# Optimizing a Trainium2 kernel written in Bass

```python
import numpy as np
import jax
import jax.numpy as jnp

def _softmax(x, axis=-1):
    return jax.nn.softmax(x, axis=axis)

def _gelu(x):
    return jax.nn.gelu(x, approximate=True)

def _silu(x):
    return jax.nn.silu(x)

def _sigmoid(x):
    return jax.nn.sigmoid(x)

def _layernorm(x, axis=-1, eps=1e-05):
    m = jnp.mean(x, axis=axis, keepdims=True)
    v = jnp.var(x, axis=axis, keepdims=True)
    return (x - m) / jnp.sqrt(v + eps)

def _scatter_add(tgt, idx, src, axis=0):
    return tgt.at[idx].add(src)

def _segment_sum(src, seg, n):
    return jax.ops.segment_sum(src, seg, n)
kernel_name = 'mk_gnn_ffn_d4_gnn_r16_f70b1a'

def setup_inputs(seed: int=0):
    np.random.seed(seed)
    _w = jnp.asarray

    def _rec_inputs():
        import jax
        import jax.numpy as jnp
        _gk = jax.random.key(seed)
        x = -0.0002117 + 1 * jax.random.normal(jax.random.fold_in(_gk, 1), (3125, 256), jnp.float32)
        _s = jax.random.randint(jax.random.fold_in(_gk, 2), (50000,), 0, 3125, jnp.int32)
        _d = jax.random.randint(jax.random.fold_in(_gk, 3), (50000,), 0, 3125, jnp.int32)
        _loop = jnp.arange(3125, dtype=jnp.int32)
        src = jnp.concatenate([_s, _d, _loop])
        dst = jnp.concatenate([_d, _s, _loop])
        _o = jnp.argsort(dst, stable=True)
        src = src[_o]
        dst = dst[_o]
        edge_attr_64 = -9.77346e-05 + 0.999888 * jax.random.normal(jax.random.fold_in(_gk, 12), (103125, 64), jnp.float32)
        edge_type_8 = jax.random.randint(jax.random.fold_in(_gk, 14), (103125,), 0, 8, jnp.int32)
        edge_weight = jax.random.uniform(jax.random.fold_in(_gk, 15), (103125,), jnp.float32, 0.0, 1)
        node_type_4 = jax.random.randint(jax.random.fold_in(_gk, 16), (3125,), 0, 4, jnp.int32)
        return (x, src, dst, edge_attr_64, edge_type_8, edge_weight, node_type_4)
    x, src, dst, edge_attr_64, edge_type_8, edge_weight, node_type_4 = _rec_inputs()

    def _L0_gnn_setup():
        import jax, jax.numpy as jnp
        import numpy as np
        N_NODES = 6250
        N_EDGES = 200000
        D_FEAT = 256
        FILTERS = 256
        key = jax.random.key(seed)
        k1, k2, k3, k4, k5 = jax.random.split(key, 5)
        x = jax.random.normal(k1, (N_NODES, D_FEAT), dtype=jnp.float32)
        edge_row = jax.random.randint(k2, (N_EDGES,), 0, N_NODES, dtype=jnp.int32)
        edge_col = jax.random.randint(k3, (N_EDGES,), 0, N_NODES, dtype=jnp.int32)
        edge_vals = jnp.ones((N_EDGES,), dtype=jnp.float32)
        w = jax.random.normal(k4, (D_FEAT, FILTERS), dtype=jnp.float32) * (2.0 / D_FEAT) ** 0.5
        b = jax.random.normal(k5, (FILTERS,), dtype=jnp.float32) * 0.05
        return {'x': x, 'edge_row': edge_row, 'edge_col': edge_col, 'edge_vals': edge_vals, 'w': w, 'b': b}
    _L0_gnn_all = _L0_gnn_setup()
    _L0_gnn_in = {k: v for k, v in _L0_gnn_all.items() if k in ('w', 'b')}
    del _L0_gnn_all

    def _L0_ffn_setup():
        import jax, jax.numpy as jnp
        import numpy as np
        B, A = (256, 8)
        IN, OUT = (256, 256)
        SH1, SH2 = (256, 128)
        EH1, EH2 = (128, 64)
        E, TOPK = (4, 2)

        def _shared_mlp(x, W1, b1, W2, b2, W3, b3):
            h = jax.nn.relu(x @ W1 + b1)
            h = jax.nn.relu(h @ W2 + b2)
            return h @ W3 + b3

        def _experts_mlp(x, eW1, eb1, eW2, eb2, eW3, eb3):
            h = jax.nn.relu(jnp.einsum('baf,efh->ebah', x, eW1) + eb1[:, None, None, :])
            h = jax.nn.relu(jnp.einsum('ebah,ehg->ebag', h, eW2) + eb2[:, None, None, :])
            o = jnp.einsum('ebag,ego->ebao', h, eW3) + eb3[:, None, None, :]
            return jnp.moveaxis(o, 0, -1)
        key = jax.random.key(seed)
        ks = jax.random.split(key, 16)
        s = 0.05
        return {'x': jax.random.normal(ks[0], (B, A, IN), jnp.float32), 'sW1': jax.random.normal(ks[1], (IN, SH1), jnp.float32) * s, 'sb1': jnp.zeros((SH1,), jnp.float32), 'sW2': jax.random.normal(ks[2], (SH1, SH2), jnp.float32) * s, 'sb2': jnp.zeros((SH2,), jnp.float32), 'sW3': jax.random.normal(ks[3], (SH2, OUT), jnp.float32) * s, 'sb3': jnp.zeros((OUT,), jnp.float32), 'eW1': jax.random.normal(ks[4], (E, IN, EH1), jnp.float32) * s, 'eb1': jnp.zeros((E, EH1), jnp.float32), 'eW2': jax.random.normal(ks[5], (E, EH1, EH2), jnp.float32) * s, 'eb2': jnp.zeros((E, EH2), jnp.float32), 'eW3': jax.random.normal(ks[6], (E, EH2, OUT), jnp.float32) * s, 'eb3': jnp.zeros((E, OUT), jnp.float32), 'gW': jax.random.normal(ks[7], (IN, E), jnp.float32) * s, 'gb': jnp.zeros((E,), jnp.float32)}
    _L0_ffn_all = _L0_ffn_setup()
    _L0_ffn_in = {k: v for k, v in _L0_ffn_all.items() if k in ('sW1', 'sb1', 'sW2', 'sb2', 'sW3', 'sb3', 'eW1', 'eb1', 'eW2', 'eb2', 'eW3', 'eb3', 'gW', 'gb')}
    del _L0_ffn_all

    def _L1_gnn_setup():
        import jax, jax.numpy as jnp
        import numpy as np
        N_NODES = 1250
        N_EDGES = 20000
        IN_DIM = 256
        OUT_DIM = 256
        N_HEADS = 4
        D_K = OUT_DIM // N_HEADS
        N_NTYPES = 4
        N_RELS = 8
        SQRT_DK = float(np.sqrt(D_K))

        def _typed_matmul(x, W, node_type):
            all_t = jnp.einsum('ni,tio->tno', x, W)
            return all_t[node_type, jnp.arange(x.shape[0])]
        key = jax.random.key(seed)
        ks = jax.random.split(key, 12)
        xav = lambda k, shape, fan: jax.random.normal(k, shape, jnp.float32) * (1.0 / np.sqrt(fan))
        return {'h': jax.random.normal(ks[0], (N_NODES, IN_DIM), jnp.float32), 'k_linears': xav(ks[1], (N_NTYPES, IN_DIM, OUT_DIM), IN_DIM), 'q_linears': xav(ks[2], (N_NTYPES, IN_DIM, OUT_DIM), IN_DIM), 'v_linears': xav(ks[3], (N_NTYPES, IN_DIM, OUT_DIM), IN_DIM), 'a_linears': xav(ks[4], (N_NTYPES, OUT_DIM, OUT_DIM), OUT_DIM), 'relation_att': xav(ks[5], (N_RELS, N_HEADS, D_K, D_K), D_K), 'relation_msg': xav(ks[6], (N_RELS, N_HEADS, D_K, D_K), D_K), 'relation_pri': jnp.ones((N_RELS, N_HEADS), jnp.float32), 'skip': jnp.ones((N_NTYPES,), jnp.float32), 'node_type': jax.random.randint(ks[7], (N_NODES,), 0, N_NTYPES), 'etype': jnp.sort(jax.random.randint(ks[8], (N_EDGES,), 0, N_RELS)), 'row_idx': jax.random.randint(ks[9], (N_EDGES,), 0, N_NODES), 'col_idx': jax.random.randint(ks[10], (N_EDGES,), 0, N_NODES)}
    _L1_gnn_all = _L1_gnn_setup()
    _L1_gnn_in = {k: v for k, v in _L1_gnn_all.items() if k in ('k_linears', 'q_linears', 'v_linears', 'a_linears', 'relation_att', 'relation_msg', 'relation_pri', 'skip')}
    del _L1_gnn_all

    def _L1_ffn_setup():
        import jax, jax.numpy as jnp
        import numpy as np
        E = 8
        K = 2
        D = 256
        H = 512
        DOUT = 256
        EPS = 1e-05
        key = jax.random.key(seed)
        ks = jax.random.split(key, 9)
        s = 0.02
        return {'x': jax.random.normal(ks[0], (4, 512, D), jnp.float32), 'gamma': 1.0 + 0.05 * jax.random.normal(ks[1], (D,), jnp.float32), 'beta': 0.05 * jax.random.normal(ks[2], (D,), jnp.float32), 'Wr': 0.01 * jax.random.normal(ks[3], (D, E), jnp.float32), 'br': jnp.zeros((E,), jnp.float32), 'W1': s * jax.random.normal(ks[4], (E, D, H), jnp.float32), 'b1': s * jax.random.normal(ks[5], (E, H), jnp.float32), 'W2': s * jax.random.normal(ks[6], (E, H, DOUT), jnp.float32), 'b2': s * jax.random.normal(ks[7], (E, DOUT), jnp.float32)}
    _L1_ffn_all = _L1_ffn_setup()
    _L1_ffn_in = {k: v for k, v in _L1_ffn_all.items() if k in ('gamma', 'beta', 'Wr', 'br', 'W1', 'b1', 'W2', 'b2')}
    del _L1_ffn_all

    def _L2_gnn_setup():
        import jax, jax.numpy as jnp
        import numpy as np
        N, E, D, H, FE = (3125, 50000, 256, 8, 64)
        HD = D // H
        key = jax.random.key(seed)
        ks = jax.random.split(key, 14)
        sD = 1.0 / np.sqrt(D)
        sF = 1.0 / np.sqrt(FE)
        return {'h': jax.random.normal(ks[0], (N, D), jnp.float32), 'efeat': jax.random.normal(ks[1], (E, FE), jnp.float32), 'src': jax.random.randint(ks[2], (E,), 0, N), 'dst': jax.random.randint(ks[3], (E,), 0, N), 'Wq': jax.random.normal(ks[4], (D, D), jnp.float32) * sD, 'Wk': jax.random.normal(ks[5], (D, D), jnp.float32) * sD, 'Wv': jax.random.normal(ks[6], (D, D), jnp.float32) * sD, 'W1': jax.random.normal(ks[7], (FE, D), jnp.float32) * sF, 'b1': jnp.zeros((D,), jnp.float32), 'W2': jax.random.normal(ks[8], (D, H), jnp.float32) * sD, 'b2': jnp.zeros((H,), jnp.float32), 'Wo': jax.random.normal(ks[9], (D, D), jnp.float32) * sD, 'bo': jnp.zeros((D,), jnp.float32)}
    _L2_gnn_all = _L2_gnn_setup()
    _L2_gnn_in = {k: v for k, v in _L2_gnn_all.items() if k in ('Wq', 'Wk', 'Wv', 'W1', 'b1', 'W2', 'b2', 'Wo', 'bo')}
    del _L2_gnn_all

    def _L2_ffn_setup():
        import jax, jax.numpy as jnp
        import numpy as np
        TOP_K = 2
        LN_EPS = 1e-05
        key = jax.random.key(seed)
        ks = jax.random.split(key, 8)
        B, S, D, E, H = (16, 1024, 256, 8, 1024)
        x = jax.random.normal(ks[0], (B, S, D), dtype=jnp.float32)
        Wr = jax.random.normal(ks[1], (D, E), dtype=jnp.float32) * 0.1
        br = jnp.zeros((E,), dtype=jnp.float32)
        ln_g = jnp.ones((E, D), dtype=jnp.float32)
        ln_b = jnp.zeros((E, D), dtype=jnp.float32)
        W1 = jax.random.normal(ks[2], (E, D, H), dtype=jnp.float32) * (1.0 / np.sqrt(D))
        b1 = jnp.zeros((E, H), dtype=jnp.float32)
        W2 = jax.random.normal(ks[3], (E, H, D), dtype=jnp.float32) * (1.0 / np.sqrt(H))
        b2 = jnp.zeros((E, D), dtype=jnp.float32)
        return {'x': x, 'Wr': Wr, 'br': br, 'ln_g': ln_g, 'ln_b': ln_b, 'W1': W1, 'b1': b1, 'W2': W2, 'b2': b2}
    _L2_ffn_all = _L2_ffn_setup()
    _L2_ffn_in = {k: v for k, v in _L2_ffn_all.items() if k in ('Wr', 'br', 'ln_g', 'ln_b', 'W1', 'b1', 'W2', 'b2')}
    del _L2_ffn_all

    def _L3_gnn_setup():
        import jax, jax.numpy as jnp
        import numpy as np
        N_NODES = 625
        N_EDGES = 20000
        DIM = 256
        key = jax.random.key(seed)
        k = jax.random.split(key, 6)
        scale = 1.0 / np.sqrt(DIM)
        x = jax.random.normal(k[0], (N_NODES, DIM), dtype=jnp.float32)
        W = jax.random.normal(k[1], (DIM, DIM), dtype=jnp.float32) * scale
        a_src = jax.random.normal(k[2], (DIM,), dtype=jnp.float32) * scale
        a_dst = jax.random.normal(k[3], (DIM,), dtype=jnp.float32) * scale
        bias = jnp.zeros((DIM,), dtype=jnp.float32)
        edge_index = jax.random.randint(k[4], (2, N_EDGES), 0, N_NODES, dtype=jnp.int64)
        return {'x': x, 'W': W, 'a_src': a_src, 'a_dst': a_dst, 'bias': bias, 'edge_index': edge_index}
    _L3_gnn_all = _L3_gnn_setup()
    _L3_gnn_in = {k: v for k, v in _L3_gnn_all.items() if k in ('W', 'a_src', 'a_dst', 'bias')}
    del _L3_gnn_all

    def _L3_ffn_setup():
        import jax, jax.numpy as jnp
        import numpy as np
        BN_EPS = 0.001

        def _bn(h, g, b, m, v):
            return g * (h - m) * jax.lax.rsqrt(v + BN_EPS) + b
        key = jax.random.key(seed)
        ks = jax.random.split(key, 8)
        B, F, Df = (256, 64, 256)
        E, H, D = (8, 256, 256)
        s1 = 1.0 / np.sqrt(Df)
        s2 = 1.0 / np.sqrt(H)
        return {'x': jax.random.normal(ks[0], (B, F, Df), jnp.float32), 'Wr': jax.random.normal(ks[1], (Df, E), jnp.float32) * s1, 'br': jnp.zeros((E,), jnp.float32), 'W1': jax.random.normal(ks[2], (E, Df, H), jnp.float32) * s1, 'b1': jnp.zeros((E, H), jnp.float32), 'g1': jnp.ones((E, H), jnp.float32), 'be1': jnp.zeros((E, H), jnp.float32), 'm1': jnp.zeros((E, H), jnp.float32), 'v1': jnp.ones((E, H), jnp.float32), 'W2': jax.random.normal(ks[3], (E, H, H), jnp.float32) * s2, 'b2': jnp.zeros((E, H), jnp.float32), 'g2': jnp.ones((E, H), jnp.float32), 'be2': jnp.zeros((E, H), jnp.float32), 'm2': jnp.zeros((E, H), jnp.float32), 'v2': jnp.ones((E, H), jnp.float32), 'Wo': jax.random.normal(ks[4], (E, H, D), jnp.float32) * s2, 'bo': jnp.zeros((E, D), jnp.float32)}
    _L3_ffn_all = _L3_ffn_setup()
    _L3_ffn_in = {k: v for k, v in _L3_ffn_all.items() if k in ('Wr', 'br', 'W1', 'b1', 'g1', 'be1', 'm1', 'v1', 'W2', 'b2', 'g2', 'be2', 'm2', 'v2', 'Wo', 'bo')}
    del _L3_ffn_all
    return {'x': x, 'src': src, 'dst': dst, 'edge_attr_64': edge_attr_64, 'edge_type_8': edge_type_8, 'edge_weight': edge_weight, 'node_type_4': node_type_4, 'L0_gnn_w': _L0_gnn_in['w'], 'L0_gnn_b': _L0_gnn_in['b'], 'L0_ffn_sW1': _L0_ffn_in['sW1'], 'L0_ffn_sb1': _L0_ffn_in['sb1'], 'L0_ffn_sW2': _L0_ffn_in['sW2'], 'L0_ffn_sb2': _L0_ffn_in['sb2'], 'L0_ffn_sW3': _L0_ffn_in['sW3'], 'L0_ffn_sb3': _L0_ffn_in['sb3'], 'L0_ffn_eW1': _L0_ffn_in['eW1'], 'L0_ffn_eb1': _L0_ffn_in['eb1'], 'L0_ffn_eW2': _L0_ffn_in['eW2'], 'L0_ffn_eb2': _L0_ffn_in['eb2'], 'L0_ffn_eW3': _L0_ffn_in['eW3'], 'L0_ffn_eb3': _L0_ffn_in['eb3'], 'L0_ffn_gW': _L0_ffn_in['gW'], 'L0_ffn_gb': _L0_ffn_in['gb'], 'L1_gnn_k_linears': _L1_gnn_in['k_linears'], 'L1_gnn_q_linears': _L1_gnn_in['q_linears'], 'L1_gnn_v_linears': _L1_gnn_in['v_linears'], 'L1_gnn_a_linears': _L1_gnn_in['a_linears'], 'L1_gnn_relation_att': _L1_gnn_in['relation_att'], 'L1_gnn_relation_msg': _L1_gnn_in['relation_msg'], 'L1_gnn_relation_pri': _L1_gnn_in['relation_pri'], 'L1_gnn_skip': _L1_gnn_in['skip'], 'L1_ffn_gamma': _L1_ffn_in['gamma'], 'L1_ffn_beta': _L1_ffn_in['beta'], 'L1_ffn_Wr': _L1_ffn_in['Wr'], 'L1_ffn_br': _L1_ffn_in['br'], 'L1_ffn_W1': _L1_ffn_in['W1'], 'L1_ffn_b1': _L1_ffn_in['b1'], 'L1_ffn_W2': _L1_ffn_in['W2'], 'L1_ffn_b2': _L1_ffn_in['b2'], 'L2_gnn_Wq': _L2_gnn_in['Wq'], 'L2_gnn_Wk': _L2_gnn_in['Wk'], 'L2_gnn_Wv': _L2_gnn_in['Wv'], 'L2_gnn_W1': _L2_gnn_in['W1'], 'L2_gnn_b1': _L2_gnn_in['b1'], 'L2_gnn_W2': _L2_gnn_in['W2'], 'L2_gnn_b2': _L2_gnn_in['b2'], 'L2_gnn_Wo': _L2_gnn_in['Wo'], 'L2_gnn_bo': _L2_gnn_in['bo'], 'L2_ffn_Wr': _L2_ffn_in['Wr'], 'L2_ffn_br': _L2_ffn_in['br'], 'L2_ffn_ln_g': _L2_ffn_in['ln_g'], 'L2_ffn_ln_b': _L2_ffn_in['ln_b'], 'L2_ffn_W1': _L2_ffn_in['W1'], 'L2_ffn_b1': _L2_ffn_in['b1'], 'L2_ffn_W2': _L2_ffn_in['W2'], 'L2_ffn_b2': _L2_ffn_in['b2'], 'L3_gnn_W': _L3_gnn_in['W'], 'L3_gnn_a_src': _L3_gnn_in['a_src'], 'L3_gnn_a_dst': _L3_gnn_in['a_dst'], 'L3_gnn_bias': _L3_gnn_in['bias'], 'L3_ffn_Wr': _L3_ffn_in['Wr'], 'L3_ffn_br': _L3_ffn_in['br'], 'L3_ffn_W1': _L3_ffn_in['W1'], 'L3_ffn_b1': _L3_ffn_in['b1'], 'L3_ffn_g1': _L3_ffn_in['g1'], 'L3_ffn_be1': _L3_ffn_in['be1'], 'L3_ffn_m1': _L3_ffn_in['m1'], 'L3_ffn_v1': _L3_ffn_in['v1'], 'L3_ffn_W2': _L3_ffn_in['W2'], 'L3_ffn_b2': _L3_ffn_in['b2'], 'L3_ffn_g2': _L3_ffn_in['g2'], 'L3_ffn_be2': _L3_ffn_in['be2'], 'L3_ffn_m2': _L3_ffn_in['m2'], 'L3_ffn_v2': _L3_ffn_in['v2'], 'L3_ffn_Wo': _L3_ffn_in['Wo'], 'L3_ffn_bo': _L3_ffn_in['bo']}

def reference(x, src, dst, edge_attr_64, edge_type_8, edge_weight, node_type_4, L0_gnn_w, L0_gnn_b, L0_ffn_sW1, L0_ffn_sb1, L0_ffn_sW2, L0_ffn_sb2, L0_ffn_sW3, L0_ffn_sb3, L0_ffn_eW1, L0_ffn_eb1, L0_ffn_eW2, L0_ffn_eb2, L0_ffn_eW3, L0_ffn_eb3, L0_ffn_gW, L0_ffn_gb, L1_gnn_k_linears, L1_gnn_q_linears, L1_gnn_v_linears, L1_gnn_a_linears, L1_gnn_relation_att, L1_gnn_relation_msg, L1_gnn_relation_pri, L1_gnn_skip, L1_ffn_gamma, L1_ffn_beta, L1_ffn_Wr, L1_ffn_br, L1_ffn_W1, L1_ffn_b1, L1_ffn_W2, L1_ffn_b2, L2_gnn_Wq, L2_gnn_Wk, L2_gnn_Wv, L2_gnn_W1, L2_gnn_b1, L2_gnn_W2, L2_gnn_b2, L2_gnn_Wo, L2_gnn_bo, L2_ffn_Wr, L2_ffn_br, L2_ffn_ln_g, L2_ffn_ln_b, L2_ffn_W1, L2_ffn_b1, L2_ffn_W2, L2_ffn_b2, L3_gnn_W, L3_gnn_a_src, L3_gnn_a_dst, L3_gnn_bias, L3_ffn_Wr, L3_ffn_br, L3_ffn_W1, L3_ffn_b1, L3_ffn_g1, L3_ffn_be1, L3_ffn_m1, L3_ffn_v1, L3_ffn_W2, L3_ffn_b2, L3_ffn_g2, L3_ffn_be2, L3_ffn_m2, L3_ffn_v2, L3_ffn_Wo, L3_ffn_bo):
    import jax
    import jax.numpy as jnp

    def _L0_gnn_ref(x, edge_row, edge_col, edge_vals, w, b):
        import jax, jax.numpy as jnp
        import numpy as np
        N_NODES = 6250
        N_EDGES = 200000
        D_FEAT = 256
        FILTERS = 256
        n = x.shape[0]
        deg = jax.ops.segment_sum(edge_vals, edge_row, num_segments=n)
        dinv = jnp.where(deg > 0, deg ** (-0.5), 0.0)
        norm_vals = edge_vals * dinv[edge_row] * dinv[edge_col]
        h = x @ w
        msg = norm_vals[:, None] * h[edge_col]
        agg = jax.ops.segment_sum(msg, edge_row, num_segments=n)
        return jax.nn.relu(agg + b)

    def _L0_ffn_ref(x, sW1, sb1, sW2, sb2, sW3, sb3, eW1, eb1, eW2, eb2, eW3, eb3, gW, gb):
        import jax, jax.numpy as jnp
        import numpy as np
        B, A = (256, 8)
        IN, OUT = (256, 256)
        SH1, SH2 = (256, 128)
        EH1, EH2 = (128, 64)
        E, TOPK = (4, 2)

        def _shared_mlp(x, W1, b1, W2, b2, W3, b3):
            h = jax.nn.relu(x @ W1 + b1)
            h = jax.nn.relu(h @ W2 + b2)
            return h @ W3 + b3

        def _experts_mlp(x, eW1, eb1, eW2, eb2, eW3, eb3):
            h = jax.nn.relu(jnp.einsum('baf,efh->ebah', x, eW1) + eb1[:, None, None, :])
            h = jax.nn.relu(jnp.einsum('ebah,ehg->ebag', h, eW2) + eb2[:, None, None, :])
            o = jnp.einsum('ebag,ego->ebao', h, eW3) + eb3[:, None, None, :]
            return jnp.moveaxis(o, 0, -1)
        all_out = _experts_mlp(x, eW1, eb1, eW2, eb2, eW3, eb3)
        shared = _shared_mlp(x, sW1, sb1, sW2, sb2, sW3, sb3)
        gates = jax.nn.softmax(x @ gW + gb, axis=-1)
        topv, topi = jax.lax.top_k(gates, TOPK)
        topw = jax.nn.softmax(topv, axis=-1)
        sel = jnp.take_along_axis(all_out, topi[:, :, None, :], axis=-1)
        gated = jnp.sum(sel * topw[:, :, None, :], axis=-1)
        return shared + gated

    def _L1_gnn_ref(h, k_linears, q_linears, v_linears, a_linears, relation_att, relation_msg, relation_pri, skip, node_type, etype, row_idx, col_idx):
        import jax, jax.numpy as jnp
        import numpy as np
        N_NODES = 1250
        N_EDGES = 20000
        IN_DIM = 256
        OUT_DIM = 256
        N_HEADS = 4
        D_K = OUT_DIM // N_HEADS
        N_NTYPES = 4
        N_RELS = 8
        SQRT_DK = float(np.sqrt(D_K))

        def _typed_matmul(x, W, node_type):
            all_t = jnp.einsum('ni,tio->tno', x, W)
            return all_t[node_type, jnp.arange(x.shape[0])]
        n = h.shape[0]
        k = _typed_matmul(h, k_linears, node_type).reshape(n, N_HEADS, D_K)
        q = _typed_matmul(h, q_linears, node_type).reshape(n, N_HEADS, D_K)
        v = _typed_matmul(h, v_linears, node_type).reshape(n, N_HEADS, D_K)
        q_att = jnp.einsum('nhd,rhde->rnhe', q, relation_att)
        v_msg = jnp.einsum('nhd,rhde->rnhe', v, relation_msg)
        aw_q_edge = q_att[etype, col_idx]
        msg_edge = v_msg[etype, row_idx]
        attn_score = jnp.sum(aw_q_edge * k[row_idx], axis=-1)
        score = attn_score * (relation_pri[etype] / SQRT_DK)
        m = jax.ops.segment_max(score, col_idx, num_segments=n)
        ex = jnp.exp(score - m[col_idx])
        denom = jax.ops.segment_sum(ex, col_idx, num_segments=n)
        alpha = ex / denom[col_idx]
        agg = jax.ops.segment_sum(alpha[..., None] * msg_edge, col_idx, num_segments=n)
        agg = agg.reshape(n, OUT_DIM)
        out = _typed_matmul(agg, a_linears, node_type)
        out = jax.nn.sigmoid(skip)[node_type][:, None] * out
        return out

    def _L1_ffn_ref(x, gamma, beta, Wr, br, W1, b1, W2, b2):
        import jax, jax.numpy as jnp
        import numpy as np
        E = 8
        K = 2
        D = 256
        H = 512
        DOUT = 256
        EPS = 1e-05
        mu = jnp.mean(x, axis=-1, keepdims=True)
        var = jnp.mean(jnp.square(x - mu), axis=-1, keepdims=True)
        xn = (x - mu) * jax.lax.rsqrt(var + EPS) * gamma + beta
        logits = jnp.einsum('bsd,de->bse', xn, Wr) + br
        top_vals, top_idx = jax.lax.top_k(logits, K)
        w = jax.nn.softmax(top_vals, axis=-1)
        w_full = jnp.einsum('bsk,bske->bse', w, jax.nn.one_hot(top_idx, E, dtype=w.dtype))
        y = jnp.zeros(x.shape[:-1] + (DOUT,), x.dtype)
        for e in range(E):
            h = jax.nn.gelu(jnp.einsum('bsd,dh->bsh', xn, W1[e]) + b1[e], approximate=False)
            y_e = jnp.einsum('bsh,hd->bsd', h, W2[e]) + b2[e]
            y = y + y_e * w_full[..., e, None]
        return y

    def _L2_gnn_ref(h, efeat, src, dst, Wq, Wk, Wv, W1, b1, W2, b2, Wo, bo):
        import jax, jax.numpy as jnp
        import numpy as np
        N, E, D, H, FE = (3125, 50000, 256, 8, 64)
        HD = D // H
        n = h.shape[0]
        Q = (h @ Wq).reshape(n, H, HD)
        K = (h @ Wk).reshape(n, H, HD)
        V = (h @ Wv).reshape(n, H, HD)
        score = jnp.einsum('ehd,ehd->eh', Q[dst], K[src]) / np.sqrt(HD)
        score = score + jax.nn.relu(efeat @ W1 + b1) @ W2 + b2
        m = jax.ops.segment_max(score, dst, num_segments=n)
        ex = jnp.exp(score - m[dst])
        denom = jax.ops.segment_sum(ex, dst, num_segments=n)
        alpha = ex / denom[dst]
        out = jax.ops.segment_sum(alpha[:, :, None] * V[src], dst, num_segments=n)
        out = out.reshape(n, D)
        return out @ Wo + bo

    def _L2_ffn_ref(x, Wr, br, ln_g, ln_b, W1, b1, W2, b2):
        import jax, jax.numpy as jnp
        import numpy as np
        TOP_K = 2
        LN_EPS = 1e-05
        B, S, D = x.shape
        N = B * S
        xt = x.reshape(N, D)
        logits = xt @ Wr + br
        probs = jax.nn.softmax(logits, axis=-1)
        top_p, top_idx = jax.lax.top_k(probs, TOP_K)
        weights = top_p / top_p.sum(axis=-1, keepdims=True)
        mu = xt.mean(axis=-1, keepdims=True)
        var = ((xt - mu) ** 2).mean(axis=-1, keepdims=True)
        xn = (xt - mu) * jax.lax.rsqrt(var + LN_EPS)
        xe = xn[None, :, :] * ln_g[:, None, :] + ln_b[:, None, :]
        h = jax.nn.gelu(jnp.einsum('end,edh->enh', xe, W1) + b1[:, None, :], approximate=False)
        y = jnp.einsum('enh,ehd->end', h, W2) + b2[:, None, :]
        y_tok = jnp.transpose(y, (1, 0, 2))
        sel = jnp.take_along_axis(y_tok, top_idx[:, :, None], axis=1)
        out = (weights[:, :, None] * sel).sum(axis=1)
        return out.reshape(B, S, D)

    def _L3_gnn_ref(x, W, a_src, a_dst, bias, edge_index):
        import jax, jax.numpy as jnp
        import numpy as np
        N_NODES = 625
        N_EDGES = 20000
        DIM = 256
        N, D = x.shape
        loop = jnp.arange(N, dtype=edge_index.dtype)
        src = jnp.concatenate([edge_index[0], loop])
        dst = jnp.concatenate([edge_index[1], loop])
        h = x @ W.T
        alpha_s = h @ a_src
        alpha_d = h @ a_dst
        e = jax.nn.leaky_relu(alpha_s[src] + alpha_d[dst], negative_slope=0.2)
        m = jax.ops.segment_max(e, dst, num_segments=N)
        p = jnp.exp(e - m[dst])
        s = jax.ops.segment_sum(p, dst, num_segments=N)
        alpha = p / s[dst]
        out = jax.ops.segment_sum(h[src] * alpha[:, None], dst, num_segments=N)
        out = out + bias
        out = jax.nn.relu(out)
        return x + out

    def _L3_ffn_ref(x, Wr, br, W1, b1, g1, be1, m1, v1, W2, b2, g2, be2, m2, v2, Wo, bo):
        import jax, jax.numpy as jnp
        import numpy as np
        BN_EPS = 0.001

        def _bn(h, g, b, m, v):
            return g * (h - m) * jax.lax.rsqrt(v + BN_EPS) + b
        feat = jnp.mean(x, axis=0)
        w = jax.nn.softmax(feat @ Wr + br, axis=-1)
        h = jnp.einsum('bfd,edh->bfeh', x, W1) + b1
        h = jax.nn.relu(_bn(h, g1, be1, m1, v1))
        h = jnp.einsum('bfeh,ehk->bfek', h, W2) + b2
        h = jax.nn.relu(_bn(h, g2, be2, m2, v2))
        y = jnp.einsum('bfeh,ehd->bfed', h, Wo) + bo
        return jnp.einsum('bfed,fe->bfd', y, w)
    edge_index = jnp.stack([src, dst])
    x = x + _L0_gnn_ref(_layernorm(x, axis=-1), src, dst, edge_weight, L0_gnn_w, L0_gnn_b)
    x = x + _L0_ffn_ref(_layernorm(x, axis=-1)[None], L0_ffn_sW1, L0_ffn_sb1, L0_ffn_sW2, L0_ffn_sb2, L0_ffn_sW3, L0_ffn_sb3, L0_ffn_eW1, L0_ffn_eb1, L0_ffn_eW2, L0_ffn_eb2, L0_ffn_eW3, L0_ffn_eb3, L0_ffn_gW, L0_ffn_gb)[0]
    x = x + _L1_gnn_ref(_layernorm(x, axis=-1), L1_gnn_k_linears, L1_gnn_q_linears, L1_gnn_v_linears, L1_gnn_a_linears, L1_gnn_relation_att, L1_gnn_relation_msg, L1_gnn_relation_pri, L1_gnn_skip, node_type_4, edge_type_8, src, dst)
    x = x + _L1_ffn_ref(_layernorm(x, axis=-1)[None], L1_ffn_gamma, L1_ffn_beta, L1_ffn_Wr, L1_ffn_br, L1_ffn_W1, L1_ffn_b1, L1_ffn_W2, L1_ffn_b2)[0]
    x = x + _L2_gnn_ref(_layernorm(x, axis=-1), edge_attr_64, src, dst, L2_gnn_Wq, L2_gnn_Wk, L2_gnn_Wv, L2_gnn_W1, L2_gnn_b1, L2_gnn_W2, L2_gnn_b2, L2_gnn_Wo, L2_gnn_bo)
    x = x + _L2_ffn_ref(_layernorm(x, axis=-1)[None], L2_ffn_Wr, L2_ffn_br, L2_ffn_ln_g, L2_ffn_ln_b, L2_ffn_W1, L2_ffn_b1, L2_ffn_W2, L2_ffn_b2)[0]
    x = x + _L3_gnn_ref(_layernorm(x, axis=-1), L3_gnn_W, L3_gnn_a_src, L3_gnn_a_dst, L3_gnn_bias, edge_index)
    x = x + _L3_ffn_ref(_layernorm(x, axis=-1)[None], L3_ffn_Wr, L3_ffn_br, L3_ffn_W1, L3_ffn_b1, L3_ffn_g1, L3_ffn_be1, L3_ffn_m1, L3_ffn_v1, L3_ffn_W2, L3_ffn_b2, L3_ffn_g2, L3_ffn_be2, L3_ffn_m2, L3_ffn_v2, L3_ffn_Wo, L3_ffn_bo)[0]
    return x

_drawn_inputs = setup_inputs


def setup_inputs(seed=0):
    import zlib

    import numpy as np

    out = dict(_drawn_inputs(seed))
    spreads = {'L0_ffn_sb1': (0.0, 0.1),
     'L0_ffn_sb2': (0.0, 0.1),
     'L0_ffn_sb3': (0.0, 0.1),
     'L0_ffn_eb1': (0.0, 0.292),
     'L0_ffn_eb2': (0.0, 0.1),
     'L0_ffn_eb3': (0.0, 0.1),
     'L0_ffn_gb': (0.0, 0.1),
     'L1_gnn_relation_pri': (1.0, 0.2),
     'L1_gnn_skip': (1.0, 0.2),
     'L1_ffn_br': (0.0, 0.1),
     'L2_gnn_b1': (0.0, 0.1),
     'L2_gnn_b2': (0.0, 0.8),
     'L2_gnn_bo': (0.0, 0.1),
     'L2_ffn_br': (0.0, 0.1),
     'L2_ffn_ln_g': (1.0, 0.2),
     'L2_ffn_ln_b': (0.0, 0.1),
     'L2_ffn_b1': (0.0, 0.1),
     'L2_ffn_b2': (0.0, 0.1),
     'L3_gnn_bias': (0.0, 0.276),
     'L3_ffn_br': (0.0, 0.8),
     'L3_ffn_b1': (0.0, 0.737),
     'L3_ffn_g1': (1.0, 0.6),
     'L3_ffn_be1': (0.0, 0.777),
     'L3_ffn_m1': (0.0, 0.723),
     'L3_ffn_v1': (1.0, 0.6),
     'L3_ffn_b2': (0.0, 0.529),
     'L3_ffn_g2': (1.0, 0.6),
     'L3_ffn_be2': (0.0, 0.55),
     'L3_ffn_m2': (0.0, 0.511),
     'L3_ffn_v2': (1.0, 0.6),
     'L3_ffn_bo': (0.0, 0.384)}
    factors = {'L1_ffn_b1': 4.012, 'L3_gnn_a_dst': 3.874}
    for name, (base, spread) in spreads.items():
        noise = np.random.default_rng([zlib.crc32(name.encode()), seed]).standard_normal(out[name].shape)
        drawn = base * np.exp(spread * noise) if base else spread * noise
        out[name] = jnp.asarray(drawn.astype(out[name].dtype))
    for name, factor in factors.items():
        out[name] = (out[name] * factor).astype(out[name].dtype)
    return out
```

```python
from contextlib import ExitStack

import numpy as np

import concourse.bass as bass
from concourse import mybir

F32 = mybir.dt.float32
I32 = mybir.dt.int32
ACT = mybir.ActivationFunctionType
ALU = mybir.AluOpType
AX = mybir.AxisListType

P = 128
NODES, EDGES, D = 3125, 103125, 256
KK = D // P
TILES = -(-NODES // P)
NPAD = TILES * P
NWIN = NPAD + P
CHUNKS = -(-EDGES // P)
EPAD = CHUNKS * P
BATCH = 13
BATCHES = CHUNKS // BATCH
PAIRS = [(j, min(2, BATCH - j)) for j in range(0, BATCH, 2)]
UNROLL = 5
GROUP = UNROLL * P
HALF = GROUP // 2
BIG = 1.0e38
NO_NODE = 8191


class Kernel:

    def __init__(self, nc, a):
        self.nc, self.a = nc, a
        self.uid = 0

    def phase(self):
        return Phase(self)


class Phase:

    def __init__(self, k):
        self.k, self.nc, self.stack, self.sems = k, k.nc, ExitStack(), []

    def __enter__(self):
        return self

    def __exit__(self, *exc):
        self.stack.close()
        if exc[0] is None:
            self.nc.clear_and_free_semaphores(self.sems)
            self.nc.all_engine_barrier()

    def _name(self, name):
        self.k.uid += 1
        return f"{name}_{self.k.uid}"

    def sb(self, name, shape, dt=F32):
        return self.stack.enter_context(self.nc.sbuf_tensor(self._name(name), shape, dt))

    def ps(self, name, shape, dt=F32):
        return self.stack.enter_context(self.nc.psum_tensor(self._name(name), shape, dt))

    def sem(self, name):
        s = self.nc.alloc_semaphore(self._name(name))
        self.sems.append(s)
        return s


class Chain:

    def __init__(self, eng, sem):
        self.eng, self.sem, self.n, self.base = eng, sem, 0, 0

    def __call__(self, ins):
        self.n += 1
        ins.then_inc(self.sem, 1)
        self.eng.wait_ge(self.sem, self.base + self.n)


def hot_by(eng, k, out, values, width):
    shape = [P, BATCH, width]
    return eng.tensor_tensor(out, k.lane_iota[:, 0:width].unsqueeze(1).to_broadcast(shape),
                             values.unsqueeze(2).to_broadcast(shape), ALU.is_equal)


def row_table(k, lanes, row):
    blocks = [(c, min(P, CHUNKS - c)) for c in range(0, CHUNKS, P)]
    with k.phase() as ph:
        turned = [ph.ps(f"turned{q}", [P, P]) for q in range(len(blocks))]
        kept = ph.sb("kept", [P, len(blocks), P])
        full, copied, stored = ph.sem("full"), ph.sem("copied"), ph.sem("stored")
        with k.nc.Block() as block:

            @block.tensor
            def _(pe):
                for q, (c, n) in enumerate(blocks):
                    pe.transpose(turned[q][0:n, :], lanes[:, c:c + n], k.ident[:, :]).then_inc(full, 1)

            @block.scalar
            def _(act):
                for q, (c, n) in enumerate(blocks):
                    act.wait_ge(full, q + 1)
                    act.activation(kept[0:n, q, :], turned[q][0:n, :], ACT.Copy).then_inc(copied, 1)

            @block.sync
            def _(sp):
                for q, (c, n) in enumerate(blocks):
                    sp.wait_ge(copied, q + 1)
                    sp.dma_start(row[:, c * P:(c + n) * P].rearrange("o (c e) -> (o c) e", e=P), kept[0:n, q, :]
                                 ).then_inc(stored, 16)
                sp.wait_ge(stored, 16 * len(blocks))


def setup(k):
    nc, a = k.nc, k.a
    k.x = nc.alloc_sbuf_tensor("x_res", [P, TILES, D], F32)
    k.ident = nc.alloc_sbuf_tensor("ident", [P, P], F32)
    k.lane_iota = nc.alloc_sbuf_tensor("lane_iota", [P, P], F32)
    k.lane_col = nc.alloc_sbuf_tensor("lane_col", [P, 1], F32)
    k.rel_row = nc.dram_tensor("rel_row", [1, EPAD], F32, kind="Internal").ap()
    k.lane_row = nc.dram_tensor("src_lane_row", [1, EPAD], F32, kind="Internal").ap()
    k.src_tile = nc.alloc_sbuf_tensor("src_tile", [P, CHUNKS], F32)
    k.src = nc.alloc_sbuf_tensor("src_idx", [P, CHUNKS], I32)
    k.dst = nc.alloc_sbuf_tensor("dst_idx", [P, CHUNKS], I32)
    k.rel = nc.alloc_sbuf_tensor("rel_pos", [P, CHUNKS], F32)
    k.dinv = nc.alloc_sbuf_tensor("dinv", [P, TILES], F32)
    k.weight = nc.alloc_sbuf_tensor("edge_w", [P, CHUNKS], F32)
    with k.phase() as outer:
        lane_of = outer.sb("lane_of", [P, CHUNKS])
        edge_tables(k, lane_of)
        row_table(k, k.rel, k.rel_row)
        row_table(k, lane_of, k.lane_row)


def edge_tables(k, lane_of):
    nc, a = k.nc, k.a
    with k.phase() as ph:
        loaded, made, chained = ph.sem("loaded"), ph.sem("made"), ph.sem("chained")
        based, hot, summed = ph.sem("based"), ph.sem("hot"), ph.sem("summed")
        hot_free, tiled = ph.sem("hot_free"), ph.sem("tiled")
        dstf, basef = ph.sb("dstf", [P, CHUNKS]), ph.sb("basef", [1, CHUNKS])
        tile_of, low_of = k.src_tile, ph.sb("low_of", [P, CHUNKS])
        ints = ph.sb("ints", [P, CHUNKS], I32)
        ones = ph.sb("ones", [1, P])
        hot_lane = ph.sb("hot_lane", [P, 2, BATCH, P])
        hot_tile = ph.sb("hot_tile", [P, 2, BATCH, TILES])
        degree = ph.ps("degree", [P, 512])
        bases = ph.ps("bases", [P, 2, 512])
        deg = ph.sb("deg", [P, TILES])
        has = ph.sb("has", [P, TILES])
        HC = CHUNKS // 2
        with nc.Block() as block:

            @block.sync
            def _(sp):
                sp.dma_start(k.dst[:, :], a["dst_lanes"]).then_inc(loaded, 16)
                sp.dma_start(k.weight[:, :], a["weight_lanes"]).then_inc(loaded, 16)
                sp.dma_start(k.src[:, :], a["src_lanes"]).then_inc(loaded, 16)
                sp.dma_start(k.x[:, :, :], a["x_lanes"]).then_inc(loaded, 16)
                sp.wait_ge(loaded, 64)

            @block.gpsimd
            def _(pool):
                pool.memset(ones[:, :], 1.0).then_inc(made, 1)
                pool.memset(k.ident[:, :], 0.0).then_inc(made, 1)
                pool.iota(k.lane_iota[:, :], [[1, P]], base=0, channel_multiplier=0,
                          allow_small_or_imprecise_dtypes=True).then_inc(made, 1)
                pool.iota(k.lane_col[:, :], [[0, 1]], base=0, channel_multiplier=1,
                          allow_small_or_imprecise_dtypes=True).then_inc(made, 1)
                pool.wait_ge(made, 4)
                pool.affine_select(out=k.ident[:, :], in_=k.ident[:, :], compare_op=ALU.not_equal, fill=1.0,
                                   base=0, pattern=[[-1, P]], channel_multiplier=1).then_inc(made, 1)

            @block.vector
            def _(dve):
                step = Chain(dve, chained)
                dve.wait_ge(loaded, 64)
                dve.wait_ge(made, 4)
                step(dve.tensor_copy(dstf[:, :], k.dst[:, :]))
                dve.tensor_copy(basef[0:1, :], dstf[0:1, :]).then_inc(based, 1)
                step(dve.tensor_scalar(ints[:, :], k.src[:, :], 7, None, ALU.logical_shift_right))
                step(dve.tensor_copy(tile_of[:, :], ints[:, :]))
                step(dve.tensor_copy(low_of[:, :], k.src[:, :]))
                step(dve.scalar_tensor_tensor(lane_of[:, :], tile_of[:, :], -float(P), low_of[:, :], ALU.mult, ALU.add))
                with dve.Fori(0, BATCHES // 2) as i:
                    for u in range(2):
                        b = i * 2 + u
                        c = i * (2 * BATCH) + u * BATCH
                        dve.wait_ge(hot_free, b + 1)
                        hot_by(dve, k, hot_lane[:, u, :, :], lane_of[:, bass.ds(c, BATCH)], P)
                        hot_by(dve, k, hot_tile[:, u, :, :], tile_of[:, bass.ds(c, BATCH)], TILES).then_inc(tiled, 1)
                        dve.wait_ge(tiled, b + 1)
                        w = k.weight[:, bass.ds(c, BATCH)].unsqueeze(2).to_broadcast([P, BATCH, TILES])
                        dve.tensor_tensor(hot_tile[:, u, :, :], hot_tile[:, u, :, :], w, ALU.mult).then_inc(hot, 1)
                dve.wait_ge(summed, 1)
                for h in range(2):
                    step(dve.tensor_tensor(k.rel[:, h * HC:(h + 1) * HC], dstf[:, h * HC:(h + 1) * HC],
                                           bases[:, h, 0:HC], ALU.subtract))
                dve.wait_ge(summed, 2)
                step(dve.tensor_copy(deg[:, :], degree[:, 0:TILES]))
                step(dve.tensor_scalar(has[:, :], deg[:, :], 0.0, None, ALU.is_gt))
                step(dve.tensor_scalar(low_of[:, 0:TILES], has[:, :], -1.0, 1.0, ALU.mult, ALU.add))
                step(dve.tensor_tensor(deg[:, :], deg[:, :], low_of[:, 0:TILES], ALU.add))
                step(dve.reciprocal(deg[:, :], deg[:, :]))
                dve.wait_ge(made, 5)
                dve.tensor_copy(deg[:, :], deg[:, :]).then_inc(made, 1)
                dve.wait_ge(made, 7)
                step(dve.tensor_tensor(k.dinv[:, :], k.dinv[:, :], has[:, :], ALU.mult))

            @block.scalar
            def _(act):
                act.wait_ge(made, 6)
                act.activation(k.dinv[:, :], deg[:, :], ACT.Sqrt).then_inc(made, 1)

            @block.tensor
            def _(pe):
                pe.sem_inc(hot_free, 2)
                pe.wait_ge(based, 1)
                for h in range(2):
                    ins = pe.matmul(bases[:, h, 0:HC], ones[0:1, :], basef[0:1, h * HC:(h + 1) * HC],
                                    start=True, stop=True)
                ins.then_inc(summed, 1)

                def add(u, first, last):
                    for j in range(BATCH):
                        ins = pe.matmul(degree[:, 0:TILES], hot_lane[:, u, j, :], hot_tile[:, u, j, :],
                                        start=first and j == 0, stop=last and j == BATCH - 1)
                    return ins

                for n in range(2):
                    pe.wait_ge(hot, n + 1)
                    add(n % 2, n == 0, False).then_inc(hot_free, 1)
                with pe.Fori(1, BATCHES // 2 - 1) as i:
                    for u in range(2):
                        pe.wait_ge(hot, i * 2 + (u + 1))
                        add(u, False, False).then_inc(hot_free, 1)
                for n in range(BATCHES - 2, BATCHES):
                    pe.wait_ge(hot, n + 1)
                    ins = add(n % 2, False, n == BATCHES - 1)
                ins.then_inc(summed, 1)



def normalize(k, src, out, eps=1e-5, gamma=None, beta=None):
    nc = k.nc
    with k.phase() as ph:
        stats = ph.sb("stats", [P, TILES, 6])
        mv = ph.sb("mv", [P, TILES, 2])
        std = ph.sb("std", [P, TILES])
        counted, aggregated, rooted, done = (ph.sem(n) for n in ("counted", "aggregated", "rooted", "done"))
        loaded = ph.sem("affine_loaded")
        if gamma is not None:
            gb = ph.sb("gamma_beta", [P, 2, D])
        with nc.Block() as block:
            if gamma is not None:
                @block.sync
                def _(sp):
                    sp.dma_start(gb[:, 0, :], gamma.to_broadcast([P, D])).then_inc(loaded, 16)
                    sp.dma_start(gb[:, 1, :], beta.to_broadcast([P, D])).then_inc(loaded, 16)

            @block.vector
            def _(dve):
                with dve.Fori(0, TILES) as t:
                    dve.bn_stats(stats[:, bass.ds(t, 1), :], src[:, bass.ds(t, 1), :]).then_inc(counted, 1)
                for t in range(TILES):
                    dve.wait_ge(counted, t + 1)
                    ins = dve.bn_aggr(mv[:, t, :], stats[:, t, :])
                ins.then_inc(aggregated, 1)
                dve.wait_ge(aggregated, 1)
                dve.tensor_scalar(std[:, :], mv[:, :, 1], eps, None, ALU.add).then_inc(rooted, 1)
                dve.wait_ge(rooted, 2)
                dve.reciprocal(std[:, :], std[:, :]).then_inc(rooted, 1)
                dve.wait_ge(rooted, 3)
                with dve.Fori(0, TILES) as t:
                    o = out[:, bass.ds(t, 1), :]
                    dve.tensor_scalar(o, src[:, bass.ds(t, 1), :], mv[:, bass.ds(t, 1), 0], std[:, bass.ds(t, 1)],
                                      ALU.subtract, ALU.mult).then_inc(done, 1)
                if gamma is not None:
                    dve.wait_ge(loaded, 32)
                    dve.wait_ge(done, TILES)
                    g = gb[:, 0, :].unsqueeze(1).to_broadcast([P, TILES, D])
                    b = gb[:, 1, :].unsqueeze(1).to_broadcast([P, TILES, D])
                    dve.tensor_tensor(out[:, :, :], out[:, :, :], g, ALU.mult).then_inc(done, 1)
                    dve.wait_ge(done, TILES + 1)
                    dve.tensor_tensor(out[:, :, :], out[:, :, :], b, ALU.add).then_inc(done, 1)

            @block.scalar
            def _(act):
                act.wait_ge(rooted, 1)
                act.activation(std[:, :], std[:, :], ACT.Sqrt).then_inc(rooted, 1)



def node_tiles(k, ph, src, width, load, rhs, evacuate, store=None, stores=0, xT=None, links=0):
    nc = k.nc
    ring = ph.sb("tile_ring", [P, UNROLL, D])
    ringT = ph.sb("tileT_ring", [P, UNROLL, KK, P])
    stage = ph.sb("stage", [P, UNROLL, width]) if store else None
    banks = -(-width // 512)
    turned = [ph.ps(f"turned{i}", [P, 512]) for i in range(2)]
    products = [ph.ps(f"product{i}", [P, banks, 512]) for i in range(3)]
    weights_in, ring_full, turned_full = ph.sem("weights_in"), ph.sem("ring_full"), ph.sem("turned_full")
    ringT_full, multiplied, kept = ph.sem("ringT_full"), ph.sem("multiplied"), ph.sem("kept")
    product_out, chained = ph.sem("product_out"), ph.sem("chained")
    stored = [ph.sem(f"stored{u}") for u in range(UNROLL)]
    bodies = TILES // UNROLL
    weights_count = []
    with nc.Block() as block:

        @block.sync
        def _(sp):
            weights_count.append(load(sp, weights_in))
            if store:
                with sp.Fori(0, bodies) as i:
                    for u in range(UNROLL):
                        t = i * UNROLL + u
                        sp.wait_ge(product_out, t + 2)
                        store(sp, t, stage[:, u, :], stored[u])
                for u in range(UNROLL):
                    sp.wait_ge(stored[u], 16 * stores * bodies)

        @block.scalar
        def _(act):
            with act.Fori(0, bodies) as i:
                for u in range(UNROLL):
                    act.activation(ring[:, u, :], src[:, bass.ds(i * UNROLL + u, 1), :], ACT.Copy
                                   ).then_inc(ring_full, 1)
                for u in range(UNROLL):
                    t = i * UNROLL + u
                    act.wait_ge(turned_full, t + 1)
                    act.wait_ge(multiplied, i * UNROLL)
                    if xT is not None:
                        act.wait_ge(kept, i * UNROLL)
                    act.activation(ringT[:, u, :, :], turned[u % 2][:, 0:D], ACT.Copy).then_inc(ringT_full, 1)

        if xT is not None:
            @block.gpsimd
            def _(pool):
                with pool.Fori(0, bodies) as i:
                    for u in range(UNROLL):
                        t = i * UNROLL + u
                        pool.wait_ge(ringT_full, t + 1)
                        pool.tensor_copy(xT[:, :, bass.ds(t * P, P)], ringT[:, u, :, :]).then_inc(kept, 1)

        @block.tensor
        def _(pe):
            pe.wait_ge(weights_in, weights_count[0])
            with pe.Fori(0, bodies) as i:
                for u in range(UNROLL):
                    t = i * UNROLL + u
                    pe.wait_ge(ring_full, t + 1)
                    pe.wait_ge(ringT_full, t)
                    for kk in range(KK):
                        ins = pe.transpose(turned[u % 2][:, kk * P:(kk + 1) * P],
                                           ring[:, u, kk * P:(kk + 1) * P], k.ident[:, :])
                    ins.then_inc(turned_full, 1)
                for u in range(UNROLL):
                    t = i * UNROLL + u
                    pe.wait_ge(ringT_full, t + 1)
                    pe.wait_ge(product_out, t)
                    for b in range(banks):
                        n = min(512, width - b * 512)
                        for kk in range(KK):
                            ins = pe.matmul(products[u % 3][:, b, 0:n], ringT[:, u, kk, :],
                                            rhs[:, kk, b * 512:b * 512 + n], start=kk == 0, stop=kk == KK - 1)
                    ins.then_inc(multiplied, 1)

        @block.vector
        def _(dve):
            dve.sem_inc(product_out, 1)
            step = Chain(dve, chained)
            with dve.Fori(0, bodies) as i:
                for u in range(UNROLL):
                    t = i * UNROLL + u
                    dve.wait_ge(multiplied, t + 1)
                    if store:
                        dve.wait_ge(stored[u], i * (16 * stores))
                    step.base, step.n = t * links, 0
                    last = evacuate(dve, t, products[u % 3], stage[:, u, :] if store else None, step)
                    assert step.n == links
                    last.then_inc(product_out, 1)


def aggregate(k, table, index, accT, weights=None, alpha=None, heads=1, elem=D):
    nc = k.nc
    with k.phase() as ph:
        staged = ph.sb("index_staged", [P, 2, BATCH], I32)
        odd = ph.sb("odd_sums", [P, KK, NWIN])
        rows = ph.sb("rows", [P, 2, BATCH, D])
        hot = ph.sb("hot", [P, 2, BATCH, P])
        messages = ph.sb("messages", [P, 2, BATCH, D]) if alpha else rows
        sums = [ph.ps(f"sums{j}", [P, 2, KK, P]) for j in range(len(PAIRS))]
        index_staged, cleared, hot_full = ph.sem("index_staged"), ph.sem("cleared"), ph.sem("hot_full")
        gathering, go = ph.sem("gathering"), ph.sem("go")
        rows_in = [ph.sem(f"rows_in{u}") for u in range(2)]
        weighted, multiplied, added, chained = (ph.sem(n) for n in ("weighted", "multiplied", "added", "chained"))
        NPAIR = len(PAIRS)
        with nc.Block() as block:

            @block.scalar
            def _(act):
                with act.Fori(0, BATCHES // 2) as i:
                    for u in range(2):
                        act.wait_ge(rows_in[u], i * (16 * BATCH))
                        act.sem_inc(go, 1)
                        act.activation(staged[:, u, :], index[:, bass.ds(i * (2 * BATCH) + u * BATCH, BATCH)],
                                       ACT.Copy).then_inc(index_staged, 1)

            @block.gpsimd
            def _(pool):
                with pool.Fori(0, BATCHES // 2) as i:
                    for u in range(2):
                        pool.wait_ge(index_staged, i * 2 + (u + 1))
                        if alpha:
                            pool.wait_ge(weighted, i * 2 + (u + 1))
                        else:
                            pool.wait_ge(multiplied, (i * 2 + (u + 1)) * NPAIR)
                        pool.sem_inc(gathering, 1)
                        for j in range(BATCH):
                            pool.indirect_dma_start(
                                out=rows[:, u, j, :], out_offset=None, in_=table,
                                in_offset=bass.IndirectOffsetOnAxis(ap=staged[:, u, j:j + 1], axis=0)
                            ).then_inc(rows_in[u], 16)

            @block.tensor
            def _(pe):
                pe.sem_inc(multiplied, 2 * NPAIR)
                with pe.Fori(0, BATCHES // 2) as i:
                    for u in range(2):
                        b = i * 2 + u
                        pe.wait_ge(hot_full, b + 1)
                        if alpha:
                            pe.wait_ge(weighted, b + 3)
                        else:
                            pe.wait_ge(rows_in[u], (i + 1) * (16 * BATCH))
                        for p, (j0, n) in enumerate(PAIRS):
                            pe.wait_ge(added, b * BATCH + (j0 + n))
                            for j in range(j0, j0 + n):
                                for kk in range(KK):
                                    ins = pe.matmul(sums[p][:, j - j0, kk, :], messages[:, u, j, kk * P:(kk + 1) * P],
                                                    hot[:, u, j, :], start=True, stop=True)
                            ins.then_inc(multiplied, 1)

            @block.vector
            def _(dve):
                dve.sem_inc(added, BATCH)
                dve.sem_inc(weighted, 2)
                dve.memset(accT[:, :, :], 0.0).then_inc(cleared, 1)
                dve.memset(odd[:, :, :], 0.0).then_inc(cleared, 1)
                dve.wait_ge(cleared, 2)
                base = dve.alloc_register(ph._name("window_base"))

                def prepare(i, u):
                    b = i * 2 + u
                    dve.wait_ge(multiplied, (b + 1) * NPAIR)
                    c = i * (2 * BATCH) + u * BATCH
                    if weights is not None:
                        for j in range(BATCH):
                            ins = dve.tensor_scalar(hot[:, u, j, :], k.lane_iota[:, :], k.rel[:, bass.ds(c + j, 1)],
                                                    weights[:, bass.ds(c + j, 1)], ALU.is_equal, ALU.mult)
                    else:
                        ins = hot_by(dve, k, hot[:, u, :, :], k.rel[:, bass.ds(c, BATCH)], P)
                    ins.then_inc(hot_full, 1)
                    if alpha:
                        dve.wait_ge(rows_in[u], (i + 1) * (16 * BATCH))
                        a = alpha(i, u).rearrange("p h j -> p j h").unsqueeze(3).to_broadcast([P, BATCH, heads, D // heads])
                        dve.tensor_tensor(messages[:, u, :, :].rearrange("p j (h d) -> p j h d", h=heads),
                                          rows[:, u, :, :].rearrange("p j (h d) -> p j h d", h=heads), a, ALU.mult
                                          ).then_inc(weighted, 1)

                def add(i, u):
                    b = i * 2 + u
                    for p, (j0, n) in enumerate(PAIRS):
                        dve.wait_ge(multiplied, b * NPAIR + (2 * NPAIR + p + 1))
                        for j in range(j0, j0 + n):
                            dve.reg_load(base, k.dst[0:1, bass.ds(i * (2 * BATCH) + (u * BATCH + j), 1)])
                            acc = odd if (j + u) % 2 else accT
                            window = acc[:, :, bass.ds(nc.snap(base, min_val=0, max_val=NPAD), P)]
                            dve.wait_ge(added, b * BATCH + (BATCH + j - 1))
                            dve.tensor_tensor(window, window, sums[p][:, j - j0, :, :], ALU.add).then_inc(added, 1)

                last = BATCHES // 2 - 1
                prepare(0, 0)
                with dve.Fori(0, last) as i:
                    prepare(i, 1)
                    add(i, 0)
                    prepare(i + 1, 0)
                    add(i, 1)
                prepare(last, 1)
                add(last, 0)
                add(last, 1)
                dve.wait_ge(added, CHUNKS + BATCH)
                dve.tensor_tensor(accT[:, :, :], accT[:, :, :], odd[:, :, :], ALU.add).then_inc(chained, 1)


QUADS = [(j, min(4, BATCH - j)) for j in range(0, BATCH, 4)]
SUM_COPIES = 4
COPY_OF = [[(j + 2 * u) % SUM_COPIES for j in range(BATCH)] for u in range(2)]
SCATTERS = [[COPY_OF[u].count(m) for m in range(SUM_COPIES)] for u in range(2)]


def scatter_sum(k, table, copies):
    nc = k.nc
    with k.phase() as ph:
        zeros = ph.sb("zeros", [P, D])
        srcf = ph.sb("srcf", [P, CHUNKS])
        src_row = ph.sb("src_row", [P, 2, BATCH * P], I32)
        mixed = ph.sb("mixed", [P, BATCH])
        earlier = ph.sb("earlier", [P, P])
        lane = ph.sb("lane", [P, 1])
        before = ph.sb("before", [P, 2, BATCH])
        junk = ph.sb("junk", [P, BATCH, P])
        target = ph.sb("target", [P, 2, BATCH], I32)
        window = ph.sb("window", [P, 2, BATCH, D])
        hot = ph.sb("hot", [P, 2, BATCH, P])
        same = ph.sb("same", [P, 2, BATCH, P])
        gmat = ph.sb("gmat", [P, 2, BATCH, P])
        out = ph.sb("out", [P, 2, BATCH, D])
        g_ps = [ph.ps(f"g{q}", [P, 4, P]) for q in range(4)]
        o_ps = [ph.ps(f"o{q}", [P, 2, D]) for q in range(4)]
        zeroed, cleared, consts = ph.sem("zeroed"), ph.sem("cleared"), ph.sem("consts")
        row_in = [ph.sem(f"row_in{u}") for u in range(2)]
        window_in = [ph.sem(f"window_in{u}") for u in range(2)]
        hot_full, chained, targeted, g_full, g_out = (ph.sem(n) for n in
                                                      ("hot_full", "chained", "targeted", "g_full", "g_out"))
        o_full, o_out, scattering = ph.sem("o_full"), ph.sem("o_out"), ph.sem("scattering")
        scattered = [[ph.sem(f"scattered{u}_{m}") for m in range(SUM_COPIES)] for u in range(2)]
        NQ, NP2 = len(QUADS), len(PAIRS)
        with nc.Block() as block:

            @block.sync
            def _(sp):
                base = sp.alloc_register(ph._name("window_base"))
                with sp.Fori(0, BATCHES // 2) as i:
                    for u in range(2):
                        b = i * 2 + u
                        c = i * (2 * BATCH) + u * BATCH
                        sp.wait_ge(hot_full, b + 1)
                        row = k.a["src_row"][:, bass.ds(c * P, BATCH * P)]
                        sp.dma_start(src_row[:, u, :], row.to_broadcast([P, BATCH * P])).then_inc(row_in[u], 16)
                        sp.wait_ge(o_full, (b + 1) * NP2)
                        for j in range(BATCH):
                            sp.reg_load(base, k.dst[0:1, bass.ds(c + j, 1)])
                            first = nc.snap(base, min_val=0, max_val=NPAD)
                            sp.dma_start(window[:, u, j, :], table[bass.ds(first, P), :]).then_inc(window_in[u], 16)

            @block.scalar
            def _(act):
                act.sem_inc(o_out, 2)
                act.sem_inc(g_out, NQ)
                act.wait_ge(zeroed, 1)
                for m in range(SUM_COPIES):
                    for t in range(NWIN // P):
                        act.dma_start(copies[m][t * P:(t + 1) * P, :], zeros[:, :]).then_inc(cleared, 16)
                with act.Fori(0, BATCHES // 2) as i:
                    for u in range(2):
                        b = i * 2 + u
                        for q, (j0, n) in enumerate(QUADS):
                            act.wait_ge(g_full, b * NQ + (q + 1))
                            act.wait_ge(o_full, (b + 1) * NP2)
                            act.activation(gmat[:, u, j0:j0 + n, :], g_ps[q][:, 0:n, :], ACT.Copy).then_inc(g_out, 1)
                        for m in range(SUM_COPIES):
                            act.wait_ge(scattered[u][m], i * (16 * SCATTERS[u][m]))
                        for p, (j0, n) in enumerate(PAIRS):
                            act.wait_ge(o_full, b * NP2 + (2 * NP2 + p + 1))
                            act.activation(out[:, u, j0:j0 + n, :], o_ps[p % 4][:, 0:n, :], ACT.Copy).then_inc(o_out, 1)

            @block.gpsimd
            def _(pool):
                pool.memset(zeros[:, :], 0.0).then_inc(zeroed, 1)
                pool.memset(earlier[:, :], 1.0).then_inc(consts, 1)
                pool.iota(lane[:, :], [[0, 1]], base=NPAD, channel_multiplier=1,
                          allow_small_or_imprecise_dtypes=True).then_inc(consts, 1)
                pool.wait_ge(consts, 2)
                pool.affine_select(out=earlier[:, :], in_=earlier[:, :], compare_op=ALU.is_gt, fill=0.0,
                                   base=0, pattern=[[-1, P]], channel_multiplier=1).then_inc(consts, 1)
                pool.wait_ge(cleared, 16 * SUM_COPIES * (NWIN // P))
                with pool.Fori(0, BATCHES // 2) as i:
                    for u in range(2):
                        b = i * 2 + u
                        pool.wait_ge(targeted, b + 1)
                        for j in range(BATCH):
                            m, before_j = COPY_OF[u][j], COPY_OF[u][:j].count(COPY_OF[u][j])
                            pool.wait_ge(o_out, b * NP2 + (j // 2 + 3))
                            if before_j:
                                pool.wait_ge(scattered[u][m], (i * SCATTERS[u][m] + before_j) * 16)
                            else:
                                pool.wait_ge(scattered[1 - u][m], (i + u) * (16 * SCATTERS[1 - u][m]))
                            pool.sem_inc(scattering, 1)
                            pool.indirect_dma_start(
                                out=copies[m], out_offset=bass.IndirectOffsetOnAxis(ap=target[:, u, j:j + 1], axis=0),
                                in_=out[:, u, j, :], in_offset=None, compute_op=ALU.add).then_inc(scattered[u][m], 16)
                for u in range(2):
                    for m in range(SUM_COPIES):
                        pool.wait_ge(scattered[u][m], 16 * SCATTERS[u][m] * (BATCHES // 2))

            @block.tensor
            def _(pe):
                pe.sem_inc(o_full, 2 * NP2)
                with pe.Fori(0, BATCHES // 2) as i:
                    for u in range(2):
                        b = i * 2 + u
                        pe.wait_ge(hot_full, b + 3)
                        for q, (j0, n) in enumerate(QUADS):
                            pe.wait_ge(g_out, b * NQ + (q + 1))
                            for j in range(j0, j0 + n):
                                ins = pe.matmul(g_ps[q][:, j - j0, :], hot[:, u, j, :], same[:, u, j, :],
                                                start=True, stop=True)
                            ins.then_inc(g_full, 1)
                        pe.wait_ge(window_in[u], (i + 1) * (16 * BATCH))
                        for p, (j0, n) in enumerate(PAIRS):
                            pe.wait_ge(g_out, b * NQ + (NQ + (j0 + n - 1) // 4 + 1))
                            pe.wait_ge(o_out, b * NP2 + p)
                            for j in range(j0, j0 + n):
                                ins = pe.matmul(o_ps[p % 4][:, j - j0, :], gmat[:, u, j, :], window[:, u, j, :],
                                                start=True, stop=True)
                            ins.then_inc(o_full, 1)

            @block.vector
            def _(dve):
                dve.sem_inc(hot_full, 2)
                dve.wait_ge(consts, 3)
                step = Chain(dve, chained)
                step(dve.tensor_copy(srcf[:, :], k.src[:, :]))
                links = 4
                with dve.Fori(0, BATCHES // 2) as i:
                    for u in range(2):
                        b = i * 2 + u
                        c = i * (2 * BATCH) + u * BATCH
                        step.base, step.n = b * links + 1, 0
                        dve.wait_ge(row_in[u], (i + 1) * 16)
                        dve.wait_ge(g_out, b * NQ)
                        hot_by(dve, k, hot[:, u, :, :], k.rel[:, bass.ds(c, BATCH)], P)
                        for j in range(BATCH):
                            mine = srcf[:, bass.ds(c + j, 1)]
                            others = src_row[:, u, j * P:(j + 1) * P]
                            dve.tensor_scalar(same[:, u, j, :], others, mine, k.weight[:, bass.ds(c + j, 1)],
                                              ALU.is_equal, ALU.mult)
                            ins = dve.scalar_tensor_tensor(junk[:, j, :], others, mine, earlier[:, :], ALU.is_equal,
                                                           ALU.mult, accum_out=before[:, u, j:j + 1])
                        step(ins)
                        for m in range(SUM_COPIES):
                            dve.wait_ge(scattered[u][m], i * (16 * SCATTERS[u][m]))
                        step(dve.tensor_scalar(before[:, u, :], before[:, u, :], 0.0, None, ALU.is_gt))
                        s0 = srcf[:, bass.ds(c, BATCH)]
                        step(dve.tensor_scalar(mixed[:, 0:BATCH], s0, -1.0, lane[:, 0:1], ALU.mult, ALU.add))
                        step(dve.tensor_tensor(mixed[:, 0:BATCH], mixed[:, 0:BATCH], before[:, u, :], ALU.mult))
                        dve.tensor_tensor(target[:, u, :], mixed[:, 0:BATCH], s0, ALU.add).then_inc(targeted, 1)
                        dve.wait_ge(targeted, b + 1)
                        dve.sem_inc(hot_full, 1)


def layer0_gnn(k):
    nc, a = k.nc, k.a
    table = nc.dram_tensor("gcn_rows", [NWIN, D], F32, kind="Internal").ap()
    copies = [nc.dram_tensor(f"gcn_sums{m}", [NWIN, D], F32, kind="Internal").ap() for m in range(SUM_COPIES)]
    with k.phase() as ph:
        xn = ph.sb("xn", [P, TILES, D])
        normalize(k, k.x, xn)
        w = ph.sb("gcn_w", [P, KK, D])
        clear_tail(k, table)

        def load(sp, sem):
            sp.dma_start(w[:, :, :], a["L0_gnn_w"]).then_inc(sem, 16)
            return 16

        def evacuate(dve, t, product, stage, step):
            return dve.tensor_scalar(stage, product[:, 0, 0:D], k.dinv[:, bass.ds(t, 1)], None, ALU.mult)

        def store(sp, t, stage, sem):
            sp.dma_start(table[bass.ds(t * P, P), :], stage).then_inc(sem, 16)

        with k.phase() as inner:
            node_tiles(k, inner, xn, D, load, w, evacuate, store, 1)
    scatter_sum(k, table, copies)
    with k.phase() as ph:
        parts = ph.sb("parts", [P, SUM_COPIES, TILES, D])
        bias = ph.sb("gcn_bias", [P, D])
        loaded, chained = ph.sem("loaded"), ph.sem("chained")
        with nc.Block() as block:

            @block.sync
            def _(sp):
                sp.dma_start(bias[:, :], a["L0_gnn_b"].to_broadcast([P, D])).then_inc(loaded, 16)
                for m in range(SUM_COPIES):
                    sp.dma_start(parts[:, m, :, :], copies[m][0:NPAD, :].rearrange("(t p) d -> p t d", p=P)
                                 ).then_inc(loaded, 16)

            @block.vector
            def _(dve):
                step = Chain(dve, chained)
                dve.wait_ge(loaded, 16 * (1 + SUM_COPIES))
                total = parts[:, 0, :, :]
                for m in range(1, SUM_COPIES):
                    step(dve.tensor_tensor(total, total, parts[:, m, :, :], ALU.add))
                step(dve.tensor_tensor(total, total, k.dinv[:, :].unsqueeze(2).to_broadcast([P, TILES, D]), ALU.mult))
                step(dve.tensor_tensor(total, total, bias[:, :].unsqueeze(1).to_broadcast([P, TILES, D]), ALU.add))
                step(dve.tensor_scalar(total, total, 0.0, None, ALU.max))
                step(dve.tensor_tensor(k.x[:, :, :], k.x[:, :, :], total, ALU.add))


def clear_tail(k, table):
    with k.phase() as ph:
        zeros, zeroed, stored = ph.sb("zeros", [P, D]), ph.sem("zeroed"), ph.sem("stored")
        with k.nc.Block() as block:

            @block.gpsimd
            def _(pool):
                pool.memset(zeros[:, :], 0.0).then_inc(zeroed, 1)

            @block.sync
            def _(sp):
                sp.wait_ge(zeroed, 1)
                sp.dma_start(table[NPAD:NWIN, :], zeros[:, :]).then_inc(stored, 16)
                sp.wait_ge(stored, 16)


def from_sums(k, ph, accT, load, update, links):
    nc = k.nc
    ring = ph.sb("sum_ring", [P, UNROLL, KK, P])
    turned = [ph.ps(f"turned{i}", [P, 512]) for i in range(3)]
    loaded, ring_full, turned_full = ph.sem("loaded"), ph.sem("ring_full"), ph.sem("turned_full")
    turned_out, chained = ph.sem("turned_out"), ph.sem("chained")
    bodies = TILES // UNROLL
    count = []
    with nc.Block() as block:

        @block.sync
        def _(sp):
            count.append(load(sp, loaded))

        @block.scalar
        def _(act):
            with act.Fori(0, bodies) as i:
                act.wait_ge(turned_full, i * UNROLL)
                for u in range(UNROLL):
                    act.activation(ring[:, u, :, :], accT[:, :, bass.ds((i * UNROLL + u) * P, P)], ACT.Copy
                                   ).then_inc(ring_full, 1)

        @block.tensor
        def _(pe):
            with pe.Fori(0, bodies) as i:
                for u in range(UNROLL):
                    t = i * UNROLL + u
                    pe.wait_ge(ring_full, t + 1)
                    pe.wait_ge(turned_out, t)
                    for kk in range(KK):
                        ins = pe.transpose(turned[u % 3][:, kk * P:(kk + 1) * P], ring[:, u, kk, :], k.ident[:, :])
                    ins.then_inc(turned_full, 1)

        @block.vector
        def _(dve):
            dve.sem_inc(turned_out, 1)
            dve.wait_ge(loaded, count[0])
            step = Chain(dve, chained)
            with dve.Fori(0, bodies) as i:
                for u in range(UNROLL):
                    t = i * UNROLL + u
                    dve.wait_ge(turned_full, t + 1)
                    step.base, step.n = t * links, 0
                    last = update(dve, t, turned[u % 3][:, 0:D], step)
                    assert step.n == links
                    last.then_inc(turned_out, 1)


def gate_weights(k, logits, gates, experts, kind, bias=None):
    nc = k.nc
    E = experts
    shape = [P, TILES, E]
    pair = [P, TILES, E, E]
    with k.phase() as ph:
        br = ph.sb("router_bias", [P, E])
        low = ph.sb("low", [P, E, E])
        probs, work = ph.sb("probs", shape), ph.sb("work", shape)
        top, total = ph.sb("top", [P, TILES]), ph.sb("total", [P, TILES])
        above, ties = ph.sb("above", pair), ph.sb("ties", pair)
        loaded, consts, chained, exps, exp_in = (ph.sem(n) for n in ("loaded", "consts", "chained", "exps", "exp_in"))
        n_exp = {"softmax": 1, "top2": 1, "top2_of_softmax": 2, "top2_renormalized": 1}[kind]
        with nc.Block() as block:

            @block.sync
            def _(sp):
                sp.dma_start(br[:, :], bias.to_broadcast([P, E])).then_inc(loaded, 16)

            @block.gpsimd
            def _(pool):
                pool.memset(low[:, :, :], 1.0).then_inc(consts, 1)
                pool.wait_ge(consts, 1)
                pool.affine_select(out=low[:, :, :], in_=low[:, :, :], compare_op=ALU.is_gt, fill=0.0,
                                   base=0, pattern=[[1, E], [-1, E]], channel_multiplier=0).then_inc(consts, 1)

            @block.scalar
            def _(act):
                for n in range(n_exp):
                    act.wait_ge(exp_in, n + 1)
                    act.activation(work[:, :, :], work[:, :, :], ACT.Exp).then_inc(exps, 1)

            @block.vector
            def _(dve):
                step = Chain(dve, chained)

                def spread(v):
                    return v[:, :].unsqueeze(2).to_broadcast(shape)

                def exponentials(values, n):
                    step(dve.tensor_reduce(top[:, :], values, AX.X, ALU.max))
                    dve.tensor_tensor(work[:, :, :], values, spread(top), ALU.subtract).then_inc(exp_in, 1)
                    dve.wait_ge(exps, n)

                def divide(out):
                    step(dve.tensor_reduce(total[:, :], work[:, :, :], AX.X, ALU.add))
                    step(dve.reciprocal(total[:, :], total[:, :]))
                    step(dve.tensor_tensor(out, work[:, :, :], spread(total), ALU.mult))

                dve.wait_ge(loaded, 16)
                dve.wait_ge(consts, 2)
                step(dve.tensor_tensor(logits[:, :, :], logits[:, :, :],
                                       br[:, :].unsqueeze(1).to_broadcast(shape), ALU.add))
                values = logits[:, :, :]
                if kind != "top2":
                    exponentials(values, 1)
                    divide(probs[:, :, :] if kind != "softmax" else gates[:, :, :])
                    values = probs[:, :, :]
                if kind == "softmax":
                    return
                for t in range(TILES):
                    rivals = values[:, t, :].unsqueeze(1).to_broadcast([P, E, E])
                    own = values[:, t, :].unsqueeze(2).to_broadcast([P, E, E])
                    dve.tensor_tensor(above[:, t, :, :], rivals, own, ALU.is_gt)
                    ins = dve.tensor_tensor(ties[:, t, :, :], rivals, own, ALU.is_equal)
                step(ins)
                flat = "p t e j -> p t (e j)"
                step(dve.tensor_tensor(ties[:, :, :, :].rearrange(flat), ties[:, :, :, :].rearrange(flat),
                                       low[:, :, :].rearrange("p e j -> p (e j)").unsqueeze(1).to_broadcast([P, TILES, E * E]),
                                       ALU.mult))
                step(dve.tensor_tensor(above[:, :, :, :], above[:, :, :, :], ties[:, :, :, :], ALU.add))
                taken = gates[:, :, :]
                step(dve.tensor_reduce(taken, above[:, :, :, :], AX.X, ALU.add))
                step(dve.tensor_scalar(taken, taken, 2.0, None, ALU.is_lt))
                if kind == "top2_renormalized":
                    step(dve.tensor_tensor(work[:, :, :], values, taken, ALU.mult))
                else:
                    exponentials(values, 2 if kind == "top2_of_softmax" else 1)
                    step(dve.tensor_tensor(work[:, :, :], work[:, :, :], taken, ALU.mult))
                divide(gates[:, :, :])


class Experts:

    def __init__(self, count, dims):
        self.count, self.dims = count, dims
        self.at, col = [], 0
        for n_in, n_out in zip(dims, dims[1:]):
            self.at.append(col)
            col += -(-n_in // P) * n_out
        self.columns = col
        self.chunks = [(l, c) for l, n in enumerate(dims[1:-1]) for c in range(-(-n // P))]

    def matrix(self, weights, layer, kk, lo, hi):
        n_in, n_out = self.dims[layer], self.dims[layer + 1]
        c = self.at[layer] + kk * n_out
        return weights[0:min(P, n_in - kk * P), c + lo:c + hi]


def mixture(k, xT, spec, weights, out_bias, act_func, bias, scale=None, gates=None, prescale=None):
    nc = k.nc
    E, chunks = spec.count, spec.chunks
    J = 2 * len(chunks)
    SLOTS = 4 if J % 4 == 0 else 3
    slots = min(2, E)
    GROUPS = TILES // UNROLL
    with k.phase() as ph:
        w = ph.sb("expert_w", [P, slots, spec.columns])
        wide = max(-(-n // P) for n in spec.dims[1:-1])
        hidden = [ph.sb(f"hidden{l}", [P, -(-n // P), GROUP]) for l, n in enumerate(spec.dims[1:-1])]
        b_out = ph.sb("out_bias", [P, E, D])
        bias_e = ph.sb("bias_e", [P, 2, len(chunks)])
        scale_e = ph.sb("scale_e", [P, 2, len(chunks)]) if scale is not None else None
        staged, started = ph.sem("staged"), ph.sem("started")
        units = [ph.ps(f"unit{i}", [P, 512]) for i in range(SLOTS)]
        outs = [ph.ps(f"out{i}", [P, 512]) for i in range(3)]
        w_in = [ph.sem(f"w_in{s}") for s in range(slots)]
        w_ready, bias_in = ph.sem("w_ready"), ph.sem("bias_in")
        unit_full, unit_out, out_full, out_out, chained = (ph.sem(n) for n in (
            "unit_full", "unit_out", "out_full", "out_out", "chained"))

        def experts(eng, body):
            if E == 1:
                body(0, 0, 0)
            else:
                with eng.Fori(0, E // 2) as pair:
                    for s in range(2):
                        body(pair * 2 + s, s, pair)

        def groups(eng, e, body):
            with eng.Fori(0, GROUPS) as g:
                body(g, e * GROUPS + g)

        with nc.Block() as block:

            @block.sync
            def _(sp):
                sp.dma_start(b_out[:, :, :], out_bias.rearrange("o (e d) -> o e d", e=E).to_broadcast([P, E, D])
                             ).then_inc(bias_in, 16)

                def load(e, s, pair):
                    sp.wait_ge(out_full, e * TILES)
                    sp.dma_start(w[:, s, :], weights[bass.ds(e, 1), :, :].rearrange("o p c -> (o p) c")
                                 ).then_inc(w_in[s], 16)

                experts(sp, load)

            @block.scalar
            def _(act):
                act.sem_inc(unit_out, SLOTS - 1)

                def expert(e, s, pair):
                    ins = act.activation(bias_e[:, s, :], bias[:, bass.ds(e, 1), :], ACT.Copy)
                    if scale is not None:
                        ins.then_inc(staged, 1)
                        ins = act.activation(scale_e[:, s, :], scale[:, bass.ds(e, 1), :], ACT.Copy)
                    ins.then_inc(staged, 1)

                    def group(g, n):
                        act.wait_ge(staged, (e + 1) * (1 if scale is None else 2))
                        act.wait_ge(out_full, n * UNROLL + TILES)
                        for j in range(J):
                            l, c = chunks[j // 2]
                            m = min(P, spec.dims[l + 1] - c * P)
                            half = slice((j % 2) * HALF, (j % 2 + 1) * HALF)
                            act.wait_ge(unit_full, n * J + (j + 1))
                            col = (slice(0, m), s, slice(j // 2, j // 2 + 1))
                            act.activation(hidden[l][0:m, c, half], units[j % SLOTS][0:m, 0:HALF], act_func,
                                           bias=bias_e[col], **({"scale": scale_e[col]} if scale is not None else {})
                                           ).then_inc(unit_out, 1)
                    groups(act, e, group)
                experts(act, expert)

            @block.tensor
            def _(pe):
                pe.sem_inc(out_full, TILES)

                def expert(e, s, pair):
                    if prescale is not None:
                        pe.wait_ge(w_ready, e + 1)
                    else:
                        pe.wait_ge(w_in[s], pair * 16 + 16)
                    pe.sem_inc(started, 1)

                    def group(g, n):
                        for j in range(J):
                            l, c = chunks[j // 2]
                            m = min(P, spec.dims[l + 1] - c * P)
                            K = -(-spec.dims[l] // P)
                            pe.wait_ge(unit_out, n * J + j)
                            for kk in range(K):
                                rows = min(P, spec.dims[l] - kk * P)
                                if l == 0:
                                    rhs = xT[:, kk, bass.ds(g * GROUP + (j % 2) * HALF, HALF)]
                                else:
                                    src = chunks.index((l - 1, kk)) * 2 + j % 2
                                    pe.wait_ge(unit_out, n * J + (src + SLOTS))
                                    rhs = hidden[l - 1][0:rows, kk, (j % 2) * HALF:(j % 2 + 1) * HALF]
                                ins = pe.matmul(units[j % SLOTS][0:m, 0:HALF],
                                                spec.matrix(w[:, s, :], l, kk, c * P, c * P + m), rhs,
                                                start=kk == 0, stop=kk == K - 1)
                            ins.then_inc(unit_full, 1)
                        L = len(spec.dims) - 2
                        K = -(-spec.dims[L] // P)
                        for u in range(UNROLL):
                            pe.wait_ge(out_out, n * UNROLL + u)
                            for kk in range(K):
                                rows = min(P, spec.dims[L] - kk * P)
                                if u in (0, 2):
                                    src = chunks.index((L - 1, kk)) * 2 + (u == 2)
                                    pe.wait_ge(unit_out, n * J + (src + SLOTS))
                                ins = pe.matmul(outs[u % 3][:, 0:D], hidden[L - 1][0:rows, kk, u * P:(u + 1) * P],
                                                spec.matrix(w[:, s, :], L, kk, 0, D), start=kk == 0, stop=kk == K - 1)
                            ins.then_inc(out_full, 1)
                    groups(pe, e, group)
                experts(pe, expert)

            @block.vector
            def _(dve):
                dve.sem_inc(out_out, 1)
                dve.wait_ge(bias_in, 16)

                def expert(e, s, pair):
                    if prescale is not None:
                        dve.wait_ge(w_in[s], pair * 16 + 16)
                        H = spec.dims[1]
                        for kk in range(KK):
                            part = w[:, s, kk * H:(kk + 1) * H]
                            ins = dve.tensor_scalar(part, part, prescale[:, kk, bass.ds(e, 1)], None, ALU.mult)
                        ins.then_inc(w_ready, 1)

                    def group(g, n):
                        for u in range(UNROLL):
                            t = g * UNROLL + u
                            xt = k.x[:, bass.ds(t, 1), :]
                            bt = b_out[:, bass.ds(e, 1), :]
                            dve.wait_ge(out_out, n * UNROLL + (u + 1))
                            if gates is not None:
                                gate = gates[:, bass.ds(t, 1), bass.ds(e, 1)].rearrange("p a b -> p (a b)")
                                ins = dve.scalar_tensor_tensor(xt, bt, gate, xt, ALU.mult, ALU.add)
                            else:
                                ins = dve.tensor_tensor(xt, bt, xt, ALU.add)
                            ins.then_inc(chained, 1)
                            dve.wait_ge(chained, n * UNROLL + (u + 1))
                            dve.wait_ge(out_full, n * UNROLL + (TILES + u + 1))
                            part = outs[u % 3][:, 0:D]
                            if gates is not None:
                                ins = dve.scalar_tensor_tensor(xt, part, gate, xt, ALU.mult, ALU.add)
                            else:
                                ins = dve.tensor_tensor(xt, part, xt, ALU.add)
                            ins.then_inc(out_out, 1)
                    groups(dve, e, group)
                experts(dve, expert)


def routed(k, xn, xT, router, experts, logits):
    with k.phase() as ph:
        wr = ph.sb("router", [P, KK, experts])

        def load(sp, sem):
            sp.dma_start(wr[:, :, :], router).then_inc(sem, 16)
            return 16

        def evacuate(dve, t, product, stage, step):
            return dve.tensor_copy(logits[:, bass.ds(t, 1), :], product[:, 0, 0:experts])

        node_tiles(k, ph, xn, experts, load, wr, evacuate, xT=xT)


def load_small(k, pairs):
    with k.phase() as ph:
        loaded = ph.sem("loaded")
        with k.nc.Block() as block:

            @block.sync
            def _(sp):
                for dst, src in pairs:
                    sp.dma_start(dst, src).then_inc(loaded, 16)
                sp.wait_ge(loaded, 16 * len(pairs))


def edge_order(dram_row, g, ci):
    return dram_row.rearrange("o (g c e) -> (o c) g e", g=g, c=ci)


def attention_scores(k, ktable, kindex, qtable, heads, scores):
    nc = k.nc
    CI = 104 // heads
    R = CI * heads
    G = CHUNKS // CI
    per_body = 2 * BATCH // CI
    DH = D // heads
    with k.phase() as ph:
        staged = ph.sb("index_staged", [P, 2, BATCH], I32)
        rows = ph.sb("rows", [P, 2, BATCH, D])
        window = ph.sb("window", [P, 2, BATCH, D])
        rel = ph.sb("rel_row", [P, 2, BATCH * P])
        spread = ph.sb("spread", [P, 2, BATCH, P])
        prod = ph.sb("prod", [P, BATCH, D])
        sc = ph.sb("sc", [P, per_body, heads, CI])
        kept = ph.sb("kept", [R, G, P])
        q_ps = [ph.ps(f"q{q}", [P, 2, D]) for q in range(len(PAIRS))]
        s_ps = ph.ps("s", [P, 512])
        index_staged, gathering, spread_full = ph.sem("index_staged"), ph.sem("gathering"), ph.sem("spread_full")
        q_full, q_out = ph.sem("q_full"), ph.sem("q_out")
        rel_in = [ph.sem(f"rel_in{u}") for u in range(2)]
        reduced, s_full, s_out, stored = (ph.sem(n) for n in ("reduced", "s_full", "s_out", "stored"))
        go = ph.sem("go")
        rows_in = [ph.sem(f"rows_in{u}") for u in range(2)]
        window_in = [ph.sem(f"window_in{u}") for u in range(2)]
        NP2 = len(PAIRS)
        with nc.Block() as block:

            @block.sync
            def _(sp):
                base = sp.alloc_register(ph._name("window_base"))
                with sp.Fori(0, BATCHES // 2) as i:
                    for u in range(2):
                        b = i * 2 + u
                        c = i * (2 * BATCH) + u * BATCH
                        sp.wait_ge(spread_full, b + 1)
                        sp.dma_start(rel[:, u, :], k.rel_row[:, bass.ds(c * P, BATCH * P)].to_broadcast([P, BATCH * P])
                                     ).then_inc(rel_in[u], 16)
                        sp.wait_ge(q_full, (b + 1) * NP2)
                        for j in range(BATCH):
                            sp.reg_load(base, k.dst[0:1, bass.ds(c + j, 1)])
                            first = nc.snap(base, min_val=0, max_val=NPAD)
                            sp.dma_start(window[:, u, j, :], qtable[bass.ds(first, P), :]).then_inc(window_in[u], 16)
                sp.wait_ge(s_out, G + 1)
                for h in range(heads):
                    sp.dma_start(edge_order(scores[h:h + 1, :], G, CI), kept[h * CI:(h + 1) * CI, :, :]
                                 ).then_inc(stored, 16)
                sp.wait_ge(stored, 16 * heads)

            @block.scalar
            def _(act):
                act.sem_inc(s_out, 1)

                def stage(i, u):
                    act.wait_ge(rows_in[u], i * (16 * BATCH))
                    act.sem_inc(go, 1)
                    act.activation(staged[:, u, :], kindex[:, bass.ds(i * (2 * BATCH) + u * BATCH, BATCH)],
                                   ACT.Copy).then_inc(index_staged, 1)

                def keep(i):
                    for v in range(per_body):
                        act.wait_ge(s_full, i * per_body + (v + 1))
                        act.sem_inc(go, 1)
                        act.activation(kept[:, bass.ds(i * per_body + v, 1), :], s_ps[0:R, 0:P], ACT.Copy
                                       ).then_inc(s_out, 1)

                last = BATCHES // 2 - 1
                stage(0, 0)
                stage(0, 1)
                with act.Fori(0, last) as i:
                    stage(i + 1, 0)
                    stage(i + 1, 1)
                    keep(i)
                keep(last)

            @block.gpsimd
            def _(pool):
                with pool.Fori(0, BATCHES // 2) as i:
                    for u in range(2):
                        b = i * 2 + u
                        pool.wait_ge(index_staged, b + 1)
                        pool.wait_ge(reduced, b + 1)
                        pool.sem_inc(gathering, 1)
                        for j in range(BATCH):
                            pool.indirect_dma_start(
                                out=rows[:, u, j, :], out_offset=None, in_=ktable,
                                in_offset=bass.IndirectOffsetOnAxis(ap=staged[:, u, j:j + 1], axis=0)
                            ).then_inc(rows_in[u], 16)

            @block.tensor
            def _(pe):
                pe.sem_inc(q_full, 2 * NP2)
                with pe.Fori(0, BATCHES // 2) as i:
                    for u in range(2):
                        b = i * 2 + u
                        pe.wait_ge(spread_full, b + 3)
                        pe.wait_ge(window_in[u], (i + 1) * (16 * BATCH))
                        for p, (j0, n) in enumerate(PAIRS):
                            pe.wait_ge(q_out, b * NP2 + (p + 1))
                            for j in range(j0, j0 + n):
                                ins = pe.matmul(q_ps[p][:, j - j0, :], spread[:, u, j, :], window[:, u, j, :],
                                                start=True, stop=True)
                            ins.then_inc(q_full, 1)
                    for v in range(per_body):
                        pe.wait_ge(reduced, i * 2 + (2 + (v + 1) * 2 // per_body))
                        pe.wait_ge(s_out, i * per_body + (v + 1))
                        pe.transpose(s_ps[0:R, 0:P], sc[:, v, :, :].rearrange("p h c -> p (h c)"), k.ident[:, :]
                                     ).then_inc(s_full, 1)

            @block.vector
            def _(dve):
                dve.sem_inc(q_out, NP2)
                dve.sem_inc(reduced, 2)
                dve.sem_inc(spread_full, 2)

                def spread_out(i, u):
                    b = i * 2 + u
                    dve.wait_ge(rel_in[u], (i + 1) * 16)
                    dve.wait_ge(q_full, (b + 1) * NP2)
                    dve.tensor_scalar(spread[:, u, :, :].rearrange("p j e -> p (j e)"), rel[:, u, :], k.lane_col[:, 0:1],
                                      None, ALU.is_equal).then_inc(spread_full, 1)

                def score(i, u):
                    b = i * 2 + u
                    dve.wait_ge(rows_in[u], (i + 1) * (16 * BATCH))
                    dve.wait_ge(reduced, b + 2)
                    for p, (j0, n) in enumerate(PAIRS):
                        dve.wait_ge(q_full, b * NP2 + (2 * NP2 + p + 1))
                        dve.tensor_tensor(prod[:, j0:j0 + n, :], q_ps[p][:, 0:n, :], rows[:, u, j0:j0 + n, :],
                                          ALU.mult).then_inc(q_out, 1)
                    dve.wait_ge(q_out, (b + 2) * NP2)
                    dve.wait_ge(s_full, i * per_body)
                    v, j0 = (u, 0) if per_body == 2 else (0, u * BATCH)
                    dve.tensor_reduce(sc[:, v, :, j0:j0 + BATCH].rearrange("p h j -> p j h"),
                                      prod[:, :, :].rearrange("p j (h d) -> p j h d", h=heads), AX.X, ALU.add
                                      ).then_inc(reduced, 1)

                last = BATCHES // 2 - 1
                spread_out(0, 0)
                with dve.Fori(0, last) as i:
                    spread_out(i, 1)
                    score(i, 0)
                    spread_out(i + 1, 0)
                    score(i, 1)
                spread_out(last, 1)
                score(last, 0)
                score(last, 1)


def segment_softmax(k, scores, heads, alphas, scale=1.0, bias=None, more_loops=False):
    nc = k.nc
    H, N = heads, CHUNKS
    with k.phase() as ph:
        sc, run, seg = ph.sb("sc", [P, H, N]), ph.sb("run", [P, N]), ph.sb("seg", [P, H, N])
        dst = ph.sb("dst_rows_f", [P, N])
        dst_i = ph.sb("dst_rows", [P, N], I32)
        same, pen = ph.sb("same", [P, N + 1]), ph.sb("pen", [P, N + 1])
        ends = [ph.sb(f"end_{n}", [P, N]) for n in ("first", "last")]
        end_pens = [ph.sb(f"end_pen_{n}", [P, N]) for n in ("first", "last")]
        edge_vals = ph.sb("edge_vals", [P, 4, H])
        rowed = ph.sb("rowed", [H, 4, P])
        cont, whole = ph.sb("cont", [H, P + 1]), ph.sb("whole", [H, P])
        link, link_pen = ph.sb("link", [H, 2, P]), ph.sb("link_pen", [H, 2, P])
        cont_pen = ph.sb("cont_pen", [H, P + 1])
        carried = ph.sb("carried", [H, 2, P + 1])
        carry_in = ph.sb("carry_in", [H, 2, P])
        carry = ph.sb("carry", [P, 2, H])
        ends_ps = ph.ps("ends_ps", [P, 4, P])
        carry_ps = ph.ps("carry_ps", [P, 512])
        loaded, chained, at_pe, from_pe = (ph.sem(n) for n in ("loaded", "chained", "at_pe", "from_pe"))
        exp_in, exp_out, stored = ph.sem("exp_in"), ph.sem("exp_out"), ph.sem("stored")
        rows = "h (p i) -> p h i"
        loads = 2 + (bias is not None) + more_loops
        if more_loops:
            src_i, loops = ph.sb("src_rows", [P, N], I32), ph.sb("loops", [P, H, N])
        with nc.Block() as block:

            @block.sync
            def _(sp):
                sp.dma_start(dst_i[:, :], k.a["dst_rows"]).then_inc(loaded, 16)
                sp.dma_start(sc[:, :, :], scores.rearrange(rows, p=P)).then_inc(loaded, 16)
                if bias is not None:
                    sp.dma_start(seg[:, :, :], bias.rearrange(rows, p=P)).then_inc(loaded, 16)
                if more_loops:
                    sp.dma_start(src_i[:, :], k.a["src_row"].rearrange("o (p i) -> (o p) i", p=P)).then_inc(loaded, 16)
                sp.wait_ge(exp_out, 2)
                sp.dma_start(alphas.rearrange(rows, p=P), sc[:, :, :]).then_inc(stored, 16)
                sp.wait_ge(stored, 16)

            @block.scalar
            def _(act):
                act.wait_ge(exp_in, 1)
                act.activation(sc[:, :, :], sc[:, :, :], ACT.Exp).then_inc(exp_out, 1)

            @block.tensor
            def _(pe):
                for n in range(3 if more_loops else 2):
                    pe.wait_ge(at_pe, 2 * n + 1)
                    for q in range(4):
                        ins = pe.transpose(ends_ps[0:H, q, :], edge_vals[:, q, :], k.ident[:, :])
                    ins.then_inc(from_pe, 1)
                    pe.wait_ge(at_pe, 2 * n + 2)
                    for q in range(2):
                        ins = pe.transpose(carry_ps[:, q * H:(q + 1) * H], carry_in[:, q, :], k.ident[0:H, 0:H])
                    ins.then_inc(from_pe, 1)

            @block.vector
            def _(dve):
                step = Chain(dve, chained)
                dve.wait_ge(loaded, 16 * loads)
                step(dve.tensor_copy(dst[:, :], dst_i[:, :]))
                dve.memset(same[:, 0:1], 0.0)
                dve.memset(same[:, N:N + 1], 0.0)
                step(dve.tensor_tensor(same[:, 1:N], dst[:, 1:N], dst[:, 0:N - 1], ALU.is_equal))
                step(dve.tensor_scalar(pen[:, :], same[:, :], 1.0, BIG, ALU.subtract, ALU.mult))
                for n, at in enumerate((0, N - 1)):
                    step(dve.tensor_scalar(ends[n][:, :], dst[:, :], dst[:, at:at + 1], None, ALU.is_equal))
                    step(dve.tensor_scalar(end_pens[n][:, :], ends[n][:, :], 1.0, BIG, ALU.subtract, ALU.mult))
                    step(dve.tensor_copy(edge_vals[:, 2 + n, :], dst[:, at:at + 1].to_broadcast([P, H])))
                if scale != 1.0:
                    step(dve.tensor_scalar(sc[:, :, :], sc[:, :, :], scale, None, ALU.mult))
                if bias is not None:
                    step(dve.tensor_tensor(sc[:, :, :], sc[:, :, :], seg[:, :, :], ALU.add))

                def combine(n, maximum, values):
                    masks = pen if maximum else same
                    join, op = (ALU.add, ALU.max) if maximum else (ALU.mult, ALU.add)
                    for h in range(H):
                        step(dve.tensor_tensor_scan(run[:, :], masks[:, 0:N], values[:, h, :], -BIG if maximum else 0.0,
                                                    join, op))
                        step(dve.tensor_tensor_scan(seg[:, h, ::-1], masks[:, N:0:-1], run[:, ::-1],
                                                    -BIG if maximum else 0.0, join, ALU.max))
                    step(dve.tensor_copy(edge_vals[:, 0, :], seg[:, :, 0]))
                    dve.tensor_copy(edge_vals[:, 1, :], seg[:, :, N - 1]).then_inc(at_pe, 1)
                    dve.wait_ge(from_pe, 2 * n + 1)
                    step(dve.tensor_copy(rowed[:, :, :], ends_ps[0:H, :, :]))
                    firsts, lasts, dst_first, dst_last = (rowed[:, q, :] for q in range(4))
                    if n == 0:
                        dve.memset(cont[:, 0:1], 0.0)
                        dve.memset(cont[:, P:P + 1], 0.0)
                        step(dve.tensor_tensor(cont[:, 1:P], dst_first[:, 1:P], dst_last[:, 0:P - 1], ALU.is_equal))
                        step(dve.tensor_tensor(whole[:, :], dst_first, dst_last, ALU.is_equal))
                        step(dve.tensor_tensor(link[:, 0, :], whole[:, :], cont[:, 0:P], ALU.mult))
                        step(dve.tensor_tensor(link[:, 1, :], whole[:, :], cont[:, 1:P + 1], ALU.mult))
                        step(dve.tensor_scalar(link_pen[:, :, :], link[:, :, :], 1.0, BIG, ALU.subtract, ALU.mult))
                        step(dve.tensor_scalar(cont_pen[:, :], cont[:, :], 1.0, BIG, ALU.subtract, ALU.mult))
                    links = link_pen if maximum else link
                    none = -BIG if maximum else 0.0
                    step(dve.memset(carried[:, :, :], none))
                    step(dve.tensor_tensor_scan(carried[:, 0, 1:P + 1], links[:, 0, :], lasts, none, join, op))
                    step(dve.tensor_tensor_scan(carried[:, 1, P - 1::-1], links[:, 1, ::-1], firsts[:, ::-1], none,
                                                join, op))
                    c = cont_pen if maximum else cont
                    step(dve.tensor_tensor(carry_in[:, 0, :], carried[:, 0, 0:P], c[:, 0:P], join))
                    dve.tensor_tensor(carry_in[:, 1, :], carried[:, 1, 1:P + 1], c[:, 1:P + 1], join).then_inc(at_pe, 1)
                    dve.wait_ge(from_pe, 2 * n + 2)
                    step(dve.tensor_copy(carry[:, :, :], carry_ps[:, 0:2 * H].rearrange("p (q h) -> p q h", q=2)))
                    masks = end_pens if maximum else ends
                    for h in range(H):
                        for q in range(2):
                            step(dve.scalar_tensor_tensor(seg[:, h, :], masks[q][:, :], carry[:, q, h:h + 1],
                                                          seg[:, h, :], join, op))

                combine(0, True, sc)
                step(dve.tensor_tensor(sc[:, :, :], sc[:, :, :], seg[:, :, :], ALU.subtract))
                dve.sem_inc(exp_in, 1)
                if more_loops:
                    step(dve.tensor_copy(loops[:, 0, :], src_i[:, :]))
                    step(dve.tensor_tensor(loops[:, 0, :], loops[:, 0, :], dst[:, :], ALU.is_equal))
                    combine(1, False, loops)
                    step(dve.tensor_scalar(seg[:, :, :], seg[:, :, :], 1.0, None, ALU.max))
                    step(dve.reciprocal(seg[:, :, :], seg[:, :, :]))
                    step(dve.tensor_tensor(loops[:, :, :], loops[:, :, :], seg[:, :, :], ALU.mult))
                    step(dve.tensor_scalar(loops[:, :, :], loops[:, :, :], 1.0, None, ALU.add))
                dve.wait_ge(exp_out, 1)
                if more_loops:
                    step(dve.tensor_tensor(sc[:, :, :], sc[:, :, :], loops[:, :, :], ALU.mult))
                combine(2 if more_loops else 1, False, sc)
                step(dve.reciprocal(seg[:, :, :], seg[:, :, :]))
                dve.tensor_tensor(sc[:, :, :], sc[:, :, :], seg[:, :, :], ALU.mult).then_inc(exp_out, 1)


def load_alphas(k, alphas, heads, ci, out):
    nc = k.nc
    R, G = heads * ci, CHUNKS // ci
    quads = [(g, min(4, G - g)) for g in range(0, G, 4)]
    with k.phase() as ph:
        kept = ph.sb("kept", [R, G, P])
        ps = [ph.ps(f"turned{q}", [P, 4, P]) for q in range(2)]
        loaded, full, emptied = ph.sem("loaded"), ph.sem("full"), ph.sem("emptied")
        with nc.Block() as block:

            @block.sync
            def _(sp):
                for h in range(heads):
                    sp.dma_start(kept[h * ci:(h + 1) * ci, :, :], edge_order(alphas[h:h + 1, :], G, ci)
                                 ).then_inc(loaded, 16)

            @block.tensor
            def _(pe):
                pe.wait_ge(loaded, 16 * heads)
                for q, (g0, n) in enumerate(quads):
                    if q >= 2:
                        pe.wait_ge(emptied, q - 1)
                    for g in range(g0, g0 + n):
                        ins = pe.transpose(ps[q % 2][:, g - g0, 0:R], kept[:, g, :], k.ident[0:R, 0:R])
                    ins.then_inc(full, 1)

            @block.scalar
            def _(act):
                for q, (g0, n) in enumerate(quads):
                    act.wait_ge(full, q + 1)
                    act.activation(out[:, g0:g0 + n, :], ps[q % 2][:, 0:n, 0:R], ACT.Copy).then_inc(emptied, 1)


def edge_bias(k, out):
    nc, a = k.nc, k.a
    N, H, F = 496, 8, 64
    COLS = EPAD // 2
    BLOCKS = 4
    BODIES = COLS // (N * BLOCKS)
    with k.phase() as ph:
        w1, w2 = ph.sb("w1", [P, D]), ph.sb("w2", [P, KK, H])
        b1, b2 = ph.sb("b1", [P, KK]), ph.sb("b2", [H, 1])
        attr = ph.sb("attr", [P, 2, BLOCKS * N])
        hid = ph.sb("hid", [P, 2, KK, N])
        res = ph.sb("res", [H, 2, 2, BLOCKS, N])
        h_ps = [ph.ps(f"h{q}", [P, 512]) for q in range(4)]
        r_ps = [ph.ps(f"r{q}", [P, 512]) for q in range(2)]
        w_in, h_full, h_out, r_full, r_out = (ph.sem(n) for n in ("w_in", "h_full", "h_out", "r_full", "r_out"))
        attr_in = [ph.sem(f"attr_in{u}") for u in range(2)]
        stored = [ph.sem(f"stored{u}") for u in range(2)]
        storing = ph.sem("storing")
        J = 2 * BLOCKS
        with nc.Block() as block:

            @block.sync
            def _(sp):
                for dst, src in ((w1[:, :], a["L2_gnn_W1"]), (w2[:, :, :], a["L2_gnn_W2"]), (b1[:, :], a["L2_gnn_b1"]),
                                 (b2[:, :], a["L2_gnn_b2"])):
                    sp.dma_start(dst, src).then_inc(w_in, 16)
                with sp.Fori(0, BODIES // 2) as i:
                    for u in range(2):
                        n = i * 2 + u
                        sp.wait_ge(r_full, n * J)
                        sp.dma_start(attr[:, u, :], a["attr"][:, bass.ds(n * (BLOCKS * N), BLOCKS * N)]
                                     ).then_inc(attr_in[u], 16)

            @block.tensor
            def _(pe):
                pe.sem_inc(r_full, J)
                pe.wait_ge(w_in, 64)
                with pe.Fori(0, BODIES // 2) as i:
                    for u in range(2):
                        n = i * 2 + u
                        pe.wait_ge(attr_in[u], i * 16 + 16)

                        def hidden(j):
                            half, blk = j % 2, j // 2
                            for kk in range(KK):
                                q = (2 * j + kk) % 4
                                pe.wait_ge(h_out, n * (2 * J) + (2 * j + kk))
                                pe.matmul(h_ps[q][:, 0:N], w1[half * F:(half + 1) * F, kk * P:(kk + 1) * P],
                                          attr[half * F:(half + 1) * F, u, blk * N:(blk + 1) * N],
                                          start=True, stop=True).then_inc(h_full, 1)

                        def result(j):
                            pe.wait_ge(r_out, n * J + j)
                            for kk in range(KK):
                                pe.wait_ge(h_out, n * (2 * J) + (2 * j + kk + 4))
                                ins = pe.matmul(r_ps[j % 2][0:H, 0:N], w2[:, kk, :], hid[:, j % 2, kk, :],
                                                start=kk == 0, stop=kk == KK - 1)
                            ins.then_inc(r_full, 1)

                        hidden(0)
                        for j in range(J):
                            if j + 1 < J:
                                hidden(j + 1)
                            result(j)

            @block.scalar
            def _(act):
                act.sem_inc(h_out, 3)
                act.wait_ge(w_in, 64)
                with act.Fori(0, BODIES // 2) as i:
                    for u in range(2):
                        n = i * 2 + u
                        for j in range(J):
                            for kk in range(KK):
                                act.wait_ge(h_full, n * (2 * J) + (2 * j + kk + 1))
                                act.wait_ge(r_full, n * J + (J + j - 1))
                                act.activation(hid[:, j % 2, kk, :], h_ps[(2 * j + kk) % 4][:, 0:N], ACT.Relu,
                                               bias=b1[:, kk:kk + 1]).then_inc(h_out, 1)

            @block.vector
            def _(dve):
                dve.sem_inc(r_out, 1)
                dve.wait_ge(w_in, 64)
                with dve.Fori(0, BODIES // 2) as i:
                    for u in range(2):
                        n = i * 2 + u
                        dve.wait_ge(stored[u], i * 32)
                        for j in range(J):
                            dve.wait_ge(r_full, n * J + (J + j + 1))
                            dve.tensor_scalar(res[:, u, j % 2, j // 2, :], r_ps[j % 2][0:H, 0:N], b2[:, 0:1], None, ALU.add
                                              ).then_inc(r_out, 1)

            @block.gpsimd
            def _(pool):
                with pool.Fori(0, BODIES // 2) as i:
                    for u in range(2):
                        n = i * 2 + u
                        for half in range(2):
                            pool.wait_ge(r_out, n * J + (J + 1))
                            pool.sem_inc(storing, 1)
                            pool.dma_start(out[:, bass.ds(n * (BLOCKS * N) + half * COLS, BLOCKS * N)],
                                           res[:, u, half, :, :].rearrange("h b n -> h (b n)")).then_inc(stored[u], 16)
                for u in range(2):
                    pool.wait_ge(stored[u], 32 * (BODIES // 2))


def project_sums(k, ph, accT, count, load, rhs, update, links):
    nc = k.nc
    ring = ph.sb("sum_ring", [P, UNROLL, KK, P])
    ps = [ph.ps(f"product{i}", [P, 512]) for i in range(4)]
    loaded, ring_full, full, emptied, chained = (ph.sem(n) for n in ("loaded", "ring_full", "full", "emptied", "chained"))
    bodies = TILES // UNROLL
    count_in = []
    with nc.Block() as block:

        @block.sync
        def _(sp):
            count_in.append(load(sp, loaded))

        @block.scalar
        def _(act):
            go = ph.sem("go")
            with act.Fori(0, bodies) as i:
                act.wait_ge(full, i * (UNROLL * count))
                act.sem_inc(go, 1)
                for u in range(UNROLL):
                    act.activation(ring[:, u, :, :], accT[:, :, bass.ds((i * UNROLL + u) * P, P)], ACT.Copy
                                   ).then_inc(ring_full, 1)

        @block.tensor
        def _(pe):
            pe.wait_ge(loaded, count_in[0])
            with pe.Fori(0, bodies) as i:
                for u in range(UNROLL):
                    t = i * UNROLL + u
                    pe.wait_ge(ring_full, t + 1)
                    for y in range(count):
                        m = u * count + y
                        pe.wait_ge(emptied, t * count + y)
                        for kk in range(KK):
                            ins = pe.matmul(ps[m % 4 if count == 4 else m % 3][:, 0:D], ring[:, u, kk, :],
                                            rhs[:, y, kk, :], start=kk == 0, stop=kk == KK - 1)
                        ins.then_inc(full, 1)

        @block.vector
        def _(dve):
            dve.sem_inc(emptied, 3 if count == 4 else 1)
            dve.wait_ge(loaded, count_in[0])
            step = Chain(dve, chained)
            with dve.Fori(0, bodies) as i:
                for u in range(UNROLL):
                    t = i * UNROLL + u
                    step.base, step.n = t * links, 0

                    def product(y):
                        m = u * count + y
                        dve.wait_ge(full, t * count + (y + 1))
                        return ps[m % 4 if count == 4 else m % 3][:, 0:D]

                    update(dve, t, product, step, emptied)
                    assert step.n == links


TYPES, RELS, L1_HEADS = 4, 8, 4


def typed_tables(k, xn, kinds, qtab, ktab, vtab):
    nc, a = k.nc, k.a
    HD = D // L1_HEADS
    R4 = RELS // 2
    with k.phase() as ph:
        weights = ph.sb("typed_w", [P, 3, TYPES, KK, D])
        blocks = ph.sb("relation_blocks", [P, 2, KK, RELS, P])
        pri = ph.sb("pri", [P, KK, RELS])
        ring = ph.sb("tile_ring", [P, D])
        diag = ph.sb("diag", [P, TYPES, P])
        masked = ph.sb("masked", [P, KK, TYPES, P])
        kvT = ph.sb("kvT", [P, 2, KK, P])
        stage = ph.sb("stage", [P, 2, 2, RELS, D])
        q_stage = ph.sb("q_stage", [P, 2, D])
        m_ps = [ph.ps(f"masked{kk}", [P, TYPES, P]) for kk in range(KK)]
        kv_ps, q_ps = ph.ps("kv", [P, 2, KK, P]), ph.ps("q", [P, 512])
        r_ps = [ph.ps(f"related{i}", [P, R4, P]) for i in range(4)]
        loaded, zeroed, blocked, ready = ph.sem("loaded"), ph.sem("zeroed"), ph.sem("blocked"), ph.sem("ready")
        ring_full, diag_full, m_full, m_out = (ph.sem(n) for n in ("ring_full", "diag_full", "m_full", "m_out"))
        kv_full, kv_out, q_full, q_out = (ph.sem(n) for n in ("kv_full", "kv_out", "q_full", "q_out"))
        r_full, k_out, v_out = ph.sem("r_full"), ph.sem("k_out"), ph.sem("v_out")
        stored = [ph.sem(f"stored{u}") for u in range(2)]
        TURNS = (TILES - 1) // 2
        J = 8

        def tiles(eng, body):
            with eng.Fori(0, TURNS) as i:
                for u in range(2):
                    body(i * 2 + u, u, i, True)
            body(TILES - 1, 0, TURNS, False)

        def part(j):
            return j // 4, j // 2 % 2, slice(j % 2 * R4, j % 2 * R4 + R4)

        with nc.Block() as block:

            @block.sync
            def _(sp):
                sp.dma_start(weights[:, :, :, :, :], a["L1_gnn_w"]).then_inc(loaded, 16)
                sp.dma_start(pri[:, :, :], a["L1_gnn_pri"]).then_inc(loaded, 16)
                sp.wait_ge(zeroed, 1)
                for n, name in enumerate(("L1_gnn_att", "L1_gnn_msg")):
                    for h in range(2):
                        at = slice(h * HD, (h + 1) * HD)
                        for o in range(KK):
                            sp.dma_start(blocks[at, n, o, :, at], a[name][at, o, :, :]).then_inc(blocked, 16)

                def store(t, u, turn, more):
                    sp.wait_ge(q_out, t + 1)
                    sp.dma_start(qtab[bass.ds(t * P, P), :], q_stage[:, u, :]).then_inc(stored[u], 16)
                    for n, (tab, out) in enumerate(((ktab, k_out), (vtab, v_out))):
                        sp.wait_ge(out, (t + 1) * 4)
                        sp.dma_start(tab.rearrange("(r n) d -> n r d", r=RELS)[bass.ds(t * P, P), :, :],
                                     stage[:, u, n, :, :]).then_inc(stored[u], 16)
                tiles(sp, store)
                for u in range(2):
                    sp.wait_ge(stored[u], 48 * (TURNS + 1 - u))

            @block.gpsimd
            def _(pool):
                pool.memset(blocks[:, :, :, :, :], 0.0).then_inc(zeroed, 1)
                pool.memset(xn[:, TILES, :], 0.0).then_inc(zeroed, 1)

            @block.scalar
            def _(act):
                def fetch(t):
                    act.activation(ring[:, :], xn[:, bass.ds(t, 1), :], ACT.Copy).then_inc(ring_full, 1)

                def empty(t):
                    for kk in range(KK):
                        act.wait_ge(m_full, t * KK + (kk + 1))
                        act.activation(masked[:, kk, :, :], m_ps[kk][:, :, :], ACT.Copy).then_inc(m_out, 1)

                def tile(t, u, turn, more):
                    act.wait_ge(kv_full, t + 1)
                    act.activation(kvT[:, :, :, :], kv_ps[:, :, :, :], ACT.Copy).then_inc(kv_out, 1)
                    act.wait_ge(q_full, t + 1)
                    if more:
                        empty(t + 1)
                        act.sem_inc(ready, 1)
                        fetch(t + 2)
                    act.wait_ge(stored[u], turn * 48)
                    for j in range(4):
                        _, o, rels = part(j)
                        act.wait_ge(r_full, t * J + (j + 1))
                        act.activation(stage[:, u, 0, rels, o * P:(o + 1) * P], r_ps[j % 4][:, :, :], ACT.Copy
                                       ).then_inc(k_out, 1)

                act.wait_ge(zeroed, 2)
                fetch(0)
                empty(0)
                fetch(1)
                tiles(act, tile)

            @block.vector
            def _(dve):
                dve.wait_ge(loaded, 32)
                dve.wait_ge(blocked, 16 * 8)
                p4 = pri[:, :, :].unsqueeze(3).to_broadcast([P, KK, RELS, P])
                for o in range(KK):
                    dve.scalar_tensor_tensor(blocks[:, 0, o, :, :], blocks[:, 0, o, :, :], 1.0 / HD ** 0.5,
                                             p4[:, o, :, :], ALU.mult, ALU.mult).then_inc(blocked, 1)

                def mask(t):
                    types = kinds[:, bass.ds(t, 1), :].rearrange("p o y -> p (o y)").unsqueeze(2)
                    dve.tensor_tensor(diag[:, :, :], k.ident[:, :].unsqueeze(1).to_broadcast([P, TYPES, P]),
                                      types.to_broadcast([P, TYPES, P]), ALU.mult).then_inc(diag_full, 1)

                def tile(t, u, turn, more):
                    dve.wait_ge(q_full, t + 1)
                    dve.wait_ge(stored[u], turn * 48)
                    dve.tensor_copy(q_stage[:, u, :], q_ps[:, 0:D]).then_inc(q_out, 1)
                    if more:
                        dve.wait_ge(m_full, (t + 2) * KK)
                        mask(t + 2)
                    for j in range(4, J):
                        _, o, rels = part(j)
                        dve.wait_ge(r_full, t * J + (j + 1))
                        dve.tensor_copy(stage[:, u, 1, rels, o * P:(o + 1) * P], r_ps[j % 4][:, :, :]).then_inc(v_out, 1)

                mask(0)
                dve.wait_ge(m_full, KK)
                mask(1)
                tiles(dve, tile)

            @block.tensor
            def _(pe):
                def turn_masked(t):
                    pe.wait_ge(ring_full, t + 1)
                    pe.wait_ge(diag_full, t + 1)
                    pe.wait_ge(m_out, t * KK)
                    for kk in range(KK):
                        pe.matmul(m_ps[kk][:, :, :], ring[:, kk * P:(kk + 1) * P], diag[:, :, :], start=True, stop=True
                                  ).then_inc(m_full, 1)

                def tile(t, u, turn, more):
                    pe.wait_ge(m_out, (t + 1) * KK)
                    pe.wait_ge(kv_out, t)
                    for n in range(2):
                        for o in range(KK):
                            for kk in range(KK):
                                for y in range(TYPES):
                                    ins = pe.matmul(kv_ps[:, n, o, :], weights[:, n, y, kk, o * P:(o + 1) * P],
                                                    masked[:, kk, y, :], start=kk == 0 and y == 0,
                                                    stop=kk == KK - 1 and y == TYPES - 1)
                    ins.then_inc(kv_full, 1)
                    pe.wait_ge(q_out, t)
                    for kk in range(KK):
                        for y in range(TYPES):
                            ins = pe.matmul(q_ps[:, 0:D], masked[:, kk, y, :], weights[:, 2, y, kk, :],
                                            start=kk == 0 and y == 0, stop=kk == KK - 1 and y == TYPES - 1)
                    ins.then_inc(q_full, 1)
                    if more:
                        turn_masked(t + 1)
                    pe.wait_ge(kv_out, t + 1)
                    for j in range(J):
                        n, o, rels = part(j)
                        if n == 0:
                            pe.wait_ge(v_out, t * 4)
                        else:
                            pe.wait_ge(k_out, t * 4 + (j - 3))
                        pe.matmul(r_ps[j % 4][:, :, :], kvT[:, n, o, :], blocks[:, n, o, rels, :], start=True, stop=True
                                  ).then_inc(r_full, 1)

                pe.wait_ge(loaded, 32)
                pe.wait_ge(blocked, 16 * 8 + 2)
                turn_masked(0)
                tiles(pe, tile)


def layer1_gnn(k):
    nc, a = k.nc, k.a
    H, CI = L1_HEADS, 2 * BATCH

    def dram(name, shape):
        return nc.dram_tensor(name, shape, F32, kind="Internal").ap()

    ktab, vtab, qtab = dram("l1_k", [RELS * NPAD, D]), dram("l1_v", [RELS * NPAD, D]), dram("l1_q", [NWIN, D])
    scores, alphas = dram("l1_scores", [H, EPAD]), dram("l1_alpha", [H, EPAD])
    with k.phase() as ph:
        index = ph.sb("row_index", [P, CHUNKS], I32)
        kinds = ph.sb("kinds", [P, TILES + 1, TYPES])
        gains = ph.sb("gains", [P, TILES, TYPES])
        with k.phase() as inner:
            etype, types = inner.sb("etype", [P, CHUNKS], I32), inner.sb("types", [P, TILES], I32)
            etype_f, src_f = inner.sb("etype_f", [P, CHUNKS]), inner.sb("src_f", [P, CHUNKS])
            types_f, skip = inner.sb("types_f", [P, TILES]), inner.sb("skip", [P, TYPES])
            loaded, chained, squashed = inner.sem("loaded"), inner.sem("chained"), inner.sem("squashed")
            with nc.Block() as block:

                @block.sync
                def _(sp):
                    for dst, src in ((etype, a["etype_lanes"]), (types, a["type_lanes"])):
                        sp.dma_start(dst[:, :], src).then_inc(loaded, 16)
                    sp.dma_start(skip[:, :], a["L1_gnn_skip"].to_broadcast([P, TYPES])).then_inc(loaded, 16)

                @block.scalar
                def _(act):
                    act.wait_ge(loaded, 48)
                    act.activation(skip[:, :], skip[:, :], ACT.Sigmoid).then_inc(squashed, 1)

                @block.vector
                def _(dve):
                    step = Chain(dve, chained)
                    dve.wait_ge(loaded, 48)
                    dve.tensor_copy(types_f[:, :], types[:, :])
                    dve.tensor_copy(etype_f[:, :], etype[:, :])
                    step(dve.tensor_copy(src_f[:, :], k.src[:, :]))
                    dve.scalar_tensor_tensor(index[:, :], etype_f[:, :], float(NPAD), src_f[:, :], ALU.mult, ALU.add)
                    dve.memset(kinds[:, TILES, :], 0.0)
                    for y in range(TYPES):
                        ins = dve.tensor_scalar(kinds[:, 0:TILES, y], types_f[:, :], float(y), None, ALU.is_equal)
                    step(ins)
                    dve.wait_ge(squashed, 1)
                    step(dve.tensor_tensor(gains[:, :, :], kinds[:, 0:TILES, :],
                                           skip[:, :].unsqueeze(1).to_broadcast([P, TILES, TYPES]), ALU.mult))
        clear_tail(k, qtab)
        with k.phase() as inner:
            xn = inner.sb("xn", [P, TILES + 1, D])
            normalize(k, k.x, xn)
            typed_tables(k, xn, kinds, qtab, ktab, vtab)
        attention_scores(k, ktab, index, qtab, H, scores)
        segment_softmax(k, scores, H, alphas)
        accT = ph.sb("accT", [P, KK, NWIN])
        with k.phase() as inner:
            alpha = inner.sb("alpha", [P, CHUNKS // CI, H * CI])
            load_alphas(k, alphas, H, CI, alpha)
            aggregate(k, vtab, index, accT, heads=H,
                      alpha=lambda i, u: alpha[:, bass.ds(i, 1), :].rearrange("p o (h c) -> p (o h) c", h=H)
                      [:, :, u * BATCH:(u + 1) * BATCH])
        wa = ph.sb("wa", [P, TYPES, KK, D])

        def load(sp, sem):
            sp.dma_start(wa[:, :, :, :], a["L1_gnn_wa"]).then_inc(sem, 16)
            return 16

        def update(dve, t, product, step, emptied):
            xt = k.x[:, bass.ds(t, 1), :]
            for y in range(TYPES):
                dve.wait_ge(emptied, t * TYPES + (y + 3))
                gain = gains[:, bass.ds(t, 1), y]
                dve.scalar_tensor_tensor(xt, product(y), gain, xt, ALU.mult, ALU.add).then_inc(emptied, 1)

        with k.phase() as inner:
            project_sums(k, inner, accT, TYPES, load, wa, update, 0)


def layer2_gnn(k):
    nc, a = k.nc, k.a
    H, CI = 8, BATCH

    def dram(name, shape):
        return nc.dram_tensor(name, shape, F32, kind="Internal").ap()

    ktab, vtab, qtab = dram("l2_k", [NPAD, D]), dram("l2_v", [NPAD, D]), dram("l2_q", [NWIN, D])
    scores, biases, alphas = dram("l2_scores", [H, EPAD]), dram("l2_bias", [H, EPAD]), dram("l2_alpha", [H, EPAD])
    edge_bias(k, biases)
    clear_tail(k, qtab)
    with k.phase() as ph:
        xn = ph.sb("xn", [P, TILES, D])
        normalize(k, k.x, xn)
        w = ph.sb("kvq_w", [P, KK, 3 * D])

        def load(sp, sem):
            sp.dma_start(w[:, :, :], a["L2_gnn_kvq"]).then_inc(sem, 16)
            return 16

        def evacuate(dve, t, product, stage, step):
            return dve.tensor_copy(stage, product[:, :, :].rearrange("p b n -> p (b n)")[:, 0:3 * D])

        def store(sp, t, stage, sem):
            for n, tab in enumerate((ktab, vtab, qtab)):
                sp.dma_start(tab[bass.ds(t * P, P), :], stage[:, n * D:(n + 1) * D]).then_inc(sem, 16)

        with k.phase() as inner:
            node_tiles(k, inner, xn, 3 * D, load, w, evacuate, store, 3)
    attention_scores(k, ktab, k.src, qtab, H, scores)
    segment_softmax(k, scores, H, alphas, float(1.0 / np.sqrt(D // H)), biases)
    with k.phase() as ph:
        accT = ph.sb("accT", [P, KK, NWIN])
        with k.phase() as inner:
            alpha = inner.sb("alpha", [P, CHUNKS // CI, H * CI])
            load_alphas(k, alphas, H, CI, alpha)
            aggregate(k, vtab, k.src, accT, heads=H,
                      alpha=lambda i, u: alpha[:, bass.ds(i * 2 + u, 1), :].rearrange("p o (h j) -> p (o h) j", h=H))
        wo, bo = ph.sb("wo", [P, 1, KK, D]), ph.sb("bo", [P, D])

        def load(sp, sem):
            sp.dma_start(wo[:, 0, :, :], a["L2_gnn_Wo"]).then_inc(sem, 16)
            sp.dma_start(bo[:, :], a["L2_gnn_bo"].to_broadcast([P, D])).then_inc(sem, 16)
            return 32

        def update(dve, t, product, step, emptied):
            xt = k.x[:, bass.ds(t, 1), :]
            step(dve.tensor_tensor(xt, xt, bo[:, :], ALU.add))
            dve.tensor_tensor(xt, product(0), xt, ALU.add).then_inc(emptied, 1)

        with k.phase() as inner:
            project_sums(k, inner, accT, 1, load, wo, update, 1)


def layer3_gnn(k):
    nc, a = k.nc, k.a

    def dram(name, shape):
        return nc.dram_tensor(name, shape, F32, kind="Internal").ap()

    htab, dtab = dram("l3_h", [NPAD, D]), dram("l3_d", [NWIN, 1])
    scores, alphas = dram("l3_scores", [1, EPAD]), dram("l3_alpha", [1, EPAD])
    with k.phase() as ph:
        s_nodes = ph.sb("s_nodes", [P, TILES])
        xn = ph.sb("xn", [P, TILES, D])
        normalize(k, k.x, xn)
        wt, wo, att = ph.sb("w_t", [P, KK, D + 2]), ph.sb("w_o", [P, KK, D]), ph.sb("att", [P, KK, 2])
        load_small(k, [(wt[:, :, 0:D], a["L3_gnn_WT"]), (wo[:, :, :], a["L3_gnn_W"]), (att[:, :, :], a["L3_gnn_att"])])
        with k.phase() as inner:
            zeros, zeroed, stored = inner.sb("zeros", [P, 1]), inner.sem("zeroed"), inner.sem("stored")
            ps, folded, copied = inner.ps("folded", [P, 512]), inner.sem("folded"), inner.sem("copied")
            with nc.Block() as block:

                @block.tensor
                def _(pe):
                    for kk in range(KK):
                        for o in range(KK):
                            ins = pe.matmul(ps[:, 2 * kk:2 * kk + 2], wo[:, o, kk * P:(kk + 1) * P], att[:, o, :],
                                            start=o == 0, stop=o == KK - 1)
                    ins.then_inc(folded, 1)

                @block.vector
                def _(dve):
                    dve.memset(zeros[:, :], 0.0).then_inc(zeroed, 1)
                    dve.wait_ge(folded, 1)
                    for kk in range(KK):
                        dve.tensor_copy(wt[:, kk, D:D + 2], ps[:, 2 * kk:2 * kk + 2])
                    dve.tensor_tensor(k.x[:, :, :], k.x[:, :, :], xn[:, :, :], ALU.add).then_inc(copied, 1)
                    dve.wait_ge(copied, 1)

                @block.sync
                def _(sp):
                    sp.wait_ge(zeroed, 1)
                    sp.dma_start(dtab[NPAD:NWIN, :], zeros[:, :]).then_inc(stored, 16)
                    sp.wait_ge(stored, 16)

        def load(sp, sem):
            return 0

        def evacuate(dve, t, product, stage, step):
            dve.tensor_copy(s_nodes[:, bass.ds(t, 1)], product[:, 0, D:D + 1])
            return dve.tensor_copy(stage, product[:, 0, 0:D + 2])

        def store(sp, t, stage, sem):
            for tab, lo, n in ((htab, 0, D), (dtab, D + 1, 1)):
                sp.dma_start(tab[bass.ds(t * P, P), :], stage[:, lo:lo + n]).then_inc(sem, 16)

        with k.phase() as inner:
            node_tiles(k, inner, xn, D + 2, load, wt, evacuate, store, 2)
        gat_scores(k, s_nodes, dtab, scores)
    segment_softmax(k, scores, 1, alphas, more_loops=True)
    with k.phase() as ph:
        accT = ph.sb("accT", [P, KK, NWIN])
        with k.phase() as inner:
            alpha = inner.sb("alpha", [P, CHUNKS // 62, 62])
            load_alphas(k, alphas, 1, 62, alpha)
            aggregate(k, htab, k.src, accT, weights=alpha[:, :, :].rearrange("p g c -> p (g c)"))
        bias = ph.sb("bias", [P, D])

        def load(sp, sem):
            sp.dma_start(bias[:, :], a["L3_gnn_bias"].to_broadcast([P, D])).then_inc(sem, 16)
            return 16

        def update(dve, t, tile, step):
            xt = k.x[:, bass.ds(t, 1), :]
            step(dve.tensor_tensor(tile, tile, bias[:, :], ALU.add))
            return dve.scalar_tensor_tensor(xt, tile, 0.0, xt, ALU.max, ALU.add)

        with k.phase() as inner:
            from_sums(k, inner, accT, load, update, links=1)


def gat_scores(k, s_nodes, dtab, scores):
    nc = k.nc
    with k.phase() as ph:
        lanes = ph.sb("src_lanes", [P, 2, BATCH * P])
        hot_lane = ph.sb("hot_lane", [P, 2, BATCH, P])
        hot_tile = ph.sb("hot_tile", [P, 2, BATCH, TILES])
        d_all = ph.sb("d_all", [P, NWIN])
        s_edges, d_edges = ph.sb("s_edges", [P, 2, BATCH]), ph.sb("d_edges", [P, 2, BATCH])
        junk = ph.sb("junk", [P, 2, BATCH, P])
        sc = ph.sb("sc", [P, CHUNKS])
        kept = ph.sb("kept", [62, BATCH, P])
        by_lane = [ph.ps(f"by_lane{u}", [P, 512]) for u in range(2)]
        ps = [ph.ps(f"turned{q}", [P, 512]) for q in range(2)]
        d_in, lane_hot, by_lane_full, chained = (ph.sem(n) for n in ("d_in", "lane_hot", "by_lane_full", "chained"))
        scored, full, emptied, stored = (ph.sem(n) for n in ("scored", "full", "emptied", "stored"))
        lanes_in = [ph.sem(f"lanes_in{u}") for u in range(2)]
        with nc.Block() as block:

            @block.sync
            def _(sp):
                sp.dma_start(d_all[:, :], dtab.rearrange("n o -> o n").to_broadcast([P, NWIN])).then_inc(d_in, 16)
                with sp.Fori(0, BATCHES // 2) as i:
                    for u in range(2):
                        c = i * (2 * BATCH) + u * BATCH
                        sp.wait_ge(lane_hot, i * 2 + (u + 1))
                        sp.dma_start(lanes[:, u, :], k.lane_row[:, bass.ds(c * P, BATCH * P)].to_broadcast([P, BATCH * P])
                                     ).then_inc(lanes_in[u], 16)
                sp.wait_ge(emptied, BATCH)
                sp.dma_start(edge_order(scores, BATCH, 62), kept[:, :, :]).then_inc(stored, 16)
                sp.wait_ge(stored, 16)

            @block.tensor
            def _(pe):
                with pe.Fori(0, BATCHES // 2) as i:
                    for u in range(2):
                        b = i * 2 + u
                        pe.wait_ge(lane_hot, b + 3)
                        pe.wait_ge(scored, b + 1)
                        for j in range(BATCH):
                            ins = pe.matmul(by_lane[u][:, j * TILES:(j + 1) * TILES], hot_lane[:, u, j, :], s_nodes[:, :],
                                            start=True, stop=True)
                        ins.then_inc(by_lane_full, 1)
                pe.wait_ge(scored, 2 + BATCHES)
                for g in range(BATCH):
                    if g >= 2:
                        pe.wait_ge(emptied, g - 1)
                    pe.transpose(ps[g % 2][0:62, 0:P], sc[:, g * 62:(g + 1) * 62], k.ident[:, :]).then_inc(full, 1)

            @block.scalar
            def _(act):
                for g in range(BATCH):
                    act.wait_ge(full, g + 1)
                    act.activation(kept[:, g, :], ps[g % 2][0:62, 0:P], ACT.Copy).then_inc(emptied, 1)

            @block.vector
            def _(dve):
                base = dve.alloc_register(ph._name("window_base"))
                step = Chain(dve, chained)
                dve.sem_inc(scored, 2)
                dve.sem_inc(lane_hot, 2)
                dve.wait_ge(d_in, 16)

                def compare(i, u):
                    dve.wait_ge(lanes_in[u], (i + 1) * 16)
                    dve.tensor_scalar(hot_lane[:, u, :, :].rearrange("p j e -> p (j e)"), lanes[:, u, :], k.lane_col[:, 0:1],
                                      None, ALU.is_equal).then_inc(lane_hot, 1)

                def score(i, u):
                    b = i * 2 + u
                    c = i * (2 * BATCH) + u * BATCH
                    step.base, step.n = b * 4, 0
                    for j in range(BATCH):
                        dve.reg_load(base, k.dst[0:1, bass.ds(c + j, 1)])
                        window = d_all[:, bass.ds(nc.snap(base, min_val=0, max_val=NPAD), P)]
                        dve.scalar_tensor_tensor(junk[:, u, j, :], k.lane_iota[:, :], k.rel[:, bass.ds(c + j, 1)], window,
                                                 ALU.is_equal, ALU.mult, accum_out=d_edges[:, u, j:j + 1])
                    step(hot_by(dve, k, hot_tile[:, u, :, :], k.src_tile[:, bass.ds(c, BATCH)], TILES))
                    dve.wait_ge(by_lane_full, b + 1)
                    step(dve.tensor_tensor(hot_tile[:, u, :, :].rearrange("p j t -> p (j t)"),
                                           hot_tile[:, u, :, :].rearrange("p j t -> p (j t)"),
                                           by_lane[u][:, 0:BATCH * TILES], ALU.mult))
                    step(dve.tensor_reduce(s_edges[:, u, :], hot_tile[:, u, :, :], AX.X, ALU.add))
                    step(dve.tensor_tensor(d_edges[:, u, :], d_edges[:, u, :], s_edges[:, u, :], ALU.add))
                    dve.scalar_tensor_tensor(sc[:, bass.ds(c, BATCH)], d_edges[:, u, :], 0.2, d_edges[:, u, :],
                                             ALU.mult, ALU.max).then_inc(scored, 1)

                last = BATCHES // 2 - 1
                compare(0, 0)
                with dve.Fori(0, last) as i:
                    compare(i, 1)
                    score(i, 0)
                    compare(i + 1, 0)
                    score(i, 1)
                compare(last, 1)
                score(last, 0)
                score(last, 1)


SHARED0 = Experts(1, [D, 256, 128, D])
EXPERTS0 = Experts(4, [D, 128, 64, D])
EXPERTS1 = Experts(8, [D, 512, D])
EXPERTS2 = Experts(8, [D, 1024, D])
EXPERTS3 = Experts(8, [D, 256, 256, D])


def layer0_ffn(k):
    a = k.a
    with k.phase() as ph:
        xT, gates, logits = ph.sb("xT", [P, KK, NPAD]), ph.sb("gates", [P, TILES, 4]), ph.sb("logits", [P, TILES, 4])
        with k.phase() as inner:
            xn = inner.sb("xn", [P, TILES, D])
            normalize(k, k.x, xn)
            routed(k, xn, xT, a["L0_ffn_gW"], 4, logits)
        gate_weights(k, logits, gates, 4, "top2_of_softmax", a["L0_ffn_gb"])
        bs, be = ph.sb("shared_bias", [P, 1, len(SHARED0.chunks)]), ph.sb("expert_bias", [P, 4, len(EXPERTS0.chunks)])
        load_small(k, [(bs[:, :, :], a["L0_ffn_sb"]), (be[:, :, :], a["L0_ffn_eb"])])
        mixture(k, xT, SHARED0, a["L0_ffn_sW"], a["L0_ffn_sb3"], ACT.Relu, bs)
        mixture(k, xT, EXPERTS0, a["L0_ffn_eW"], a["L0_ffn_eb3"], ACT.Relu, be, gates=gates)


def layer1_ffn(k):
    a = k.a
    with k.phase() as ph:
        xT, gates, logits = ph.sb("xT", [P, KK, NPAD]), ph.sb("gates", [P, TILES, 8]), ph.sb("logits", [P, TILES, 8])
        with k.phase() as inner:
            xn = inner.sb("xn", [P, TILES, D])
            normalize(k, k.x, xn)
            normalize(k, xn, xn, gamma=a["L1_ffn_gamma"], beta=a["L1_ffn_beta"])
            routed(k, xn, xT, a["L1_ffn_Wr"], 8, logits)
        gate_weights(k, logits, gates, 8, "top2", a["L1_ffn_br"])
        b1 = ph.sb("expert_bias", [P, 8, len(EXPERTS1.chunks)])
        load_small(k, [(b1[:, :, :], a["L1_ffn_b1"])])
        mixture(k, xT, EXPERTS1, a["L1_ffn_W"], a["L1_ffn_b2"], ACT.Gelu, b1, gates=gates)


def layer2_ffn(k):
    nc, a = k.nc, k.a
    E, C = 8, len(EXPERTS2.chunks)
    with k.phase() as ph:
        xT, gates, logits = ph.sb("xT", [P, KK, NPAD]), ph.sb("gates", [P, TILES, E]), ph.sb("logits", [P, TILES, E])
        with k.phase() as inner:
            xn = inner.sb("xn", [P, TILES, D])
            normalize(k, k.x, xn)
            routed(k, xn, None, a["L2_ffn_Wr"], E, logits)
            normalize(k, xn, xn)
            unused = inner.sb("unused", [P, TILES, E])
            routed(k, xn, xT, a["L2_ffn_Wr"], E, unused)
        gate_weights(k, logits, gates, E, "top2_renormalized", a["L2_ffn_br"])
        b1, g, b = ph.sb("b1", [P, E, C]), ph.sb("ln_g", [P, KK, E]), ph.sb("ln_b", [P, KK, E])
        load_small(k, [(b1[:, :, :], a["L2_ffn_b1"]), (g[:, :, :], a["L2_ffn_ln_g"]), (b[:, :, :], a["L2_ffn_ln_b"])])
        with k.phase() as inner:
            H = EXPERTS2.dims[1]
            w = inner.sb("w1", [P, 2, KK * H])
            folded = [inner.ps(f"folded{s}", [P, 512]) for s in range(2)]
            w_in = [inner.sem(f"w_in{s}") for s in range(2)]
            multiplied, added = inner.sem("multiplied"), inner.sem("added")
            with nc.Block() as block:

                @block.sync
                def _(sp):
                    for e in range(E):
                        if e >= 2:
                            sp.wait_ge(multiplied, e - 1)
                        sp.dma_start(w[:, e % 2, :], a["L2_ffn_W"][e, :, 0:KK * H]).then_inc(w_in[e % 2], 16)

                @block.tensor
                def _(pe):
                    for e in range(E):
                        pe.wait_ge(w_in[e % 2], 16 * (e // 2 + 1))
                        if e >= 2:
                            pe.wait_ge(added, e - 1)
                        for c in range(C):
                            for kk in range(KK):
                                ins = pe.matmul(folded[e % 2][:, c:c + 1], w[:, e % 2, kk * H + c * P:kk * H + (c + 1) * P],
                                                b[:, kk, e:e + 1], start=kk == 0, stop=kk == KK - 1)
                        ins.then_inc(multiplied, 1)

                @block.vector
                def _(dve):
                    for e in range(E):
                        dve.wait_ge(multiplied, e + 1)
                        dve.tensor_tensor(b1[:, e, :], b1[:, e, :], folded[e % 2][:, 0:C], ALU.add).then_inc(added, 1)
        mixture(k, xT, EXPERTS2, a["L2_ffn_W"], a["L2_ffn_b2"], ACT.Gelu, b1, gates=gates, prescale=g)


def layer3_ffn(k):
    nc, a = k.nc, k.a
    E, C = 8, len(EXPERTS3.chunks)
    with k.phase() as ph:
        xT, gates, logits = ph.sb("xT", [P, KK, NPAD]), ph.sb("gates", [P, TILES, E]), ph.sb("logits", [P, TILES, E])
        with k.phase() as inner:
            xn = inner.sb("xn", [P, TILES, D])
            normalize(k, k.x, xn)
            routed(k, xn, xT, a["L3_ffn_Wr"], E, logits)
        gate_weights(k, logits, gates, E, "softmax", a["L3_ffn_br"])
        b, g, be, m, v = (ph.sb(n, [P, E, C]) for n in ("b", "g", "be", "m", "v"))
        load_small(k, [(t[:, :, :], a[f"L3_ffn_{n}"]) for t, n in ((b, "b"), (g, "g"), (be, "be"), (m, "m"), (v, "v"))])
        with k.phase() as inner:
            chained, rooted = inner.sem("chained"), inner.sem("rooted")
            with nc.Block() as block:

                @block.vector
                def _(dve):
                    step = Chain(dve, chained)
                    dve.tensor_scalar(v[:, :, :], v[:, :, :], 1e-3, None, ALU.add).then_inc(rooted, 1)
                    dve.wait_ge(rooted, 2)
                    step(dve.reciprocal(v[:, :, :], v[:, :, :]))
                    step(dve.tensor_tensor(g[:, :, :], g[:, :, :], v[:, :, :], ALU.mult))
                    step(dve.tensor_tensor(b[:, :, :], b[:, :, :], m[:, :, :], ALU.subtract))
                    step(dve.tensor_tensor(b[:, :, :], b[:, :, :], g[:, :, :], ALU.mult))
                    step(dve.tensor_tensor(b[:, :, :], b[:, :, :], be[:, :, :], ALU.add))

                @block.scalar
                def _(act):
                    act.wait_ge(rooted, 1)
                    act.activation(v[:, :, :], v[:, :, :], ACT.Sqrt).then_inc(rooted, 1)
        mixture(k, xT, EXPERTS3, a["L3_ffn_W"], a["L3_ffn_bo"], ACT.Relu, b, scale=g, gates=gates)


LAYERS = [layer0_gnn, layer0_ffn, layer1_gnn, layer1_ffn, layer2_gnn, layer2_ffn, layer3_gnn, layer3_ffn]


def program(nc, a, out, upto=99):
    k = Kernel(nc, a)
    setup(k)
    for layer in LAYERS[:upto]:
        layer(k)
    with k.phase() as ph:
        stored = ph.sem("stored")
        with nc.Block() as block:

            @block.sync
            def _(sp):
                full = NODES // P
                sp.dma_start(out[0:full * P, :].rearrange("(t p) d -> p t d", p=P), k.x[:, 0:full, :]
                             ).then_inc(stored, 16)
                sp.dma_start(out[full * P:NODES, :], k.x[0:NODES - full * P, full, :]).then_inc(stored, 16)
                sp.wait_ge(stored, 32)




def lay_out(i):
    o = {}

    def padded(a, rows, fill=0):
        a = np.asarray(a)
        return np.concatenate([a, np.full((rows - a.shape[0],) + a.shape[1:], fill, a.dtype)])

    def lanes(a, fill=0):
        return np.ascontiguousarray(padded(a, EPAD, fill).reshape(CHUNKS, P).T)

    def halves(w):
        w = np.asarray(w)
        s = w.shape
        w = w.reshape(s[:-2] + (s[-2] // P, P, s[-1]))
        return np.ascontiguousarray(np.swapaxes(w, -3, -2))

    def row(b):
        return np.ascontiguousarray(np.asarray(b).reshape(1, -1))

    o["x_lanes"] = np.ascontiguousarray(padded(i["x"], NPAD).reshape(TILES, P, D).transpose(1, 0, 2))
    o["src_row"] = row(padded(i["src"], EPAD))
    o["src_lanes"] = lanes(i["src"])
    o["dst_lanes"] = lanes(i["dst"], NO_NODE)
    o["weight_lanes"] = lanes(i["edge_weight"])
    o["L0_gnn_w"] = halves(i["L0_gnn_w"])
    o["L0_gnn_b"] = row(i["L0_gnn_b"])

    def packed(*matrices):
        cols = []
        for w in matrices:
            w = np.asarray(w)
            w = w.reshape((-1,) + w.shape[-2:])
            rows = -(-w.shape[1] // P) * P
            w = np.concatenate([w, np.zeros((w.shape[0], rows - w.shape[1], w.shape[2]), w.dtype)], axis=1)
            cols.append(halves(w).reshape(w.shape[0], P, -1))
        return np.ascontiguousarray(np.concatenate(cols, axis=2))

    def columns(*vectors):
        cols = []
        for v in vectors:
            v = np.asarray(v)
            v = v.reshape(-1, v.shape[-1])
            n = -(-v.shape[1] // P) * P
            v = np.concatenate([v, np.zeros((v.shape[0], n - v.shape[1]), v.dtype)], axis=1)
            cols.append(v.reshape(v.shape[0], -1, P).transpose(2, 0, 1))
        return np.ascontiguousarray(np.concatenate(cols, axis=2))

    def typed(name):
        return halves(i[name]).transpose(1, 0, 2, 3)

    def by_head(relation, order):
        r = np.asarray(relation).transpose(order)
        return np.ascontiguousarray(r.reshape(KK, P, r.shape[2], r.shape[3]).transpose(1, 0, 2, 3))

    o["etype_lanes"] = lanes(i["edge_type_8"])
    o["type_lanes"] = np.ascontiguousarray(padded(i["node_type_4"], NPAD).reshape(TILES, P).T)
    o["L1_gnn_w"] = np.ascontiguousarray(np.stack([typed(f"L1_gnn_{n}_linears") for n in "kvq"], axis=1))
    o["L1_gnn_wa"] = np.ascontiguousarray(typed("L1_gnn_a_linears"))
    o["L1_gnn_att"] = by_head(i["L1_gnn_relation_att"], (1, 3, 0, 2))
    o["L1_gnn_msg"] = by_head(i["L1_gnn_relation_msg"], (1, 2, 0, 3))
    pri = np.repeat(np.asarray(i["L1_gnn_relation_pri"]).T, P // 2, axis=0)
    o["L1_gnn_pri"] = np.ascontiguousarray(pri.reshape(KK, P, -1).transpose(1, 0, 2))
    o["L1_gnn_skip"] = row(i["L1_gnn_skip"])
    o["dst_rows"] = np.ascontiguousarray(padded(i["dst"], EPAD, NO_NODE).reshape(P, CHUNKS))
    attr = padded(i["edge_attr_64"], EPAD).T
    o["attr"] = np.ascontiguousarray(np.concatenate([attr[:, :EPAD // 2], attr[:, EPAD // 2:]]))
    o["L2_gnn_kvq"] = np.ascontiguousarray(np.concatenate([halves(i[f"L2_gnn_W{n}"]) for n in "kvq"], axis=2))
    o["L2_gnn_W1"] = np.concatenate([np.asarray(i["L2_gnn_W1"])] * 2)
    o["L2_gnn_W2"] = halves(i["L2_gnn_W2"])
    o["L2_gnn_b1"] = np.ascontiguousarray(np.asarray(i["L2_gnn_b1"]).reshape(KK, P).T)
    o["L2_gnn_b2"] = np.asarray(i["L2_gnn_b2"]).reshape(-1, 1)
    o["L2_gnn_Wo"], o["L2_gnn_bo"] = halves(i["L2_gnn_Wo"]), row(i["L2_gnn_bo"])
    o["L3_gnn_W"], o["L3_gnn_WT"] = halves(i["L3_gnn_W"]), halves(np.asarray(i["L3_gnn_W"]).T)
    o["L3_gnn_att"] = halves(np.stack([np.asarray(i["L3_gnn_a_src"]), np.asarray(i["L3_gnn_a_dst"])], axis=1))
    o["L3_gnn_bias"] = row(i["L3_gnn_bias"])
    o["L0_ffn_gW"], o["L0_ffn_gb"] = halves(i["L0_ffn_gW"]), row(i["L0_ffn_gb"])
    o["L0_ffn_sW"] = packed(i["L0_ffn_sW1"], i["L0_ffn_sW2"], i["L0_ffn_sW3"])
    o["L0_ffn_eW"] = packed(i["L0_ffn_eW1"], i["L0_ffn_eW2"], i["L0_ffn_eW3"])
    o["L0_ffn_sb"], o["L0_ffn_sb3"] = columns(i["L0_ffn_sb1"], i["L0_ffn_sb2"]), row(i["L0_ffn_sb3"])
    o["L0_ffn_eb"], o["L0_ffn_eb3"] = columns(i["L0_ffn_eb1"], i["L0_ffn_eb2"]), row(i["L0_ffn_eb3"])
    o["L1_ffn_gamma"], o["L1_ffn_beta"] = row(i["L1_ffn_gamma"]), row(i["L1_ffn_beta"])
    o["L1_ffn_Wr"], o["L1_ffn_br"] = halves(i["L1_ffn_Wr"]), row(i["L1_ffn_br"])
    o["L1_ffn_W"] = packed(i["L1_ffn_W1"], i["L1_ffn_W2"])
    o["L1_ffn_b1"], o["L1_ffn_b2"] = columns(i["L1_ffn_b1"]), row(i["L1_ffn_b2"])
    o["L2_ffn_Wr"], o["L2_ffn_br"] = halves(i["L2_ffn_Wr"]), row(i["L2_ffn_br"])
    o["L2_ffn_W"] = packed(i["L2_ffn_W1"], i["L2_ffn_W2"])
    o["L2_ffn_b1"], o["L2_ffn_b2"] = columns(i["L2_ffn_b1"]), row(i["L2_ffn_b2"])
    for n in ("ln_g", "ln_b"):
        o[f"L2_ffn_{n}"] = np.ascontiguousarray(columns(i[f"L2_ffn_{n}"]).transpose(0, 2, 1))
    o["L3_ffn_Wr"], o["L3_ffn_br"] = halves(i["L3_ffn_Wr"]), row(i["L3_ffn_br"])
    o["L3_ffn_W"] = packed(i["L3_ffn_W1"], i["L3_ffn_W2"], i["L3_ffn_Wo"])
    o["L3_ffn_bo"] = row(i["L3_ffn_bo"])
    for n in ("b", "g", "be", "m", "v"):
        o[f"L3_ffn_{n}"] = columns(i[f"L3_ffn_{n}1"], i[f"L3_ffn_{n}2"])
    return o


def kernel(**inputs):
    import concourse.bacc as bacc
    from concourse.bass_utils import run_bass_kernel_spmd as run

    nc = bacc.Bacc("TRN2", target_bir_lowering=False, num_devices=1)
    arrays = lay_out(inputs)
    a = {n: nc.dram_tensor(f"in_{n}", v.shape, mybir.dt.from_np(v.dtype), kind="ExternalInput").ap()
         for n, v in arrays.items()}
    out = nc.dram_tensor("out_x", (NODES, D), F32, kind="ExternalOutput").ap()
    program(nc, a, out)
    r = run(nc, [{f"in_{n}": v for n, v in arrays.items()}], core_ids=[0])
    return r.results[0]["out_x"]
```

```python
from contextlib import ExitStack

import numpy as np

import concourse.bass as bass
from concourse import mybir

F32 = mybir.dt.float32
BF16 = mybir.dt.bfloat16
I32 = mybir.dt.int32
ACT = mybir.ActivationFunctionType
ALU = mybir.AluOpType
AX = mybir.AxisListType

P = 128
NODES, EDGES, D = 3125, 103125, 256
KK = D // P
TILES = -(-NODES // P)
NPAD = TILES * P
NWIN = NPAD + P
CHUNKS = -(-EDGES // P)
EPAD = CHUNKS * P
BATCH = 13
BATCHES = CHUNKS // BATCH
PAIRS = [(j, min(2, BATCH - j)) for j in range(0, BATCH, 2)]
UNROLL = 5
GROUP = UNROLL * P
HALF = GROUP // 2
BIG = 1.0e38
NO_NODE = 8191


class Kernel:

    def __init__(self, nc, a):
        self.nc, self.a = nc, a
        self.uid = 0

    def phase(self):
        return Phase(self)


class Phase:

    def __init__(self, k):
        self.k, self.nc, self.stack, self.sems = k, k.nc, ExitStack(), []

    def __enter__(self):
        return self

    def __exit__(self, *exc):
        self.stack.close()
        if exc[0] is None:
            self.nc.clear_and_free_semaphores(self.sems)
            self.nc.all_engine_barrier()

    def _name(self, name):
        self.k.uid += 1
        return f"{name}_{self.k.uid}"

    def sb(self, name, shape, dt=F32):
        return self.stack.enter_context(self.nc.sbuf_tensor(self._name(name), shape, dt))

    def ps(self, name, shape, dt=F32):
        return self.stack.enter_context(self.nc.psum_tensor(self._name(name), shape, dt))

    def sem(self, name):
        s = self.nc.alloc_semaphore(self._name(name))
        self.sems.append(s)
        return s


class Chain:

    def __init__(self, eng, sem):
        self.eng, self.sem, self.n, self.base = eng, sem, 0, 0

    def __call__(self, ins):
        self.n += 1
        ins.then_inc(self.sem, 1)
        self.eng.wait_ge(self.sem, self.base + self.n)


def hot_by(eng, k, out, values, width):
    shape = [P, BATCH, width]
    return eng.tensor_tensor(out, k.lane_iota[:, 0:width].unsqueeze(1).to_broadcast(shape),
                             values.unsqueeze(2).to_broadcast(shape), ALU.is_equal)


def row_table(k, lanes, row):
    blocks = [(c, min(P, CHUNKS - c)) for c in range(0, CHUNKS, P)]
    with k.phase() as ph:
        turned = [ph.ps(f"turned{q}", [P, P]) for q in range(len(blocks))]
        kept = ph.sb("kept", [P, len(blocks), P], BF16)
        full, copied, stored = ph.sem("full"), ph.sem("copied"), ph.sem("stored")
        with k.nc.Block() as block:

            @block.tensor
            def _(pe):
                for q, (c, n) in enumerate(blocks):
                    pe.transpose(turned[q][0:n, :], lanes[:, c:c + n], k.ident[:, :]).then_inc(full, 1)

            @block.scalar
            def _(act):
                for q, (c, n) in enumerate(blocks):
                    act.wait_ge(full, q + 1)
                    act.activation(kept[0:n, q, :], turned[q][0:n, :], ACT.Copy).then_inc(copied, 1)

            @block.sync
            def _(sp):
                for q, (c, n) in enumerate(blocks):
                    sp.wait_ge(copied, q + 1)
                    sp.dma_start(row[:, c * P:(c + n) * P].rearrange("o (c e) -> (o c) e", e=P), kept[0:n, q, :]
                                 ).then_inc(stored, 16)
                sp.wait_ge(stored, 16 * len(blocks))


def setup(k):
    nc, a = k.nc, k.a
    k.x = nc.alloc_sbuf_tensor("x_res", [P, TILES, D], F32)
    k.ident = nc.alloc_sbuf_tensor("ident", [P, P], F32)
    k.lane_iota = nc.alloc_sbuf_tensor("lane_iota", [P, P], F32)
    k.lane_col = nc.alloc_sbuf_tensor("lane_col", [P, 1], F32)
    k.rel_row, k.src_lane_row, k.dst_lane_row = (nc.dram_tensor(n, [1, EPAD], BF16, kind="Internal").ap()
                                                 for n in ("rel_row", "src_lane_row", "dst_lane_row"))
    k.src_tile = nc.alloc_sbuf_tensor("src_tile", [P, CHUNKS], F32)
    k.dst_tile = nc.alloc_sbuf_tensor("dst_tile", [P, CHUNKS], F32)
    k.src = nc.alloc_sbuf_tensor("src_idx", [P, CHUNKS], I32)
    k.dst = nc.alloc_sbuf_tensor("dst_idx", [P, CHUNKS], I32)
    k.rel = nc.alloc_sbuf_tensor("rel_pos", [P, CHUNKS], F32)
    k.dinv = nc.alloc_sbuf_tensor("dinv", [P, TILES], F32)
    k.weight = nc.alloc_sbuf_tensor("edge_w", [P, CHUNKS], F32)
    with k.phase() as outer:
        src_lane, dst_lane = outer.sb("src_lane", [P, CHUNKS]), outer.sb("dst_lane", [P, CHUNKS])
        edge_tables(k, src_lane, dst_lane)
        for lanes, table in ((k.rel, k.rel_row), (src_lane, k.src_lane_row), (dst_lane, k.dst_lane_row)):
            row_table(k, lanes, table)


def split(step, dve, value, rest, parts):
    step(dve.tensor_copy(parts[0], value))
    step(dve.tensor_tensor(rest, value, parts[0], ALU.subtract))
    step(dve.tensor_copy(parts[1], rest))
    step(dve.tensor_tensor(rest, rest, parts[1], ALU.subtract))
    step(dve.tensor_copy(parts[2], rest))


def edge_tables(k, src_lane, dst_lane):
    nc, a = k.nc, k.a
    with k.phase() as ph:
        loaded, made, chained = ph.sem("loaded"), ph.sem("made"), ph.sem("chained")
        based, hot, summed = ph.sem("based"), ph.sem("hot"), ph.sem("summed")
        hot_free, tiled = ph.sem("hot_free"), ph.sem("tiled")
        dstf, basef = ph.sb("dstf", [P, CHUNKS]), ph.sb("basef", [1, CHUNKS])
        low_of = ph.sb("low_of", [P, CHUNKS])
        weight_parts = ph.sb("weight_parts", [P, 3, CHUNKS], BF16)
        ints = ph.sb("ints", [P, CHUNKS], I32)
        ones = ph.sb("ones", [1, P])
        hot_lane = ph.sb("hot_lane", [P, 2, BATCH, P], BF16)
        hot_tile = ph.sb("hot_tile", [P, BATCH, TILES], BF16)
        tile_w = ph.sb("tile_w", [P, 2, 3, BATCH, TILES], BF16)
        degree = ph.ps("degree", [P, 512])
        bases = ph.ps("bases", [P, 2, 512])
        deg = ph.sb("deg", [P, TILES])
        has = ph.sb("has", [P, TILES])
        HC = CHUNKS // 2
        with nc.Block() as block:

            @block.sync
            def _(sp):
                sp.dma_start(k.dst[:, :], a["dst_lanes"]).then_inc(loaded, 16)
                sp.dma_start(k.weight[:, :], a["weight_lanes"]).then_inc(loaded, 16)
                sp.dma_start(k.src[:, :], a["src_lanes"]).then_inc(loaded, 16)
                sp.dma_start(k.x[:, :, :], a["x_lanes"]).then_inc(loaded, 16)
                sp.wait_ge(loaded, 64)

            @block.gpsimd
            def _(pool):
                pool.memset(ones[:, :], 1.0).then_inc(made, 1)
                pool.memset(k.ident[:, :], 0.0).then_inc(made, 1)
                pool.iota(k.lane_iota[:, :], [[1, P]], base=0, channel_multiplier=0,
                          allow_small_or_imprecise_dtypes=True).then_inc(made, 1)
                pool.iota(k.lane_col[:, :], [[0, 1]], base=0, channel_multiplier=1,
                          allow_small_or_imprecise_dtypes=True).then_inc(made, 1)
                pool.wait_ge(made, 4)
                pool.affine_select(out=k.ident[:, :], in_=k.ident[:, :], compare_op=ALU.not_equal, fill=1.0,
                                   base=0, pattern=[[-1, P]], channel_multiplier=1).then_inc(made, 1)

            @block.vector
            def _(dve):
                step = Chain(dve, chained)
                dve.wait_ge(loaded, 64)
                dve.wait_ge(made, 4)
                step(dve.tensor_copy(dstf[:, :], k.dst[:, :]))
                dve.tensor_copy(basef[0:1, :], dstf[0:1, :]).then_inc(based, 1)
                for nodes, tile_of, lane_of in ((k.src, k.src_tile, src_lane), (k.dst, k.dst_tile, dst_lane)):
                    step(dve.tensor_scalar(ints[:, :], nodes[:, :], 7, None, ALU.logical_shift_right))
                    step(dve.tensor_copy(tile_of[:, :], ints[:, :]))
                    step(dve.tensor_copy(low_of[:, :], nodes[:, :]))
                    step(dve.scalar_tensor_tensor(lane_of[:, :], tile_of[:, :], -float(P), low_of[:, :], ALU.mult, ALU.add))
                split(step, dve, k.weight[:, :], low_of[:, :], [weight_parts[:, n, :] for n in range(3)])
                with dve.Fori(0, BATCHES // 2) as i:
                    for u in range(2):
                        b = i * 2 + u
                        c = i * (2 * BATCH) + u * BATCH
                        dve.wait_ge(hot_free, b + 1)
                        hot_by(dve, k, hot_lane[:, u, :, :], src_lane[:, bass.ds(c, BATCH)], P)
                        hot_by(dve, k, hot_tile[:, :, :], k.src_tile[:, bass.ds(c, BATCH)], TILES).then_inc(tiled, 1)
                        dve.wait_ge(tiled, b + 1)
                        for n in range(3):
                            w = weight_parts[:, n, bass.ds(c, BATCH)].unsqueeze(2).to_broadcast([P, BATCH, TILES])
                            ins = dve.tensor_tensor(tile_w[:, u, n, :, :], hot_tile[:, :, :], w, ALU.mult)
                        ins.then_inc(hot, 1)
                        dve.wait_ge(hot, b + 1)
                dve.wait_ge(summed, 1)
                for h in range(2):
                    step(dve.tensor_tensor(k.rel[:, h * HC:(h + 1) * HC], dstf[:, h * HC:(h + 1) * HC],
                                           bases[:, h, 0:HC], ALU.subtract))
                dve.wait_ge(summed, 2)
                step(dve.tensor_copy(deg[:, :], degree[:, 0:TILES]))
                step(dve.tensor_scalar(has[:, :], deg[:, :], 0.0, None, ALU.is_gt))
                step(dve.tensor_scalar(low_of[:, 0:TILES], has[:, :], -1.0, 1.0, ALU.mult, ALU.add))
                step(dve.tensor_tensor(deg[:, :], deg[:, :], low_of[:, 0:TILES], ALU.add))
                step(dve.reciprocal(deg[:, :], deg[:, :]))
                dve.wait_ge(made, 5)
                dve.tensor_copy(deg[:, :], deg[:, :]).then_inc(made, 1)
                dve.wait_ge(made, 7)
                step(dve.tensor_tensor(k.dinv[:, :], k.dinv[:, :], has[:, :], ALU.mult))

            @block.scalar
            def _(act):
                act.wait_ge(made, 6)
                act.activation(k.dinv[:, :], deg[:, :], ACT.Sqrt).then_inc(made, 1)

            @block.tensor
            def _(pe):
                pe.sem_inc(hot_free, 2)
                pe.wait_ge(based, 1)
                for h in range(2):
                    ins = pe.matmul(bases[:, h, 0:HC], ones[0:1, :], basef[0:1, h * HC:(h + 1) * HC],
                                    start=True, stop=True)
                ins.then_inc(summed, 1)

                def add(u, first, last):
                    for j in range(BATCH):
                        for n in range(3):
                            ins = pe.matmul(degree[:, 0:TILES], hot_lane[:, u, j, :], tile_w[:, u, n, j, :],
                                            start=first and j == n == 0, stop=last and j == BATCH - 1 and n == 2)
                    return ins

                for n in range(2):
                    pe.wait_ge(hot, n + 1)
                    add(n % 2, n == 0, False).then_inc(hot_free, 1)
                with pe.Fori(1, BATCHES // 2 - 1) as i:
                    for u in range(2):
                        pe.wait_ge(hot, i * 2 + (u + 1))
                        add(u, False, False).then_inc(hot_free, 1)
                for n in range(BATCHES - 2, BATCHES):
                    pe.wait_ge(hot, n + 1)
                    ins = add(n % 2, False, n == BATCHES - 1)
                ins.then_inc(summed, 1)



def normalize(k, src, out, eps=1e-5, gamma=None, beta=None):
    nc = k.nc
    with k.phase() as ph:
        stats = ph.sb("stats", [P, TILES, 6])
        mv = ph.sb("mv", [P, TILES, 2])
        std = ph.sb("std", [P, TILES])
        counted, aggregated, rooted, done = (ph.sem(n) for n in ("counted", "aggregated", "rooted", "done"))
        loaded = ph.sem("affine_loaded")
        if gamma is not None:
            gb = ph.sb("gamma_beta", [P, 2, D])
        with nc.Block() as block:
            if gamma is not None:
                @block.sync
                def _(sp):
                    sp.dma_start(gb[:, 0, :], gamma.to_broadcast([P, D])).then_inc(loaded, 16)
                    sp.dma_start(gb[:, 1, :], beta.to_broadcast([P, D])).then_inc(loaded, 16)

            @block.vector
            def _(dve):
                for t in range(TILES):
                    dve.bn_stats(stats[:, t, :], src[:, t, :]).then_inc(counted, 1)
                for t in range(TILES):
                    dve.wait_ge(counted, t + 1)
                    ins = dve.bn_aggr(mv[:, t, :], stats[:, t, :])
                ins.then_inc(aggregated, 1)
                dve.wait_ge(aggregated, 1)
                dve.tensor_scalar(std[:, :], mv[:, :, 1], eps, None, ALU.add).then_inc(rooted, 1)
                dve.wait_ge(rooted, 2)
                dve.reciprocal(std[:, :], std[:, :]).then_inc(rooted, 1)
                dve.wait_ge(rooted, 3)
                for t in range(TILES):
                    dve.tensor_scalar(out[:, t, :], src[:, t, :], mv[:, t, 0:1], std[:, t:t + 1],
                                      ALU.subtract, ALU.mult).then_inc(done, 1)
                if gamma is not None:
                    dve.wait_ge(loaded, 32)
                    dve.wait_ge(done, TILES)
                    g = gb[:, 0, :].unsqueeze(1).to_broadcast([P, TILES, D])
                    b = gb[:, 1, :].unsqueeze(1).to_broadcast([P, TILES, D])
                    dve.tensor_tensor(out[:, :, :], out[:, :, :], g, ALU.mult).then_inc(done, 1)
                    dve.wait_ge(done, TILES + 1)
                    dve.tensor_tensor(out[:, :, :], out[:, :, :], b, ALU.add).then_inc(done, 1)

            @block.scalar
            def _(act):
                act.wait_ge(rooted, 1)
                act.activation(std[:, :], std[:, :], ACT.Sqrt).then_inc(rooted, 1)



def node_tiles(k, ph, src, width, load, rhs, evacuate, store=None, stores=0, xT=None, links=0):
    nc = k.nc
    ring = ph.sb("tile_ring", [P, UNROLL, D])
    ringT = ph.sb("tileT_ring", [P, UNROLL, KK, P])
    stage = ph.sb("stage", [P, UNROLL, width // D * D]) if store else None
    banks = -(-width // 512)
    turned = [ph.ps(f"turned{i}", [P, 512]) for i in range(8 - 3 * banks)]
    products = [ph.ps(f"product{i}", [P, banks, 512]) for i in range(3)]
    weights_in, ring_full, turned_full = ph.sem("weights_in"), ph.sem("ring_full"), ph.sem("turned_full")
    ringT_full, multiplied, kept = ph.sem("ringT_full"), ph.sem("multiplied"), ph.sem("kept")
    product_out, chained = ph.sem("product_out"), ph.sem("chained")
    stored = [ph.sem(f"stored{u}") for u in range(UNROLL)]
    bodies = TILES // UNROLL
    weights_count = []
    with nc.Block() as block:

        @block.sync
        def _(sp):
            weights_count.append(load(sp, weights_in))
            if store:
                with sp.Fori(0, bodies) as i:
                    for u in range(UNROLL):
                        t = i * UNROLL + u
                        sp.wait_ge(product_out, t + 2)
                        store(sp, t, stage[:, u, :], stored[u])
                for u in range(UNROLL):
                    sp.wait_ge(stored[u], 16 * stores * bodies)

        @block.scalar
        def _(act):
            with act.Fori(0, bodies) as i:
                for u in range(UNROLL):
                    act.activation(ring[:, u, :], src[:, bass.ds(i * UNROLL + u, 1), :], ACT.Copy
                                   ).then_inc(ring_full, 1)
                for u in range(UNROLL):
                    t = i * UNROLL + u
                    act.wait_ge(turned_full, t + 1)
                    act.wait_ge(multiplied, i * UNROLL)
                    if xT is not None:
                        act.wait_ge(kept, i * UNROLL)
                    act.activation(ringT[:, u, :, :], turned[u % len(turned)][:, 0:D], ACT.Copy
                                   ).then_inc(ringT_full, 1)

        if xT is not None:
            @block.gpsimd
            def _(pool):
                with pool.Fori(0, bodies) as i:
                    for u in range(UNROLL):
                        t = i * UNROLL + u
                        pool.wait_ge(ringT_full, t + 1)
                        pool.tensor_copy(xT[:, :, bass.ds(t * P, P)], ringT[:, u, :, :]).then_inc(kept, 1)

        @block.tensor
        def _(pe):
            pe.wait_ge(weights_in, weights_count[0])
            with pe.Fori(0, bodies) as i:
                for u in range(UNROLL):
                    t = i * UNROLL + u
                    pe.wait_ge(ring_full, t + 1)
                    pe.wait_ge(ringT_full, i * UNROLL + max(0, u - len(turned) + 1))
                    for kk in range(KK):
                        ins = pe.transpose(turned[u % len(turned)][:, kk * P:(kk + 1) * P],
                                           ring[:, u, kk * P:(kk + 1) * P], k.ident[:, :])
                    ins.then_inc(turned_full, 1)
                for u in range(UNROLL):
                    t = i * UNROLL + u
                    pe.wait_ge(ringT_full, t + 1)
                    pe.wait_ge(product_out, t)
                    for b in range(banks):
                        n = min(512, width - b * 512)
                        for kk in range(KK):
                            ins = pe.matmul(products[u % 3][:, b, 0:n], ringT[:, u, kk, :],
                                            rhs[:, kk, b * 512:b * 512 + n], start=kk == 0, stop=kk == KK - 1)
                    ins.then_inc(multiplied, 1)

        @block.vector
        def _(dve):
            dve.sem_inc(product_out, 1)
            step = Chain(dve, chained)
            with dve.Fori(0, bodies) as i:
                for u in range(UNROLL):
                    t = i * UNROLL + u
                    dve.wait_ge(multiplied, t + 1)
                    if store:
                        dve.wait_ge(stored[u], i * (16 * stores))
                    step.base, step.n = t * links, 0
                    last = evacuate(dve, t, products[u % 3], stage[:, u, :] if store else None, step)
                    assert step.n == links
                    last.then_inc(product_out, 1)


def aggregate(k, table, index, accT, weights=None, alpha=None, heads=1, elem=D):
    nc = k.nc
    with k.phase() as ph:
        staged = ph.sb("index_staged", [P, 2, BATCH], I32)
        odd = ph.sb("odd_sums", [P, KK, NWIN])
        rows = ph.sb("rows", [P, 2, BATCH, D])
        hot = ph.sb("hot", [P, 2, BATCH, P])
        messages = ph.sb("messages", [P, 2, BATCH, D]) if alpha else rows
        sums = [ph.ps(f"sums{j}", [P, 2, KK, P]) for j in range(len(PAIRS))]
        index_staged, cleared, hot_full = ph.sem("index_staged"), ph.sem("cleared"), ph.sem("hot_full")
        gathering, go = ph.sem("gathering"), ph.sem("go")
        rows_in = [ph.sem(f"rows_in{u}") for u in range(2)]
        weighted, multiplied, added, chained = (ph.sem(n) for n in ("weighted", "multiplied", "added", "chained"))
        NPAIR = len(PAIRS)
        with nc.Block() as block:

            @block.scalar
            def _(act):
                with act.Fori(0, BATCHES // 2) as i:
                    for u in range(2):
                        act.wait_ge(rows_in[u], i * (16 * BATCH))
                        act.sem_inc(go, 1)
                        act.activation(staged[:, u, :], index[:, bass.ds(i * (2 * BATCH) + u * BATCH, BATCH)],
                                       ACT.Copy).then_inc(index_staged, 1)

            @block.gpsimd
            def _(pool):
                with pool.Fori(0, BATCHES // 2) as i:
                    for u in range(2):
                        pool.wait_ge(index_staged, i * 2 + (u + 1))
                        if alpha:
                            pool.wait_ge(weighted, i * 2 + (u + 1))
                        else:
                            pool.wait_ge(multiplied, (i * 2 + (u + 1)) * NPAIR)
                        pool.sem_inc(gathering, 1)
                        for j in range(BATCH):
                            pool.indirect_dma_start(
                                out=rows[:, u, j, :], out_offset=None, in_=table,
                                in_offset=bass.IndirectOffsetOnAxis(ap=staged[:, u, j:j + 1], axis=0)
                            ).then_inc(rows_in[u], 16)

            @block.tensor
            def _(pe):
                pe.sem_inc(multiplied, 2 * NPAIR)
                with pe.Fori(0, BATCHES // 2) as i:
                    for u in range(2):
                        b = i * 2 + u
                        pe.wait_ge(hot_full, b + 1)
                        if alpha:
                            pe.wait_ge(weighted, b + 3)
                        else:
                            pe.wait_ge(rows_in[u], (i + 1) * (16 * BATCH))
                        for p, (j0, n) in enumerate(PAIRS):
                            pe.wait_ge(added, b * BATCH + (j0 + n))
                            for j in range(j0, j0 + n):
                                for kk in range(KK):
                                    ins = pe.matmul(sums[p][:, j - j0, kk, :], messages[:, u, j, kk * P:(kk + 1) * P],
                                                    hot[:, u, j, :], start=True, stop=True)
                            ins.then_inc(multiplied, 1)

            @block.vector
            def _(dve):
                dve.sem_inc(added, BATCH)
                dve.sem_inc(weighted, 2)
                dve.memset(accT[:, :, :], 0.0).then_inc(cleared, 1)
                dve.memset(odd[:, :, :], 0.0).then_inc(cleared, 1)
                dve.wait_ge(cleared, 2)
                base = dve.alloc_register(ph._name("window_base"))

                def prepare(i, u):
                    b = i * 2 + u
                    dve.wait_ge(multiplied, (b + 1) * NPAIR)
                    c = i * (2 * BATCH) + u * BATCH
                    if weights is not None:
                        for j in range(BATCH):
                            ins = dve.tensor_scalar(hot[:, u, j, :], k.lane_iota[:, :], k.rel[:, bass.ds(c + j, 1)],
                                                    weights[:, bass.ds(c + j, 1)], ALU.is_equal, ALU.mult)
                    else:
                        ins = hot_by(dve, k, hot[:, u, :, :], k.rel[:, bass.ds(c, BATCH)], P)
                    ins.then_inc(hot_full, 1)
                    if alpha:
                        dve.wait_ge(rows_in[u], (i + 1) * (16 * BATCH))
                        a = alpha(i, u).rearrange("p h j -> p j h").unsqueeze(3).to_broadcast([P, BATCH, heads, D // heads])
                        dve.tensor_tensor(messages[:, u, :, :].rearrange("p j (h d) -> p j h d", h=heads),
                                          rows[:, u, :, :].rearrange("p j (h d) -> p j h d", h=heads), a, ALU.mult
                                          ).then_inc(weighted, 1)

                def add(i, u):
                    b = i * 2 + u
                    for p, (j0, n) in enumerate(PAIRS):
                        dve.wait_ge(multiplied, b * NPAIR + (2 * NPAIR + p + 1))
                        for j in range(j0, j0 + n):
                            dve.reg_load(base, k.dst[0:1, bass.ds(i * (2 * BATCH) + (u * BATCH + j), 1)])
                            acc = odd if (j + u) % 2 else accT
                            window = acc[:, :, bass.ds(nc.snap(base, min_val=0, max_val=NPAD), P)]
                            dve.wait_ge(added, b * BATCH + (BATCH + j - 1))
                            dve.tensor_tensor(window, window, sums[p][:, j - j0, :, :], ALU.add).then_inc(added, 1)

                last = BATCHES // 2 - 1
                prepare(0, 0)
                with dve.Fori(0, last) as i:
                    prepare(i, 1)
                    add(i, 0)
                    prepare(i + 1, 0)
                    add(i, 1)
                prepare(last, 1)
                add(last, 0)
                add(last, 1)
                dve.wait_ge(added, CHUNKS + BATCH)
                dve.tensor_tensor(accT[:, :, :], accT[:, :, :], odd[:, :, :], ALU.add).then_inc(chained, 1)


QUADS = [(j, min(4, BATCH - j)) for j in range(0, BATCH, 4)]
SUM_COPIES = 4
COPY_OF = [[(j + 2 * u) % SUM_COPIES for j in range(BATCH)] for u in range(2)]
SCATTERS = [[COPY_OF[u].count(m) for m in range(SUM_COPIES)] for u in range(2)]


def scatter_sum(k, table, copies):
    nc = k.nc
    with k.phase() as ph:
        zeros = ph.sb("zeros", [P, D])
        srcf = ph.sb("srcf", [P, CHUNKS])
        src_row = ph.sb("src_row", [P, 2, BATCH * P], I32)
        mixed = ph.sb("mixed", [P, BATCH])
        earlier = ph.sb("earlier", [P, P])
        lane = ph.sb("lane", [P, 1])
        before = ph.sb("before", [P, 2, BATCH])
        junk = ph.sb("junk", [P, BATCH, P])
        target = ph.sb("target", [P, 2, BATCH], I32)
        window = ph.sb("window", [P, 2, BATCH, D])
        hot = ph.sb("hot", [P, 2, BATCH, P])
        same = ph.sb("same", [P, 2, BATCH, P])
        gmat = ph.sb("gmat", [P, 2, BATCH, P])
        out = ph.sb("out", [P, 2, BATCH, D])
        g_ps = [ph.ps(f"g{q}", [P, 4, P]) for q in range(4)]
        o_ps = [ph.ps(f"o{q}", [P, 2, D]) for q in range(4)]
        zeroed, cleared, consts = ph.sem("zeroed"), ph.sem("cleared"), ph.sem("consts")
        row_in = [ph.sem(f"row_in{u}") for u in range(2)]
        window_in = [ph.sem(f"window_in{u}") for u in range(2)]
        hot_full, chained, targeted, g_full, g_out = (ph.sem(n) for n in
                                                      ("hot_full", "chained", "targeted", "g_full", "g_out"))
        o_full, o_out, scattering = ph.sem("o_full"), ph.sem("o_out"), ph.sem("scattering")
        scattered = [[ph.sem(f"scattered{u}_{m}") for m in range(SUM_COPIES)] for u in range(2)]
        NQ, NP2 = len(QUADS), len(PAIRS)
        with nc.Block() as block:

            @block.sync
            def _(sp):
                base = sp.alloc_register(ph._name("window_base"))
                with sp.Fori(0, BATCHES // 2) as i:
                    for u in range(2):
                        b = i * 2 + u
                        c = i * (2 * BATCH) + u * BATCH
                        sp.wait_ge(hot_full, b + 1)
                        row = k.a["src_row"][:, bass.ds(c * P, BATCH * P)]
                        sp.dma_start(src_row[:, u, :], row.to_broadcast([P, BATCH * P])).then_inc(row_in[u], 16)
                        sp.wait_ge(o_full, (b + 1) * NP2)
                        for j in range(BATCH):
                            sp.reg_load(base, k.dst[0:1, bass.ds(c + j, 1)])
                            first = nc.snap(base, min_val=0, max_val=NPAD)
                            sp.dma_start(window[:, u, j, :], table[bass.ds(first, P), :]).then_inc(window_in[u], 16)

            @block.scalar
            def _(act):
                act.sem_inc(o_out, 2)
                act.sem_inc(g_out, NQ)
                act.wait_ge(zeroed, 1)
                for m in range(SUM_COPIES):
                    for t in range(NWIN // P):
                        act.dma_start(copies[m][t * P:(t + 1) * P, :], zeros[:, :]).then_inc(cleared, 16)
                with act.Fori(0, BATCHES // 2) as i:
                    for u in range(2):
                        b = i * 2 + u
                        for q, (j0, n) in enumerate(QUADS):
                            act.wait_ge(g_full, b * NQ + (q + 1))
                            act.wait_ge(o_full, (b + 1) * NP2)
                            act.activation(gmat[:, u, j0:j0 + n, :], g_ps[q][:, 0:n, :], ACT.Copy).then_inc(g_out, 1)
                        for m in range(SUM_COPIES):
                            act.wait_ge(scattered[u][m], i * (16 * SCATTERS[u][m]))
                        for p, (j0, n) in enumerate(PAIRS):
                            act.wait_ge(o_full, b * NP2 + (2 * NP2 + p + 1))
                            act.activation(out[:, u, j0:j0 + n, :], o_ps[p % 4][:, 0:n, :], ACT.Copy).then_inc(o_out, 1)

            @block.gpsimd
            def _(pool):
                pool.memset(zeros[:, :], 0.0).then_inc(zeroed, 1)
                pool.memset(earlier[:, :], 1.0).then_inc(consts, 1)
                pool.iota(lane[:, :], [[0, 1]], base=NPAD, channel_multiplier=1,
                          allow_small_or_imprecise_dtypes=True).then_inc(consts, 1)
                pool.wait_ge(consts, 2)
                pool.affine_select(out=earlier[:, :], in_=earlier[:, :], compare_op=ALU.is_gt, fill=0.0,
                                   base=0, pattern=[[-1, P]], channel_multiplier=1).then_inc(consts, 1)
                pool.wait_ge(cleared, 16 * SUM_COPIES * (NWIN // P))
                with pool.Fori(0, BATCHES // 2) as i:
                    for u in range(2):
                        b = i * 2 + u
                        pool.wait_ge(targeted, b + 1)
                        for j in range(BATCH):
                            m, before_j = COPY_OF[u][j], COPY_OF[u][:j].count(COPY_OF[u][j])
                            pool.wait_ge(o_out, b * NP2 + (j // 2 + 3))
                            if before_j:
                                pool.wait_ge(scattered[u][m], (i * SCATTERS[u][m] + before_j) * 16)
                            else:
                                pool.wait_ge(scattered[1 - u][m], (i + u) * (16 * SCATTERS[1 - u][m]))
                            pool.sem_inc(scattering, 1)
                            pool.indirect_dma_start(
                                out=copies[m], out_offset=bass.IndirectOffsetOnAxis(ap=target[:, u, j:j + 1], axis=0),
                                in_=out[:, u, j, :], in_offset=None, compute_op=ALU.add).then_inc(scattered[u][m], 16)
                for u in range(2):
                    for m in range(SUM_COPIES):
                        pool.wait_ge(scattered[u][m], 16 * SCATTERS[u][m] * (BATCHES // 2))

            @block.tensor
            def _(pe):
                pe.sem_inc(o_full, 2 * NP2)
                with pe.Fori(0, BATCHES // 2) as i:
                    for u in range(2):
                        b = i * 2 + u
                        pe.wait_ge(hot_full, b + 3)
                        for q, (j0, n) in enumerate(QUADS):
                            pe.wait_ge(g_out, b * NQ + (q + 1))
                            for j in range(j0, j0 + n):
                                ins = pe.matmul(g_ps[q][:, j - j0, :], hot[:, u, j, :], same[:, u, j, :],
                                                start=True, stop=True)
                            ins.then_inc(g_full, 1)
                        pe.wait_ge(window_in[u], (i + 1) * (16 * BATCH))
                        for p, (j0, n) in enumerate(PAIRS):
                            pe.wait_ge(g_out, b * NQ + (NQ + (j0 + n - 1) // 4 + 1))
                            pe.wait_ge(o_out, b * NP2 + p)
                            for j in range(j0, j0 + n):
                                ins = pe.matmul(o_ps[p % 4][:, j - j0, :], gmat[:, u, j, :], window[:, u, j, :],
                                                start=True, stop=True)
                            ins.then_inc(o_full, 1)

            @block.vector
            def _(dve):
                dve.sem_inc(hot_full, 2)
                dve.wait_ge(consts, 3)
                step = Chain(dve, chained)
                step(dve.tensor_copy(srcf[:, :], k.src[:, :]))
                links = 4
                with dve.Fori(0, BATCHES // 2) as i:
                    for u in range(2):
                        b = i * 2 + u
                        c = i * (2 * BATCH) + u * BATCH
                        step.base, step.n = b * links + 1, 0
                        dve.wait_ge(row_in[u], (i + 1) * 16)
                        dve.wait_ge(g_out, b * NQ)
                        hot_by(dve, k, hot[:, u, :, :], k.rel[:, bass.ds(c, BATCH)], P)
                        for j in range(BATCH):
                            mine = srcf[:, bass.ds(c + j, 1)]
                            others = src_row[:, u, j * P:(j + 1) * P]
                            dve.tensor_scalar(same[:, u, j, :], others, mine, k.weight[:, bass.ds(c + j, 1)],
                                              ALU.is_equal, ALU.mult)
                            ins = dve.scalar_tensor_tensor(junk[:, j, :], others, mine, earlier[:, :], ALU.is_equal,
                                                           ALU.mult, accum_out=before[:, u, j:j + 1])
                        step(ins)
                        for m in range(SUM_COPIES):
                            dve.wait_ge(scattered[u][m], i * (16 * SCATTERS[u][m]))
                        step(dve.tensor_scalar(before[:, u, :], before[:, u, :], 0.0, None, ALU.is_gt))
                        s0 = srcf[:, bass.ds(c, BATCH)]
                        step(dve.tensor_scalar(mixed[:, 0:BATCH], s0, -1.0, lane[:, 0:1], ALU.mult, ALU.add))
                        step(dve.tensor_tensor(mixed[:, 0:BATCH], mixed[:, 0:BATCH], before[:, u, :], ALU.mult))
                        dve.tensor_tensor(target[:, u, :], mixed[:, 0:BATCH], s0, ALU.add).then_inc(targeted, 1)
                        dve.wait_ge(targeted, b + 1)
                        dve.sem_inc(hot_full, 1)


def layer0_gnn(k):
    nc, a = k.nc, k.a
    table = nc.dram_tensor("gcn_rows", [NWIN, D], F32, kind="Internal").ap()
    copies = [nc.dram_tensor(f"gcn_sums{m}", [NWIN, D], F32, kind="Internal").ap() for m in range(SUM_COPIES)]
    with k.phase() as ph:
        xn = ph.sb("xn", [P, TILES, D])
        normalize(k, k.x, xn)
        w = ph.sb("gcn_w", [P, KK, D])
        clear_tail(k, table)

        def load(sp, sem):
            sp.dma_start(w[:, :, :], a["L0_gnn_w"]).then_inc(sem, 16)
            return 16

        def evacuate(dve, t, product, stage, step):
            return dve.tensor_scalar(stage, product[:, 0, 0:D], k.dinv[:, bass.ds(t, 1)], None, ALU.mult)

        def store(sp, t, stage, sem):
            sp.dma_start(table[bass.ds(t * P, P), :], stage).then_inc(sem, 16)

        with k.phase() as inner:
            node_tiles(k, inner, xn, D, load, w, evacuate, store, 1)
    scatter_sum(k, table, copies)
    with k.phase() as ph:
        parts = ph.sb("parts", [P, SUM_COPIES, TILES, D])
        bias = ph.sb("gcn_bias", [P, D])
        loaded, chained = ph.sem("loaded"), ph.sem("chained")
        with nc.Block() as block:

            @block.sync
            def _(sp):
                sp.dma_start(bias[:, :], a["L0_gnn_b"].to_broadcast([P, D])).then_inc(loaded, 16)
                for m in range(SUM_COPIES):
                    sp.dma_start(parts[:, m, :, :], copies[m][0:NPAD, :].rearrange("(t p) d -> p t d", p=P)
                                 ).then_inc(loaded, 16)

            @block.vector
            def _(dve):
                step = Chain(dve, chained)
                dve.wait_ge(loaded, 16 * (1 + SUM_COPIES))
                total = parts[:, 0, :, :]
                for m in range(1, SUM_COPIES):
                    step(dve.tensor_tensor(total, total, parts[:, m, :, :], ALU.add))
                step(dve.tensor_tensor(total, total, k.dinv[:, :].unsqueeze(2).to_broadcast([P, TILES, D]), ALU.mult))
                step(dve.tensor_tensor(total, total, bias[:, :].unsqueeze(1).to_broadcast([P, TILES, D]), ALU.add))
                step(dve.tensor_scalar(total, total, 0.0, None, ALU.max))
                step(dve.tensor_tensor(k.x[:, :, :], k.x[:, :, :], total, ALU.add))


def clear_tail(k, table):
    with k.phase() as ph:
        zeros, zeroed, stored = ph.sb("zeros", [P, D]), ph.sem("zeroed"), ph.sem("stored")
        with k.nc.Block() as block:

            @block.gpsimd
            def _(pool):
                pool.memset(zeros[:, :], 0.0).then_inc(zeroed, 1)

            @block.sync
            def _(sp):
                sp.wait_ge(zeroed, 1)
                sp.dma_start(table[NPAD:NWIN, :], zeros[:, :]).then_inc(stored, 16)
                sp.wait_ge(stored, 16)


def from_sums(k, ph, accT, load, update, links):
    nc = k.nc
    ring = ph.sb("sum_ring", [P, UNROLL, KK, P])
    turned = [ph.ps(f"turned{i}", [P, 512]) for i in range(3)]
    loaded, ring_full, turned_full = ph.sem("loaded"), ph.sem("ring_full"), ph.sem("turned_full")
    turned_out, chained = ph.sem("turned_out"), ph.sem("chained")
    bodies = TILES // UNROLL
    count = []
    with nc.Block() as block:

        @block.sync
        def _(sp):
            count.append(load(sp, loaded))

        @block.scalar
        def _(act):
            with act.Fori(0, bodies) as i:
                act.wait_ge(turned_full, i * UNROLL)
                for u in range(UNROLL):
                    act.activation(ring[:, u, :, :], accT[:, :, bass.ds((i * UNROLL + u) * P, P)], ACT.Copy
                                   ).then_inc(ring_full, 1)

        @block.tensor
        def _(pe):
            with pe.Fori(0, bodies) as i:
                for u in range(UNROLL):
                    t = i * UNROLL + u
                    pe.wait_ge(ring_full, t + 1)
                    pe.wait_ge(turned_out, t)
                    for kk in range(KK):
                        ins = pe.transpose(turned[u % 3][:, kk * P:(kk + 1) * P], ring[:, u, kk, :], k.ident[:, :])
                    ins.then_inc(turned_full, 1)

        @block.vector
        def _(dve):
            dve.sem_inc(turned_out, 1)
            dve.wait_ge(loaded, count[0])
            step = Chain(dve, chained)
            with dve.Fori(0, bodies) as i:
                for u in range(UNROLL):
                    t = i * UNROLL + u
                    dve.wait_ge(turned_full, t + 1)
                    step.base, step.n = t * links, 0
                    last = update(dve, t, turned[u % 3][:, 0:D], step)
                    assert step.n == links
                    last.then_inc(turned_out, 1)


def gate_weights(k, logits, gates, experts, kind, bias=None, chosen=None):
    nc = k.nc
    E = experts
    shape = [P, TILES, E]
    pair = [P, TILES, E, E]
    with k.phase() as ph:
        br = ph.sb("router_bias", [P, E])
        low = ph.sb("low", [P, E, E])
        probs, work = ph.sb("probs", shape), ph.sb("work", shape)
        top, total = ph.sb("top", [P, TILES]), ph.sb("total", [P, TILES])
        above, ties = ph.sb("above", pair), ph.sb("ties", pair)
        loaded, consts, chained, exps, exp_in = (ph.sem(n) for n in ("loaded", "consts", "chained", "exps", "exp_in"))
        n_exp = {"softmax": 1, "top2": 1, "top2_of_softmax": 2, "top2_renormalized": 1}[kind]
        with nc.Block() as block:

            @block.sync
            def _(sp):
                sp.dma_start(br[:, :], bias.to_broadcast([P, E])).then_inc(loaded, 16)

            @block.gpsimd
            def _(pool):
                pool.memset(low[:, :, :], 1.0).then_inc(consts, 1)
                pool.wait_ge(consts, 1)
                pool.affine_select(out=low[:, :, :], in_=low[:, :, :], compare_op=ALU.is_gt, fill=0.0,
                                   base=0, pattern=[[1, E], [-1, E]], channel_multiplier=0).then_inc(consts, 1)

            @block.scalar
            def _(act):
                for n in range(n_exp):
                    act.wait_ge(exp_in, n + 1)
                    act.activation(work[:, :, :], work[:, :, :], ACT.Exp).then_inc(exps, 1)

            @block.vector
            def _(dve):
                step = Chain(dve, chained)

                def spread(v):
                    return v[:, :].unsqueeze(2).to_broadcast(shape)

                def exponentials(values, n):
                    step(dve.tensor_reduce(top[:, :], values, AX.X, ALU.max))
                    dve.tensor_tensor(work[:, :, :], values, spread(top), ALU.subtract).then_inc(exp_in, 1)
                    dve.wait_ge(exps, n)

                def divide(out):
                    step(dve.tensor_reduce(total[:, :], work[:, :, :], AX.X, ALU.add))
                    step(dve.reciprocal(total[:, :], total[:, :]))
                    step(dve.tensor_tensor(out, work[:, :, :], spread(total), ALU.mult))

                dve.wait_ge(loaded, 16)
                dve.wait_ge(consts, 2)
                step(dve.tensor_tensor(logits[:, :, :], logits[:, :, :],
                                       br[:, :].unsqueeze(1).to_broadcast(shape), ALU.add))
                values = logits[:, :, :]
                if kind != "top2":
                    exponentials(values, 1)
                    divide(probs[:, :, :] if kind != "softmax" else gates[:, :, :])
                    values = probs[:, :, :]
                if kind == "softmax":
                    return
                for t in range(TILES):
                    rivals = values[:, t, :].unsqueeze(1).to_broadcast([P, E, E])
                    own = values[:, t, :].unsqueeze(2).to_broadcast([P, E, E])
                    dve.tensor_tensor(above[:, t, :, :], rivals, own, ALU.is_gt)
                    ins = dve.tensor_tensor(ties[:, t, :, :], rivals, own, ALU.is_equal)
                step(ins)
                flat = "p t e j -> p t (e j)"
                step(dve.tensor_tensor(ties[:, :, :, :].rearrange(flat), ties[:, :, :, :].rearrange(flat),
                                       low[:, :, :].rearrange("p e j -> p (e j)").unsqueeze(1).to_broadcast([P, TILES, E * E]),
                                       ALU.mult))
                step(dve.tensor_tensor(above[:, :, :, :], above[:, :, :, :], ties[:, :, :, :], ALU.add))
                taken = gates[:, :, :]
                step(dve.tensor_reduce(taken, above[:, :, :, :], AX.X, ALU.add))
                step(dve.tensor_scalar(taken, taken, 2.0, None, ALU.is_lt))
                if chosen is not None:
                    step(dve.tensor_copy(chosen[:, :, :], taken))
                if kind == "top2_renormalized":
                    step(dve.tensor_tensor(work[:, :, :], values, taken, ALU.mult))
                else:
                    exponentials(values, 2 if kind == "top2_of_softmax" else 1)
                    step(dve.tensor_tensor(work[:, :, :], work[:, :, :], taken, ALU.mult))
                divide(gates[:, :, :])


class Experts:

    def __init__(self, count, dims):
        self.count, self.dims = count, dims
        self.at, col = [], 0
        for n_in, n_out in zip(dims, dims[1:]):
            self.at.append(col)
            col += -(-n_in // P) * n_out
        self.columns = col
        self.chunks = [(l, c) for l, n in enumerate(dims[1:-1]) for c in range(-(-n // P))]

    def matrix(self, weights, layer, kk, lo, hi):
        n_in, n_out = self.dims[layer], self.dims[layer + 1]
        c = self.at[layer] + kk * n_out
        return weights[0:min(P, n_in - kk * P), c + lo:c + hi]


def mixture(k, xT, spec, weights, out_bias, act_func, bias, scale=None, gates=None, prescale=None):
    nc = k.nc
    E, chunks = spec.count, spec.chunks
    J = 2 * len(chunks)
    SLOTS = 4 if J % 4 == 0 else 3
    slots = min(2, E)
    GROUPS = TILES // UNROLL
    with k.phase() as ph:
        w = ph.sb("expert_w", [P, slots, spec.columns])
        wide = max(-(-n // P) for n in spec.dims[1:-1])
        hidden = [ph.sb(f"hidden{l}", [P, -(-n // P), GROUP]) for l, n in enumerate(spec.dims[1:-1])]
        b_out = ph.sb("out_bias", [P, E, D])
        bias_e = ph.sb("bias_e", [P, 2, len(chunks)])
        scale_e = ph.sb("scale_e", [P, 2, len(chunks)]) if scale is not None else None
        staged, started = ph.sem("staged"), ph.sem("started")
        units = [ph.ps(f"unit{i}", [P, 512]) for i in range(SLOTS)]
        outs = [ph.ps(f"out{i}", [P, 512]) for i in range(3)]
        w_in = [ph.sem(f"w_in{s}") for s in range(slots)]
        w_ready, bias_in = ph.sem("w_ready"), ph.sem("bias_in")
        unit_full, unit_out, out_full, out_out, chained = (ph.sem(n) for n in (
            "unit_full", "unit_out", "out_full", "out_out", "chained"))

        def experts(eng, body):
            if E == 1:
                body(0, 0, 0)
            else:
                with eng.Fori(0, E // 2) as pair:
                    for s in range(2):
                        body(pair * 2 + s, s, pair)

        def groups(eng, e, body):
            with eng.Fori(0, GROUPS) as g:
                body(g, e * GROUPS + g)

        with nc.Block() as block:

            @block.sync
            def _(sp):
                sp.dma_start(b_out[:, :, :], out_bias.rearrange("o (e d) -> o e d", e=E).to_broadcast([P, E, D])
                             ).then_inc(bias_in, 16)

                def load(e, s, pair):
                    sp.wait_ge(out_full, e * TILES)
                    sp.dma_start(w[:, s, :], weights[bass.ds(e, 1), :, :].rearrange("o p c -> (o p) c")
                                 ).then_inc(w_in[s], 16)

                experts(sp, load)

            @block.scalar
            def _(act):
                act.sem_inc(unit_out, SLOTS - 1)

                def expert(e, s, pair):
                    ins = act.activation(bias_e[:, s, :], bias[:, bass.ds(e, 1), :], ACT.Copy)
                    if scale is not None:
                        ins.then_inc(staged, 1)
                        ins = act.activation(scale_e[:, s, :], scale[:, bass.ds(e, 1), :], ACT.Copy)
                    ins.then_inc(staged, 1)

                    def group(g, n):
                        act.wait_ge(staged, (e + 1) * (1 if scale is None else 2))
                        act.wait_ge(out_full, n * UNROLL + TILES)
                        for j in range(J):
                            l, c = chunks[j // 2]
                            m = min(P, spec.dims[l + 1] - c * P)
                            half = slice((j % 2) * HALF, (j % 2 + 1) * HALF)
                            act.wait_ge(unit_full, n * J + (j + 1))
                            col = (slice(0, m), s, slice(j // 2, j // 2 + 1))
                            act.activation(hidden[l][0:m, c, half], units[j % SLOTS][0:m, 0:HALF], act_func,
                                           bias=bias_e[col], **({"scale": scale_e[col]} if scale is not None else {})
                                           ).then_inc(unit_out, 1)
                    groups(act, e, group)
                experts(act, expert)

            @block.tensor
            def _(pe):
                pe.sem_inc(out_full, TILES)

                def expert(e, s, pair):
                    if prescale is not None:
                        pe.wait_ge(w_ready, e + 1)
                    else:
                        pe.wait_ge(w_in[s], pair * 16 + 16)
                    pe.sem_inc(started, 1)

                    def group(g, n):
                        for j in range(J):
                            l, c = chunks[j // 2]
                            m = min(P, spec.dims[l + 1] - c * P)
                            K = -(-spec.dims[l] // P)
                            pe.wait_ge(unit_out, n * J + j)
                            for kk in range(K):
                                rows = min(P, spec.dims[l] - kk * P)
                                if l == 0:
                                    rhs = xT[:, kk, bass.ds(g * GROUP + (j % 2) * HALF, HALF)]
                                else:
                                    src = chunks.index((l - 1, kk)) * 2 + j % 2
                                    pe.wait_ge(unit_out, n * J + (src + SLOTS))
                                    rhs = hidden[l - 1][0:rows, kk, (j % 2) * HALF:(j % 2 + 1) * HALF]
                                ins = pe.matmul(units[j % SLOTS][0:m, 0:HALF],
                                                spec.matrix(w[:, s, :], l, kk, c * P, c * P + m), rhs,
                                                start=kk == 0, stop=kk == K - 1)
                            ins.then_inc(unit_full, 1)
                        L = len(spec.dims) - 2
                        K = -(-spec.dims[L] // P)
                        for u in range(UNROLL):
                            pe.wait_ge(out_out, n * UNROLL + u)
                            for kk in range(K):
                                rows = min(P, spec.dims[L] - kk * P)
                                if u in (0, 2):
                                    src = chunks.index((L - 1, kk)) * 2 + (u == 2)
                                    pe.wait_ge(unit_out, n * J + (src + SLOTS))
                                ins = pe.matmul(outs[u % 3][:, 0:D], hidden[L - 1][0:rows, kk, u * P:(u + 1) * P],
                                                spec.matrix(w[:, s, :], L, kk, 0, D), start=kk == 0, stop=kk == K - 1)
                            ins.then_inc(out_full, 1)
                    groups(pe, e, group)
                experts(pe, expert)

            @block.vector
            def _(dve):
                dve.sem_inc(out_out, 1)
                dve.wait_ge(bias_in, 16)

                def expert(e, s, pair):
                    if prescale is not None:
                        dve.wait_ge(w_in[s], pair * 16 + 16)
                        H = spec.dims[1]
                        for kk in range(KK):
                            part = w[:, s, kk * H:(kk + 1) * H]
                            ins = dve.tensor_scalar(part, part, prescale[:, kk, bass.ds(e, 1)], None, ALU.mult)
                        ins.then_inc(w_ready, 1)

                    def group(g, n):
                        for u in range(UNROLL):
                            t = g * UNROLL + u
                            xt = k.x[:, bass.ds(t, 1), :]
                            bt = b_out[:, bass.ds(e, 1), :]
                            dve.wait_ge(out_out, n * UNROLL + (u + 1))
                            if gates is not None:
                                gate = gates[:, bass.ds(t, 1), bass.ds(e, 1)].rearrange("p a b -> p (a b)")
                                ins = dve.scalar_tensor_tensor(xt, bt, gate, xt, ALU.mult, ALU.add)
                            else:
                                ins = dve.tensor_tensor(xt, bt, xt, ALU.add)
                            ins.then_inc(chained, 1)
                            dve.wait_ge(chained, n * UNROLL + (u + 1))
                            dve.wait_ge(out_full, n * UNROLL + (TILES + u + 1))
                            part = outs[u % 3][:, 0:D]
                            if gates is not None:
                                ins = dve.scalar_tensor_tensor(xt, part, gate, xt, ALU.mult, ALU.add)
                            else:
                                ins = dve.tensor_tensor(xt, part, xt, ALU.add)
                            ins.then_inc(out_out, 1)
                    groups(dve, e, group)
                experts(dve, expert)


BLOCK = 2 * P


class Dispatch:

    def __init__(self, k, ph, experts, hidden, affine):
        self.experts, self.hidden, self.affine = experts, hidden, affine
        self.blocks = (2 * NPAD + experts * (BLOCK - 1)) // BLOCK
        assert self.blocks % 2 == 0
        self.chunks = hidden // P
        self.bias_at = KK * hidden
        self.affine_at = self.bias_at + self.chunks
        self.columns = self.affine_at + (2 * KK if affine else 0)
        k.uid += 1
        self.rows = k.nc.dram_tensor(f"slot_rows_{k.uid}", [self.blocks * BLOCK, D], F32, kind="Internal").ap()
        self.results = k.nc.dram_tensor(f"slot_results_{k.uid}", [self.blocks * BLOCK, D], F32, kind="Internal").ap()
        self.slots = ph.sb("slots", [P, 2, TILES], I32)
        self.gates = ph.sb("slot_gates", [P, 2, TILES])
        self.block_expert = ph.sb("block_expert", [P, self.blocks], I32)


def assign_slots(k, d, chosen, gates):
    nc = k.nc
    E, NB = d.experts, d.blocks
    per_dma = 8
    with k.phase() as ph:
        before_me, ones = ph.sb("before_me", [P, P]), ph.sb("ones", [P, P])
        zeros = ph.sb("zeros", [P, per_dma * D])
        block_no = ph.sb("block_no", [P, NB])
        rank, ends = ph.sb("rank", [P, E, TILES]), ph.sb("ends", [P, E, TILES + 1])
        blocks, block_end, first = (ph.sb(n, [P, E]) for n in ("blocks", "block_end", "first"))
        blocks_i = ph.sb("blocks_i", [P, E], I32)
        work, slot = ph.sb("work", [P, E, TILES]), ph.sb("slot", [P, 2, TILES])
        passed = ph.sb("passed", [P, NB, E])
        number = ph.sb("number", [P, NB])
        lanes_ps, tiles_ps = (ph.ps(n, [P, TILES, E]) for n in ("lanes_before", "tile_totals"))
        consts, counted, chained = ph.sem("consts"), ph.sem("counted"), ph.sem("chained")
        zeroed, cleared = ph.sem("zeroed"), ph.sem("cleared")
        with nc.Block() as block:

            @block.gpsimd
            def _(pool):
                pool.memset(ones[:, :], 1.0).then_inc(consts, 1)
                pool.memset(before_me[:, :], 1.0).then_inc(consts, 1)
                pool.iota(block_no[:, :], [[1, NB]], base=0, channel_multiplier=0,
                          allow_small_or_imprecise_dtypes=True).then_inc(consts, 1)
                pool.wait_ge(consts, 3)
                pool.affine_select(out=before_me[:, :], in_=before_me[:, :], compare_op=ALU.is_gt, fill=0.0,
                                   base=0, pattern=[[1, P]], channel_multiplier=-1).then_inc(consts, 1)
                pool.memset(zeros[:, :], 0.0).then_inc(zeroed, 1)

            @block.sync
            def _(sp):
                sp.wait_ge(zeroed, 1)
                step = P * per_dma
                n = d.rows.shape[0] // step
                for m in range(n):
                    sp.dma_start(d.rows[m * step:(m + 1) * step, :].rearrange("(p r) d -> p (r d)", p=P), zeros[:, :]
                                 ).then_inc(cleared, 16)
                sp.wait_ge(cleared, 16 * n)

            @block.tensor
            def _(pe):
                pe.wait_ge(consts, 4)
                flat = chosen[:, :, :].rearrange("p t e -> p (t e)")
                pe.matmul(lanes_ps[:, :, :].rearrange("p t e -> p (t e)"), before_me[:, :], flat, start=True, stop=True)
                pe.matmul(tiles_ps[:, :, :].rearrange("p t e -> p (t e)"), ones[:, :], flat, start=True, stop=True
                          ).then_inc(counted, 1)

            @block.vector
            def _(dve):
                step = Chain(dve, chained)
                by_tile = "p e t -> p t e"
                dve.wait_ge(consts, 4)
                step(dve.memset(ends[:, :, :], 0.0))
                dve.wait_ge(counted, 1)
                for e in range(E):
                    step(dve.tensor_tensor_scan(ends[:, e, 1:TILES + 1], ones[:, 0:TILES], tiles_ps[:, :, e], 0.0,
                                                ALU.mult, ALU.add))
                step(dve.tensor_tensor(rank[:, :, :], ends[:, :, 0:TILES], lanes_ps[:, :, :].rearrange("p t e -> p e t"),
                                       ALU.add))
                step(dve.tensor_scalar(blocks[:, :], ends[:, :, TILES], float(BLOCK - 1), None, ALU.add))
                step(dve.tensor_copy(blocks_i[:, :], blocks[:, :]))
                step(dve.tensor_scalar(blocks_i[:, :], blocks_i[:, :], BLOCK.bit_length() - 1, None, ALU.logical_shift_right))
                step(dve.tensor_copy(blocks[:, :], blocks_i[:, :]))
                step(dve.tensor_tensor_scan(block_end[:, :], ones[:, 0:E], blocks[:, :], 0.0, ALU.mult, ALU.add))
                step(dve.tensor_tensor(first[:, :], block_end[:, :], blocks[:, :], ALU.subtract))
                step(dve.scalar_tensor_tensor(rank[:, :, :], first[:, :].unsqueeze(2).to_broadcast([P, E, TILES]),
                                              float(BLOCK), rank[:, :, :], ALU.mult, ALU.add))
                took = chosen[:, :, :].rearrange("p t e -> p e t")
                step(dve.tensor_scalar(work[:, :, :], took, -1.0, -float(2 ** 20), ALU.add, ALU.mult))
                step(dve.tensor_tensor(work[:, :, :], work[:, :, :], rank[:, :, :], ALU.add))
                step(dve.tensor_reduce(slot[:, 0, :], work[:, :, :].rearrange(by_tile), AX.X, ALU.min))
                step(dve.tensor_tensor(work[:, :, :], rank[:, :, :], took, ALU.mult))
                step(dve.tensor_reduce(slot[:, 1, :], work[:, :, :].rearrange(by_tile), AX.X, ALU.max))
                step(dve.tensor_copy(d.slots[:, :, :], slot[:, :, :]))
                for n in range(2):
                    step(dve.tensor_tensor(work[:, :, :], rank[:, :, :],
                                           slot[:, n, :].unsqueeze(1).to_broadcast([P, E, TILES]), ALU.is_equal))
                    step(dve.tensor_tensor(work[:, :, :], work[:, :, :], gates[:, :, :].rearrange("p t e -> p e t"), ALU.mult))
                    step(dve.tensor_reduce(d.gates[:, n, :], work[:, :, :].rearrange(by_tile), AX.X, ALU.add))
                step(dve.tensor_tensor(passed[:, :, :], block_no[:, :].unsqueeze(2).to_broadcast([P, NB, E]),
                                       block_end[:, :].unsqueeze(1).to_broadcast([P, NB, E]), ALU.is_ge))
                step(dve.tensor_reduce(number[:, :], passed[:, :, :], AX.X, ALU.add))
                step(dve.tensor_scalar(number[:, :], number[:, :], float(E - 1), None, ALU.min))
                step(dve.tensor_copy(d.block_expert[:, :], number[:, :]))


def scatter_rows(k, d, xn):
    with k.phase() as ph:
        moved = ph.sem("moved")
        with k.nc.Block() as block:

            @block.gpsimd
            def _(pool):
                for t in range(TILES):
                    for n in range(2):
                        pool.indirect_dma_start(
                            out=d.rows, out_offset=bass.IndirectOffsetOnAxis(ap=d.slots[:, n, t:t + 1], axis=0),
                            in_=xn[:, t, :], in_offset=None).then_inc(moved, 16)
                pool.wait_ge(moved, 16 * 2 * TILES)


def expert_blocks(k, d, first_part, second_part, out_bias):
    nc = k.nc
    E, C, H, NB = d.experts, d.chunks, d.hidden, d.blocks
    UNITS = 4
    with k.phase() as ph:
        w1, w2 = ph.sb("first_part", [P, 2, d.columns]), ph.sb("second_part", [P, E, C * D])
        b2 = ph.sb("out_bias", [P, E, D])
        rows = ph.sb("rows", [P, 2, 2, D])
        xT = ph.sb("xT", [P, KK, BLOCK])
        hid = ph.sb("hidden", [P, C, BLOCK])
        res = ph.sb("results", [P, 2, 2, D])
        t_ps = ph.ps("turned", [P, KK, BLOCK])
        units = [ph.ps(f"unit{n}", [P, 512]) for n in range(UNITS)]
        outs = [ph.ps(f"out{h}", [P, 512]) for h in range(2)]
        w1_in = [ph.sem(f"first_part_in{u}") for u in range(2)]
        rows_in = [ph.sem(f"rows_in{u}") for u in range(2)]
        stored = [ph.sem(f"stored{u}") for u in range(2)]
        w2_in, turned, xT_full = ph.sem("second_part_in"), ph.sem("turned"), ph.sem("xT_full")
        unit_full, unit_out, out_full, out_out = (ph.sem(n) for n in ("unit_full", "unit_out", "out_full", "out_out"))
        storing = ph.sem("storing")

        def expert_of(eng, reg, s):
            eng.reg_load(reg, d.block_expert[0:1, bass.ds(s, 1)])
            return nc.snap(reg, min_val=0, max_val=E - 1)

        def blocks(eng, body):
            with eng.Fori(0, NB // 2 - 1) as i:
                for u in range(2):
                    body(i * 2 + u, u, i, True)
            for u in range(2):
                body(NB - 2 + u, u, NB // 2 - 1, u == 0)

        with nc.Block() as block:

            @block.sync
            def _(sp):
                reg = sp.alloc_register(ph._name("expert"))

                def load(s, u, turn, more):
                    sp.wait_ge(out_full, s * 2 + 2)
                    sp.dma_start(rows[:, u, :, :], d.rows[bass.ds(s * BLOCK, BLOCK), :].rearrange("(h p) d -> p h d", p=P)
                                 ).then_inc(rows_in[u], 16)
                    e = expert_of(sp, reg, s)
                    sp.dma_start(w1[:, u, :], first_part[bass.ds(e, 1), :, :].rearrange("o p c -> (o p) c")
                                 ).then_inc(w1_in[u], 16)
                blocks(sp, load)

            @block.gpsimd
            def _(pool):
                pool.dma_start(b2[:, :, :], out_bias.rearrange("o (e d) -> o e d", e=E).to_broadcast([P, E, D])
                               ).then_inc(w2_in, 16)
                for e in range(E):
                    pool.dma_start(w2[:, e, :], second_part[e, :, :]).then_inc(w2_in, 16)

                def store(s, u, turn, more):
                    pool.wait_ge(out_out, s * 2 + 4)
                    pool.sem_inc(storing, 1)
                    pool.dma_start(d.results[bass.ds(s * BLOCK, BLOCK), :].rearrange("(h p) d -> p h d", p=P),
                                   res[:, u, :, :]).then_inc(stored[u], 16)
                blocks(pool, store)
                for u in range(2):
                    pool.wait_ge(stored[u], 16 * (NB // 2))

            @block.tensor
            def _(pe):
                reg = pe.alloc_register(ph._name("expert"))
                pe.sem_inc(out_full, 4)

                def turn_rows(s, u, turn):
                    pe.wait_ge(rows_in[u], turn * 16 + 16)
                    for kk in range(KK):
                        for h in range(2):
                            ins = pe.transpose(t_ps[:, kk, h * P:(h + 1) * P], rows[:, u, h, kk * P:(kk + 1) * P],
                                               k.ident[:, :])
                    ins.then_inc(turned, 1)

                def compute(s, u, turn, more):
                    pe.wait_ge(xT_full, s + 1)
                    pe.wait_ge(w1_in[u], turn * 16 + 16)
                    for c in range(C):
                        pe.wait_ge(unit_out, s * C + c)
                        for kk in range(KK):
                            ins = pe.matmul(units[c % UNITS][:, 0:BLOCK], w1[:, u, kk * H + c * P:kk * H + (c + 1) * P],
                                            xT[:, kk, :], start=kk == 0, stop=kk == KK - 1)
                        ins.then_inc(unit_full, 1)
                    if more:
                        turn_rows(s + 1, 1 - u, turn + u)
                    pe.wait_ge(w2_in, 16 * (1 + E))
                    pe.wait_ge(unit_out, s * C + (C + UNITS - 1))
                    e = expert_of(pe, reg, s)
                    for h in range(2):
                        pe.wait_ge(out_out, s * 2 + (h + 1))
                        for c in range(C):
                            ins = pe.matmul(outs[h][:, 0:D], hid[:, c, h * P:(h + 1) * P],
                                            w2[:, bass.ds(e, 1), c * D:(c + 1) * D], start=c == 0, stop=c == C - 1)
                        ins.then_inc(out_full, 1)

                turn_rows(0, 0, 0)
                blocks(pe, compute)

            @block.scalar
            def _(act):
                act.sem_inc(unit_out, UNITS - 1)

                def hidden(s, u, turn, more):
                    act.wait_ge(out_full, s * 2 + 4)
                    for c in range(C):
                        act.wait_ge(unit_full, s * C + (c + 1))
                        act.activation(hid[:, c, :], units[c % UNITS][:, 0:BLOCK], ACT.Gelu,
                                       bias=w1[:, u, d.bias_at + c:d.bias_at + c + 1]).then_inc(unit_out, 1)
                blocks(act, hidden)

            @block.vector
            def _(dve):
                reg = dve.alloc_register(ph._name("expert"))
                dve.sem_inc(out_out, 2)
                dve.wait_ge(w2_in, 16 * (1 + E))

                def keep_rows(s, u, turn):
                    dve.wait_ge(turned, s + 1)
                    if not d.affine:
                        dve.tensor_copy(xT[:, :, :], t_ps[:, :, :]).then_inc(xT_full, 1)
                        return
                    dve.wait_ge(w1_in[u], turn * 16 + 16)
                    for kk in range(KK):
                        at = d.affine_at + 2 * kk
                        ins = dve.tensor_scalar(xT[:, kk, :], t_ps[:, kk, :], w1[:, u, at:at + 1], w1[:, u, at + 1:at + 2],
                                                ALU.mult, ALU.add)
                    ins.then_inc(xT_full, 1)

                def results(s, u, turn, more):
                    if more:
                        keep_rows(s + 1, 1 - u, turn + u)
                    dve.wait_ge(stored[u], turn * 16)
                    e = expert_of(dve, reg, s)
                    for h in range(2):
                        dve.wait_ge(out_full, s * 2 + (h + 5))
                        dve.tensor_tensor(res[:, u, h, :], outs[h][:, 0:D], b2[:, bass.ds(e, 1), :].rearrange("p o d -> p (o d)"),
                                          ALU.add).then_inc(out_out, 1)

                keep_rows(0, 0, 0)
                blocks(dve, results)


def combine_visits(k, d):
    GROUPS = TILES // UNROLL
    with k.phase() as ph:
        got = ph.sb("got", [P, 2, TILES, D])
        got_in = [ph.sem(f"got_in{g}") for g in range(GROUPS)]
        added = ph.sem("added")
        with k.nc.Block() as block:

            @block.gpsimd
            def _(pool):
                for t in range(TILES):
                    for n in range(2):
                        pool.indirect_dma_start(
                            out=got[:, n, t, :], out_offset=None, in_=d.results,
                            in_offset=bass.IndirectOffsetOnAxis(ap=d.slots[:, n, t:t + 1], axis=0)
                        ).then_inc(got_in[t // UNROLL], 16)

            @block.vector
            def _(dve):
                for g in range(GROUPS):
                    dve.wait_ge(got_in[g], 16 * 2 * UNROLL)
                    for n in range(2):
                        if n == 1:
                            dve.wait_ge(added, (2 * g + 1) * UNROLL)
                        for t in range(g * UNROLL, (g + 1) * UNROLL):
                            xt = k.x[:, t, :]
                            dve.scalar_tensor_tensor(xt, got[:, n, t, :], d.gates[:, n, t:t + 1], xt, ALU.mult, ALU.add
                                                     ).then_inc(added, 1)


def sparse_mixture(k, xn, chosen, gates, experts, hidden, parts, out_bias, affine):
    with k.phase() as ph:
        d = Dispatch(k, ph, experts, hidden, affine)
        assign_slots(k, d, chosen, gates)
        scatter_rows(k, d, xn)
        expert_blocks(k, d, parts[0], parts[1], out_bias)
        combine_visits(k, d)


def routed(k, xn, xT, router, experts, logits):
    with k.phase() as ph:
        wr = ph.sb("router", [P, KK, experts])

        def load(sp, sem):
            sp.dma_start(wr[:, :, :], router).then_inc(sem, 16)
            return 16

        def evacuate(dve, t, product, stage, step):
            return dve.tensor_copy(logits[:, bass.ds(t, 1), :], product[:, 0, 0:experts])

        node_tiles(k, ph, xn, experts, load, wr, evacuate, xT=xT)


def load_small(k, pairs):
    with k.phase() as ph:
        loaded = ph.sem("loaded")
        with k.nc.Block() as block:

            @block.sync
            def _(sp):
                for dst, src in pairs:
                    sp.dma_start(dst, src).then_inc(loaded, 16)
                sp.wait_ge(loaded, 16 * len(pairs))


def edge_order(dram_row, g, ci):
    return dram_row.rearrange("o (g c e) -> (o c) g e", g=g, c=ci)


def attention_scores(k, ktable, kindex, qtable, heads, scores):
    nc = k.nc
    CI = 104 // heads
    R = CI * heads
    G = CHUNKS // CI
    per_body = 2 * BATCH // CI
    DH = D // heads
    with k.phase() as ph:
        staged = ph.sb("index_staged", [P, 2, BATCH], I32)
        rows = ph.sb("rows", [P, 2, BATCH, D])
        window = ph.sb("window", [P, 2, BATCH, D])
        rel = ph.sb("rel_row", [P, 2, BATCH * P], BF16)
        spread = ph.sb("spread", [P, 2, BATCH, P])
        prod = ph.sb("prod", [P, BATCH, D])
        sc = ph.sb("sc", [P, per_body, heads, CI])
        kept = ph.sb("kept", [R, G, P])
        q_ps = [ph.ps(f"q{q}", [P, 2, D]) for q in range(len(PAIRS))]
        s_ps = ph.ps("s", [P, 512])
        index_staged, gathering, spread_full = ph.sem("index_staged"), ph.sem("gathering"), ph.sem("spread_full")
        q_full, q_out = ph.sem("q_full"), ph.sem("q_out")
        rel_in = [ph.sem(f"rel_in{u}") for u in range(2)]
        reduced, s_full, s_out, stored = (ph.sem(n) for n in ("reduced", "s_full", "s_out", "stored"))
        go = ph.sem("go")
        rows_in = [ph.sem(f"rows_in{u}") for u in range(2)]
        window_in = [ph.sem(f"window_in{u}") for u in range(2)]
        NP2 = len(PAIRS)
        with nc.Block() as block:

            @block.sync
            def _(sp):
                base = sp.alloc_register(ph._name("window_base"))
                with sp.Fori(0, BATCHES // 2) as i:
                    for u in range(2):
                        b = i * 2 + u
                        c = i * (2 * BATCH) + u * BATCH
                        sp.wait_ge(spread_full, b + 1)
                        sp.dma_start(rel[:, u, :], k.rel_row[:, bass.ds(c * P, BATCH * P)].to_broadcast([P, BATCH * P])
                                     ).then_inc(rel_in[u], 16)
                        sp.wait_ge(q_full, (b + 1) * NP2)
                        for j in range(BATCH):
                            sp.reg_load(base, k.dst[0:1, bass.ds(c + j, 1)])
                            first = nc.snap(base, min_val=0, max_val=NPAD)
                            sp.dma_start(window[:, u, j, :], qtable[bass.ds(first, P), :]).then_inc(window_in[u], 16)
                sp.wait_ge(s_out, G + 1)
                for h in range(heads):
                    sp.dma_start(edge_order(scores[h:h + 1, :], G, CI), kept[h * CI:(h + 1) * CI, :, :]
                                 ).then_inc(stored, 16)
                sp.wait_ge(stored, 16 * heads)

            @block.scalar
            def _(act):
                act.sem_inc(s_out, 1)

                def stage(i, u):
                    act.wait_ge(rows_in[u], i * (16 * BATCH))
                    act.sem_inc(go, 1)
                    act.activation(staged[:, u, :], kindex[:, bass.ds(i * (2 * BATCH) + u * BATCH, BATCH)],
                                   ACT.Copy).then_inc(index_staged, 1)

                def keep(i):
                    for v in range(per_body):
                        act.wait_ge(s_full, i * per_body + (v + 1))
                        act.sem_inc(go, 1)
                        act.activation(kept[:, bass.ds(i * per_body + v, 1), :], s_ps[0:R, 0:P], ACT.Copy
                                       ).then_inc(s_out, 1)

                last = BATCHES // 2 - 1
                stage(0, 0)
                stage(0, 1)
                with act.Fori(0, last) as i:
                    stage(i + 1, 0)
                    stage(i + 1, 1)
                    keep(i)
                keep(last)

            @block.gpsimd
            def _(pool):
                with pool.Fori(0, BATCHES // 2) as i:
                    for u in range(2):
                        b = i * 2 + u
                        pool.wait_ge(index_staged, b + 1)
                        pool.wait_ge(reduced, b + 1)
                        pool.sem_inc(gathering, 1)
                        for j in range(BATCH):
                            pool.indirect_dma_start(
                                out=rows[:, u, j, :], out_offset=None, in_=ktable,
                                in_offset=bass.IndirectOffsetOnAxis(ap=staged[:, u, j:j + 1], axis=0)
                            ).then_inc(rows_in[u], 16)

            @block.tensor
            def _(pe):
                pe.sem_inc(q_full, 2 * NP2)
                with pe.Fori(0, BATCHES // 2) as i:
                    for u in range(2):
                        b = i * 2 + u
                        pe.wait_ge(spread_full, b + 3)
                        pe.wait_ge(window_in[u], (i + 1) * (16 * BATCH))
                        for p, (j0, n) in enumerate(PAIRS):
                            pe.wait_ge(q_out, b * NP2 + (p + 1))
                            for j in range(j0, j0 + n):
                                ins = pe.matmul(q_ps[p][:, j - j0, :], spread[:, u, j, :], window[:, u, j, :],
                                                start=True, stop=True)
                            ins.then_inc(q_full, 1)
                    for v in range(per_body):
                        pe.wait_ge(reduced, i * 2 + (2 + (v + 1) * 2 // per_body))
                        pe.wait_ge(s_out, i * per_body + (v + 1))
                        pe.transpose(s_ps[0:R, 0:P], sc[:, v, :, :].rearrange("p h c -> p (h c)"), k.ident[:, :]
                                     ).then_inc(s_full, 1)

            @block.vector
            def _(dve):
                dve.sem_inc(q_out, NP2)
                dve.sem_inc(reduced, 2)
                dve.sem_inc(spread_full, 2)

                def spread_out(i, u):
                    b = i * 2 + u
                    dve.wait_ge(rel_in[u], (i + 1) * 16)
                    dve.wait_ge(q_full, (b + 1) * NP2)
                    dve.tensor_scalar(spread[:, u, :, :].rearrange("p j e -> p (j e)"), rel[:, u, :], k.lane_col[:, 0:1],
                                      None, ALU.is_equal).then_inc(spread_full, 1)

                def score(i, u):
                    b = i * 2 + u
                    dve.wait_ge(rows_in[u], (i + 1) * (16 * BATCH))
                    dve.wait_ge(reduced, b + 2)
                    for p, (j0, n) in enumerate(PAIRS):
                        dve.wait_ge(q_full, b * NP2 + (2 * NP2 + p + 1))
                        dve.tensor_tensor(prod[:, j0:j0 + n, :], q_ps[p][:, 0:n, :], rows[:, u, j0:j0 + n, :],
                                          ALU.mult).then_inc(q_out, 1)
                    dve.wait_ge(q_out, (b + 2) * NP2)
                    dve.wait_ge(s_full, i * per_body)
                    v, j0 = (u, 0) if per_body == 2 else (0, u * BATCH)
                    dve.tensor_reduce(sc[:, v, :, j0:j0 + BATCH].rearrange("p h j -> p j h"),
                                      prod[:, :, :].rearrange("p j (h d) -> p j h d", h=heads), AX.X, ALU.add
                                      ).then_inc(reduced, 1)

                last = BATCHES // 2 - 1
                spread_out(0, 0)
                with dve.Fori(0, last) as i:
                    spread_out(i, 1)
                    score(i, 0)
                    spread_out(i + 1, 0)
                    score(i, 1)
                spread_out(last, 1)
                score(last, 0)
                score(last, 1)


def segment_softmax(k, scores, heads, alphas, scale=1.0, bias=None, more_loops=False):
    nc = k.nc
    H, N = heads, CHUNKS
    with k.phase() as ph:
        sc, run, seg = ph.sb("sc", [P, H, N]), ph.sb("run", [P, N]), ph.sb("seg", [P, H, N])
        dst = ph.sb("dst_rows_f", [P, N])
        dst_i = ph.sb("dst_rows", [P, N], I32)
        same, pen = ph.sb("same", [P, N + 1]), ph.sb("pen", [P, N + 1])
        ends = [ph.sb(f"end_{n}", [P, N]) for n in ("first", "last")]
        end_pens = [ph.sb(f"end_pen_{n}", [P, N]) for n in ("first", "last")]
        edge_vals = ph.sb("edge_vals", [P, 4, H])
        rowed = ph.sb("rowed", [H, 4, P])
        cont, whole = ph.sb("cont", [H, P + 1]), ph.sb("whole", [H, P])
        link, link_pen = ph.sb("link", [H, 2, P]), ph.sb("link_pen", [H, 2, P])
        cont_pen = ph.sb("cont_pen", [H, P + 1])
        carried = ph.sb("carried", [H, 2, P + 1])
        carry_in = ph.sb("carry_in", [H, 2, P])
        carry = ph.sb("carry", [P, 2, H])
        ends_ps = ph.ps("ends_ps", [P, 4, P])
        carry_ps = ph.ps("carry_ps", [P, 512])
        loaded, chained, at_pe, from_pe = (ph.sem(n) for n in ("loaded", "chained", "at_pe", "from_pe"))
        exp_in, exp_out, stored = ph.sem("exp_in"), ph.sem("exp_out"), ph.sem("stored")
        rows = "h (p i) -> p h i"
        loads = 2 + (bias is not None) + more_loops
        if more_loops:
            src_i, loops = ph.sb("src_rows", [P, N], I32), ph.sb("loops", [P, H, N])
        with nc.Block() as block:

            @block.sync
            def _(sp):
                sp.dma_start(dst_i[:, :], k.a["dst_rows"]).then_inc(loaded, 16)
                sp.dma_start(sc[:, :, :], scores.rearrange(rows, p=P)).then_inc(loaded, 16)
                if bias is not None:
                    sp.dma_start(seg[:, :, :], bias.rearrange(rows, p=P)).then_inc(loaded, 16)
                if more_loops:
                    sp.dma_start(src_i[:, :], k.a["src_row"].rearrange("o (p i) -> (o p) i", p=P)).then_inc(loaded, 16)
                sp.wait_ge(exp_out, 2)
                sp.dma_start(alphas.rearrange(rows, p=P), sc[:, :, :]).then_inc(stored, 16)
                sp.wait_ge(stored, 16)

            @block.scalar
            def _(act):
                act.wait_ge(exp_in, 1)
                act.activation(sc[:, :, :], sc[:, :, :], ACT.Exp).then_inc(exp_out, 1)

            @block.tensor
            def _(pe):
                for n in range(3 if more_loops else 2):
                    pe.wait_ge(at_pe, 2 * n + 1)
                    for q in range(4):
                        ins = pe.transpose(ends_ps[0:H, q, :], edge_vals[:, q, :], k.ident[:, :])
                    ins.then_inc(from_pe, 1)
                    pe.wait_ge(at_pe, 2 * n + 2)
                    for q in range(2):
                        ins = pe.transpose(carry_ps[:, q * H:(q + 1) * H], carry_in[:, q, :], k.ident[0:H, 0:H])
                    ins.then_inc(from_pe, 1)

            @block.vector
            def _(dve):
                step = Chain(dve, chained)
                dve.wait_ge(loaded, 16 * loads)
                step(dve.tensor_copy(dst[:, :], dst_i[:, :]))
                dve.memset(same[:, 0:1], 0.0)
                dve.memset(same[:, N:N + 1], 0.0)
                step(dve.tensor_tensor(same[:, 1:N], dst[:, 1:N], dst[:, 0:N - 1], ALU.is_equal))
                step(dve.tensor_scalar(pen[:, :], same[:, :], 1.0, BIG, ALU.subtract, ALU.mult))
                for n, at in enumerate((0, N - 1)):
                    step(dve.tensor_scalar(ends[n][:, :], dst[:, :], dst[:, at:at + 1], None, ALU.is_equal))
                    step(dve.tensor_scalar(end_pens[n][:, :], ends[n][:, :], 1.0, BIG, ALU.subtract, ALU.mult))
                    step(dve.tensor_copy(edge_vals[:, 2 + n, :], dst[:, at:at + 1].to_broadcast([P, H])))
                if scale != 1.0:
                    step(dve.tensor_scalar(sc[:, :, :], sc[:, :, :], scale, None, ALU.mult))
                if bias is not None:
                    step(dve.tensor_tensor(sc[:, :, :], sc[:, :, :], seg[:, :, :], ALU.add))

                def combine(n, maximum, values):
                    masks = pen if maximum else same
                    join, op = (ALU.add, ALU.max) if maximum else (ALU.mult, ALU.add)
                    for h in range(H):
                        step(dve.tensor_tensor_scan(run[:, :], masks[:, 0:N], values[:, h, :], -BIG if maximum else 0.0,
                                                    join, op))
                        step(dve.tensor_tensor_scan(seg[:, h, ::-1], masks[:, N:0:-1], run[:, ::-1],
                                                    -BIG if maximum else 0.0, join, ALU.max))
                    step(dve.tensor_copy(edge_vals[:, 0, :], seg[:, :, 0]))
                    dve.tensor_copy(edge_vals[:, 1, :], seg[:, :, N - 1]).then_inc(at_pe, 1)
                    dve.wait_ge(from_pe, 2 * n + 1)
                    step(dve.tensor_copy(rowed[:, :, :], ends_ps[0:H, :, :]))
                    firsts, lasts, dst_first, dst_last = (rowed[:, q, :] for q in range(4))
                    if n == 0:
                        dve.memset(cont[:, 0:1], 0.0)
                        dve.memset(cont[:, P:P + 1], 0.0)
                        step(dve.tensor_tensor(cont[:, 1:P], dst_first[:, 1:P], dst_last[:, 0:P - 1], ALU.is_equal))
                        step(dve.tensor_tensor(whole[:, :], dst_first, dst_last, ALU.is_equal))
                        step(dve.tensor_tensor(link[:, 0, :], whole[:, :], cont[:, 0:P], ALU.mult))
                        step(dve.tensor_tensor(link[:, 1, :], whole[:, :], cont[:, 1:P + 1], ALU.mult))
                        step(dve.tensor_scalar(link_pen[:, :, :], link[:, :, :], 1.0, BIG, ALU.subtract, ALU.mult))
                        step(dve.tensor_scalar(cont_pen[:, :], cont[:, :], 1.0, BIG, ALU.subtract, ALU.mult))
                    links = link_pen if maximum else link
                    none = -BIG if maximum else 0.0
                    step(dve.memset(carried[:, :, :], none))
                    step(dve.tensor_tensor_scan(carried[:, 0, 1:P + 1], links[:, 0, :], lasts, none, join, op))
                    step(dve.tensor_tensor_scan(carried[:, 1, P - 1::-1], links[:, 1, ::-1], firsts[:, ::-1], none,
                                                join, op))
                    c = cont_pen if maximum else cont
                    step(dve.tensor_tensor(carry_in[:, 0, :], carried[:, 0, 0:P], c[:, 0:P], join))
                    dve.tensor_tensor(carry_in[:, 1, :], carried[:, 1, 1:P + 1], c[:, 1:P + 1], join).then_inc(at_pe, 1)
                    dve.wait_ge(from_pe, 2 * n + 2)
                    step(dve.tensor_copy(carry[:, :, :], carry_ps[:, 0:2 * H].rearrange("p (q h) -> p q h", q=2)))
                    masks = end_pens if maximum else ends
                    for h in range(H):
                        for q in range(2):
                            step(dve.scalar_tensor_tensor(seg[:, h, :], masks[q][:, :], carry[:, q, h:h + 1],
                                                          seg[:, h, :], join, op))

                combine(0, True, sc)
                step(dve.tensor_tensor(sc[:, :, :], sc[:, :, :], seg[:, :, :], ALU.subtract))
                dve.sem_inc(exp_in, 1)
                if more_loops:
                    step(dve.tensor_copy(loops[:, 0, :], src_i[:, :]))
                    step(dve.tensor_tensor(loops[:, 0, :], loops[:, 0, :], dst[:, :], ALU.is_equal))
                    combine(1, False, loops)
                    step(dve.tensor_scalar(seg[:, :, :], seg[:, :, :], 1.0, None, ALU.max))
                    step(dve.reciprocal(seg[:, :, :], seg[:, :, :]))
                    step(dve.tensor_tensor(loops[:, :, :], loops[:, :, :], seg[:, :, :], ALU.mult))
                    step(dve.tensor_scalar(loops[:, :, :], loops[:, :, :], 1.0, None, ALU.add))
                dve.wait_ge(exp_out, 1)
                if more_loops:
                    step(dve.tensor_tensor(sc[:, :, :], sc[:, :, :], loops[:, :, :], ALU.mult))
                combine(2 if more_loops else 1, False, sc)
                step(dve.reciprocal(seg[:, :, :], seg[:, :, :]))
                dve.tensor_tensor(sc[:, :, :], sc[:, :, :], seg[:, :, :], ALU.mult).then_inc(exp_out, 1)


def load_alphas(k, alphas, heads, ci, out):
    nc = k.nc
    R, G = heads * ci, CHUNKS // ci
    quads = [(g, min(4, G - g)) for g in range(0, G, 4)]
    with k.phase() as ph:
        kept = ph.sb("kept", [R, G, P])
        ps = [ph.ps(f"turned{q}", [P, 4, P]) for q in range(2)]
        loaded, full, emptied = ph.sem("loaded"), ph.sem("full"), ph.sem("emptied")
        with nc.Block() as block:

            @block.sync
            def _(sp):
                for h in range(heads):
                    sp.dma_start(kept[h * ci:(h + 1) * ci, :, :], edge_order(alphas[h:h + 1, :], G, ci)
                                 ).then_inc(loaded, 16)

            @block.tensor
            def _(pe):
                pe.wait_ge(loaded, 16 * heads)
                for q, (g0, n) in enumerate(quads):
                    if q >= 2:
                        pe.wait_ge(emptied, q - 1)
                    for g in range(g0, g0 + n):
                        ins = pe.transpose(ps[q % 2][:, g - g0, 0:R], kept[:, g, :], k.ident[0:R, 0:R])
                    ins.then_inc(full, 1)

            @block.scalar
            def _(act):
                for q, (g0, n) in enumerate(quads):
                    act.wait_ge(full, q + 1)
                    act.activation(out[:, g0:g0 + n, :], ps[q % 2][:, 0:n, 0:R], ACT.Copy).then_inc(emptied, 1)


def edge_bias(k, out):
    nc, a = k.nc, k.a
    N, H, F = 496, 8, 64
    COLS = EPAD // 2
    BLOCKS = 4
    BODIES = COLS // (N * BLOCKS)
    with k.phase() as ph:
        w1, w2 = ph.sb("w1", [P, D]), ph.sb("w2", [P, KK, H])
        b1, b2 = ph.sb("b1", [P, KK]), ph.sb("b2", [H, 1])
        attr = ph.sb("attr", [P, 2, BLOCKS * N])
        hid = ph.sb("hid", [P, 2, KK, N])
        res = ph.sb("res", [H, 2, 2, BLOCKS, N])
        h_ps = [ph.ps(f"h{q}", [P, 512]) for q in range(4)]
        r_ps = [ph.ps(f"r{q}", [P, 512]) for q in range(2)]
        w_in, h_full, h_out, r_full, r_out = (ph.sem(n) for n in ("w_in", "h_full", "h_out", "r_full", "r_out"))
        attr_in = [ph.sem(f"attr_in{u}") for u in range(2)]
        stored = [ph.sem(f"stored{u}") for u in range(2)]
        storing = ph.sem("storing")
        J = 2 * BLOCKS
        with nc.Block() as block:

            @block.sync
            def _(sp):
                for dst, src in ((w1[:, :], a["L2_gnn_W1"]), (w2[:, :, :], a["L2_gnn_W2"]), (b1[:, :], a["L2_gnn_b1"]),
                                 (b2[:, :], a["L2_gnn_b2"])):
                    sp.dma_start(dst, src).then_inc(w_in, 16)
                with sp.Fori(0, BODIES // 2) as i:
                    for u in range(2):
                        n = i * 2 + u
                        sp.wait_ge(r_full, n * J)
                        sp.dma_start(attr[:, u, :], a["attr"][:, bass.ds(n * (BLOCKS * N), BLOCKS * N)]
                                     ).then_inc(attr_in[u], 16)

            @block.tensor
            def _(pe):
                pe.sem_inc(r_full, J)
                pe.wait_ge(w_in, 64)
                with pe.Fori(0, BODIES // 2) as i:
                    for u in range(2):
                        n = i * 2 + u
                        pe.wait_ge(attr_in[u], i * 16 + 16)

                        def hidden(j):
                            half, blk = j % 2, j // 2
                            for kk in range(KK):
                                q = (2 * j + kk) % 4
                                pe.wait_ge(h_out, n * (2 * J) + (2 * j + kk))
                                pe.matmul(h_ps[q][:, 0:N], w1[half * F:(half + 1) * F, kk * P:(kk + 1) * P],
                                          attr[half * F:(half + 1) * F, u, blk * N:(blk + 1) * N],
                                          start=True, stop=True).then_inc(h_full, 1)

                        def result(j):
                            pe.wait_ge(r_out, n * J + j)
                            for kk in range(KK):
                                pe.wait_ge(h_out, n * (2 * J) + (2 * j + kk + 4))
                                ins = pe.matmul(r_ps[j % 2][0:H, 0:N], w2[:, kk, :], hid[:, j % 2, kk, :],
                                                start=kk == 0, stop=kk == KK - 1)
                            ins.then_inc(r_full, 1)

                        hidden(0)
                        for j in range(J):
                            if j + 1 < J:
                                hidden(j + 1)
                            result(j)

            @block.scalar
            def _(act):
                act.sem_inc(h_out, 3)
                act.wait_ge(w_in, 64)
                with act.Fori(0, BODIES // 2) as i:
                    for u in range(2):
                        n = i * 2 + u
                        for j in range(J):
                            for kk in range(KK):
                                act.wait_ge(h_full, n * (2 * J) + (2 * j + kk + 1))
                                act.wait_ge(r_full, n * J + (J + j - 1))
                                act.activation(hid[:, j % 2, kk, :], h_ps[(2 * j + kk) % 4][:, 0:N], ACT.Relu,
                                               bias=b1[:, kk:kk + 1]).then_inc(h_out, 1)

            @block.vector
            def _(dve):
                dve.sem_inc(r_out, 1)
                dve.wait_ge(w_in, 64)
                with dve.Fori(0, BODIES // 2) as i:
                    for u in range(2):
                        n = i * 2 + u
                        dve.wait_ge(stored[u], i * 32)
                        for j in range(J):
                            dve.wait_ge(r_full, n * J + (J + j + 1))
                            dve.tensor_scalar(res[:, u, j % 2, j // 2, :], r_ps[j % 2][0:H, 0:N], b2[:, 0:1], None, ALU.add
                                              ).then_inc(r_out, 1)

            @block.gpsimd
            def _(pool):
                with pool.Fori(0, BODIES // 2) as i:
                    for u in range(2):
                        n = i * 2 + u
                        for half in range(2):
                            pool.wait_ge(r_out, n * J + (J + 1))
                            pool.sem_inc(storing, 1)
                            pool.dma_start(out[:, bass.ds(n * (BLOCKS * N) + half * COLS, BLOCKS * N)],
                                           res[:, u, half, :, :].rearrange("h b n -> h (b n)")).then_inc(stored[u], 16)
                for u in range(2):
                    pool.wait_ge(stored[u], 32 * (BODIES // 2))


def project_sums(k, ph, accT, count, load, rhs, update, links):
    nc = k.nc
    ring = ph.sb("sum_ring", [P, UNROLL, KK, P])
    ps = [ph.ps(f"product{i}", [P, 512]) for i in range(4)]
    loaded, ring_full, full, emptied, chained = (ph.sem(n) for n in ("loaded", "ring_full", "full", "emptied", "chained"))
    bodies = TILES // UNROLL
    count_in = []
    with nc.Block() as block:

        @block.sync
        def _(sp):
            count_in.append(load(sp, loaded))

        @block.scalar
        def _(act):
            go = ph.sem("go")
            with act.Fori(0, bodies) as i:
                act.wait_ge(full, i * (UNROLL * count))
                act.sem_inc(go, 1)
                for u in range(UNROLL):
                    act.activation(ring[:, u, :, :], accT[:, :, bass.ds((i * UNROLL + u) * P, P)], ACT.Copy
                                   ).then_inc(ring_full, 1)

        @block.tensor
        def _(pe):
            pe.wait_ge(loaded, count_in[0])
            with pe.Fori(0, bodies) as i:
                for u in range(UNROLL):
                    t = i * UNROLL + u
                    pe.wait_ge(ring_full, t + 1)
                    for y in range(count):
                        m = u * count + y
                        pe.wait_ge(emptied, t * count + y)
                        for kk in range(KK):
                            ins = pe.matmul(ps[m % 4 if count == 4 else m % 3][:, 0:D], ring[:, u, kk, :],
                                            rhs[:, y, kk, :], start=kk == 0, stop=kk == KK - 1)
                        ins.then_inc(full, 1)

        @block.vector
        def _(dve):
            dve.sem_inc(emptied, 3 if count == 4 else 1)
            dve.wait_ge(loaded, count_in[0])
            step = Chain(dve, chained)
            with dve.Fori(0, bodies) as i:
                for u in range(UNROLL):
                    t = i * UNROLL + u
                    step.base, step.n = t * links, 0

                    def product(y):
                        m = u * count + y
                        dve.wait_ge(full, t * count + (y + 1))
                        return ps[m % 4 if count == 4 else m % 3][:, 0:D]

                    update(dve, t, product, step, emptied)
                    assert step.n == links


TYPES, RELS, L1_HEADS = 4, 8, 4


def typed_tables(k, xn, kinds, qtab, ktab, vtab):
    nc, a = k.nc, k.a
    HD = D // L1_HEADS
    R4 = RELS // 2
    with k.phase() as ph:
        weights = ph.sb("typed_w", [P, 3, TYPES, KK, D])
        blocks = ph.sb("relation_blocks", [P, 2, KK, RELS, P])
        pri = ph.sb("pri", [P, KK, RELS])
        ring = ph.sb("tile_ring", [P, D])
        diag = ph.sb("diag", [P, TYPES, P])
        masked = ph.sb("masked", [P, KK, TYPES, P])
        kvT = ph.sb("kvT", [P, 2, KK, P])
        stage = ph.sb("stage", [P, 2, 2, RELS, D])
        q_stage = ph.sb("q_stage", [P, 2, D])
        m_ps = [ph.ps(f"masked{kk}", [P, TYPES, P]) for kk in range(KK)]
        kv_ps, q_ps = ph.ps("kv", [P, 2, KK, P]), ph.ps("q", [P, 512])
        r_ps = [ph.ps(f"related{i}", [P, R4, P]) for i in range(4)]
        loaded, zeroed, blocked, ready = ph.sem("loaded"), ph.sem("zeroed"), ph.sem("blocked"), ph.sem("ready")
        ring_full, diag_full, m_full, m_out = (ph.sem(n) for n in ("ring_full", "diag_full", "m_full", "m_out"))
        kv_full, kv_out, q_full, q_out = (ph.sem(n) for n in ("kv_full", "kv_out", "q_full", "q_out"))
        r_full, k_out, v_out = ph.sem("r_full"), ph.sem("k_out"), ph.sem("v_out")
        stored = [ph.sem(f"stored{u}") for u in range(2)]
        TURNS = (TILES - 1) // 2
        J = 8

        def tiles(eng, body):
            with eng.Fori(0, TURNS) as i:
                for u in range(2):
                    body(i * 2 + u, u, i, True)
            body(TILES - 1, 0, TURNS, False)

        def part(j):
            return j // 4, j // 2 % 2, slice(j % 2 * R4, j % 2 * R4 + R4)

        with nc.Block() as block:

            @block.sync
            def _(sp):
                sp.dma_start(weights[:, :, :, :, :], a["L1_gnn_w"]).then_inc(loaded, 16)
                sp.dma_start(pri[:, :, :], a["L1_gnn_pri"]).then_inc(loaded, 16)
                sp.wait_ge(zeroed, 1)
                for n, name in enumerate(("L1_gnn_att", "L1_gnn_msg")):
                    for h in range(2):
                        at = slice(h * HD, (h + 1) * HD)
                        for o in range(KK):
                            sp.dma_start(blocks[at, n, o, :, at], a[name][at, o, :, :]).then_inc(blocked, 16)

                def store(t, u, turn, more):
                    sp.wait_ge(q_out, t + 1)
                    sp.dma_start(qtab[bass.ds(t * P, P), :], q_stage[:, u, :]).then_inc(stored[u], 16)
                    for n, (tab, out) in enumerate(((ktab, k_out), (vtab, v_out))):
                        sp.wait_ge(out, (t + 1) * 4)
                        sp.dma_start(tab.rearrange("(r n) d -> n r d", r=RELS)[bass.ds(t * P, P), :, :],
                                     stage[:, u, n, :, :]).then_inc(stored[u], 16)
                tiles(sp, store)
                for u in range(2):
                    sp.wait_ge(stored[u], 48 * (TURNS + 1 - u))

            @block.gpsimd
            def _(pool):
                pool.memset(blocks[:, :, :, :, :], 0.0).then_inc(zeroed, 1)
                pool.memset(xn[:, TILES, :], 0.0).then_inc(zeroed, 1)

            @block.scalar
            def _(act):
                def fetch(t):
                    act.activation(ring[:, :], xn[:, bass.ds(t, 1), :], ACT.Copy).then_inc(ring_full, 1)

                def empty(t):
                    for kk in range(KK):
                        act.wait_ge(m_full, t * KK + (kk + 1))
                        act.activation(masked[:, kk, :, :], m_ps[kk][:, :, :], ACT.Copy).then_inc(m_out, 1)

                def tile(t, u, turn, more):
                    act.wait_ge(kv_full, t + 1)
                    act.activation(kvT[:, :, :, :], kv_ps[:, :, :, :], ACT.Copy).then_inc(kv_out, 1)
                    act.wait_ge(q_full, t + 1)
                    if more:
                        empty(t + 1)
                        act.sem_inc(ready, 1)
                        fetch(t + 2)
                    act.wait_ge(stored[u], turn * 48)
                    for j in range(4):
                        _, o, rels = part(j)
                        act.wait_ge(r_full, t * J + (j + 1))
                        act.activation(stage[:, u, 0, rels, o * P:(o + 1) * P], r_ps[j % 4][:, :, :], ACT.Copy
                                       ).then_inc(k_out, 1)

                act.wait_ge(zeroed, 2)
                fetch(0)
                empty(0)
                fetch(1)
                tiles(act, tile)

            @block.vector
            def _(dve):
                dve.wait_ge(loaded, 32)
                dve.wait_ge(blocked, 16 * 8)
                p4 = pri[:, :, :].unsqueeze(3).to_broadcast([P, KK, RELS, P])
                for o in range(KK):
                    dve.scalar_tensor_tensor(blocks[:, 0, o, :, :], blocks[:, 0, o, :, :], 1.0 / HD ** 0.5,
                                             p4[:, o, :, :], ALU.mult, ALU.mult).then_inc(blocked, 1)

                def mask(t):
                    types = kinds[:, bass.ds(t, 1), :].rearrange("p o y -> p (o y)").unsqueeze(2)
                    dve.tensor_tensor(diag[:, :, :], k.ident[:, :].unsqueeze(1).to_broadcast([P, TYPES, P]),
                                      types.to_broadcast([P, TYPES, P]), ALU.mult).then_inc(diag_full, 1)

                def tile(t, u, turn, more):
                    dve.wait_ge(q_full, t + 1)
                    dve.wait_ge(stored[u], turn * 48)
                    dve.tensor_copy(q_stage[:, u, :], q_ps[:, 0:D]).then_inc(q_out, 1)
                    if more:
                        dve.wait_ge(m_full, (t + 2) * KK)
                        mask(t + 2)
                    for j in range(4, J):
                        _, o, rels = part(j)
                        dve.wait_ge(r_full, t * J + (j + 1))
                        dve.tensor_copy(stage[:, u, 1, rels, o * P:(o + 1) * P], r_ps[j % 4][:, :, :]).then_inc(v_out, 1)

                mask(0)
                dve.wait_ge(m_full, KK)
                mask(1)
                tiles(dve, tile)

            @block.tensor
            def _(pe):
                def turn_masked(t):
                    pe.wait_ge(ring_full, t + 1)
                    pe.wait_ge(diag_full, t + 1)
                    pe.wait_ge(m_out, t * KK)
                    for kk in range(KK):
                        pe.matmul(m_ps[kk][:, :, :], ring[:, kk * P:(kk + 1) * P], diag[:, :, :], start=True, stop=True
                                  ).then_inc(m_full, 1)

                def tile(t, u, turn, more):
                    pe.wait_ge(m_out, (t + 1) * KK)
                    pe.wait_ge(kv_out, t)
                    for n in range(2):
                        for o in range(KK):
                            for kk in range(KK):
                                for y in range(TYPES):
                                    ins = pe.matmul(kv_ps[:, n, o, :], weights[:, n, y, kk, o * P:(o + 1) * P],
                                                    masked[:, kk, y, :], start=kk == 0 and y == 0,
                                                    stop=kk == KK - 1 and y == TYPES - 1)
                    ins.then_inc(kv_full, 1)
                    pe.wait_ge(q_out, t)
                    for kk in range(KK):
                        for y in range(TYPES):
                            ins = pe.matmul(q_ps[:, 0:D], masked[:, kk, y, :], weights[:, 2, y, kk, :],
                                            start=kk == 0 and y == 0, stop=kk == KK - 1 and y == TYPES - 1)
                    ins.then_inc(q_full, 1)
                    if more:
                        turn_masked(t + 1)
                    pe.wait_ge(kv_out, t + 1)
                    for j in range(J):
                        n, o, rels = part(j)
                        if n == 0:
                            pe.wait_ge(v_out, t * 4)
                        else:
                            pe.wait_ge(k_out, t * 4 + (j - 3))
                        pe.matmul(r_ps[j % 4][:, :, :], kvT[:, n, o, :], blocks[:, n, o, rels, :], start=True, stop=True
                                  ).then_inc(r_full, 1)

                pe.wait_ge(loaded, 32)
                pe.wait_ge(blocked, 16 * 8 + 2)
                turn_masked(0)
                tiles(pe, tile)


def layer1_gnn(k):
    nc, a = k.nc, k.a
    H, CI = L1_HEADS, 2 * BATCH

    def dram(name, shape):
        return nc.dram_tensor(name, shape, F32, kind="Internal").ap()

    ktab, vtab, qtab = dram("l1_k", [RELS * NPAD, D]), dram("l1_v", [RELS * NPAD, D]), dram("l1_q", [NWIN, D])
    scores, alphas = dram("l1_scores", [H, EPAD]), dram("l1_alpha", [H, EPAD])
    with k.phase() as ph:
        index = ph.sb("row_index", [P, CHUNKS], I32)
        kinds = ph.sb("kinds", [P, TILES + 1, TYPES])
        gains = ph.sb("gains", [P, TILES, TYPES])
        with k.phase() as inner:
            etype, types = inner.sb("etype", [P, CHUNKS], I32), inner.sb("types", [P, TILES], I32)
            etype_f, src_f = inner.sb("etype_f", [P, CHUNKS]), inner.sb("src_f", [P, CHUNKS])
            types_f, skip = inner.sb("types_f", [P, TILES]), inner.sb("skip", [P, TYPES])
            loaded, chained, squashed = inner.sem("loaded"), inner.sem("chained"), inner.sem("squashed")
            with nc.Block() as block:

                @block.sync
                def _(sp):
                    for dst, src in ((etype, a["etype_lanes"]), (types, a["type_lanes"])):
                        sp.dma_start(dst[:, :], src).then_inc(loaded, 16)
                    sp.dma_start(skip[:, :], a["L1_gnn_skip"].to_broadcast([P, TYPES])).then_inc(loaded, 16)

                @block.scalar
                def _(act):
                    act.wait_ge(loaded, 48)
                    act.activation(skip[:, :], skip[:, :], ACT.Sigmoid).then_inc(squashed, 1)

                @block.vector
                def _(dve):
                    step = Chain(dve, chained)
                    dve.wait_ge(loaded, 48)
                    dve.tensor_copy(types_f[:, :], types[:, :])
                    dve.tensor_copy(etype_f[:, :], etype[:, :])
                    step(dve.tensor_copy(src_f[:, :], k.src[:, :]))
                    dve.scalar_tensor_tensor(index[:, :], etype_f[:, :], float(NPAD), src_f[:, :], ALU.mult, ALU.add)
                    dve.memset(kinds[:, TILES, :], 0.0)
                    for y in range(TYPES):
                        ins = dve.tensor_scalar(kinds[:, 0:TILES, y], types_f[:, :], float(y), None, ALU.is_equal)
                    step(ins)
                    dve.wait_ge(squashed, 1)
                    step(dve.tensor_tensor(gains[:, :, :], kinds[:, 0:TILES, :],
                                           skip[:, :].unsqueeze(1).to_broadcast([P, TILES, TYPES]), ALU.mult))
        clear_tail(k, qtab)
        with k.phase() as inner:
            xn = inner.sb("xn", [P, TILES + 1, D])
            normalize(k, k.x, xn)
            typed_tables(k, xn, kinds, qtab, ktab, vtab)
        attention_scores(k, ktab, index, qtab, H, scores)
        segment_softmax(k, scores, H, alphas)
        accT = ph.sb("accT", [P, KK, NWIN])
        with k.phase() as inner:
            alpha = inner.sb("alpha", [P, CHUNKS // CI, H * CI])
            load_alphas(k, alphas, H, CI, alpha)
            aggregate(k, vtab, index, accT, heads=H,
                      alpha=lambda i, u: alpha[:, bass.ds(i, 1), :].rearrange("p o (h c) -> p (o h) c", h=H)
                      [:, :, u * BATCH:(u + 1) * BATCH])
        wa = ph.sb("wa", [P, TYPES, KK, D])

        def load(sp, sem):
            sp.dma_start(wa[:, :, :, :], a["L1_gnn_wa"]).then_inc(sem, 16)
            return 16

        def update(dve, t, product, step, emptied):
            xt = k.x[:, bass.ds(t, 1), :]
            for y in range(TYPES):
                dve.wait_ge(emptied, t * TYPES + (y + 3))
                gain = gains[:, bass.ds(t, 1), y]
                dve.scalar_tensor_tensor(xt, product(y), gain, xt, ALU.mult, ALU.add).then_inc(emptied, 1)

        with k.phase() as inner:
            project_sums(k, inner, accT, TYPES, load, wa, update, 0)


def layer2_gnn(k):
    nc, a = k.nc, k.a
    H, CI = 8, BATCH

    def dram(name, shape):
        return nc.dram_tensor(name, shape, F32, kind="Internal").ap()

    ktab, vtab, qtab = dram("l2_k", [NPAD, D]), dram("l2_v", [NPAD, D]), dram("l2_q", [NWIN, D])
    scores, biases, alphas = dram("l2_scores", [H, EPAD]), dram("l2_bias", [H, EPAD]), dram("l2_alpha", [H, EPAD])
    edge_bias(k, biases)
    clear_tail(k, qtab)
    with k.phase() as ph:
        xn = ph.sb("xn", [P, TILES, D])
        normalize(k, k.x, xn)
        w = ph.sb("kvq_w", [P, KK, 3 * D])

        def load(sp, sem):
            sp.dma_start(w[:, :, :], a["L2_gnn_kvq"]).then_inc(sem, 16)
            return 16

        def evacuate(dve, t, product, stage, step):
            return dve.tensor_copy(stage, product[:, :, :].rearrange("p b n -> p (b n)")[:, 0:3 * D])

        def store(sp, t, stage, sem):
            for n, tab in enumerate((ktab, vtab, qtab)):
                sp.dma_start(tab[bass.ds(t * P, P), :], stage[:, n * D:(n + 1) * D]).then_inc(sem, 16)

        with k.phase() as inner:
            node_tiles(k, inner, xn, 3 * D, load, w, evacuate, store, 3)
    attention_scores(k, ktab, k.src, qtab, H, scores)
    segment_softmax(k, scores, H, alphas, float(1.0 / np.sqrt(D // H)), biases)
    with k.phase() as ph:
        accT = ph.sb("accT", [P, KK, NWIN])
        with k.phase() as inner:
            alpha = inner.sb("alpha", [P, CHUNKS // CI, H * CI])
            load_alphas(k, alphas, H, CI, alpha)
            aggregate(k, vtab, k.src, accT, heads=H,
                      alpha=lambda i, u: alpha[:, bass.ds(i * 2 + u, 1), :].rearrange("p o (h j) -> p (o h) j", h=H))
        wo, bo = ph.sb("wo", [P, 1, KK, D]), ph.sb("bo", [P, D])

        def load(sp, sem):
            sp.dma_start(wo[:, 0, :, :], a["L2_gnn_Wo"]).then_inc(sem, 16)
            sp.dma_start(bo[:, :], a["L2_gnn_bo"].to_broadcast([P, D])).then_inc(sem, 16)
            return 32

        def update(dve, t, product, step, emptied):
            xt = k.x[:, bass.ds(t, 1), :]
            step(dve.tensor_tensor(xt, xt, bo[:, :], ALU.add))
            dve.tensor_tensor(xt, product(0), xt, ALU.add).then_inc(emptied, 1)

        with k.phase() as inner:
            project_sums(k, inner, accT, 1, load, wo, update, 1)


def layer3_gnn(k):
    nc, a = k.nc, k.a

    def dram(name, shape):
        return nc.dram_tensor(name, shape, F32, kind="Internal").ap()

    htab = dram("l3_h", [NPAD, D])
    scores, alphas = dram("l3_scores", [1, EPAD]), dram("l3_alpha", [1, EPAD])
    with k.phase() as ph:
        score_parts = ph.sb("score_parts", [P, 2, TILES])
        xn = ph.sb("xn", [P, TILES, D])
        normalize(k, k.x, xn)
        wt, wo, att = ph.sb("w_t", [P, KK, D + 2]), ph.sb("w_o", [P, KK, D]), ph.sb("att", [P, KK, 2])
        load_small(k, [(wt[:, :, 0:D], a["L3_gnn_WT"]), (wo[:, :, :], a["L3_gnn_W"]), (att[:, :, :], a["L3_gnn_att"])])
        with k.phase() as inner:
            ps, folded, copied = inner.ps("folded", [P, 512]), inner.sem("folded"), inner.sem("copied")
            with nc.Block() as block:

                @block.tensor
                def _(pe):
                    for kk in range(KK):
                        for o in range(KK):
                            ins = pe.matmul(ps[:, 2 * kk:2 * kk + 2], wo[:, o, kk * P:(kk + 1) * P], att[:, o, :],
                                            start=o == 0, stop=o == KK - 1)
                    ins.then_inc(folded, 1)

                @block.vector
                def _(dve):
                    dve.wait_ge(folded, 1)
                    for kk in range(KK):
                        dve.tensor_copy(wt[:, kk, D:D + 2], ps[:, 2 * kk:2 * kk + 2])
                    dve.tensor_tensor(k.x[:, :, :], k.x[:, :, :], xn[:, :, :], ALU.add).then_inc(copied, 1)
                    dve.wait_ge(copied, 1)

        def load(sp, sem):
            return 0

        def evacuate(dve, t, product, stage, step):
            dve.tensor_copy(score_parts[:, :, bass.ds(t, 1)].rearrange("p n t -> p (n t)"), product[:, 0, D:D + 2])
            return dve.tensor_copy(stage, product[:, 0, 0:D])

        def store(sp, t, stage, sem):
            sp.dma_start(htab[bass.ds(t * P, P), :], stage).then_inc(sem, 16)

        with k.phase() as inner:
            node_tiles(k, inner, xn, D + 2, load, wt, evacuate, store, 1)
        gat_scores(k, score_parts, scores)
    segment_softmax(k, scores, 1, alphas, more_loops=True)
    with k.phase() as ph:
        accT = ph.sb("accT", [P, KK, NWIN])
        with k.phase() as inner:
            alpha = inner.sb("alpha", [P, CHUNKS // 62, 62])
            load_alphas(k, alphas, 1, 62, alpha)
            aggregate(k, htab, k.src, accT, weights=alpha[:, :, :].rearrange("p g c -> p (g c)"))
        bias = ph.sb("bias", [P, D])

        def load(sp, sem):
            sp.dma_start(bias[:, :], a["L3_gnn_bias"].to_broadcast([P, D])).then_inc(sem, 16)
            return 16

        def update(dve, t, tile, step):
            xt = k.x[:, bass.ds(t, 1), :]
            step(dve.tensor_tensor(tile, tile, bias[:, :], ALU.add))
            return dve.scalar_tensor_tensor(xt, tile, 0.0, xt, ALU.max, ALU.add)

        with k.phase() as inner:
            from_sums(k, inner, accT, load, update, links=1)


def gat_scores(k, nodes, scores):
    nc = k.nc
    with k.phase() as ph:
        lanes = ph.sb("lanes", [P, 2, 2, BATCH * P], BF16)
        hot_lane = ph.sb("hot_lane", [P, 2, 2, BATCH * P], BF16)
        hot_tile = ph.sb("hot_tile", [P, 2, 2, BATCH, TILES])
        parts, rest = ph.sb("parts", [P, 3, 2, TILES], BF16), ph.sb("rest", [P, 2, TILES])
        picked = ph.sb("picked", [P, 2, 2, BATCH])
        sc = ph.sb("sc", [P, CHUNKS])
        kept = ph.sb("kept", [62, BATCH, P])
        by_lane = [[ph.ps(f"by_lane{u}_{n}", [P, 512]) for n in range(2)] for u in range(2)]
        ps = [ph.ps(f"turned{q}", [P, 512]) for q in range(2)]
        split_up, lane_hot, by_lane_full, chained = (ph.sem(n) for n in ("split_up", "lane_hot", "by_lane_full", "chained"))
        scored, full, emptied, stored = (ph.sem(n) for n in ("scored", "full", "emptied", "stored"))
        lanes_in = [ph.sem(f"lanes_in{u}") for u in range(2)]
        with nc.Block() as block:

            @block.sync
            def _(sp):
                with sp.Fori(0, BATCHES // 2) as i:
                    for u in range(2):
                        c = i * (2 * BATCH) + u * BATCH
                        sp.wait_ge(lane_hot, i * 2 + (u + 1))
                        for n, table in enumerate((k.src_lane_row, k.dst_lane_row)):
                            sp.dma_start(lanes[:, u, n, :], table[:, bass.ds(c * P, BATCH * P)].to_broadcast([P, BATCH * P])
                                         ).then_inc(lanes_in[u], 16)
                sp.wait_ge(emptied, BATCH)
                sp.dma_start(edge_order(scores, BATCH, 62), kept[:, :, :]).then_inc(stored, 16)
                sp.wait_ge(stored, 16)

            @block.tensor
            def _(pe):
                pe.wait_ge(split_up, 1)
                with pe.Fori(0, BATCHES // 2) as i:
                    for u in range(2):
                        b = i * 2 + u
                        pe.wait_ge(lane_hot, b + 3)
                        pe.wait_ge(scored, b + 1)
                        for n in range(2):
                            for j in range(BATCH):
                                for m in range(3):
                                    ins = pe.matmul(by_lane[u][n][:, j * TILES:(j + 1) * TILES],
                                                    hot_lane[:, u, n, j * P:(j + 1) * P], parts[:, m, n, :],
                                                    start=m == 0, stop=m == 2)
                        ins.then_inc(by_lane_full, 1)
                pe.wait_ge(scored, 2 + BATCHES)
                for g in range(BATCH):
                    if g >= 2:
                        pe.wait_ge(emptied, g - 1)
                    pe.transpose(ps[g % 2][0:62, 0:P], sc[:, g * 62:(g + 1) * 62], k.ident[:, :]).then_inc(full, 1)

            @block.scalar
            def _(act):
                for g in range(BATCH):
                    act.wait_ge(full, g + 1)
                    act.activation(kept[:, g, :], ps[g % 2][0:62, 0:P], ACT.Copy).then_inc(emptied, 1)

            @block.vector
            def _(dve):
                step = Chain(dve, chained)
                links = 4
                dve.sem_inc(scored, 2)
                dve.sem_inc(lane_hot, 2)
                split(step, dve, nodes[:, :, :], rest[:, :, :], [parts[:, m, :, :] for m in range(3)])
                dve.sem_inc(split_up, 1)
                split_links = step.n

                def compare(i, u):
                    dve.wait_ge(lanes_in[u], i * 32 + 32)
                    dve.wait_ge(scored, i * 2 + (u + 1))
                    dve.tensor_scalar(hot_lane[:, u, :, :], lanes[:, u, :, :], k.lane_col[:, 0:1], None, ALU.is_equal
                                      ).then_inc(lane_hot, 1)

                def score(i, u):
                    b = i * 2 + u
                    c = i * (2 * BATCH) + u * BATCH
                    step.base, step.n = b * links + split_links, 0
                    hot_by(dve, k, hot_tile[:, u, 0, :, :], k.src_tile[:, bass.ds(c, BATCH)], TILES)
                    step(hot_by(dve, k, hot_tile[:, u, 1, :, :], k.dst_tile[:, bass.ds(c, BATCH)], TILES))
                    dve.wait_ge(by_lane_full, b + 1)
                    for n in range(2):
                        hot = hot_tile[:, u, n, :, :].rearrange("p j t -> p (j t)")
                        ins = dve.tensor_tensor(hot, hot, by_lane[u][n][:, 0:BATCH * TILES], ALU.mult)
                    step(ins)
                    step(dve.tensor_reduce(picked[:, u, :, :], hot_tile[:, u, :, :, :], AX.X, ALU.add))
                    step(dve.tensor_tensor(picked[:, u, 0, :], picked[:, u, 0, :], picked[:, u, 1, :], ALU.add))
                    dve.scalar_tensor_tensor(sc[:, bass.ds(c, BATCH)], picked[:, u, 0, :], 0.2, picked[:, u, 0, :],
                                             ALU.mult, ALU.max).then_inc(scored, 1)

                last = BATCHES // 2 - 1
                compare(0, 0)
                with dve.Fori(0, last) as i:
                    compare(i, 1)
                    score(i, 0)
                    compare(i + 1, 0)
                    score(i, 1)
                compare(last, 1)
                score(last, 0)
                score(last, 1)


SHARED0 = Experts(1, [D, 256, 128, D])
EXPERTS0 = Experts(4, [D, 128, 64, D])
EXPERTS3 = Experts(8, [D, 256, 256, D])


def layer0_ffn(k):
    a = k.a
    with k.phase() as ph:
        xT, gates, logits = ph.sb("xT", [P, KK, NPAD]), ph.sb("gates", [P, TILES, 4]), ph.sb("logits", [P, TILES, 4])
        with k.phase() as inner:
            xn = inner.sb("xn", [P, TILES, D])
            normalize(k, k.x, xn)
            routed(k, xn, xT, a["L0_ffn_gW"], 4, logits)
        gate_weights(k, logits, gates, 4, "top2_of_softmax", a["L0_ffn_gb"])
        bs, be = ph.sb("shared_bias", [P, 1, len(SHARED0.chunks)]), ph.sb("expert_bias", [P, 4, len(EXPERTS0.chunks)])
        load_small(k, [(bs[:, :, :], a["L0_ffn_sb"]), (be[:, :, :], a["L0_ffn_eb"])])
        mixture(k, xT, SHARED0, a["L0_ffn_sW"], a["L0_ffn_sb3"], ACT.Relu, bs)
        mixture(k, xT, EXPERTS0, a["L0_ffn_eW"], a["L0_ffn_eb3"], ACT.Relu, be, gates=gates)


def layer1_ffn(k):
    a, E = k.a, 8
    with k.phase() as ph:
        xn, gates, chosen, logits = (ph.sb("xn", [P, TILES, D]), ph.sb("gates", [P, TILES, E]),
                                     ph.sb("chosen", [P, TILES, E]), ph.sb("logits", [P, TILES, E]))
        normalize(k, k.x, xn)
        normalize(k, xn, xn, gamma=a["L1_ffn_gamma"], beta=a["L1_ffn_beta"])
        routed(k, xn, None, a["L1_ffn_Wr"], E, logits)
        gate_weights(k, logits, gates, E, "top2", a["L1_ffn_br"], chosen)
        sparse_mixture(k, xn, chosen, gates, E, 512, (a["L1_ffn_first"], a["L1_ffn_second"]), a["L1_ffn_b2"], False)


def layer2_ffn(k):
    a, E = k.a, 8
    with k.phase() as ph:
        xn, gates, chosen, logits = (ph.sb("xn", [P, TILES, D]), ph.sb("gates", [P, TILES, E]),
                                     ph.sb("chosen", [P, TILES, E]), ph.sb("logits", [P, TILES, E]))
        normalize(k, k.x, xn)
        routed(k, xn, None, a["L2_ffn_Wr"], E, logits)
        normalize(k, xn, xn)
        gate_weights(k, logits, gates, E, "top2_renormalized", a["L2_ffn_br"], chosen)
        sparse_mixture(k, xn, chosen, gates, E, 1024, (a["L2_ffn_first"], a["L2_ffn_second"]), a["L2_ffn_b2"], True)


def layer3_ffn(k):
    nc, a = k.nc, k.a
    E, C = 8, len(EXPERTS3.chunks)
    with k.phase() as ph:
        xT, gates, logits = ph.sb("xT", [P, KK, NPAD]), ph.sb("gates", [P, TILES, E]), ph.sb("logits", [P, TILES, E])
        with k.phase() as inner:
            xn = inner.sb("xn", [P, TILES, D])
            normalize(k, k.x, xn)
            routed(k, xn, xT, a["L3_ffn_Wr"], E, logits)
        gate_weights(k, logits, gates, E, "softmax", a["L3_ffn_br"])
        b, g, be, m, v = (ph.sb(n, [P, E, C]) for n in ("b", "g", "be", "m", "v"))
        load_small(k, [(t[:, :, :], a[f"L3_ffn_{n}"]) for t, n in ((b, "b"), (g, "g"), (be, "be"), (m, "m"), (v, "v"))])
        with k.phase() as inner:
            chained, rooted = inner.sem("chained"), inner.sem("rooted")
            with nc.Block() as block:

                @block.vector
                def _(dve):
                    step = Chain(dve, chained)
                    dve.tensor_scalar(v[:, :, :], v[:, :, :], 1e-3, None, ALU.add).then_inc(rooted, 1)
                    dve.wait_ge(rooted, 2)
                    step(dve.reciprocal(v[:, :, :], v[:, :, :]))
                    step(dve.tensor_tensor(g[:, :, :], g[:, :, :], v[:, :, :], ALU.mult))
                    step(dve.tensor_tensor(b[:, :, :], b[:, :, :], m[:, :, :], ALU.subtract))
                    step(dve.tensor_tensor(b[:, :, :], b[:, :, :], g[:, :, :], ALU.mult))
                    step(dve.tensor_tensor(b[:, :, :], b[:, :, :], be[:, :, :], ALU.add))

                @block.scalar
                def _(act):
                    act.wait_ge(rooted, 1)
                    act.activation(v[:, :, :], v[:, :, :], ACT.Sqrt).then_inc(rooted, 1)
        mixture(k, xT, EXPERTS3, a["L3_ffn_W"], a["L3_ffn_bo"], ACT.Relu, b, scale=g, gates=gates)


LAYERS = [layer0_gnn, layer0_ffn, layer1_gnn, layer1_ffn, layer2_gnn, layer2_ffn, layer3_gnn, layer3_ffn]


def program(nc, a, out, upto=99):
    k = Kernel(nc, a)
    setup(k)
    for layer in LAYERS[:upto]:
        layer(k)
    with k.phase() as ph:
        stored = ph.sem("stored")
        with nc.Block() as block:

            @block.sync
            def _(sp):
                full = NODES // P
                sp.dma_start(out[0:full * P, :].rearrange("(t p) d -> p t d", p=P), k.x[:, 0:full, :]
                             ).then_inc(stored, 16)
                sp.dma_start(out[full * P:NODES, :], k.x[0:NODES - full * P, full, :]).then_inc(stored, 16)
                sp.wait_ge(stored, 32)




def lay_out(i):
    o = {}

    def padded(a, rows, fill=0):
        a = np.asarray(a)
        return np.concatenate([a, np.full((rows - a.shape[0],) + a.shape[1:], fill, a.dtype)])

    def lanes(a, fill=0):
        return np.ascontiguousarray(padded(a, EPAD, fill).reshape(CHUNKS, P).T)

    def halves(w):
        w = np.asarray(w)
        s = w.shape
        w = w.reshape(s[:-2] + (s[-2] // P, P, s[-1]))
        return np.ascontiguousarray(np.swapaxes(w, -3, -2))

    def row(b):
        return np.ascontiguousarray(np.asarray(b).reshape(1, -1))

    o["x_lanes"] = np.ascontiguousarray(padded(i["x"], NPAD).reshape(TILES, P, D).transpose(1, 0, 2))
    o["src_row"] = row(padded(i["src"], EPAD))
    o["src_lanes"] = lanes(i["src"])
    o["dst_lanes"] = lanes(i["dst"], NO_NODE)
    o["weight_lanes"] = lanes(i["edge_weight"])
    o["L0_gnn_w"] = halves(i["L0_gnn_w"])
    o["L0_gnn_b"] = row(i["L0_gnn_b"])

    def packed(*matrices):
        cols = []
        for w in matrices:
            w = np.asarray(w)
            w = w.reshape((-1,) + w.shape[-2:])
            rows = -(-w.shape[1] // P) * P
            w = np.concatenate([w, np.zeros((w.shape[0], rows - w.shape[1], w.shape[2]), w.dtype)], axis=1)
            cols.append(halves(w).reshape(w.shape[0], P, -1))
        return np.ascontiguousarray(np.concatenate(cols, axis=2))

    def columns(*vectors):
        cols = []
        for v in vectors:
            v = np.asarray(v)
            v = v.reshape(-1, v.shape[-1])
            n = -(-v.shape[1] // P) * P
            v = np.concatenate([v, np.zeros((v.shape[0], n - v.shape[1]), v.dtype)], axis=1)
            cols.append(v.reshape(v.shape[0], -1, P).transpose(2, 0, 1))
        return np.ascontiguousarray(np.concatenate(cols, axis=2))

    def typed(name):
        return halves(i[name]).transpose(1, 0, 2, 3)

    def by_head(relation, order):
        r = np.asarray(relation).transpose(order)
        return np.ascontiguousarray(r.reshape(KK, P, r.shape[2], r.shape[3]).transpose(1, 0, 2, 3))

    o["etype_lanes"] = lanes(i["edge_type_8"])
    o["type_lanes"] = np.ascontiguousarray(padded(i["node_type_4"], NPAD).reshape(TILES, P).T)
    o["L1_gnn_w"] = np.ascontiguousarray(np.stack([typed(f"L1_gnn_{n}_linears") for n in "kvq"], axis=1))
    o["L1_gnn_wa"] = np.ascontiguousarray(typed("L1_gnn_a_linears"))
    o["L1_gnn_att"] = by_head(i["L1_gnn_relation_att"], (1, 3, 0, 2))
    o["L1_gnn_msg"] = by_head(i["L1_gnn_relation_msg"], (1, 2, 0, 3))
    pri = np.repeat(np.asarray(i["L1_gnn_relation_pri"]).T, P // 2, axis=0)
    o["L1_gnn_pri"] = np.ascontiguousarray(pri.reshape(KK, P, -1).transpose(1, 0, 2))
    o["L1_gnn_skip"] = row(i["L1_gnn_skip"])
    o["dst_rows"] = np.ascontiguousarray(padded(i["dst"], EPAD, NO_NODE).reshape(P, CHUNKS))
    attr = padded(i["edge_attr_64"], EPAD).T
    o["attr"] = np.ascontiguousarray(np.concatenate([attr[:, :EPAD // 2], attr[:, EPAD // 2:]]))
    o["L2_gnn_kvq"] = np.ascontiguousarray(np.concatenate([halves(i[f"L2_gnn_W{n}"]) for n in "kvq"], axis=2))
    o["L2_gnn_W1"] = np.concatenate([np.asarray(i["L2_gnn_W1"])] * 2)
    o["L2_gnn_W2"] = halves(i["L2_gnn_W2"])
    o["L2_gnn_b1"] = np.ascontiguousarray(np.asarray(i["L2_gnn_b1"]).reshape(KK, P).T)
    o["L2_gnn_b2"] = np.asarray(i["L2_gnn_b2"]).reshape(-1, 1)
    o["L2_gnn_Wo"], o["L2_gnn_bo"] = halves(i["L2_gnn_Wo"]), row(i["L2_gnn_bo"])
    o["L3_gnn_W"], o["L3_gnn_WT"] = halves(i["L3_gnn_W"]), halves(np.asarray(i["L3_gnn_W"]).T)
    o["L3_gnn_att"] = halves(np.stack([np.asarray(i["L3_gnn_a_src"]), np.asarray(i["L3_gnn_a_dst"])], axis=1))
    o["L3_gnn_bias"] = row(i["L3_gnn_bias"])
    o["L0_ffn_gW"], o["L0_ffn_gb"] = halves(i["L0_ffn_gW"]), row(i["L0_ffn_gb"])
    o["L0_ffn_sW"] = packed(i["L0_ffn_sW1"], i["L0_ffn_sW2"], i["L0_ffn_sW3"])
    o["L0_ffn_eW"] = packed(i["L0_ffn_eW1"], i["L0_ffn_eW2"], i["L0_ffn_eW3"])
    o["L0_ffn_sb"], o["L0_ffn_sb3"] = columns(i["L0_ffn_sb1"], i["L0_ffn_sb2"]), row(i["L0_ffn_sb3"])
    o["L0_ffn_eb"], o["L0_ffn_eb3"] = columns(i["L0_ffn_eb1"], i["L0_ffn_eb2"]), row(i["L0_ffn_eb3"])
    o["L1_ffn_gamma"], o["L1_ffn_beta"] = row(i["L1_ffn_gamma"]), row(i["L1_ffn_beta"])
    o["L1_ffn_Wr"], o["L1_ffn_br"] = halves(i["L1_ffn_Wr"]), row(i["L1_ffn_br"])
    def first_parts(w, b, *affine):
        parts = [packed(w), columns(b).transpose(1, 0, 2)]
        if affine:
            g, c = (columns(v).transpose(1, 0, 2) for v in affine)
            parts.append(np.stack([g, c], axis=3).reshape(g.shape[0], P, 2 * KK))
        return np.ascontiguousarray(np.concatenate(parts, axis=2))

    o["L1_ffn_first"] = first_parts(i["L1_ffn_W1"], i["L1_ffn_b1"])
    o["L1_ffn_second"], o["L1_ffn_b2"] = packed(i["L1_ffn_W2"]), row(i["L1_ffn_b2"])
    o["L2_ffn_Wr"], o["L2_ffn_br"] = halves(i["L2_ffn_Wr"]), row(i["L2_ffn_br"])
    o["L2_ffn_first"] = first_parts(i["L2_ffn_W1"], i["L2_ffn_b1"], i["L2_ffn_ln_g"], i["L2_ffn_ln_b"])
    o["L2_ffn_second"], o["L2_ffn_b2"] = packed(i["L2_ffn_W2"]), row(i["L2_ffn_b2"])
    o["L3_ffn_Wr"], o["L3_ffn_br"] = halves(i["L3_ffn_Wr"]), row(i["L3_ffn_br"])
    o["L3_ffn_W"] = packed(i["L3_ffn_W1"], i["L3_ffn_W2"], i["L3_ffn_Wo"])
    o["L3_ffn_bo"] = row(i["L3_ffn_bo"])
    for n in ("b", "g", "be", "m", "v"):
        o[f"L3_ffn_{n}"] = columns(i[f"L3_ffn_{n}1"], i[f"L3_ffn_{n}2"])
    return o


def kernel(**inputs):
    import concourse.bacc as bacc
    from concourse.bass_utils import run_bass_kernel_spmd as run

    nc = bacc.Bacc("TRN2", target_bir_lowering=False, num_devices=1)
    arrays = lay_out(inputs)
    a = {n: nc.dram_tensor(f"in_{n}", v.shape, mybir.dt.from_np(v.dtype), kind="ExternalInput").ap()
         for n, v in arrays.items()}
    out = nc.dram_tensor("out_x", (NODES, D), F32, kind="ExternalOutput").ap()
    program(nc, a, out)
    r = run(nc, [{f"in_{n}": v for n, v in arrays.items()}], core_ids=[0])
    return r.results[0]["out_x"]
```

```python
from contextlib import ExitStack

import numpy as np

import concourse.bass as bass
from concourse import mybir

F32 = mybir.dt.float32
BF16 = mybir.dt.bfloat16
I32 = mybir.dt.int32
ACT = mybir.ActivationFunctionType
ALU = mybir.AluOpType
AX = mybir.AxisListType

P = 128
NODES, EDGES, D = 3125, 103125, 256
KK = D // P
TILES = -(-NODES // P)
NPAD = TILES * P
NWIN = NPAD + P
CHUNKS = -(-EDGES // P)
EPAD = CHUNKS * P
BATCH = 13
BATCHES = CHUNKS // BATCH
PAIRS = [(j, min(2, BATCH - j)) for j in range(0, BATCH, 2)]
UNROLL = 5
GROUP = UNROLL * P
HALF = GROUP // 2
BLOCK = 2 * P
BIG = 1.0e38
NO_NODE = 8191


class Kernel:

    def __init__(self, nc, a):
        self.nc, self.a = nc, a
        self.uid = 0
        self.gcn_rows, self.l2_queries = (nc.dram_tensor(n, [NWIN, D], F32, kind="Internal").ap()
                                          for n in ("gcn_rows", "l2_queries"))
        self.routed_layers = 0
        self.slot_rows = [nc.dram_tensor(f"slot_rows{n}", [(2 * NPAD + 8 * (BLOCK - 1)) // BLOCK * BLOCK, D], F32,
                                         kind="Internal").ap() for n in range(2)]
        self.gcn_sums = [nc.dram_tensor(f"gcn_sums{m}", [NWIN, D], F32, kind="Internal").ap() for m in range(SUM_COPIES)]
        self.edge_bias = nc.dram_tensor("edge_bias", [8, EPAD], F32, kind="Internal").ap()

    def phase(self):
        return Phase(self)


class Phase:

    def __init__(self, k):
        self.k, self.nc, self.stack, self.sems = k, k.nc, ExitStack(), []

    def __enter__(self):
        return self

    def __exit__(self, *exc):
        self.stack.close()
        if exc[0] is None:
            self.nc.clear_and_free_semaphores(self.sems)
            self.nc.all_engine_barrier()

    def _name(self, name):
        self.k.uid += 1
        return f"{name}_{self.k.uid}"

    def sb(self, name, shape, dt=F32):
        return self.stack.enter_context(self.nc.sbuf_tensor(self._name(name), shape, dt))

    def ps(self, name, shape, dt=F32):
        return self.stack.enter_context(self.nc.psum_tensor(self._name(name), shape, dt))

    def sem(self, name):
        s = self.nc.alloc_semaphore(self._name(name))
        self.sems.append(s)
        return s


class Chain:

    def __init__(self, eng, sem):
        self.eng, self.sem, self.n, self.base = eng, sem, 0, 0

    def __call__(self, ins):
        self.n += 1
        ins.then_inc(self.sem, 1)
        self.eng.wait_ge(self.sem, self.base + self.n)


def hot_by(eng, k, out, values, width):
    shape = [P, BATCH, width]
    return eng.tensor_tensor(out, k.lane_iota[:, 0:width].unsqueeze(1).to_broadcast(shape),
                             values.unsqueeze(2).to_broadcast(shape), ALU.is_equal)


def row_tables(k, tables):
    blocks = [(c, min(P, CHUNKS - c)) for c in range(0, CHUNKS, P)]
    jobs = [(lanes, row, c, n) for lanes, row in tables for c, n in blocks]
    BANKS = 8
    with k.phase() as ph:
        turned = [ph.ps(f"turned{q}", [P, P]) for q in range(BANKS)]
        kept = ph.sb("kept", [P, len(jobs), P], BF16)
        full, copied, stored = ph.sem("full"), ph.sem("copied"), ph.sem("stored")
        with k.nc.Block() as block:

            @block.tensor
            def _(pe):
                for q, (lanes, _, c, n) in enumerate(jobs):
                    if q >= BANKS:
                        pe.wait_ge(copied, q - BANKS + 1)
                    pe.transpose(turned[q % BANKS][0:n, :], lanes[:, c:c + n], k.ident[:, :]).then_inc(full, 1)

            @block.scalar
            def _(act):
                for q, (_, _, c, n) in enumerate(jobs):
                    act.wait_ge(full, q + 1)
                    act.activation(kept[0:n, q, :], turned[q % BANKS][0:n, :], ACT.Copy).then_inc(copied, 1)

            @block.sync
            def _(sp):
                for q, (_, row, c, n) in enumerate(jobs):
                    sp.wait_ge(copied, q + 1)
                    sp.dma_start(row[:, c * P:(c + n) * P].rearrange("o (c e) -> (o c) e", e=P), kept[0:n, q, :]
                                 ).then_inc(stored, 16)
                sp.wait_ge(stored, 16 * len(jobs))


def setup(k):
    nc = k.nc
    k.x = nc.alloc_sbuf_tensor("x_res", [P, TILES, D], F32)
    k.ident = nc.alloc_sbuf_tensor("ident", [P, P], F32)
    k.lane_iota = nc.alloc_sbuf_tensor("lane_iota", [P, P], F32)
    k.lane_col = nc.alloc_sbuf_tensor("lane_col", [P, 1], F32)
    k.rel_row, k.src_lane_row, k.dst_lane_row = (nc.dram_tensor(n, [1, EPAD], BF16, kind="Internal").ap()
                                                 for n in ("rel_row", "src_lane_row", "dst_lane_row"))
    k.src_tile = nc.alloc_sbuf_tensor("src_tile", [P, CHUNKS], F32)
    k.dst_tile = nc.alloc_sbuf_tensor("dst_tile", [P, CHUNKS], F32)
    k.src = nc.alloc_sbuf_tensor("src_idx", [P, CHUNKS], I32)
    k.dst = nc.alloc_sbuf_tensor("dst_idx", [P, CHUNKS], I32)
    k.rel = nc.alloc_sbuf_tensor("rel_pos", [P, CHUNKS], F32)
    k.dinv = nc.alloc_sbuf_tensor("dinv", [P, TILES], F32)
    k.weight = nc.alloc_sbuf_tensor("edge_w", [P, CHUNKS], F32)
    with k.phase() as outer:
        src_lane, dst_lane = outer.sb("src_lane", [P, CHUNKS]), outer.sb("dst_lane", [P, CHUNKS])
        edge_tables(k, src_lane, dst_lane)
        row_tables(k, ((k.rel, k.rel_row), (src_lane, k.src_lane_row), (dst_lane, k.dst_lane_row)))


def split(step, dve, value, rest, parts):
    step(dve.tensor_copy(parts[0], value))
    step(dve.tensor_tensor(rest, value, parts[0], ALU.subtract))
    step(dve.tensor_copy(parts[1], rest))
    step(dve.tensor_tensor(rest, rest, parts[1], ALU.subtract))
    step(dve.tensor_copy(parts[2], rest))


JOBS = 4
JOB = BATCH * P // JOBS


def clear_rows(eng, tables, zeros, cleared):
    per_dma, n = zeros.shape[1] // D, 0
    for table in tables:
        for at in range(0, table.shape[0], P * per_dma):
            rows = min(per_dma, (table.shape[0] - at) // P)
            eng.dma_start(table[at:at + P * rows, :].rearrange("(p r) d -> p (r d)", p=P), zeros[:, 0:rows * D]
                          ).then_inc(cleared, 16)
            n += 1
            eng.wait_ge(cleared, 16 * n)


class EdgeMLP:

    def __init__(self, k, ph):
        self.k = k
        H, F = 8, 64
        self.w1, self.w2 = ph.sb("edge_w1", [F, D]), ph.sb("edge_w2", [P, KK, H])
        self.b1, self.b2 = ph.sb("edge_b1", [P, KK]), ph.sb("edge_b2", [H, 1])
        self.attr = ph.sb("edge_attr", [F, 2, JOBS * JOB])
        self.hid = ph.sb("edge_hid", [P, 2, KK, JOB])
        self.res = ph.sb("edge_res", [H, 2, JOBS * JOB])
        self.h_ps = [ph.ps(f"edge_h{q}", [P, 512]) for q in range(4)]
        self.r_ps = ph.ps("edge_r", [P, 512])
        self.w_in, self.h_full, self.h_out, self.r_full, self.r_out = (
            ph.sem("edge_" + n) for n in ("w_in", "h_full", "h_out", "r_full", "r_out"))
        self.attr_in = [ph.sem(f"edge_attr_in{u}") for u in range(2)]
        self.stored = [ph.sem(f"edge_stored{u}") for u in range(2)]

    def load_weights(self, sp):
        a = self.k.a
        for dst, src in ((self.w1[:, :], a["L2_gnn_W1"]), (self.w2[:, :, :], a["L2_gnn_W2"]),
                         (self.b1[:, :], a["L2_gnn_b1"]), (self.b2[:, :], a["L2_gnn_b2"])):
            sp.dma_start(dst, src).then_inc(self.w_in, 16)

    def load(self, sp, i, u):
        edges = bass.ds((i * 2 + u) * (JOBS * JOB), JOBS * JOB)
        sp.dma_start(self.attr[:, u, :], self.k.a["attr"][:, edges]).then_inc(self.attr_in[u], 16)

    def store(self, sp, i, u):
        edges = bass.ds((i * 2 + u) * (JOBS * JOB), JOBS * JOB)
        sp.wait_ge(self.r_out, i * (2 * JOBS) + ((u + 1) * JOBS + 1))
        sp.dma_start(self.k.edge_bias[:, edges], self.res[:, u, :]).then_inc(self.stored[u], 16)

    def hidden(self, pe, i, j):
        if j % JOBS == 0:
            pe.wait_ge(self.attr_in[j // JOBS], i * 16 + 16)
        for kk in range(KK):
            pe.wait_ge(self.h_out, i * (4 * JOBS) + (2 * j + kk + 1))
            pe.matmul(self.h_ps[(2 * j + kk) % 4][:, 0:JOB], self.w1[:, kk * P:(kk + 1) * P],
                      self.attr[:, j // JOBS, j % JOBS * JOB:(j % JOBS + 1) * JOB], start=True, stop=True
                      ).then_inc(self.h_full, 1)

    def result(self, pe, i, j):
        pe.wait_ge(self.h_out, i * (4 * JOBS) + (2 * j + 6))
        pe.wait_ge(self.r_out, i * (2 * JOBS) + (j + 1))
        for kk in range(KK):
            ins = pe.matmul(self.r_ps[0:8, 0:JOB], self.w2[:, kk, :], self.hid[:, j % 2, kk, :],
                            start=kk == 0, stop=kk == KK - 1)
        ins.then_inc(self.r_full, 1)

    def activate(self, act, i, j):
        act.wait_ge(self.r_full, i * (2 * JOBS) + (j + 1))
        for kk in range(KK):
            act.wait_ge(self.h_full, i * (4 * JOBS) + (2 * j + kk + 1))
            act.activation(self.hid[:, j % 2, kk, :], self.h_ps[(2 * j + kk) % 4][:, 0:JOB], ACT.Relu,
                           bias=self.b1[:, kk:kk + 1]).then_inc(self.h_out, 1)

    def keep(self, act, i, j):
        if j % JOBS == 0:
            act.wait_ge(self.stored[j // JOBS], i * 16)
        act.wait_ge(self.r_full, i * (2 * JOBS) + (j + 3))
        act.activation(self.res[:, j // JOBS, j % JOBS * JOB:(j % JOBS + 1) * JOB], self.r_ps[0:8, 0:JOB],
                       ACT.Identity, bias=self.b2[:, 0:1]).then_inc(self.r_out, 1)


def edge_tables(k, src_lane, dst_lane):
    nc, a = k.nc, k.a
    with k.phase() as ph:
        loaded, made, chained = ph.sem("loaded"), ph.sem("made"), ph.sem("chained")
        based, hot, summed = ph.sem("based"), ph.sem("hot"), ph.sem("summed")
        hot_free, tiled = ph.sem("hot_free"), ph.sem("tiled")
        dstf, basef = ph.sb("dstf", [P, CHUNKS]), ph.sb("basef", [1, CHUNKS])
        low_of = ph.sb("low_of", [P, CHUNKS])
        weight_parts = ph.sb("weight_parts", [P, 3, CHUNKS], BF16)
        ints = ph.sb("ints", [P, CHUNKS], I32)
        ones = ph.sb("ones", [1, P])
        hot_lane = ph.sb("hot_lane", [P, 2, BATCH, P], BF16)
        hot_tile = ph.sb("hot_tile", [P, BATCH, TILES], BF16)
        tile_w = ph.sb("tile_w", [P, 2, 3, BATCH, TILES], BF16)
        degree = ph.ps("degree", [P, 512])
        bases = ph.ps("bases", [P, 2, 512])
        deg = ph.sb("deg", [P, TILES])
        has = ph.sb("has", [P, TILES])
        HC = CHUNKS // 2
        mlp = EdgeMLP(k, ph)
        zeros, zeroed, cleared = ph.sb("zeros", [P, 8 * D]), ph.sem("zeroed"), ph.sem("cleared")
        with nc.Block() as block:

            @block.sync
            def _(sp):
                mlp.load_weights(sp)
                mlp.load(sp, 0, 0)
                sp.dma_start(k.dst[:, :], a["dst_lanes"]).then_inc(loaded, 16)
                sp.dma_start(k.weight[:, :], a["weight_lanes"]).then_inc(loaded, 16)
                sp.dma_start(k.src[:, :], a["src_lanes"]).then_inc(loaded, 16)
                sp.dma_start(k.x[:, :, :], a["x_lanes"]).then_inc(loaded, 16)
                mlp.load(sp, 0, 1)
                with sp.Fori(0, BATCHES // 2 - 1) as i:
                    for u in range(2):
                        mlp.store(sp, i, u)
                        mlp.load(sp, i + 1, u)
                for u in range(2):
                    mlp.store(sp, BATCHES // 2 - 1, u)
                    sp.wait_ge(mlp.stored[u], 16 * (BATCHES // 2))

            @block.gpsimd
            def _(pool):
                pool.memset(ones[:, :], 1.0).then_inc(made, 1)
                pool.memset(k.ident[:, :], 0.0).then_inc(made, 1)
                pool.iota(k.lane_iota[:, :], [[1, P]], base=0, channel_multiplier=0,
                          allow_small_or_imprecise_dtypes=True).then_inc(made, 1)
                pool.iota(k.lane_col[:, :], [[0, 1]], base=0, channel_multiplier=1,
                          allow_small_or_imprecise_dtypes=True).then_inc(made, 1)
                pool.wait_ge(made, 4)
                pool.affine_select(out=k.ident[:, :], in_=k.ident[:, :], compare_op=ALU.not_equal, fill=1.0,
                                   base=0, pattern=[[-1, P]], channel_multiplier=1).then_inc(made, 1)
                pool.memset(zeros[:, :], 0.0).then_inc(zeroed, 1)
                pool.wait_ge(zeroed, 1)
                tails = [table[NPAD:NWIN, :] for table in (k.gcn_rows, k.l2_queries)]
                clear_rows(pool, k.gcn_sums + tails, zeros, cleared)

            @block.vector
            def _(dve):
                step = Chain(dve, chained)
                dve.wait_ge(loaded, 64)
                dve.wait_ge(made, 4)
                step(dve.tensor_copy(dstf[:, :], k.dst[:, :]))
                dve.tensor_copy(basef[0:1, :], dstf[0:1, :]).then_inc(based, 1)
                for nodes, tile_of, lane_of in ((k.src, k.src_tile, src_lane), (k.dst, k.dst_tile, dst_lane)):
                    step(dve.tensor_scalar(ints[:, :], nodes[:, :], 7, None, ALU.logical_shift_right))
                    step(dve.tensor_copy(tile_of[:, :], ints[:, :]))
                    step(dve.tensor_copy(low_of[:, :], nodes[:, :]))
                    step(dve.scalar_tensor_tensor(lane_of[:, :], tile_of[:, :], -float(P), low_of[:, :], ALU.mult, ALU.add))
                split(step, dve, k.weight[:, :], low_of[:, :], [weight_parts[:, n, :] for n in range(3)])
                with dve.Fori(0, BATCHES // 2) as i:
                    for u in range(2):
                        b = i * 2 + u
                        c = i * (2 * BATCH) + u * BATCH
                        dve.wait_ge(hot_free, b + 1)
                        hot_by(dve, k, hot_lane[:, u, :, :], src_lane[:, bass.ds(c, BATCH)], P)
                        hot_by(dve, k, hot_tile[:, :, :], k.src_tile[:, bass.ds(c, BATCH)], TILES).then_inc(tiled, 1)
                        dve.wait_ge(tiled, b + 1)
                        for n in range(3):
                            w = weight_parts[:, n, bass.ds(c, BATCH)].unsqueeze(2).to_broadcast([P, BATCH, TILES])
                            ins = dve.tensor_tensor(tile_w[:, u, n, :, :], hot_tile[:, :, :], w, ALU.mult)
                        ins.then_inc(hot, 1)
                        dve.wait_ge(hot, b + 1)
                dve.wait_ge(summed, 1)
                for h in range(2):
                    step(dve.tensor_tensor(k.rel[:, h * HC:(h + 1) * HC], dstf[:, h * HC:(h + 1) * HC],
                                           bases[:, h, 0:HC], ALU.subtract))
                dve.wait_ge(summed, 2)
                step(dve.tensor_copy(deg[:, :], degree[:, 0:TILES]))
                step(dve.tensor_scalar(has[:, :], deg[:, :], 0.0, None, ALU.is_gt))
                step(dve.tensor_scalar(low_of[:, 0:TILES], has[:, :], -1.0, 1.0, ALU.mult, ALU.add))
                step(dve.tensor_tensor(deg[:, :], deg[:, :], low_of[:, 0:TILES], ALU.add))
                step(dve.reciprocal(deg[:, :], deg[:, :]))
                dve.wait_ge(made, 5)
                dve.tensor_copy(deg[:, :], deg[:, :]).then_inc(made, 1)
                dve.wait_ge(made, 7)
                step(dve.tensor_tensor(k.dinv[:, :], k.dinv[:, :], has[:, :], ALU.mult))

            @block.scalar
            def _(act):
                act.sem_inc(mlp.h_out, 4)
                act.sem_inc(mlp.r_out, 1)
                act.wait_ge(mlp.w_in, 64)

                def turn(i, more):
                    for j in range(2 * JOBS):
                        if j + 1 < 2 * JOBS:
                            mlp.activate(act, i, j + 1)
                        elif more:
                            mlp.activate(act, i + 1, 0)
                        mlp.keep(act, i, j)

                mlp.activate(act, 0, 0)
                with act.Fori(0, BATCHES // 2 - 1) as i:
                    turn(i, True)
                turn(BATCHES // 2 - 1, False)
                act.wait_ge(made, 6)
                act.activation(k.dinv[:, :], deg[:, :], ACT.Sqrt).then_inc(made, 1)

            @block.tensor
            def _(pe):
                pe.sem_inc(hot_free, 2)

                def add(u, first, last):
                    for j in range(BATCH):
                        for n in range(3):
                            ins = pe.matmul(degree[:, 0:TILES], hot_lane[:, u, j, :], tile_w[:, u, n, j, :],
                                            start=first and j == n == 0, stop=last and j == BATCH - 1 and n == 2)
                    return ins

                def turn(i, first=False, last=False):
                    for j in range(2 * JOBS):
                        if j + 1 < 2 * JOBS:
                            mlp.hidden(pe, i, j + 1)
                        elif not last:
                            mlp.hidden(pe, i + 1, 0)
                        mlp.result(pe, i, j)
                        if j % JOBS == 1:
                            u = j // JOBS
                            pe.wait_ge(hot, i * 2 + (u + 1))
                            ins = add(u, first and u == 0, last and u == 1)
                            ins.then_inc(summed if last and u == 1 else hot_free, 1)

                pe.sem_inc(mlp.r_full, 2)
                pe.wait_ge(mlp.w_in, 64)
                mlp.hidden(pe, 0, 0)
                turn(0, first=True)
                pe.wait_ge(based, 1)
                for h in range(2):
                    ins = pe.matmul(bases[:, h, 0:HC], ones[0:1, :], basef[0:1, h * HC:(h + 1) * HC],
                                    start=True, stop=True)
                ins.then_inc(summed, 1)
                with pe.Fori(1, BATCHES // 2 - 1) as i:
                    turn(i)
                turn(BATCHES // 2 - 1, last=True)


def normalize(k, src, out, eps=1e-5, gamma=None, beta=None):
    nc = k.nc
    with k.phase() as ph:
        stats = ph.sb("stats", [P, TILES, 6])
        mv = ph.sb("mv", [P, TILES, 2])
        std = ph.sb("std", [P, TILES])
        shift = ph.sb("shift", [P, TILES])
        split_at = TILES * 3 // 5
        counted, aggregated, rooted, done = (ph.sem(n) for n in ("counted", "aggregated", "rooted", "done"))
        loaded = ph.sem("affine_loaded")
        if gamma is not None:
            gb = ph.sb("gamma_beta", [P, 2, D])
        with nc.Block() as block:
            if gamma is not None:
                @block.sync
                def _(sp):
                    sp.dma_start(gb[:, 0, :], gamma.to_broadcast([P, D])).then_inc(loaded, 16)
                    sp.dma_start(gb[:, 1, :], beta.to_broadcast([P, D])).then_inc(loaded, 16)

            @block.vector
            def _(dve):
                for t in range(TILES):
                    dve.bn_stats(stats[:, t, :], src[:, t, :]).then_inc(counted, 1)
                for t in range(TILES):
                    dve.wait_ge(counted, t + 1)
                    ins = dve.bn_aggr(mv[:, t, :], stats[:, t, :])
                ins.then_inc(aggregated, 1)
                dve.wait_ge(aggregated, 1)
                dve.tensor_scalar(std[:, :], mv[:, :, 1], eps, None, ALU.add).then_inc(rooted, 1)
                dve.wait_ge(rooted, 2)
                dve.reciprocal(std[:, :], std[:, :]).then_inc(rooted, 1)
                dve.wait_ge(rooted, 3)
                dve.scalar_tensor_tensor(shift[:, :], mv[:, :, 0], -1.0, std[:, :], ALU.mult, ALU.mult).then_inc(rooted, 1)
                for t in range(split_at):
                    dve.tensor_scalar(out[:, t, :], src[:, t, :], mv[:, t, 0:1], std[:, t:t + 1],
                                      ALU.subtract, ALU.mult).then_inc(done, 1)
                if gamma is not None:
                    dve.wait_ge(loaded, 32)
                    dve.wait_ge(done, TILES)
                    g = gb[:, 0, :].unsqueeze(1).to_broadcast([P, TILES, D])
                    b = gb[:, 1, :].unsqueeze(1).to_broadcast([P, TILES, D])
                    dve.tensor_tensor(out[:, :, :], out[:, :, :], g, ALU.mult).then_inc(done, 1)
                    dve.wait_ge(done, TILES + 1)
                    dve.tensor_tensor(out[:, :, :], out[:, :, :], b, ALU.add).then_inc(done, 1)

            @block.scalar
            def _(act):
                act.wait_ge(rooted, 1)
                act.activation(std[:, :], std[:, :], ACT.Sqrt).then_inc(rooted, 1)
                act.wait_ge(rooted, 4)
                for t in range(split_at, TILES):
                    act.activation(out[:, t, :], src[:, t, :], ACT.Identity, bias=shift[:, t:t + 1],
                                   scale=std[:, t:t + 1]).then_inc(done, 1)


def node_tiles(k, ph, src, width, load, rhs, evacuate, store=None, stores=0, xT=None, links=0):
    nc = k.nc
    ring = ph.sb("tile_ring", [P, UNROLL, D])
    ringT = ph.sb("tileT_ring", [P, UNROLL, KK, P])
    stage = ph.sb("stage", [P, UNROLL, width // D * D]) if store else None
    banks = -(-width // 512)
    turned = [ph.ps(f"turned{i}", [P, 512]) for i in range(8 - 3 * banks)]
    products = [ph.ps(f"product{i}", [P, banks, 512]) for i in range(3)]
    weights_in, ring_full, turned_full = ph.sem("weights_in"), ph.sem("ring_full"), ph.sem("turned_full")
    ringT_full, multiplied, kept = ph.sem("ringT_full"), ph.sem("multiplied"), ph.sem("kept")
    product_out, chained = ph.sem("product_out"), ph.sem("chained")
    stored = [ph.sem(f"stored{u}") for u in range(UNROLL)]
    bodies = TILES // UNROLL
    weights_count = []
    with nc.Block() as block:

        @block.sync
        def _(sp):
            weights_count.append(load(sp, weights_in))
            if store:
                with sp.Fori(0, bodies) as i:
                    for u in range(UNROLL):
                        t = i * UNROLL + u
                        sp.wait_ge(product_out, t + 2)
                        store(sp, t, stage[:, u, :], stored[u])
                for u in range(UNROLL):
                    sp.wait_ge(stored[u], 16 * stores * bodies)

        @block.scalar
        def _(act):
            with act.Fori(0, bodies) as i:
                for u in range(UNROLL):
                    act.activation(ring[:, u, :], src[:, bass.ds(i * UNROLL + u, 1), :], ACT.Copy
                                   ).then_inc(ring_full, 1)
                for u in range(UNROLL):
                    t = i * UNROLL + u
                    act.wait_ge(turned_full, t + 1)
                    act.wait_ge(multiplied, i * UNROLL)
                    if xT is not None:
                        act.wait_ge(kept, i * UNROLL)
                    act.activation(ringT[:, u, :, :], turned[u % len(turned)][:, 0:D], ACT.Copy
                                   ).then_inc(ringT_full, 1)

        if xT is not None:
            @block.gpsimd
            def _(pool):
                with pool.Fori(0, bodies) as i:
                    for u in range(UNROLL):
                        t = i * UNROLL + u
                        pool.wait_ge(ringT_full, t + 1)
                        pool.tensor_copy(xT[:, :, bass.ds(t * P, P)], ringT[:, u, :, :]).then_inc(kept, 1)

        @block.tensor
        def _(pe):
            pe.wait_ge(weights_in, weights_count[0])
            with pe.Fori(0, bodies) as i:
                for u in range(UNROLL):
                    t = i * UNROLL + u
                    pe.wait_ge(ring_full, t + 1)
                    pe.wait_ge(ringT_full, i * UNROLL + max(0, u - len(turned) + 1))
                    for kk in range(KK):
                        ins = pe.transpose(turned[u % len(turned)][:, kk * P:(kk + 1) * P],
                                           ring[:, u, kk * P:(kk + 1) * P], k.ident[:, :])
                    ins.then_inc(turned_full, 1)
                for u in range(UNROLL):
                    t = i * UNROLL + u
                    pe.wait_ge(ringT_full, t + 1)
                    pe.wait_ge(product_out, t)
                    for b in range(banks):
                        n = min(512, width - b * 512)
                        for kk in range(KK):
                            ins = pe.matmul(products[u % 3][:, b, 0:n], ringT[:, u, kk, :],
                                            rhs[:, kk, b * 512:b * 512 + n], start=kk == 0, stop=kk == KK - 1)
                    ins.then_inc(multiplied, 1)

        @block.vector
        def _(dve):
            dve.sem_inc(product_out, 1)
            step = Chain(dve, chained)
            with dve.Fori(0, bodies) as i:
                for u in range(UNROLL):
                    t = i * UNROLL + u
                    dve.wait_ge(multiplied, t + 1)
                    if store:
                        dve.wait_ge(stored[u], i * (16 * stores))
                    step.base, step.n = t * links, 0
                    last = evacuate(dve, t, products[u % 3], stage[:, u, :] if store else None, step)
                    assert step.n == links
                    last.then_inc(product_out, 1)


def aggregate(k, table, index, accT, weights=None, alpha=None, heads=1):
    nc = k.nc
    with k.phase() as ph:
        staged = ph.sb("index_staged", [P, 2, BATCH], I32)
        odd = ph.sb("odd_sums", [P, KK, NWIN])
        rows = ph.sb("rows", [P, 2, BATCH, D])
        hot = ph.sb("hot", [P, 2, BATCH, P])
        messages = ph.sb("messages", [P, 2, BATCH, D]) if alpha else rows
        sums = [ph.ps(f"sums{j}", [P, 2, KK, P]) for j in range(len(PAIRS))]
        index_staged, cleared, hot_full = ph.sem("index_staged"), ph.sem("cleared"), ph.sem("hot_full")
        gathering, go = ph.sem("gathering"), ph.sem("go")
        rows_in = [ph.sem(f"rows_in{u}") for u in range(2)]
        weighted, multiplied, added, chained = (ph.sem(n) for n in ("weighted", "multiplied", "added", "chained"))
        NPAIR = len(PAIRS)
        with nc.Block() as block:

            @block.scalar
            def _(act):
                with act.Fori(0, BATCHES // 2) as i:
                    for u in range(2):
                        act.wait_ge(rows_in[u], i * (16 * BATCH))
                        act.sem_inc(go, 1)
                        act.activation(staged[:, u, :], index[:, bass.ds(i * (2 * BATCH) + u * BATCH, BATCH)],
                                       ACT.Copy).then_inc(index_staged, 1)

            @block.gpsimd
            def _(pool):
                with pool.Fori(0, BATCHES // 2) as i:
                    for u in range(2):
                        pool.wait_ge(index_staged, i * 2 + (u + 1))
                        if alpha:
                            pool.wait_ge(weighted, i * 2 + (u + 1))
                        else:
                            pool.wait_ge(multiplied, (i * 2 + (u + 1)) * NPAIR)
                        pool.sem_inc(gathering, 1)
                        for j in range(BATCH):
                            pool.indirect_dma_start(
                                out=rows[:, u, j, :], out_offset=None, in_=table,
                                in_offset=bass.IndirectOffsetOnAxis(ap=staged[:, u, j:j + 1], axis=0)
                            ).then_inc(rows_in[u], 16)

            @block.tensor
            def _(pe):
                pe.sem_inc(multiplied, 2 * NPAIR)
                with pe.Fori(0, BATCHES // 2) as i:
                    for u in range(2):
                        b = i * 2 + u
                        pe.wait_ge(hot_full, b + 1)
                        if alpha:
                            pe.wait_ge(weighted, b + 3)
                        else:
                            pe.wait_ge(rows_in[u], (i + 1) * (16 * BATCH))
                        for p, (j0, n) in enumerate(PAIRS):
                            pe.wait_ge(added, b * BATCH + (j0 + n))
                            for j in range(j0, j0 + n):
                                for kk in range(KK):
                                    ins = pe.matmul(sums[p][:, j - j0, kk, :], messages[:, u, j, kk * P:(kk + 1) * P],
                                                    hot[:, u, j, :], start=True, stop=True)
                            ins.then_inc(multiplied, 1)

            @block.vector
            def _(dve):
                dve.sem_inc(added, BATCH)
                dve.sem_inc(weighted, 2)
                dve.memset(accT[:, :, :], 0.0).then_inc(cleared, 1)
                dve.memset(odd[:, :, :], 0.0).then_inc(cleared, 1)
                dve.wait_ge(cleared, 2)
                bases = [dve.alloc_register(ph._name(f"window_base{j}")) for j in range(BATCH)]

                def prepare(i, u):
                    b = i * 2 + u
                    dve.wait_ge(multiplied, (b + 1) * NPAIR)
                    c = i * (2 * BATCH) + u * BATCH
                    if weights is not None:
                        for j in range(BATCH):
                            ins = dve.tensor_scalar(hot[:, u, j, :], k.lane_iota[:, :], k.rel[:, bass.ds(c + j, 1)],
                                                    weights[:, bass.ds(c + j, 1)], ALU.is_equal, ALU.mult)
                    else:
                        ins = hot_by(dve, k, hot[:, u, :, :], k.rel[:, bass.ds(c, BATCH)], P)
                    ins.then_inc(hot_full, 1)
                    if alpha:
                        dve.wait_ge(rows_in[u], (i + 1) * (16 * BATCH))
                        a = alpha(i, u).rearrange("p h j -> p j h").unsqueeze(3).to_broadcast([P, BATCH, heads, D // heads])
                        dve.tensor_tensor(messages[:, u, :, :].rearrange("p j (h d) -> p j h d", h=heads),
                                          rows[:, u, :, :].rearrange("p j (h d) -> p j h d", h=heads), a, ALU.mult
                                          ).then_inc(weighted, 1)

                def add(i, u):
                    b = i * 2 + u
                    for j in range(BATCH):
                        dve.reg_load(bases[j], k.dst[0:1, bass.ds(i * (2 * BATCH) + (u * BATCH + j), 1)])
                    for p, (j0, n) in enumerate(PAIRS):
                        dve.wait_ge(multiplied, b * NPAIR + (2 * NPAIR + p + 1))
                        for j in range(j0, j0 + n):
                            acc = odd if (j + u) % 2 else accT
                            window = acc[:, :, bass.ds(nc.snap(bases[j], min_val=0, max_val=NPAD), P)]
                            dve.wait_ge(added, b * BATCH + (BATCH + j - 1))
                            dve.tensor_tensor(window, window, sums[p][:, j - j0, :, :], ALU.add).then_inc(added, 1)

                last = BATCHES // 2 - 1
                prepare(0, 0)
                with dve.Fori(0, last) as i:
                    prepare(i, 1)
                    add(i, 0)
                    prepare(i + 1, 0)
                    add(i, 1)
                prepare(last, 1)
                add(last, 0)
                add(last, 1)
                dve.wait_ge(added, CHUNKS + BATCH)
                dve.tensor_tensor(accT[:, :, :], accT[:, :, :], odd[:, :, :], ALU.add).then_inc(chained, 1)


QUADS = [(j, min(4, BATCH - j)) for j in range(0, BATCH, 4)]
SUM_COPIES = 5
COPY_OF = [4 if j == BATCH - 1 else j % 4 for j in range(BATCH)]
SCATTERS = [COPY_OF.count(m) for m in range(SUM_COPIES)]


def scatter_sum(k, table, copies):
    nc = k.nc
    with k.phase() as ph:
        srcf = ph.sb("srcf", [P, CHUNKS])
        src_row = ph.sb("src_row", [P, 2, BATCH * P], I32)
        mixed = ph.sb("mixed", [P, BATCH])
        earlier = ph.sb("earlier", [P, P])
        lane = ph.sb("lane", [P, 1])
        before = ph.sb("before", [P, 2, BATCH])
        junk = ph.sb("junk", [P, BATCH, P])
        target = ph.sb("target", [P, 2, BATCH], I32)
        window = ph.sb("window", [P, 2, BATCH, D])
        hot = ph.sb("hot", [P, 2, BATCH, P])
        same = ph.sb("same", [P, 2, BATCH, P])
        gmat = ph.sb("gmat", [P, 2, BATCH, P])
        out = ph.sb("out", [P, 2, BATCH, D])
        g_ps = [ph.ps(f"g{q}", [P, 4, P]) for q in range(4)]
        o_ps = [ph.ps(f"o{q}", [P, 2, D]) for q in range(4)]
        consts = ph.sem("consts")
        row_in = [ph.sem(f"row_in{u}") for u in range(2)]
        window_in = [ph.sem(f"window_in{u}") for u in range(2)]
        hot_full, chained, targeted, g_full, g_out = (ph.sem(n) for n in
                                                      ("hot_full", "chained", "targeted", "g_full", "g_out"))
        o_full, o_out, scattering = ph.sem("o_full"), ph.sem("o_out"), ph.sem("scattering")
        scattered = [[ph.sem(f"scattered{u}_{m}") for m in range(SUM_COPIES)] for u in range(2)]
        NQ, NP2 = len(QUADS), len(PAIRS)
        with nc.Block() as block:

            @block.sync
            def _(sp):
                base = sp.alloc_register(ph._name("window_base"))
                with sp.Fori(0, BATCHES // 2) as i:
                    for u in range(2):
                        b = i * 2 + u
                        c = i * (2 * BATCH) + u * BATCH
                        sp.wait_ge(hot_full, b + 1)
                        row = k.a["src_row"][:, bass.ds(c * P, BATCH * P)]
                        sp.dma_start(src_row[:, u, :], row.to_broadcast([P, BATCH * P])).then_inc(row_in[u], 16)
                        sp.wait_ge(o_full, (b + 1) * NP2)
                        for j in range(BATCH):
                            sp.reg_load(base, k.dst[0:1, bass.ds(c + j, 1)])
                            first = nc.snap(base, min_val=0, max_val=NPAD)
                            sp.dma_start(window[:, u, j, :], table[bass.ds(first, P), :]).then_inc(window_in[u], 16)

            @block.scalar
            def _(act):
                act.sem_inc(o_out, 2)
                act.sem_inc(g_out, NQ)
                with act.Fori(0, BATCHES // 2) as i:
                    for u in range(2):
                        b = i * 2 + u
                        for q, (j0, n) in enumerate(QUADS):
                            act.wait_ge(g_full, b * NQ + (q + 1))
                            act.wait_ge(o_full, (b + 1) * NP2)
                            act.activation(gmat[:, u, j0:j0 + n, :], g_ps[q][:, 0:n, :], ACT.Copy).then_inc(g_out, 1)
                        for m in range(SUM_COPIES):
                            act.wait_ge(scattered[u][m], i * (16 * SCATTERS[m]))
                        for p, (j0, n) in enumerate(PAIRS):
                            act.wait_ge(o_full, b * NP2 + (2 * NP2 + p + 1))
                            act.activation(out[:, u, j0:j0 + n, :], o_ps[p % 4][:, 0:n, :], ACT.Copy).then_inc(o_out, 1)

            @block.gpsimd
            def _(pool):
                pool.memset(earlier[:, :], 1.0).then_inc(consts, 1)
                pool.iota(lane[:, :], [[0, 1]], base=NPAD, channel_multiplier=1,
                          allow_small_or_imprecise_dtypes=True).then_inc(consts, 1)
                pool.wait_ge(consts, 2)
                pool.affine_select(out=earlier[:, :], in_=earlier[:, :], compare_op=ALU.is_gt, fill=0.0,
                                   base=0, pattern=[[-1, P]], channel_multiplier=1).then_inc(consts, 1)
                with pool.Fori(0, BATCHES // 2) as i:
                    for u in range(2):
                        b = i * 2 + u
                        pool.wait_ge(targeted, b + 1)
                        for j in range(BATCH):
                            m, before_j = COPY_OF[j], COPY_OF[:j].count(COPY_OF[j])
                            pool.wait_ge(o_out, b * NP2 + (j // 2 + 3))
                            if before_j:
                                pool.wait_ge(scattered[u][m], (i * SCATTERS[m] + before_j) * 16)
                            else:
                                pool.wait_ge(scattered[1 - u][m], (i + u) * (16 * SCATTERS[m]))
                            pool.sem_inc(scattering, 1)
                            pool.indirect_dma_start(
                                out=copies[m], out_offset=bass.IndirectOffsetOnAxis(ap=target[:, u, j:j + 1], axis=0),
                                in_=out[:, u, j, :], in_offset=None, compute_op=ALU.add).then_inc(scattered[u][m], 16)
                for u in range(2):
                    for m in range(SUM_COPIES):
                        pool.wait_ge(scattered[u][m], 16 * SCATTERS[m] * (BATCHES // 2))

            @block.tensor
            def _(pe):
                pe.sem_inc(o_full, 2 * NP2)
                with pe.Fori(0, BATCHES // 2) as i:
                    for u in range(2):
                        b = i * 2 + u
                        pe.wait_ge(hot_full, b + 3)
                        for q, (j0, n) in enumerate(QUADS):
                            pe.wait_ge(g_out, b * NQ + (q + 1))
                            for j in range(j0, j0 + n):
                                ins = pe.matmul(g_ps[q][:, j - j0, :], hot[:, u, j, :], same[:, u, j, :],
                                                start=True, stop=True)
                            ins.then_inc(g_full, 1)
                        pe.wait_ge(window_in[u], (i + 1) * (16 * BATCH))
                        for p, (j0, n) in enumerate(PAIRS):
                            pe.wait_ge(g_out, b * NQ + (NQ + (j0 + n - 1) // 4 + 1))
                            pe.wait_ge(o_out, b * NP2 + p)
                            for j in range(j0, j0 + n):
                                ins = pe.matmul(o_ps[p % 4][:, j - j0, :], gmat[:, u, j, :], window[:, u, j, :],
                                                start=True, stop=True)
                            ins.then_inc(o_full, 1)

            @block.vector
            def _(dve):
                dve.sem_inc(hot_full, 2)
                dve.wait_ge(consts, 3)
                step = Chain(dve, chained)
                step(dve.tensor_copy(srcf[:, :], k.src[:, :]))
                links = 4
                with dve.Fori(0, BATCHES // 2) as i:
                    for u in range(2):
                        b = i * 2 + u
                        c = i * (2 * BATCH) + u * BATCH
                        step.base, step.n = b * links + 1, 0
                        dve.wait_ge(row_in[u], (i + 1) * 16)
                        dve.wait_ge(g_out, b * NQ)
                        hot_by(dve, k, hot[:, u, :, :], k.rel[:, bass.ds(c, BATCH)], P)
                        for j in range(BATCH):
                            mine = srcf[:, bass.ds(c + j, 1)]
                            others = src_row[:, u, j * P:(j + 1) * P]
                            dve.tensor_scalar(same[:, u, j, :], others, mine, k.weight[:, bass.ds(c + j, 1)],
                                              ALU.is_equal, ALU.mult)
                            ins = dve.scalar_tensor_tensor(junk[:, j, :], others, mine, earlier[:, :], ALU.is_equal,
                                                           ALU.mult, accum_out=before[:, u, j:j + 1])
                        step(ins)
                        for m in range(SUM_COPIES):
                            dve.wait_ge(scattered[u][m], i * (16 * SCATTERS[m]))
                        step(dve.tensor_scalar(before[:, u, :], before[:, u, :], 0.0, None, ALU.is_gt))
                        s0 = srcf[:, bass.ds(c, BATCH)]
                        step(dve.tensor_scalar(mixed[:, 0:BATCH], s0, -1.0, lane[:, 0:1], ALU.mult, ALU.add))
                        step(dve.tensor_tensor(mixed[:, 0:BATCH], mixed[:, 0:BATCH], before[:, u, :], ALU.mult))
                        dve.tensor_tensor(target[:, u, :], mixed[:, 0:BATCH], s0, ALU.add).then_inc(targeted, 1)
                        dve.wait_ge(targeted, b + 1)
                        dve.sem_inc(hot_full, 1)


def layer0_gnn(k):
    nc, a = k.nc, k.a
    table, copies = k.gcn_rows, k.gcn_sums
    with k.phase() as ph:
        xn = ph.sb("xn", [P, TILES, D])
        normalize(k, k.x, xn)
        w = ph.sb("gcn_w", [P, KK, D])

        def load(sp, sem):
            sp.dma_start(w[:, :, :], a["L0_gnn_w"]).then_inc(sem, 16)
            return 16

        def evacuate(dve, t, product, stage, step):
            return dve.tensor_scalar(stage, product[:, 0, 0:D], k.dinv[:, bass.ds(t, 1)], None, ALU.mult)

        def store(sp, t, stage, sem):
            sp.dma_start(table[bass.ds(t * P, P), :], stage).then_inc(sem, 16)

        with k.phase() as inner:
            node_tiles(k, inner, xn, D, load, w, evacuate, store, 1)
    scatter_sum(k, table, copies)
    with k.phase() as ph:
        parts = ph.sb("parts", [P, SUM_COPIES, TILES, D])
        bias = ph.sb("gcn_bias", [P, D])
        loaded, chained = ph.sem("loaded"), ph.sem("chained")
        GROUPS = TILES // UNROLL
        parts_in = [ph.sem(f"parts_in{g}") for g in range(GROUPS)]
        with nc.Block() as block:

            @block.sync
            def _(sp):
                sp.dma_start(bias[:, :], a["L0_gnn_b"].to_broadcast([P, D])).then_inc(loaded, 16)
                for g in range(GROUPS):
                    rows = slice(g * GROUP, (g + 1) * GROUP)
                    for m in range(SUM_COPIES):
                        sp.dma_start(parts[:, m, g * UNROLL:(g + 1) * UNROLL, :],
                                     copies[m][rows, :].rearrange("(t p) d -> p t d", p=P)).then_inc(parts_in[g], 16)

            @block.vector
            def _(dve):
                step = Chain(dve, chained)
                shape = [P, UNROLL, D]
                dve.wait_ge(loaded, 16)
                for g in range(GROUPS):
                    dve.wait_ge(parts_in[g], 16 * SUM_COPIES)
                    at = slice(g * UNROLL, (g + 1) * UNROLL)
                    total = parts[:, 0, at, :]
                    for m in range(1, SUM_COPIES):
                        step(dve.tensor_tensor(total, total, parts[:, m, at, :], ALU.add))
                    step(dve.tensor_tensor(total, total, k.dinv[:, at].unsqueeze(2).to_broadcast(shape), ALU.mult))
                    step(dve.tensor_tensor(total, total, bias[:, :].unsqueeze(1).to_broadcast(shape), ALU.add))
                    step(dve.scalar_tensor_tensor(k.x[:, at, :], total, 0.0, k.x[:, at, :], ALU.max, ALU.add))


def from_sums(k, ph, accT, load, update, links):
    nc = k.nc
    ring = ph.sb("sum_ring", [P, UNROLL, KK, P])
    turned = [ph.ps(f"turned{i}", [P, 512]) for i in range(3)]
    loaded, ring_full, turned_full = ph.sem("loaded"), ph.sem("ring_full"), ph.sem("turned_full")
    turned_out, chained = ph.sem("turned_out"), ph.sem("chained")
    bodies = TILES // UNROLL
    count = []
    with nc.Block() as block:

        @block.sync
        def _(sp):
            count.append(load(sp, loaded))

        @block.scalar
        def _(act):
            with act.Fori(0, bodies) as i:
                act.wait_ge(turned_full, i * UNROLL)
                for u in range(UNROLL):
                    act.activation(ring[:, u, :, :], accT[:, :, bass.ds((i * UNROLL + u) * P, P)], ACT.Copy
                                   ).then_inc(ring_full, 1)

        @block.tensor
        def _(pe):
            with pe.Fori(0, bodies) as i:
                for u in range(UNROLL):
                    t = i * UNROLL + u
                    pe.wait_ge(ring_full, t + 1)
                    pe.wait_ge(turned_out, t)
                    for kk in range(KK):
                        ins = pe.transpose(turned[u % 3][:, kk * P:(kk + 1) * P], ring[:, u, kk, :], k.ident[:, :])
                    ins.then_inc(turned_full, 1)

        @block.vector
        def _(dve):
            dve.sem_inc(turned_out, 1)
            dve.wait_ge(loaded, count[0])
            step = Chain(dve, chained)
            with dve.Fori(0, bodies) as i:
                for u in range(UNROLL):
                    t = i * UNROLL + u
                    dve.wait_ge(turned_full, t + 1)
                    step.base, step.n = t * links, 0
                    last = update(dve, t, turned[u % 3][:, 0:D], step)
                    assert step.n == links
                    last.then_inc(turned_out, 1)


def gate_weights(k, logits, gates, experts, kind, bias=None, chosen=None):
    nc = k.nc
    E = experts
    shape = [P, TILES, E]
    pair = [P, TILES, E, E]
    with k.phase() as ph:
        br = ph.sb("router_bias", [P, E])
        low = ph.sb("low", [P, E, E])
        probs, work = ph.sb("probs", shape), ph.sb("work", shape)
        top, total = ph.sb("top", [P, TILES]), ph.sb("total", [P, TILES])
        above, ties = ph.sb("above", pair), ph.sb("ties", pair)
        loaded, consts, chained, exps, exp_in = (ph.sem(n) for n in ("loaded", "consts", "chained", "exps", "exp_in"))
        n_exp = {"softmax": 1, "top2": 1, "top2_of_softmax": 2, "top2_renormalized": 1}[kind]
        with nc.Block() as block:

            @block.sync
            def _(sp):
                sp.dma_start(br[:, :], bias.to_broadcast([P, E])).then_inc(loaded, 16)

            @block.gpsimd
            def _(pool):
                pool.memset(low[:, :, :], 1.0).then_inc(consts, 1)
                pool.wait_ge(consts, 1)
                pool.affine_select(out=low[:, :, :], in_=low[:, :, :], compare_op=ALU.is_gt, fill=0.0,
                                   base=0, pattern=[[1, E], [-1, E]], channel_multiplier=0).then_inc(consts, 1)

            @block.scalar
            def _(act):
                for n in range(n_exp):
                    act.wait_ge(exp_in, n + 1)
                    act.activation(work[:, :, :], work[:, :, :], ACT.Exp).then_inc(exps, 1)

            @block.vector
            def _(dve):
                step = Chain(dve, chained)

                def spread(v):
                    return v[:, :].unsqueeze(2).to_broadcast(shape)

                def exponentials(values, n):
                    step(dve.tensor_reduce(top[:, :], values, AX.X, ALU.max))
                    dve.tensor_tensor(work[:, :, :], values, spread(top), ALU.subtract).then_inc(exp_in, 1)
                    dve.wait_ge(exps, n)

                def divide(out):
                    step(dve.tensor_reduce(total[:, :], work[:, :, :], AX.X, ALU.add))
                    step(dve.reciprocal(total[:, :], total[:, :]))
                    step(dve.tensor_tensor(out, work[:, :, :], spread(total), ALU.mult))

                dve.wait_ge(loaded, 16)
                dve.wait_ge(consts, 2)
                step(dve.tensor_tensor(logits[:, :, :], logits[:, :, :],
                                       br[:, :].unsqueeze(1).to_broadcast(shape), ALU.add))
                values = logits[:, :, :]
                if kind != "top2":
                    exponentials(values, 1)
                    divide(probs[:, :, :] if kind != "softmax" else gates[:, :, :])
                    values = probs[:, :, :]
                if kind == "softmax":
                    return
                for t in range(TILES):
                    rivals = values[:, t, :].unsqueeze(1).to_broadcast([P, E, E])
                    own = values[:, t, :].unsqueeze(2).to_broadcast([P, E, E])
                    dve.tensor_tensor(above[:, t, :, :], rivals, own, ALU.is_gt)
                    ins = dve.tensor_tensor(ties[:, t, :, :], rivals, own, ALU.is_equal)
                step(ins)
                flat = "p t e j -> p t (e j)"
                step(dve.tensor_tensor(ties[:, :, :, :].rearrange(flat), ties[:, :, :, :].rearrange(flat),
                                       low[:, :, :].rearrange("p e j -> p (e j)").unsqueeze(1).to_broadcast([P, TILES, E * E]),
                                       ALU.mult))
                step(dve.tensor_tensor(above[:, :, :, :], above[:, :, :, :], ties[:, :, :, :], ALU.add))
                taken = gates[:, :, :]
                step(dve.tensor_reduce(taken, above[:, :, :, :], AX.X, ALU.add))
                step(dve.tensor_scalar(taken, taken, 2.0, None, ALU.is_lt))
                if chosen is not None:
                    step(dve.tensor_copy(chosen[:, :, :], taken))
                if kind == "top2_renormalized":
                    step(dve.tensor_tensor(work[:, :, :], values, taken, ALU.mult))
                else:
                    exponentials(values, 2 if kind == "top2_of_softmax" else 1)
                    step(dve.tensor_tensor(work[:, :, :], work[:, :, :], taken, ALU.mult))
                divide(gates[:, :, :])


class Experts:

    def __init__(self, count, dims):
        self.count, self.dims = count, dims
        self.at, col = [], 0
        for n_in, n_out in zip(dims, dims[1:]):
            self.at.append(col)
            col += -(-n_in // P) * n_out
        self.columns = col
        self.chunks = [(l, c) for l, n in enumerate(dims[1:-1]) for c in range(-(-n // P))]

    def matrix(self, weights, layer, kk, lo, hi):
        n_in, n_out = self.dims[layer], self.dims[layer + 1]
        c = self.at[layer] + kk * n_out
        return weights[0:min(P, n_in - kk * P), c + lo:c + hi]


def mixture(k, xT, spec, weights, out_bias, act_func, bias, scale=None, gates=None):
    nc = k.nc
    E, chunks = spec.count, spec.chunks
    J = 2 * len(chunks)
    SLOTS = 4 if J % 4 == 0 else 3
    slots = min(2, E)
    GROUPS = TILES // UNROLL
    with k.phase() as ph:
        w = ph.sb("expert_w", [P, slots, spec.columns])
        hidden = [ph.sb(f"hidden{l}", [P, -(-n // P), GROUP]) for l, n in enumerate(spec.dims[1:-1])]
        b_out = ph.sb("out_bias", [P, E, D])
        bias_e = ph.sb("bias_e", [P, 2, len(chunks)])
        scale_e = ph.sb("scale_e", [P, 2, len(chunks)]) if scale is not None else None
        staged, started = ph.sem("staged"), ph.sem("started")
        units = [ph.ps(f"unit{i}", [P, 512]) for i in range(SLOTS)]
        outs = [ph.ps(f"out{i}", [P, 512]) for i in range(3)]
        w_in = [ph.sem(f"w_in{s}") for s in range(slots)]
        bias_in = ph.sem("bias_in")
        unit_full, unit_out, out_full, out_out, chained = (ph.sem(n) for n in (
            "unit_full", "unit_out", "out_full", "out_out", "chained"))

        def experts(eng, body):
            if E == 1:
                body(0, 0, 0)
            else:
                with eng.Fori(0, E // 2) as pair:
                    for s in range(2):
                        body(pair * 2 + s, s, pair)

        def groups(eng, e, body):
            with eng.Fori(0, GROUPS) as g:
                body(g, e * GROUPS + g)

        with nc.Block() as block:

            @block.sync
            def _(sp):
                sp.dma_start(b_out[:, :, :], out_bias.rearrange("o (e d) -> o e d", e=E).to_broadcast([P, E, D])
                             ).then_inc(bias_in, 16)

                def load(e, s, pair):
                    sp.wait_ge(out_full, e * TILES)
                    sp.dma_start(w[:, s, :], weights[bass.ds(e, 1), :, :].rearrange("o p c -> (o p) c")
                                 ).then_inc(w_in[s], 16)

                experts(sp, load)

            @block.scalar
            def _(act):
                act.sem_inc(unit_out, SLOTS - 1)

                def expert(e, s, pair):
                    ins = act.activation(bias_e[:, s, :], bias[:, bass.ds(e, 1), :], ACT.Copy)
                    if scale is not None:
                        ins.then_inc(staged, 1)
                        ins = act.activation(scale_e[:, s, :], scale[:, bass.ds(e, 1), :], ACT.Copy)
                    ins.then_inc(staged, 1)

                    def group(g, n):
                        act.wait_ge(staged, (e + 1) * (1 if scale is None else 2))
                        act.wait_ge(out_full, n * UNROLL + TILES)
                        for j in range(J):
                            l, c = chunks[j // 2]
                            m = min(P, spec.dims[l + 1] - c * P)
                            half = slice((j % 2) * HALF, (j % 2 + 1) * HALF)
                            act.wait_ge(unit_full, n * J + (j + 1))
                            col = (slice(0, m), s, slice(j // 2, j // 2 + 1))
                            act.activation(hidden[l][0:m, c, half], units[j % SLOTS][0:m, 0:HALF], act_func,
                                           bias=bias_e[col], **({"scale": scale_e[col]} if scale is not None else {})
                                           ).then_inc(unit_out, 1)
                    groups(act, e, group)
                experts(act, expert)

            @block.tensor
            def _(pe):
                pe.sem_inc(out_full, TILES)

                def expert(e, s, pair):
                    pe.wait_ge(w_in[s], pair * 16 + 16)
                    pe.sem_inc(started, 1)

                    def group(g, n):
                        for j in range(J):
                            l, c = chunks[j // 2]
                            m = min(P, spec.dims[l + 1] - c * P)
                            K = -(-spec.dims[l] // P)
                            pe.wait_ge(unit_out, n * J + j)
                            for kk in range(K):
                                rows = min(P, spec.dims[l] - kk * P)
                                if l == 0:
                                    rhs = xT[:, kk, bass.ds(g * GROUP + (j % 2) * HALF, HALF)]
                                else:
                                    src = chunks.index((l - 1, kk)) * 2 + j % 2
                                    pe.wait_ge(unit_out, n * J + (src + SLOTS))
                                    rhs = hidden[l - 1][0:rows, kk, (j % 2) * HALF:(j % 2 + 1) * HALF]
                                ins = pe.matmul(units[j % SLOTS][0:m, 0:HALF],
                                                spec.matrix(w[:, s, :], l, kk, c * P, c * P + m), rhs,
                                                start=kk == 0, stop=kk == K - 1)
                            ins.then_inc(unit_full, 1)
                        L = len(spec.dims) - 2
                        K = -(-spec.dims[L] // P)
                        for u in range(UNROLL):
                            pe.wait_ge(out_out, n * UNROLL + u)
                            for kk in range(K):
                                rows = min(P, spec.dims[L] - kk * P)
                                if u in (0, 2):
                                    src = chunks.index((L - 1, kk)) * 2 + (u == 2)
                                    pe.wait_ge(unit_out, n * J + (src + SLOTS))
                                ins = pe.matmul(outs[u % 3][:, 0:D], hidden[L - 1][0:rows, kk, u * P:(u + 1) * P],
                                                spec.matrix(w[:, s, :], L, kk, 0, D), start=kk == 0, stop=kk == K - 1)
                            ins.then_inc(out_full, 1)
                    groups(pe, e, group)
                experts(pe, expert)

            @block.vector
            def _(dve):
                dve.sem_inc(out_out, 1)
                dve.wait_ge(bias_in, 16)

                def expert(e, s, pair):
                    def group(g, n):
                        for u in range(UNROLL):
                            t = g * UNROLL + u
                            xt = k.x[:, bass.ds(t, 1), :]
                            bt = b_out[:, bass.ds(e, 1), :]
                            dve.wait_ge(out_out, n * UNROLL + (u + 1))
                            if gates is not None:
                                gate = gates[:, bass.ds(t, 1), bass.ds(e, 1)].rearrange("p a b -> p (a b)")
                                ins = dve.scalar_tensor_tensor(xt, bt, gate, xt, ALU.mult, ALU.add)
                            else:
                                ins = dve.tensor_tensor(xt, bt, xt, ALU.add)
                            ins.then_inc(chained, 1)
                            dve.wait_ge(chained, n * UNROLL + (u + 1))
                            dve.wait_ge(out_full, n * UNROLL + (TILES + u + 1))
                            part = outs[u % 3][:, 0:D]
                            if gates is not None:
                                ins = dve.scalar_tensor_tensor(xt, part, gate, xt, ALU.mult, ALU.add)
                            else:
                                ins = dve.tensor_tensor(xt, part, xt, ALU.add)
                            ins.then_inc(out_out, 1)
                    groups(dve, e, group)
                experts(dve, expert)


class Dispatch:

    def __init__(self, k, ph, experts, hidden, affine):
        self.experts, self.hidden, self.affine = experts, hidden, affine
        self.blocks = (2 * NPAD + experts * (BLOCK - 1)) // BLOCK
        assert self.blocks % 2 == 0
        self.chunks = hidden // P
        self.bias_at = KK * hidden
        self.affine_at = self.bias_at + self.chunks
        self.columns = self.affine_at + (2 * KK if affine else 0)
        k.uid += 1
        self.rows = k.slot_rows[k.routed_layers]
        k.routed_layers += 1
        assert self.rows.shape[0] == self.blocks * BLOCK
        self.results = k.nc.dram_tensor(f"slot_results_{k.uid}", [self.blocks * BLOCK, D], F32, kind="Internal").ap()
        self.slots = ph.sb("slots", [P, 2, TILES], I32)
        self.gates = ph.sb("slot_gates", [P, 2, TILES])
        self.block_expert = ph.sb("block_expert", [P, self.blocks], I32)


def assign_slots(k, d, chosen, gates):
    nc = k.nc
    E, NB = d.experts, d.blocks
    with k.phase() as ph:
        before_me, ones = ph.sb("before_me", [P, P]), ph.sb("ones", [P, P])
        block_no = ph.sb("block_no", [P, NB])
        rank, ends = ph.sb("rank", [P, E, TILES]), ph.sb("ends", [P, E, TILES + 1])
        blocks, block_end, first = (ph.sb(n, [P, E]) for n in ("blocks", "block_end", "first"))
        blocks_i = ph.sb("blocks_i", [P, E], I32)
        work, slot = ph.sb("work", [P, E, TILES]), ph.sb("slot", [P, 2, TILES])
        passed = ph.sb("passed", [P, NB, E])
        number = ph.sb("number", [P, NB])
        lanes_ps, tiles_ps = (ph.ps(n, [P, TILES, E]) for n in ("lanes_before", "tile_totals"))
        consts, counted, chained = ph.sem("consts"), ph.sem("counted"), ph.sem("chained")
        with nc.Block() as block:

            @block.gpsimd
            def _(pool):
                pool.memset(ones[:, :], 1.0).then_inc(consts, 1)
                pool.memset(before_me[:, :], 1.0).then_inc(consts, 1)
                pool.iota(block_no[:, :], [[1, NB]], base=0, channel_multiplier=0,
                          allow_small_or_imprecise_dtypes=True).then_inc(consts, 1)
                pool.wait_ge(consts, 3)
                pool.affine_select(out=before_me[:, :], in_=before_me[:, :], compare_op=ALU.is_gt, fill=0.0,
                                   base=0, pattern=[[1, P]], channel_multiplier=-1).then_inc(consts, 1)

            @block.tensor
            def _(pe):
                pe.wait_ge(consts, 4)
                flat = chosen[:, :, :].rearrange("p t e -> p (t e)")
                pe.matmul(lanes_ps[:, :, :].rearrange("p t e -> p (t e)"), before_me[:, :], flat, start=True, stop=True)
                pe.matmul(tiles_ps[:, :, :].rearrange("p t e -> p (t e)"), ones[:, :], flat, start=True, stop=True
                          ).then_inc(counted, 1)

            @block.vector
            def _(dve):
                step = Chain(dve, chained)
                by_tile = "p e t -> p t e"
                dve.wait_ge(consts, 4)
                step(dve.memset(ends[:, :, :], 0.0))
                dve.wait_ge(counted, 1)
                for e in range(E):
                    step(dve.tensor_tensor_scan(ends[:, e, 1:TILES + 1], ones[:, 0:TILES], tiles_ps[:, :, e], 0.0,
                                                ALU.mult, ALU.add))
                step(dve.tensor_tensor(rank[:, :, :], ends[:, :, 0:TILES], lanes_ps[:, :, :].rearrange("p t e -> p e t"),
                                       ALU.add))
                step(dve.tensor_scalar(blocks[:, :], ends[:, :, TILES], float(BLOCK - 1), None, ALU.add))
                step(dve.tensor_copy(blocks_i[:, :], blocks[:, :]))
                step(dve.tensor_scalar(blocks_i[:, :], blocks_i[:, :], BLOCK.bit_length() - 1, None, ALU.logical_shift_right))
                step(dve.tensor_copy(blocks[:, :], blocks_i[:, :]))
                step(dve.tensor_tensor_scan(block_end[:, :], ones[:, 0:E], blocks[:, :], 0.0, ALU.mult, ALU.add))
                step(dve.tensor_tensor(first[:, :], block_end[:, :], blocks[:, :], ALU.subtract))
                step(dve.scalar_tensor_tensor(rank[:, :, :], first[:, :].unsqueeze(2).to_broadcast([P, E, TILES]),
                                              float(BLOCK), rank[:, :, :], ALU.mult, ALU.add))
                took = chosen[:, :, :].rearrange("p t e -> p e t")
                step(dve.tensor_scalar(work[:, :, :], took, -1.0, -float(2 ** 20), ALU.add, ALU.mult))
                step(dve.tensor_tensor(work[:, :, :], work[:, :, :], rank[:, :, :], ALU.add))
                step(dve.tensor_reduce(slot[:, 0, :], work[:, :, :].rearrange(by_tile), AX.X, ALU.min))
                step(dve.tensor_tensor(work[:, :, :], rank[:, :, :], took, ALU.mult))
                step(dve.tensor_reduce(slot[:, 1, :], work[:, :, :].rearrange(by_tile), AX.X, ALU.max))
                step(dve.tensor_copy(d.slots[:, :, :], slot[:, :, :]))
                for n in range(2):
                    step(dve.tensor_tensor(work[:, :, :], rank[:, :, :],
                                           slot[:, n, :].unsqueeze(1).to_broadcast([P, E, TILES]), ALU.is_equal))
                    step(dve.tensor_tensor(work[:, :, :], work[:, :, :], gates[:, :, :].rearrange("p t e -> p e t"), ALU.mult))
                    step(dve.tensor_reduce(d.gates[:, n, :], work[:, :, :].rearrange(by_tile), AX.X, ALU.add))
                step(dve.tensor_tensor(passed[:, :, :], block_no[:, :].unsqueeze(2).to_broadcast([P, NB, E]),
                                       block_end[:, :].unsqueeze(1).to_broadcast([P, NB, E]), ALU.is_ge))
                step(dve.tensor_reduce(number[:, :], passed[:, :, :], AX.X, ALU.add))
                step(dve.tensor_scalar(number[:, :], number[:, :], float(E - 1), None, ALU.min))
                step(dve.tensor_copy(d.block_expert[:, :], number[:, :]))


def expert_blocks(k, d, xn, first_part, second_part, out_bias):
    nc = k.nc
    E, C, H, NB = d.experts, d.chunks, d.hidden, d.blocks
    UNITS = 4
    with k.phase() as ph:
        w1, w2 = ph.sb("first_part", [P, 2, d.columns]), ph.sb("second_part", [P, E, C * D])
        b2 = ph.sb("out_bias", [P, E, D])
        rows = ph.sb("rows", [P, 2, 2, D])
        xT = ph.sb("xT", [P, KK, BLOCK])
        hid = ph.sb("hidden", [P, C, BLOCK])
        res = ph.sb("results", [P, 2, 2, D])
        t_ps = ph.ps("turned", [P, KK, BLOCK])
        units = [ph.ps(f"unit{n}", [P, 512]) for n in range(UNITS)]
        outs = [ph.ps(f"out{h}", [P, 512]) for h in range(2)]
        w1_in = [ph.sem(f"first_part_in{u}") for u in range(2)]
        rows_in = [ph.sem(f"rows_in{u}") for u in range(2)]
        stored = [ph.sem(f"stored{u}") for u in range(2)]
        w2_in, turned, xT_full = ph.sem("second_part_in"), ph.sem("turned"), ph.sem("xT_full")
        unit_full, unit_out, out_full, out_out = (ph.sem(n) for n in ("unit_full", "unit_out", "out_full", "out_out"))
        storing, moved = ph.sem("storing"), ph.sem("rows_moved")

        def expert_of(eng, reg, s):
            eng.reg_load(reg, d.block_expert[0:1, bass.ds(s, 1)])
            return nc.snap(reg, min_val=0, max_val=E - 1)

        def blocks(eng, body):
            with eng.Fori(0, NB // 2 - 1) as i:
                for u in range(2):
                    body(i * 2 + u, u, i, True)
            for u in range(2):
                body(NB - 2 + u, u, NB // 2 - 1, u == 0)

        with nc.Block() as block:

            @block.sync
            def _(sp):
                reg = sp.alloc_register(ph._name("expert"))

                def load(s, u, turn, more):
                    sp.wait_ge(out_full, s * 2 + 2)
                    sp.dma_start(rows[:, u, :, :], d.rows[bass.ds(s * BLOCK, BLOCK), :].rearrange("(h p) d -> p h d", p=P)
                                 ).then_inc(rows_in[u], 16)
                    e = expert_of(sp, reg, s)
                    sp.dma_start(w1[:, u, :], first_part[bass.ds(e, 1), :, :].rearrange("o p c -> (o p) c")
                                 ).then_inc(w1_in[u], 16)
                sp.dma_start(b2[:, :, :], out_bias.rearrange("o (e d) -> o e d", e=E).to_broadcast([P, E, D])
                             ).then_inc(w2_in, 16)
                for e in range(E):
                    sp.dma_start(w2[:, e, :], second_part[e, :, :]).then_inc(w2_in, 16)
                sp.wait_ge(moved, 16 * 2 * TILES)
                blocks(sp, load)

            @block.gpsimd
            def _(pool):
                for t in range(TILES):
                    for n in range(2):
                        pool.indirect_dma_start(
                            out=d.rows, out_offset=bass.IndirectOffsetOnAxis(ap=d.slots[:, n, t:t + 1], axis=0),
                            in_=xn[:, t, :], in_offset=None).then_inc(moved, 16)

                def store(s, u, turn, more):
                    pool.wait_ge(out_out, s * 2 + 4)
                    pool.sem_inc(storing, 1)
                    pool.dma_start(d.results[bass.ds(s * BLOCK, BLOCK), :].rearrange("(h p) d -> p h d", p=P),
                                   res[:, u, :, :]).then_inc(stored[u], 16)
                blocks(pool, store)
                for u in range(2):
                    pool.wait_ge(stored[u], 16 * (NB // 2))

            @block.tensor
            def _(pe):
                reg = pe.alloc_register(ph._name("expert"))
                pe.sem_inc(out_full, 4)

                def turn_rows(s, u, turn):
                    pe.wait_ge(rows_in[u], turn * 16 + 16)
                    for kk in range(KK):
                        for h in range(2):
                            ins = pe.transpose(t_ps[:, kk, h * P:(h + 1) * P], rows[:, u, h, kk * P:(kk + 1) * P],
                                               k.ident[:, :])
                    ins.then_inc(turned, 1)

                def compute(s, u, turn, more):
                    pe.wait_ge(xT_full, s + 1)
                    pe.wait_ge(w1_in[u], turn * 16 + 16)
                    for c in range(C):
                        pe.wait_ge(unit_out, s * C + c)
                        for kk in range(KK):
                            ins = pe.matmul(units[c % UNITS][:, 0:BLOCK], w1[:, u, kk * H + c * P:kk * H + (c + 1) * P],
                                            xT[:, kk, :], start=kk == 0, stop=kk == KK - 1)
                        ins.then_inc(unit_full, 1)
                    if more:
                        turn_rows(s + 1, 1 - u, turn + u)
                    pe.wait_ge(w2_in, 16 * (1 + E))
                    pe.wait_ge(unit_out, s * C + (C + UNITS - 1))
                    e = expert_of(pe, reg, s)
                    for h in range(2):
                        pe.wait_ge(out_out, s * 2 + (h + 1))
                        for c in range(C):
                            ins = pe.matmul(outs[h][:, 0:D], hid[:, c, h * P:(h + 1) * P],
                                            w2[:, bass.ds(e, 1), c * D:(c + 1) * D], start=c == 0, stop=c == C - 1)
                        ins.then_inc(out_full, 1)

                turn_rows(0, 0, 0)
                blocks(pe, compute)

            @block.scalar
            def _(act):
                act.sem_inc(unit_out, UNITS - 1)

                def hidden(s, u, turn, more):
                    act.wait_ge(out_full, s * 2 + 4)
                    for c in range(C):
                        act.wait_ge(unit_full, s * C + (c + 1))
                        act.activation(hid[:, c, :], units[c % UNITS][:, 0:BLOCK], ACT.Gelu,
                                       bias=w1[:, u, d.bias_at + c:d.bias_at + c + 1]).then_inc(unit_out, 1)
                blocks(act, hidden)

            @block.vector
            def _(dve):
                reg = dve.alloc_register(ph._name("expert"))
                dve.sem_inc(out_out, 2)
                dve.wait_ge(w2_in, 16 * (1 + E))

                def keep_rows(s, u, turn):
                    dve.wait_ge(turned, s + 1)
                    if not d.affine:
                        dve.tensor_copy(xT[:, :, :], t_ps[:, :, :]).then_inc(xT_full, 1)
                        return
                    dve.wait_ge(w1_in[u], turn * 16 + 16)
                    for kk in range(KK):
                        at = d.affine_at + 2 * kk
                        ins = dve.tensor_scalar(xT[:, kk, :], t_ps[:, kk, :], w1[:, u, at:at + 1], w1[:, u, at + 1:at + 2],
                                                ALU.mult, ALU.add)
                    ins.then_inc(xT_full, 1)

                def results(s, u, turn, more):
                    if more:
                        keep_rows(s + 1, 1 - u, turn + u)
                    dve.wait_ge(stored[u], turn * 16)
                    e = expert_of(dve, reg, s)
                    for h in range(2):
                        dve.wait_ge(out_full, s * 2 + (h + 5))
                        dve.tensor_tensor(res[:, u, h, :], outs[h][:, 0:D], b2[:, bass.ds(e, 1), :].rearrange("p o d -> p (o d)"),
                                          ALU.add).then_inc(out_out, 1)

                keep_rows(0, 0, 0)
                blocks(dve, results)


def combine_visits(k, d):
    GROUPS = TILES // UNROLL
    with k.phase() as ph:
        got = ph.sb("got", [P, 2, TILES, D])
        got_in = [ph.sem(f"got_in{g}") for g in range(GROUPS)]
        added = ph.sem("added")
        with k.nc.Block() as block:

            @block.gpsimd
            def _(pool):
                for t in range(TILES):
                    for n in range(2):
                        pool.indirect_dma_start(
                            out=got[:, n, t, :], out_offset=None, in_=d.results,
                            in_offset=bass.IndirectOffsetOnAxis(ap=d.slots[:, n, t:t + 1], axis=0)
                        ).then_inc(got_in[t // UNROLL], 16)

            @block.vector
            def _(dve):
                for g in range(GROUPS):
                    dve.wait_ge(got_in[g], 16 * 2 * UNROLL)
                    for n in range(2):
                        if n == 1:
                            dve.wait_ge(added, (2 * g + 1) * UNROLL)
                        for t in range(g * UNROLL, (g + 1) * UNROLL):
                            xt = k.x[:, t, :]
                            dve.scalar_tensor_tensor(xt, got[:, n, t, :], d.gates[:, n, t:t + 1], xt, ALU.mult, ALU.add
                                                     ).then_inc(added, 1)


def sparse_mixture(k, xn, chosen, gates, experts, hidden, parts, out_bias, affine):
    with k.phase() as ph:
        d = Dispatch(k, ph, experts, hidden, affine)
        assign_slots(k, d, chosen, gates)
        expert_blocks(k, d, xn, parts[0], parts[1], out_bias)
        combine_visits(k, d)


def routed(k, xn, xT, router, experts, logits):
    with k.phase() as ph:
        wr = ph.sb("router", [P, KK, experts])

        def load(sp, sem):
            sp.dma_start(wr[:, :, :], router).then_inc(sem, 16)
            return 16

        def evacuate(dve, t, product, stage, step):
            return dve.tensor_copy(logits[:, bass.ds(t, 1), :], product[:, 0, 0:experts])

        node_tiles(k, ph, xn, experts, load, wr, evacuate, xT=xT)


def load_small(k, pairs):
    with k.phase() as ph:
        loaded = ph.sem("loaded")
        with k.nc.Block() as block:

            @block.sync
            def _(sp):
                for dst, src in pairs:
                    sp.dma_start(dst, src).then_inc(loaded, 16)
                sp.wait_ge(loaded, 16 * len(pairs))


def edge_order(dram_row, g, ci):
    return dram_row.rearrange("o (g c e) -> (o c) g e", g=g, c=ci)


def attention_scores(k, ktable, kindex, qtable, heads, scores):
    nc = k.nc
    CI = 104 // heads
    R = CI * heads
    G = CHUNKS // CI
    per_body = 2 * BATCH // CI
    with k.phase() as ph:
        staged = ph.sb("index_staged", [P, 2, BATCH], I32)
        rows = ph.sb("rows", [P, 2, BATCH, D])
        window = ph.sb("window", [P, 2, BATCH, D])
        rel = ph.sb("rel_row", [P, 2, BATCH * P], BF16)
        spread = ph.sb("spread", [P, 2, BATCH, P])
        prod = ph.sb("prod", [P, BATCH, D])
        sc = ph.sb("sc", [P, per_body, heads, CI])
        kept = ph.sb("kept", [R, G, P])
        q_ps = [ph.ps(f"q{q}", [P, 2, D]) for q in range(len(PAIRS))]
        s_ps = ph.ps("s", [P, 512])
        index_staged, gathering, spread_full = ph.sem("index_staged"), ph.sem("gathering"), ph.sem("spread_full")
        q_full, q_out = ph.sem("q_full"), ph.sem("q_out")
        rel_in = [ph.sem(f"rel_in{u}") for u in range(2)]
        reduced, s_full, s_out, stored = (ph.sem(n) for n in ("reduced", "s_full", "s_out", "stored"))
        go = ph.sem("go")
        rows_in = [ph.sem(f"rows_in{u}") for u in range(2)]
        window_in = [ph.sem(f"window_in{u}") for u in range(2)]
        NP2 = len(PAIRS)
        with nc.Block() as block:

            @block.sync
            def _(sp):
                base = sp.alloc_register(ph._name("window_base"))
                with sp.Fori(0, BATCHES // 2) as i:
                    for u in range(2):
                        b = i * 2 + u
                        c = i * (2 * BATCH) + u * BATCH
                        sp.wait_ge(spread_full, b + 1)
                        sp.dma_start(rel[:, u, :], k.rel_row[:, bass.ds(c * P, BATCH * P)].to_broadcast([P, BATCH * P])
                                     ).then_inc(rel_in[u], 16)
                        sp.wait_ge(q_full, (b + 1) * NP2)
                        for j in range(BATCH):
                            sp.reg_load(base, k.dst[0:1, bass.ds(c + j, 1)])
                            first = nc.snap(base, min_val=0, max_val=NPAD)
                            sp.dma_start(window[:, u, j, :], qtable[bass.ds(first, P), :]).then_inc(window_in[u], 16)
                sp.wait_ge(s_out, G + 1)
                for h in range(heads):
                    sp.dma_start(edge_order(scores[h:h + 1, :], G, CI), kept[h * CI:(h + 1) * CI, :, :]
                                 ).then_inc(stored, 16)
                sp.wait_ge(stored, 16 * heads)

            @block.scalar
            def _(act):
                act.sem_inc(s_out, 1)

                def stage(i, u):
                    act.wait_ge(rows_in[u], i * (16 * BATCH))
                    act.sem_inc(go, 1)
                    act.activation(staged[:, u, :], kindex[:, bass.ds(i * (2 * BATCH) + u * BATCH, BATCH)],
                                   ACT.Copy).then_inc(index_staged, 1)

                def keep(i):
                    for v in range(per_body):
                        act.wait_ge(s_full, i * per_body + (v + 1))
                        act.sem_inc(go, 1)
                        act.activation(kept[:, bass.ds(i * per_body + v, 1), :], s_ps[0:R, 0:P], ACT.Copy
                                       ).then_inc(s_out, 1)

                last = BATCHES // 2 - 1
                stage(0, 0)
                stage(0, 1)
                with act.Fori(0, last) as i:
                    stage(i + 1, 0)
                    stage(i + 1, 1)
                    keep(i)
                keep(last)

            @block.gpsimd
            def _(pool):
                with pool.Fori(0, BATCHES // 2) as i:
                    for u in range(2):
                        b = i * 2 + u
                        pool.wait_ge(index_staged, b + 1)
                        pool.wait_ge(reduced, b + 1)
                        pool.sem_inc(gathering, 1)
                        for j in range(BATCH):
                            pool.indirect_dma_start(
                                out=rows[:, u, j, :], out_offset=None, in_=ktable,
                                in_offset=bass.IndirectOffsetOnAxis(ap=staged[:, u, j:j + 1], axis=0)
                            ).then_inc(rows_in[u], 16)

            @block.tensor
            def _(pe):
                pe.sem_inc(q_full, 2 * NP2)
                with pe.Fori(0, BATCHES // 2) as i:
                    for u in range(2):
                        b = i * 2 + u
                        pe.wait_ge(spread_full, b + 3)
                        pe.wait_ge(window_in[u], (i + 1) * (16 * BATCH))
                        for p, (j0, n) in enumerate(PAIRS):
                            pe.wait_ge(q_out, b * NP2 + (p + 1))
                            for j in range(j0, j0 + n):
                                ins = pe.matmul(q_ps[p][:, j - j0, :], spread[:, u, j, :], window[:, u, j, :],
                                                start=True, stop=True)
                            ins.then_inc(q_full, 1)
                    for v in range(per_body):
                        pe.wait_ge(reduced, i * 2 + (2 + (v + 1) * 2 // per_body))
                        pe.wait_ge(s_out, i * per_body + (v + 1))
                        pe.transpose(s_ps[0:R, 0:P], sc[:, v, :, :].rearrange("p h c -> p (h c)"), k.ident[:, :]
                                     ).then_inc(s_full, 1)

            @block.vector
            def _(dve):
                dve.sem_inc(q_out, NP2)
                dve.sem_inc(reduced, 2)
                dve.sem_inc(spread_full, 2)

                def spread_out(i, u):
                    b = i * 2 + u
                    dve.wait_ge(rel_in[u], (i + 1) * 16)
                    dve.wait_ge(q_full, (b + 1) * NP2)
                    dve.tensor_scalar(spread[:, u, :, :].rearrange("p j e -> p (j e)"), rel[:, u, :], k.lane_col[:, 0:1],
                                      None, ALU.is_equal).then_inc(spread_full, 1)

                def score(i, u):
                    b = i * 2 + u
                    dve.wait_ge(rows_in[u], (i + 1) * (16 * BATCH))
                    dve.wait_ge(reduced, b + 2)
                    for p, (j0, n) in enumerate(PAIRS):
                        dve.wait_ge(q_full, b * NP2 + (2 * NP2 + p + 1))
                        dve.tensor_tensor(prod[:, j0:j0 + n, :], q_ps[p][:, 0:n, :], rows[:, u, j0:j0 + n, :],
                                          ALU.mult).then_inc(q_out, 1)
                    dve.wait_ge(q_out, (b + 2) * NP2)
                    dve.wait_ge(s_full, i * per_body)
                    v, j0 = (u, 0) if per_body == 2 else (0, u * BATCH)
                    dve.tensor_reduce(sc[:, v, :, j0:j0 + BATCH].rearrange("p h j -> p j h"),
                                      prod[:, :, :].rearrange("p j (h d) -> p j h d", h=heads), AX.X, ALU.add
                                      ).then_inc(reduced, 1)

                last = BATCHES // 2 - 1
                spread_out(0, 0)
                with dve.Fori(0, last) as i:
                    spread_out(i, 1)
                    score(i, 0)
                    spread_out(i + 1, 0)
                    score(i, 1)
                spread_out(last, 1)
                score(last, 0)
                score(last, 1)


def segment_softmax(k, scores, heads, alphas, scale=1.0, bias=None, more_loops=False):
    nc = k.nc
    H, N = heads, CHUNKS
    with k.phase() as ph:
        sc, run, seg = ph.sb("sc", [P, H, N]), ph.sb("run", [P, N]), ph.sb("seg", [P, H, N])
        dst = ph.sb("dst_rows_f", [P, N])
        dst_i = ph.sb("dst_rows", [P, N], I32)
        same, pen = ph.sb("same", [P, N + 1]), ph.sb("pen", [P, N + 1])
        ends = [ph.sb(f"end_{n}", [P, N]) for n in ("first", "last")]
        end_pens = [ph.sb(f"end_pen_{n}", [P, N]) for n in ("first", "last")]
        edge_vals = ph.sb("edge_vals", [P, 4, H])
        rowed = ph.sb("rowed", [H, 4, P])
        cont, whole = ph.sb("cont", [H, P + 1]), ph.sb("whole", [H, P])
        link, link_pen = ph.sb("link", [H, 2, P]), ph.sb("link_pen", [H, 2, P])
        cont_pen = ph.sb("cont_pen", [H, P + 1])
        carried = ph.sb("carried", [H, 2, P + 1])
        carry_in = ph.sb("carry_in", [H, 2, P])
        carry = ph.sb("carry", [P, 2, H])
        ends_ps = ph.ps("ends_ps", [P, 4, P])
        carry_ps = ph.ps("carry_ps", [P, 512])
        loaded, chained, at_pe, from_pe = (ph.sem(n) for n in ("loaded", "chained", "at_pe", "from_pe"))
        exp_in, exp_out, stored = ph.sem("exp_in"), ph.sem("exp_out"), ph.sem("stored")
        rows = "h (p i) -> p h i"
        loads = 2 + (bias is not None) + more_loops
        if more_loops:
            src_i, loops = ph.sb("src_rows", [P, N], I32), ph.sb("loops", [P, H, N])
        with nc.Block() as block:

            @block.sync
            def _(sp):
                sp.dma_start(dst_i[:, :], k.a["dst_rows"]).then_inc(loaded, 16)
                sp.dma_start(sc[:, :, :], scores.rearrange(rows, p=P)).then_inc(loaded, 16)
                if bias is not None:
                    sp.dma_start(seg[:, :, :], bias.rearrange(rows, p=P)).then_inc(loaded, 16)
                if more_loops:
                    sp.dma_start(src_i[:, :], k.a["src_row"].rearrange("o (p i) -> (o p) i", p=P)).then_inc(loaded, 16)
                sp.wait_ge(exp_out, 2)
                sp.dma_start(alphas.rearrange(rows, p=P), sc[:, :, :]).then_inc(stored, 16)
                sp.wait_ge(stored, 16)

            @block.scalar
            def _(act):
                act.wait_ge(exp_in, 1)
                act.activation(sc[:, :, :], sc[:, :, :], ACT.Exp).then_inc(exp_out, 1)

            @block.tensor
            def _(pe):
                for n in range(3 if more_loops else 2):
                    pe.wait_ge(at_pe, 2 * n + 1)
                    for q in range(4):
                        ins = pe.transpose(ends_ps[0:H, q, :], edge_vals[:, q, :], k.ident[:, :])
                    ins.then_inc(from_pe, 1)
                    pe.wait_ge(at_pe, 2 * n + 2)
                    for q in range(2):
                        ins = pe.transpose(carry_ps[:, q * H:(q + 1) * H], carry_in[:, q, :], k.ident[0:H, 0:H])
                    ins.then_inc(from_pe, 1)

            @block.vector
            def _(dve):
                step = Chain(dve, chained)
                dve.wait_ge(loaded, 16 * loads)
                step(dve.tensor_copy(dst[:, :], dst_i[:, :]))
                dve.memset(same[:, 0:1], 0.0)
                dve.memset(same[:, N:N + 1], 0.0)
                step(dve.tensor_tensor(same[:, 1:N], dst[:, 1:N], dst[:, 0:N - 1], ALU.is_equal))
                step(dve.tensor_scalar(pen[:, :], same[:, :], 1.0, BIG, ALU.subtract, ALU.mult))
                for n, at in enumerate((0, N - 1)):
                    step(dve.tensor_scalar(ends[n][:, :], dst[:, :], dst[:, at:at + 1], None, ALU.is_equal))
                    step(dve.tensor_scalar(end_pens[n][:, :], ends[n][:, :], 1.0, BIG, ALU.subtract, ALU.mult))
                    step(dve.tensor_copy(edge_vals[:, 2 + n, :], dst[:, at:at + 1].to_broadcast([P, H])))
                if scale != 1.0:
                    step(dve.tensor_scalar(sc[:, :, :], sc[:, :, :], scale, None, ALU.mult))
                if bias is not None:
                    step(dve.tensor_tensor(sc[:, :, :], sc[:, :, :], seg[:, :, :], ALU.add))

                def combine(n, maximum, values):
                    masks = pen if maximum else same
                    join, op = (ALU.add, ALU.max) if maximum else (ALU.mult, ALU.add)
                    for h in range(H):
                        step(dve.tensor_tensor_scan(run[:, :], masks[:, 0:N], values[:, h, :], -BIG if maximum else 0.0,
                                                    join, op))
                        step(dve.tensor_tensor_scan(seg[:, h, ::-1], masks[:, N:0:-1], run[:, ::-1],
                                                    -BIG if maximum else 0.0, join, ALU.max))
                    step(dve.tensor_copy(edge_vals[:, 0, :], seg[:, :, 0]))
                    dve.tensor_copy(edge_vals[:, 1, :], seg[:, :, N - 1]).then_inc(at_pe, 1)
                    dve.wait_ge(from_pe, 2 * n + 1)
                    step(dve.tensor_copy(rowed[:, :, :], ends_ps[0:H, :, :]))
                    firsts, lasts, dst_first, dst_last = (rowed[:, q, :] for q in range(4))
                    if n == 0:
                        dve.memset(cont[:, 0:1], 0.0)
                        dve.memset(cont[:, P:P + 1], 0.0)
                        step(dve.tensor_tensor(cont[:, 1:P], dst_first[:, 1:P], dst_last[:, 0:P - 1], ALU.is_equal))
                        step(dve.tensor_tensor(whole[:, :], dst_first, dst_last, ALU.is_equal))
                        step(dve.tensor_tensor(link[:, 0, :], whole[:, :], cont[:, 0:P], ALU.mult))
                        step(dve.tensor_tensor(link[:, 1, :], whole[:, :], cont[:, 1:P + 1], ALU.mult))
                        step(dve.tensor_scalar(link_pen[:, :, :], link[:, :, :], 1.0, BIG, ALU.subtract, ALU.mult))
                        step(dve.tensor_scalar(cont_pen[:, :], cont[:, :], 1.0, BIG, ALU.subtract, ALU.mult))
                    links = link_pen if maximum else link
                    none = -BIG if maximum else 0.0
                    step(dve.memset(carried[:, :, :], none))
                    step(dve.tensor_tensor_scan(carried[:, 0, 1:P + 1], links[:, 0, :], lasts, none, join, op))
                    step(dve.tensor_tensor_scan(carried[:, 1, P - 1::-1], links[:, 1, ::-1], firsts[:, ::-1], none,
                                                join, op))
                    c = cont_pen if maximum else cont
                    step(dve.tensor_tensor(carry_in[:, 0, :], carried[:, 0, 0:P], c[:, 0:P], join))
                    dve.tensor_tensor(carry_in[:, 1, :], carried[:, 1, 1:P + 1], c[:, 1:P + 1], join).then_inc(at_pe, 1)
                    dve.wait_ge(from_pe, 2 * n + 2)
                    step(dve.tensor_copy(carry[:, :, :], carry_ps[:, 0:2 * H].rearrange("p (q h) -> p q h", q=2)))
                    masks = end_pens if maximum else ends
                    for h in range(H):
                        for q in range(2):
                            step(dve.scalar_tensor_tensor(seg[:, h, :], masks[q][:, :], carry[:, q, h:h + 1],
                                                          seg[:, h, :], join, op))

                combine(0, True, sc)
                step(dve.tensor_tensor(sc[:, :, :], sc[:, :, :], seg[:, :, :], ALU.subtract))
                dve.sem_inc(exp_in, 1)
                if more_loops:
                    step(dve.tensor_copy(loops[:, 0, :], src_i[:, :]))
                    step(dve.tensor_tensor(loops[:, 0, :], loops[:, 0, :], dst[:, :], ALU.is_equal))
                    combine(1, False, loops)
                    step(dve.tensor_scalar(seg[:, :, :], seg[:, :, :], 1.0, None, ALU.max))
                    step(dve.reciprocal(seg[:, :, :], seg[:, :, :]))
                    step(dve.tensor_tensor(loops[:, :, :], loops[:, :, :], seg[:, :, :], ALU.mult))
                    step(dve.tensor_scalar(loops[:, :, :], loops[:, :, :], 1.0, None, ALU.add))
                dve.wait_ge(exp_out, 1)
                if more_loops:
                    step(dve.tensor_tensor(sc[:, :, :], sc[:, :, :], loops[:, :, :], ALU.mult))
                combine(2 if more_loops else 1, False, sc)
                step(dve.reciprocal(seg[:, :, :], seg[:, :, :]))
                dve.tensor_tensor(sc[:, :, :], sc[:, :, :], seg[:, :, :], ALU.mult).then_inc(exp_out, 1)


def load_alphas(k, alphas, heads, ci, out):
    nc = k.nc
    R, G = heads * ci, CHUNKS // ci
    quads = [(g, min(4, G - g)) for g in range(0, G, 4)]
    with k.phase() as ph:
        kept = ph.sb("kept", [R, G, P])
        ps = [ph.ps(f"turned{q}", [P, 4, P]) for q in range(2)]
        loaded, full, emptied = ph.sem("loaded"), ph.sem("full"), ph.sem("emptied")
        with nc.Block() as block:

            @block.sync
            def _(sp):
                for h in range(heads):
                    sp.dma_start(kept[h * ci:(h + 1) * ci, :, :], edge_order(alphas[h:h + 1, :], G, ci)
                                 ).then_inc(loaded, 16)

            @block.tensor
            def _(pe):
                pe.wait_ge(loaded, 16 * heads)
                for q, (g0, n) in enumerate(quads):
                    if q >= 2:
                        pe.wait_ge(emptied, q - 1)
                    for g in range(g0, g0 + n):
                        ins = pe.transpose(ps[q % 2][:, g - g0, 0:R], kept[:, g, :], k.ident[0:R, 0:R])
                    ins.then_inc(full, 1)

            @block.scalar
            def _(act):
                for q, (g0, n) in enumerate(quads):
                    act.wait_ge(full, q + 1)
                    act.activation(out[:, g0:g0 + n, :], ps[q % 2][:, 0:n, 0:R], ACT.Copy).then_inc(emptied, 1)


def project_sums(k, ph, accT, count, load, rhs, update, links):
    nc = k.nc
    ring = ph.sb("sum_ring", [P, UNROLL, KK, P])
    ps = [ph.ps(f"product{i}", [P, 512]) for i in range(4)]
    loaded, ring_full, full, emptied, chained = (ph.sem(n) for n in ("loaded", "ring_full", "full", "emptied", "chained"))
    bodies = TILES // UNROLL
    count_in = []
    with nc.Block() as block:

        @block.sync
        def _(sp):
            count_in.append(load(sp, loaded))

        @block.scalar
        def _(act):
            go = ph.sem("go")
            with act.Fori(0, bodies) as i:
                act.wait_ge(full, i * (UNROLL * count))
                act.sem_inc(go, 1)
                for u in range(UNROLL):
                    act.activation(ring[:, u, :, :], accT[:, :, bass.ds((i * UNROLL + u) * P, P)], ACT.Copy
                                   ).then_inc(ring_full, 1)

        @block.tensor
        def _(pe):
            pe.wait_ge(loaded, count_in[0])
            with pe.Fori(0, bodies) as i:
                for u in range(UNROLL):
                    t = i * UNROLL + u
                    pe.wait_ge(ring_full, t + 1)
                    for y in range(count):
                        m = u * count + y
                        pe.wait_ge(emptied, t * count + y)
                        for kk in range(KK):
                            ins = pe.matmul(ps[m % 4 if count == 4 else m % 3][:, 0:D], ring[:, u, kk, :],
                                            rhs[:, y, kk, :], start=kk == 0, stop=kk == KK - 1)
                        ins.then_inc(full, 1)

        @block.vector
        def _(dve):
            dve.sem_inc(emptied, 3 if count == 4 else 1)
            dve.wait_ge(loaded, count_in[0])
            step = Chain(dve, chained)
            with dve.Fori(0, bodies) as i:
                for u in range(UNROLL):
                    t = i * UNROLL + u
                    step.base, step.n = t * links, 0

                    def product(y):
                        m = u * count + y
                        dve.wait_ge(full, t * count + (y + 1))
                        return ps[m % 4 if count == 4 else m % 3][:, 0:D]

                    update(dve, t, product, step, emptied)
                    assert step.n == links


TYPES, RELS, L1_HEADS = 4, 8, 4


def typed_tables(k, xn, kinds, qtab, ktab, vtab):
    nc, a = k.nc, k.a
    HD = D // L1_HEADS
    R4 = RELS // 2
    PAIR = 2 * P
    TURNS = (TILES + 1) // 2
    with k.phase() as ph:
        weights = ph.sb("typed_w", [P, 3, TYPES, KK, D])
        blocks = ph.sb("relation_blocks", [P, 2, KK, RELS, P])
        pri = ph.sb("pri", [P, KK, RELS])
        zeros, cleared = ph.sb("zeros", [P, 8 * D]), ph.sem("cleared")
        ring = ph.sb("tile_ring", [P, 2, D])
        diag = ph.sb("diag", [P, 2, TYPES, P])
        masked = ph.sb("masked", [P, KK, TYPES, PAIR])
        kvT = ph.sb("kvT", [P, 2, KK, PAIR])
        stage = ph.sb("stage", [P, 2, 2, RELS, D])
        q_stage = ph.sb("q_stage", [P, 2, D])
        m_ps = [ph.ps(f"masked{kk}", [P, TYPES, P]) for kk in range(KK)]
        kv_ps, q_ps = ph.ps("kv", [P, 2, KK, PAIR]), ph.ps("q", [P, 2, D])
        r_ps = [ph.ps(f"related{i}", [P, R4, P]) for i in range(3)]
        loaded, zeroed, blocked = ph.sem("loaded"), ph.sem("zeroed"), ph.sem("blocked")
        ring_full, diag_full, m_full, m_out = (ph.sem(n) for n in ("ring_full", "diag_full", "m_full", "m_out"))
        kv_full, kv_out, q_full, q_out = (ph.sem(n) for n in ("kv_full", "kv_out", "q_full", "q_out"))
        r_full, outs, ready = ph.sem("r_full"), [ph.sem("k_out"), ph.sem("v_out")], ph.sem("ready")
        stored, q_stored = [ph.sem(f"stored{h}") for h in range(2)], ph.sem("q_stored")
        M, J = 2 * KK, 8

        def pairs(eng, body):
            with eng.Fori(0, TURNS - 1) as i:
                body(i, True)
            body(TURNS - 1, False)

        def job(j):
            return j // J, j % 2, j // 2 % 2, slice(j // 4 % 2 * R4, (j // 4 % 2 + 1) * R4)

        with nc.Block() as block:

            @block.sync
            def _(sp):
                sp.dma_start(weights[:, :, :, :, :], a["L1_gnn_w"]).then_inc(loaded, 16)
                sp.dma_start(pri[:, :, :], a["L1_gnn_pri"]).then_inc(loaded, 16)
                sp.wait_ge(zeroed, 1)
                for n, name in enumerate(("L1_gnn_att", "L1_gnn_msg")):
                    for h in range(2):
                        at = slice(h * HD, (h + 1) * HD)
                        for o in range(KK):
                            sp.dma_start(blocks[at, n, o, :, at], a[name][at, o, :, :]).then_inc(blocked, 16)

                def store(t, more):
                    sp.wait_ge(q_out, t + 1)
                    sp.dma_start(qtab[bass.ds(t * PAIR, PAIR), :].rearrange("(h p) d -> p h d", p=P), q_stage[:, :, :]
                                 ).then_inc(q_stored, 16)
                    for h in range(2):
                        for n, tab in enumerate((ktab, vtab)):
                            sp.wait_ge(outs[n], t * J + (h + 1) * (J // 2))
                            sp.dma_start(tab.rearrange("(r n) d -> n r d", r=RELS)[bass.ds(t * PAIR + h * P, P), :, :],
                                         stage[:, h, n, :, :]).then_inc(stored[h], 16)
                pairs(sp, store)
                sp.wait_ge(q_stored, 16 * TURNS)
                for h in range(2):
                    sp.wait_ge(stored[h], 32 * TURNS)

            @block.gpsimd
            def _(pool):
                pool.memset(blocks[:, :, :, :, :], 0.0).then_inc(zeroed, 1)
                pool.memset(xn[:, TILES, :], 0.0).then_inc(zeroed, 1)
                pool.memset(zeros[:, :], 0.0).then_inc(zeroed, 1)
                pool.wait_ge(zeroed, 3)
                clear_rows(pool, k.slot_rows, zeros, cleared)

            @block.scalar
            def _(act):
                def fetch(t):
                    act.activation(ring[:, :, :], xn[:, bass.ds(t * 2, 2), :], ACT.Copy).then_inc(ring_full, 1)

                def empty(t):
                    for m in range(M):
                        h, kk = m // KK, m % KK
                        act.wait_ge(m_full, t * M + (m + 1))
                        act.activation(masked[:, kk, :, h * P:(h + 1) * P], m_ps[kk][:, :, :], ACT.Copy).then_inc(m_out, 1)

                def pair(t, more):
                    if more:
                        act.wait_ge(m_full, t * M + M)
                        act.sem_inc(ready, 1)
                        fetch(t + 1)
                    act.wait_ge(kv_full, t + 1)
                    act.activation(kvT[:, :, :, :], kv_ps[:, :, :, :], ACT.Copy).then_inc(kv_out, 1)
                    act.wait_ge(q_full, t + 1)
                    if more:
                        empty(t + 1)
                    for j in range(0, 2 * J, 2):
                        h, _, o, rels = job(j)
                        if j % J == 0:
                            act.wait_ge(stored[h], t * 32)
                        act.wait_ge(r_full, t * (2 * J) + (j + 1))
                        act.activation(stage[:, h, 0, rels, o * P:(o + 1) * P], r_ps[j % 3][:, :, :], ACT.Copy
                                       ).then_inc(outs[0], 1)

                act.wait_ge(zeroed, 2)
                fetch(0)
                empty(0)
                pairs(act, pair)

            @block.vector
            def _(dve):
                dve.wait_ge(loaded, 32)
                dve.wait_ge(blocked, 16 * 8)
                p4 = pri[:, :, :].unsqueeze(3).to_broadcast([P, KK, RELS, P])
                for o in range(KK):
                    dve.scalar_tensor_tensor(blocks[:, 0, o, :, :], blocks[:, 0, o, :, :], 1.0 / HD ** 0.5,
                                             p4[:, o, :, :], ALU.mult, ALU.mult).then_inc(blocked, 1)

                def mask(t):
                    shape = [P, 2 * TYPES, P]
                    types = kinds[:, bass.ds(t * 2, 2), :].rearrange("p h y -> p (h y)").unsqueeze(2)
                    dve.tensor_tensor(diag[:, :, :, :].rearrange("p h y l -> p (h y) l"),
                                      k.ident[:, :].unsqueeze(1).to_broadcast(shape), types.to_broadcast(shape), ALU.mult
                                      ).then_inc(diag_full, 1)

                def pair(t, more):
                    if more:
                        dve.wait_ge(m_full, t * M + M)
                        mask(t + 1)
                    dve.wait_ge(q_full, t + 1)
                    dve.wait_ge(q_stored, t * 16)
                    dve.tensor_copy(q_stage[:, :, :], q_ps[:, :, :]).then_inc(q_out, 1)
                    for j in range(1, 2 * J, 2):
                        h, _, o, rels = job(j)
                        if j % J == 1:
                            dve.wait_ge(stored[h], t * 32)
                        dve.wait_ge(r_full, t * (2 * J) + (j + 1))
                        dve.tensor_copy(stage[:, h, 1, rels, o * P:(o + 1) * P], r_ps[j % 3][:, :, :]
                                        ).then_inc(outs[1], 1)

                mask(0)
                pairs(dve, pair)

            @block.tensor
            def _(pe):
                def turn_masked(t):
                    pe.wait_ge(ring_full, t + 1)
                    pe.wait_ge(diag_full, t + 1)
                    for m in range(M):
                        h, kk = m // KK, m % KK
                        pe.wait_ge(m_out, t * M + max(0, m - 1))
                        pe.matmul(m_ps[kk][:, :, :], ring[:, h, kk * P:(kk + 1) * P], diag[:, h, :, :],
                                  start=True, stop=True).then_inc(m_full, 1)

                def pair(t, more):
                    pe.wait_ge(m_out, t * M + M)
                    pe.wait_ge(kv_out, t)
                    for n in range(2):
                        for o in range(KK):
                            for kk in range(KK):
                                for y in range(TYPES):
                                    ins = pe.matmul(kv_ps[:, n, o, :], weights[:, n, y, kk, o * P:(o + 1) * P],
                                                    masked[:, kk, y, :], start=kk == 0 and y == 0,
                                                    stop=kk == KK - 1 and y == TYPES - 1)
                    ins.then_inc(kv_full, 1)
                    pe.wait_ge(q_out, t)
                    for h in range(2):
                        for kk in range(KK):
                            for y in range(TYPES):
                                ins = pe.matmul(q_ps[:, h, :], masked[:, kk, y, h * P:(h + 1) * P], weights[:, 2, y, kk, :],
                                                start=kk == 0 and y == 0, stop=kk == KK - 1 and y == TYPES - 1)
                    ins.then_inc(q_full, 1)
                    if more:
                        turn_masked(t + 1)
                    pe.wait_ge(kv_out, t + 1)
                    for n in range(2):
                        pe.wait_ge(outs[n], t * J)
                    for j in range(2 * J):
                        h, n, o, rels = job(j)
                        if j >= 3:
                            pe.wait_ge(outs[(j - 3) % 2], t * J + ((j - 3) // 2 + 1))
                        pe.matmul(r_ps[j % 3][:, :, :], kvT[:, n, o, h * P:(h + 1) * P], blocks[:, n, o, rels, :],
                                  start=True, stop=True).then_inc(r_full, 1)

                pe.wait_ge(loaded, 32)
                pe.wait_ge(blocked, 16 * 8 + 2)
                turn_masked(0)
                pairs(pe, pair)


def layer1_gnn(k):
    nc, a = k.nc, k.a
    H, CI = L1_HEADS, 2 * BATCH

    def dram(name, shape):
        return nc.dram_tensor(name, shape, F32, kind="Internal").ap()

    ktab, vtab, qtab = dram("l1_k", [RELS * NWIN, D]), dram("l1_v", [RELS * NWIN, D]), dram("l1_q", [NWIN, D])
    scores, alphas = dram("l1_scores", [H, EPAD]), dram("l1_alpha", [H, EPAD])
    with k.phase() as ph:
        index = ph.sb("row_index", [P, CHUNKS], I32)
        kinds = ph.sb("kinds", [P, TILES + 1, TYPES])
        gains = ph.sb("gains", [P, TILES, TYPES])
        with k.phase() as inner:
            etype, types = inner.sb("etype", [P, CHUNKS], I32), inner.sb("types", [P, TILES], I32)
            etype_f, src_f = inner.sb("etype_f", [P, CHUNKS]), inner.sb("src_f", [P, CHUNKS])
            types_f, skip = inner.sb("types_f", [P, TILES]), inner.sb("skip", [P, TYPES])
            loaded, chained, squashed = inner.sem("loaded"), inner.sem("chained"), inner.sem("squashed")
            with nc.Block() as block:

                @block.sync
                def _(sp):
                    for dst, src in ((etype, a["etype_lanes"]), (types, a["type_lanes"])):
                        sp.dma_start(dst[:, :], src).then_inc(loaded, 16)
                    sp.dma_start(skip[:, :], a["L1_gnn_skip"].to_broadcast([P, TYPES])).then_inc(loaded, 16)

                @block.scalar
                def _(act):
                    act.wait_ge(loaded, 48)
                    act.activation(skip[:, :], skip[:, :], ACT.Sigmoid).then_inc(squashed, 1)

                @block.vector
                def _(dve):
                    step = Chain(dve, chained)
                    dve.wait_ge(loaded, 48)
                    dve.tensor_copy(types_f[:, :], types[:, :])
                    dve.tensor_copy(etype_f[:, :], etype[:, :])
                    step(dve.tensor_copy(src_f[:, :], k.src[:, :]))
                    dve.scalar_tensor_tensor(index[:, :], etype_f[:, :], float(NWIN), src_f[:, :], ALU.mult, ALU.add)
                    dve.memset(kinds[:, TILES, :], 0.0)
                    for y in range(TYPES):
                        ins = dve.tensor_scalar(kinds[:, 0:TILES, y], types_f[:, :], float(y), None, ALU.is_equal)
                    step(ins)
                    dve.wait_ge(squashed, 1)
                    step(dve.tensor_tensor(gains[:, :, :], kinds[:, 0:TILES, :],
                                           skip[:, :].unsqueeze(1).to_broadcast([P, TILES, TYPES]), ALU.mult))
        with k.phase() as inner:
            xn = inner.sb("xn", [P, TILES + 1, D])
            normalize(k, k.x, xn)
            typed_tables(k, xn, kinds, qtab, ktab, vtab)
        attention_scores(k, ktab, index, qtab, H, scores)
        segment_softmax(k, scores, H, alphas)
        accT = ph.sb("accT", [P, KK, NWIN])
        with k.phase() as inner:
            alpha = inner.sb("alpha", [P, CHUNKS // CI, H * CI])
            load_alphas(k, alphas, H, CI, alpha)
            aggregate(k, vtab, index, accT, heads=H,
                      alpha=lambda i, u: alpha[:, bass.ds(i, 1), :].rearrange("p o (h c) -> p (o h) c", h=H)
                      [:, :, u * BATCH:(u + 1) * BATCH])
        wa = ph.sb("wa", [P, TYPES, KK, D])

        def load(sp, sem):
            sp.dma_start(wa[:, :, :, :], a["L1_gnn_wa"]).then_inc(sem, 16)
            return 16

        def update(dve, t, product, step, emptied):
            xt = k.x[:, bass.ds(t, 1), :]
            for y in range(TYPES):
                dve.wait_ge(emptied, t * TYPES + (y + 3))
                gain = gains[:, bass.ds(t, 1), y]
                dve.scalar_tensor_tensor(xt, product(y), gain, xt, ALU.mult, ALU.add).then_inc(emptied, 1)

        with k.phase() as inner:
            project_sums(k, inner, accT, TYPES, load, wa, update, 0)


def layer2_gnn(k):
    nc, a = k.nc, k.a
    H, CI = 8, BATCH

    def dram(name, shape):
        return nc.dram_tensor(name, shape, F32, kind="Internal").ap()

    ktab, vtab, qtab = dram("l2_k", [NPAD, D]), dram("l2_v", [NPAD, D]), k.l2_queries
    scores, alphas = dram("l2_scores", [H, EPAD]), dram("l2_alpha", [H, EPAD])
    with k.phase() as ph:
        xn = ph.sb("xn", [P, TILES, D])
        normalize(k, k.x, xn)
        w = ph.sb("kvq_w", [P, KK, 3 * D])

        def load(sp, sem):
            sp.dma_start(w[:, :, :], a["L2_gnn_kvq"]).then_inc(sem, 16)
            return 16

        def evacuate(dve, t, product, stage, step):
            return dve.tensor_copy(stage, product[:, :, :].rearrange("p b n -> p (b n)")[:, 0:3 * D])

        def store(sp, t, stage, sem):
            for n, tab in enumerate((ktab, vtab, qtab)):
                sp.dma_start(tab[bass.ds(t * P, P), :], stage[:, n * D:(n + 1) * D]).then_inc(sem, 16)

        with k.phase() as inner:
            node_tiles(k, inner, xn, 3 * D, load, w, evacuate, store, 3)
    attention_scores(k, ktab, k.src, qtab, H, scores)
    segment_softmax(k, scores, H, alphas, float(1.0 / np.sqrt(D // H)), k.edge_bias)
    with k.phase() as ph:
        accT = ph.sb("accT", [P, KK, NWIN])
        with k.phase() as inner:
            alpha = inner.sb("alpha", [P, CHUNKS // CI, H * CI])
            load_alphas(k, alphas, H, CI, alpha)
            aggregate(k, vtab, k.src, accT, heads=H,
                      alpha=lambda i, u: alpha[:, bass.ds(i * 2 + u, 1), :].rearrange("p o (h j) -> p (o h) j", h=H))
        wo, bo = ph.sb("wo", [P, 1, KK, D]), ph.sb("bo", [P, D])

        def load(sp, sem):
            sp.dma_start(wo[:, 0, :, :], a["L2_gnn_Wo"]).then_inc(sem, 16)
            sp.dma_start(bo[:, :], a["L2_gnn_bo"].to_broadcast([P, D])).then_inc(sem, 16)
            return 32

        def update(dve, t, product, step, emptied):
            xt = k.x[:, bass.ds(t, 1), :]
            step(dve.tensor_tensor(xt, xt, bo[:, :], ALU.add))
            dve.tensor_tensor(xt, product(0), xt, ALU.add).then_inc(emptied, 1)

        with k.phase() as inner:
            project_sums(k, inner, accT, 1, load, wo, update, 1)


def layer3_gnn(k):
    nc, a = k.nc, k.a

    def dram(name, shape):
        return nc.dram_tensor(name, shape, F32, kind="Internal").ap()

    htab = dram("l3_h", [NPAD, D])
    scores, alphas = dram("l3_scores", [1, EPAD]), dram("l3_alpha", [1, EPAD])
    with k.phase() as ph:
        score_parts = ph.sb("score_parts", [P, 2, TILES])
        xn = ph.sb("xn", [P, TILES, D])
        normalize(k, k.x, xn)
        wt, wo, att = ph.sb("w_t", [P, KK, D + 2]), ph.sb("w_o", [P, KK, D]), ph.sb("att", [P, KK, 2])
        load_small(k, [(wt[:, :, 0:D], a["L3_gnn_WT"]), (wo[:, :, :], a["L3_gnn_W"]), (att[:, :, :], a["L3_gnn_att"])])
        with k.phase() as inner:
            ps, folded, copied = inner.ps("folded", [P, 512]), inner.sem("folded"), inner.sem("copied")
            with nc.Block() as block:

                @block.tensor
                def _(pe):
                    for kk in range(KK):
                        for o in range(KK):
                            ins = pe.matmul(ps[:, 2 * kk:2 * kk + 2], wo[:, o, kk * P:(kk + 1) * P], att[:, o, :],
                                            start=o == 0, stop=o == KK - 1)
                    ins.then_inc(folded, 1)

                @block.vector
                def _(dve):
                    dve.wait_ge(folded, 1)
                    for kk in range(KK):
                        dve.tensor_copy(wt[:, kk, D:D + 2], ps[:, 2 * kk:2 * kk + 2])
                    dve.tensor_tensor(k.x[:, :, :], k.x[:, :, :], xn[:, :, :], ALU.add).then_inc(copied, 1)
                    dve.wait_ge(copied, 1)

        def load(sp, sem):
            return 0

        def evacuate(dve, t, product, stage, step):
            dve.tensor_copy(score_parts[:, :, bass.ds(t, 1)].rearrange("p n t -> p (n t)"), product[:, 0, D:D + 2])
            return dve.tensor_copy(stage, product[:, 0, 0:D])

        def store(sp, t, stage, sem):
            sp.dma_start(htab[bass.ds(t * P, P), :], stage).then_inc(sem, 16)

        with k.phase() as inner:
            node_tiles(k, inner, xn, D + 2, load, wt, evacuate, store, 1)
        gat_scores(k, score_parts, scores)
    segment_softmax(k, scores, 1, alphas, more_loops=True)
    with k.phase() as ph:
        accT = ph.sb("accT", [P, KK, NWIN])
        with k.phase() as inner:
            alpha = inner.sb("alpha", [P, CHUNKS // 62, 62])
            load_alphas(k, alphas, 1, 62, alpha)
            aggregate(k, htab, k.src, accT, weights=alpha[:, :, :].rearrange("p g c -> p (g c)"))
        bias = ph.sb("bias", [P, D])

        def load(sp, sem):
            sp.dma_start(bias[:, :], a["L3_gnn_bias"].to_broadcast([P, D])).then_inc(sem, 16)
            return 16

        def update(dve, t, tile, step):
            xt = k.x[:, bass.ds(t, 1), :]
            step(dve.tensor_tensor(tile, tile, bias[:, :], ALU.add))
            return dve.scalar_tensor_tensor(xt, tile, 0.0, xt, ALU.max, ALU.add)

        with k.phase() as inner:
            from_sums(k, inner, accT, load, update, links=1)


def gat_scores(k, nodes, scores):
    nc = k.nc
    with k.phase() as ph:
        lanes = ph.sb("lanes", [P, 2, 2, BATCH * P], BF16)
        hot_lane = ph.sb("hot_lane", [P, 2, 2, BATCH * P], BF16)
        hot_tile = ph.sb("hot_tile", [P, 2, 2, BATCH, TILES])
        parts, rest = ph.sb("parts", [P, 3, 2, TILES], BF16), ph.sb("rest", [P, 2, TILES])
        picked = ph.sb("picked", [P, 2, 2, BATCH])
        sc = ph.sb("sc", [P, CHUNKS])
        kept = ph.sb("kept", [62, BATCH, P])
        by_lane = [[ph.ps(f"by_lane{u}_{n}", [P, 512]) for n in range(2)] for u in range(2)]
        ps = [ph.ps(f"turned{q}", [P, 512]) for q in range(2)]
        split_up, lane_hot, by_lane_full, chained = (ph.sem(n) for n in ("split_up", "lane_hot", "by_lane_full", "chained"))
        scored, full, emptied, stored = (ph.sem(n) for n in ("scored", "full", "emptied", "stored"))
        lanes_in = [ph.sem(f"lanes_in{u}") for u in range(2)]
        with nc.Block() as block:

            @block.sync
            def _(sp):
                with sp.Fori(0, BATCHES // 2) as i:
                    for u in range(2):
                        c = i * (2 * BATCH) + u * BATCH
                        sp.wait_ge(lane_hot, i * 2 + (u + 1))
                        for n, table in enumerate((k.src_lane_row, k.dst_lane_row)):
                            sp.dma_start(lanes[:, u, n, :], table[:, bass.ds(c * P, BATCH * P)].to_broadcast([P, BATCH * P])
                                         ).then_inc(lanes_in[u], 16)
                sp.wait_ge(emptied, BATCH)
                sp.dma_start(edge_order(scores, BATCH, 62), kept[:, :, :]).then_inc(stored, 16)
                sp.wait_ge(stored, 16)

            @block.tensor
            def _(pe):
                pe.wait_ge(split_up, 1)
                with pe.Fori(0, BATCHES // 2) as i:
                    for u in range(2):
                        b = i * 2 + u
                        pe.wait_ge(lane_hot, b + 3)
                        pe.wait_ge(scored, b + 1)
                        for n in range(2):
                            for j in range(BATCH):
                                for m in range(3):
                                    ins = pe.matmul(by_lane[u][n][:, j * TILES:(j + 1) * TILES],
                                                    hot_lane[:, u, n, j * P:(j + 1) * P], parts[:, m, n, :],
                                                    start=m == 0, stop=m == 2)
                        ins.then_inc(by_lane_full, 1)
                pe.wait_ge(scored, 2 + BATCHES)
                for g in range(BATCH):
                    if g >= 2:
                        pe.wait_ge(emptied, g - 1)
                    pe.transpose(ps[g % 2][0:62, 0:P], sc[:, g * 62:(g + 1) * 62], k.ident[:, :]).then_inc(full, 1)

            @block.scalar
            def _(act):
                for g in range(BATCH):
                    act.wait_ge(full, g + 1)
                    act.activation(kept[:, g, :], ps[g % 2][0:62, 0:P], ACT.Copy).then_inc(emptied, 1)

            @block.vector
            def _(dve):
                step = Chain(dve, chained)
                links = 4
                dve.sem_inc(scored, 2)
                dve.sem_inc(lane_hot, 2)
                split(step, dve, nodes[:, :, :], rest[:, :, :], [parts[:, m, :, :] for m in range(3)])
                dve.sem_inc(split_up, 1)
                split_links = step.n

                def compare(i, u):
                    dve.wait_ge(lanes_in[u], i * 32 + 32)
                    dve.wait_ge(scored, i * 2 + (u + 1))
                    dve.tensor_scalar(hot_lane[:, u, :, :], lanes[:, u, :, :], k.lane_col[:, 0:1], None, ALU.is_equal
                                      ).then_inc(lane_hot, 1)

                def score(i, u):
                    b = i * 2 + u
                    c = i * (2 * BATCH) + u * BATCH
                    step.base, step.n = b * links + split_links, 0
                    hot_by(dve, k, hot_tile[:, u, 0, :, :], k.src_tile[:, bass.ds(c, BATCH)], TILES)
                    step(hot_by(dve, k, hot_tile[:, u, 1, :, :], k.dst_tile[:, bass.ds(c, BATCH)], TILES))
                    dve.wait_ge(by_lane_full, b + 1)
                    for n in range(2):
                        hot = hot_tile[:, u, n, :, :].rearrange("p j t -> p (j t)")
                        ins = dve.tensor_tensor(hot, hot, by_lane[u][n][:, 0:BATCH * TILES], ALU.mult)
                    step(ins)
                    step(dve.tensor_reduce(picked[:, u, :, :], hot_tile[:, u, :, :, :], AX.X, ALU.add))
                    step(dve.tensor_tensor(picked[:, u, 0, :], picked[:, u, 0, :], picked[:, u, 1, :], ALU.add))
                    dve.scalar_tensor_tensor(sc[:, bass.ds(c, BATCH)], picked[:, u, 0, :], 0.2, picked[:, u, 0, :],
                                             ALU.mult, ALU.max).then_inc(scored, 1)

                last = BATCHES // 2 - 1
                compare(0, 0)
                with dve.Fori(0, last) as i:
                    compare(i, 1)
                    score(i, 0)
                    compare(i + 1, 0)
                    score(i, 1)
                compare(last, 1)
                score(last, 0)
                score(last, 1)


SHARED0 = Experts(1, [D, 256, 128, D])
EXPERTS0 = Experts(4, [D, 128, 64, D])
EXPERTS3 = Experts(8, [D, 256, 256, D])


def layer0_ffn(k):
    a = k.a
    with k.phase() as ph:
        xT, gates, logits = ph.sb("xT", [P, KK, NPAD]), ph.sb("gates", [P, TILES, 4]), ph.sb("logits", [P, TILES, 4])
        with k.phase() as inner:
            xn = inner.sb("xn", [P, TILES, D])
            normalize(k, k.x, xn)
            routed(k, xn, xT, a["L0_ffn_gW"], 4, logits)
        gate_weights(k, logits, gates, 4, "top2_of_softmax", a["L0_ffn_gb"])
        bs, be = ph.sb("shared_bias", [P, 1, len(SHARED0.chunks)]), ph.sb("expert_bias", [P, 4, len(EXPERTS0.chunks)])
        load_small(k, [(bs[:, :, :], a["L0_ffn_sb"]), (be[:, :, :], a["L0_ffn_eb"])])
        mixture(k, xT, SHARED0, a["L0_ffn_sW"], a["L0_ffn_sb3"], ACT.Relu, bs)
        mixture(k, xT, EXPERTS0, a["L0_ffn_eW"], a["L0_ffn_eb3"], ACT.Relu, be, gates=gates)


def layer1_ffn(k):
    a, E = k.a, 8
    with k.phase() as ph:
        xn, gates, chosen, logits = (ph.sb("xn", [P, TILES, D]), ph.sb("gates", [P, TILES, E]),
                                     ph.sb("chosen", [P, TILES, E]), ph.sb("logits", [P, TILES, E]))
        normalize(k, k.x, xn)
        normalize(k, xn, xn, gamma=a["L1_ffn_gamma"], beta=a["L1_ffn_beta"])
        routed(k, xn, None, a["L1_ffn_Wr"], E, logits)
        gate_weights(k, logits, gates, E, "top2", a["L1_ffn_br"], chosen)
        sparse_mixture(k, xn, chosen, gates, E, 512, (a["L1_ffn_first"], a["L1_ffn_second"]), a["L1_ffn_b2"], False)


def layer2_ffn(k):
    a, E = k.a, 8
    with k.phase() as ph:
        xn, gates, chosen, logits = (ph.sb("xn", [P, TILES, D]), ph.sb("gates", [P, TILES, E]),
                                     ph.sb("chosen", [P, TILES, E]), ph.sb("logits", [P, TILES, E]))
        normalize(k, k.x, xn)
        routed(k, xn, None, a["L2_ffn_Wr"], E, logits)
        normalize(k, xn, xn)
        gate_weights(k, logits, gates, E, "top2_renormalized", a["L2_ffn_br"], chosen)
        sparse_mixture(k, xn, chosen, gates, E, 1024, (a["L2_ffn_first"], a["L2_ffn_second"]), a["L2_ffn_b2"], True)


def layer3_ffn(k):
    nc, a = k.nc, k.a
    E, C = 8, len(EXPERTS3.chunks)
    with k.phase() as ph:
        xT, gates, logits = ph.sb("xT", [P, KK, NPAD]), ph.sb("gates", [P, TILES, E]), ph.sb("logits", [P, TILES, E])
        with k.phase() as inner:
            xn = inner.sb("xn", [P, TILES, D])
            normalize(k, k.x, xn)
            routed(k, xn, xT, a["L3_ffn_Wr"], E, logits)
        gate_weights(k, logits, gates, E, "softmax", a["L3_ffn_br"])
        b, g, be, m, v = (ph.sb(n, [P, E, C]) for n in ("b", "g", "be", "m", "v"))
        load_small(k, [(t[:, :, :], a[f"L3_ffn_{n}"]) for t, n in ((b, "b"), (g, "g"), (be, "be"), (m, "m"), (v, "v"))])
        with k.phase() as inner:
            chained, rooted = inner.sem("chained"), inner.sem("rooted")
            with nc.Block() as block:

                @block.vector
                def _(dve):
                    step = Chain(dve, chained)
                    dve.tensor_scalar(v[:, :, :], v[:, :, :], 1e-3, None, ALU.add).then_inc(rooted, 1)
                    dve.wait_ge(rooted, 2)
                    step(dve.reciprocal(v[:, :, :], v[:, :, :]))
                    step(dve.tensor_tensor(g[:, :, :], g[:, :, :], v[:, :, :], ALU.mult))
                    step(dve.tensor_tensor(b[:, :, :], b[:, :, :], m[:, :, :], ALU.subtract))
                    step(dve.tensor_tensor(b[:, :, :], b[:, :, :], g[:, :, :], ALU.mult))
                    step(dve.tensor_tensor(b[:, :, :], b[:, :, :], be[:, :, :], ALU.add))

                @block.scalar
                def _(act):
                    act.wait_ge(rooted, 1)
                    act.activation(v[:, :, :], v[:, :, :], ACT.Sqrt).then_inc(rooted, 1)
        mixture(k, xT, EXPERTS3, a["L3_ffn_W"], a["L3_ffn_bo"], ACT.Relu, b, scale=g, gates=gates)


LAYERS = [layer0_gnn, layer0_ffn, layer1_gnn, layer1_ffn, layer2_gnn, layer2_ffn, layer3_gnn, layer3_ffn]


def program(nc, a, out, upto=99):
    k = Kernel(nc, a)
    setup(k)
    for layer in LAYERS[:upto]:
        layer(k)
    with k.phase() as ph:
        stored = ph.sem("stored")
        with nc.Block() as block:

            @block.sync
            def _(sp):
                full = NODES // P
                sp.dma_start(out[0:full * P, :].rearrange("(t p) d -> p t d", p=P), k.x[:, 0:full, :]
                             ).then_inc(stored, 16)
                sp.dma_start(out[full * P:NODES, :], k.x[0:NODES - full * P, full, :]).then_inc(stored, 16)
                sp.wait_ge(stored, 32)




def lay_out(i):
    o = {}

    def padded(a, rows, fill=0):
        a = np.asarray(a)
        return np.concatenate([a, np.full((rows - a.shape[0],) + a.shape[1:], fill, a.dtype)])

    def lanes(a, fill=0):
        return np.ascontiguousarray(padded(a, EPAD, fill).reshape(CHUNKS, P).T)

    def halves(w):
        w = np.asarray(w)
        s = w.shape
        w = w.reshape(s[:-2] + (s[-2] // P, P, s[-1]))
        return np.ascontiguousarray(np.swapaxes(w, -3, -2))

    def row(b):
        return np.ascontiguousarray(np.asarray(b).reshape(1, -1))

    o["x_lanes"] = np.ascontiguousarray(padded(i["x"], NPAD).reshape(TILES, P, D).transpose(1, 0, 2))
    o["src_row"] = row(padded(i["src"], EPAD))
    o["src_lanes"] = lanes(i["src"])
    o["dst_lanes"] = lanes(i["dst"], NO_NODE)
    o["weight_lanes"] = lanes(i["edge_weight"])
    o["L0_gnn_w"] = halves(i["L0_gnn_w"])
    o["L0_gnn_b"] = row(i["L0_gnn_b"])

    def packed(*matrices):
        cols = []
        for w in matrices:
            w = np.asarray(w)
            w = w.reshape((-1,) + w.shape[-2:])
            rows = -(-w.shape[1] // P) * P
            w = np.concatenate([w, np.zeros((w.shape[0], rows - w.shape[1], w.shape[2]), w.dtype)], axis=1)
            cols.append(halves(w).reshape(w.shape[0], P, -1))
        return np.ascontiguousarray(np.concatenate(cols, axis=2))

    def columns(*vectors):
        cols = []
        for v in vectors:
            v = np.asarray(v)
            v = v.reshape(-1, v.shape[-1])
            n = -(-v.shape[1] // P) * P
            v = np.concatenate([v, np.zeros((v.shape[0], n - v.shape[1]), v.dtype)], axis=1)
            cols.append(v.reshape(v.shape[0], -1, P).transpose(2, 0, 1))
        return np.ascontiguousarray(np.concatenate(cols, axis=2))

    def typed(name):
        return halves(i[name]).transpose(1, 0, 2, 3)

    def by_head(relation, order):
        r = np.asarray(relation).transpose(order)
        return np.ascontiguousarray(r.reshape(KK, P, r.shape[2], r.shape[3]).transpose(1, 0, 2, 3))

    o["etype_lanes"] = lanes(i["edge_type_8"])
    o["type_lanes"] = np.ascontiguousarray(padded(i["node_type_4"], NPAD).reshape(TILES, P).T)
    o["L1_gnn_w"] = np.ascontiguousarray(np.stack([typed(f"L1_gnn_{n}_linears") for n in "kvq"], axis=1))
    o["L1_gnn_wa"] = np.ascontiguousarray(typed("L1_gnn_a_linears"))
    o["L1_gnn_att"] = by_head(i["L1_gnn_relation_att"], (1, 3, 0, 2))
    o["L1_gnn_msg"] = by_head(i["L1_gnn_relation_msg"], (1, 2, 0, 3))
    pri = np.repeat(np.asarray(i["L1_gnn_relation_pri"]).T, P // 2, axis=0)
    o["L1_gnn_pri"] = np.ascontiguousarray(pri.reshape(KK, P, -1).transpose(1, 0, 2))
    o["L1_gnn_skip"] = row(i["L1_gnn_skip"])
    o["dst_rows"] = np.ascontiguousarray(padded(i["dst"], EPAD, NO_NODE).reshape(P, CHUNKS))
    o["attr"] = np.ascontiguousarray(padded(i["edge_attr_64"], EPAD).T)
    o["L2_gnn_kvq"] = np.ascontiguousarray(np.concatenate([halves(i[f"L2_gnn_W{n}"]) for n in "kvq"], axis=2))
    o["L2_gnn_W1"] = np.asarray(i["L2_gnn_W1"])
    o["L2_gnn_W2"] = halves(i["L2_gnn_W2"])
    o["L2_gnn_b1"] = np.ascontiguousarray(np.asarray(i["L2_gnn_b1"]).reshape(KK, P).T)
    o["L2_gnn_b2"] = np.asarray(i["L2_gnn_b2"]).reshape(-1, 1)
    o["L2_gnn_Wo"], o["L2_gnn_bo"] = halves(i["L2_gnn_Wo"]), row(i["L2_gnn_bo"])
    o["L3_gnn_W"], o["L3_gnn_WT"] = halves(i["L3_gnn_W"]), halves(np.asarray(i["L3_gnn_W"]).T)
    o["L3_gnn_att"] = halves(np.stack([np.asarray(i["L3_gnn_a_src"]), np.asarray(i["L3_gnn_a_dst"])], axis=1))
    o["L3_gnn_bias"] = row(i["L3_gnn_bias"])
    o["L0_ffn_gW"], o["L0_ffn_gb"] = halves(i["L0_ffn_gW"]), row(i["L0_ffn_gb"])
    o["L0_ffn_sW"] = packed(i["L0_ffn_sW1"], i["L0_ffn_sW2"], i["L0_ffn_sW3"])
    o["L0_ffn_eW"] = packed(i["L0_ffn_eW1"], i["L0_ffn_eW2"], i["L0_ffn_eW3"])
    o["L0_ffn_sb"], o["L0_ffn_sb3"] = columns(i["L0_ffn_sb1"], i["L0_ffn_sb2"]), row(i["L0_ffn_sb3"])
    o["L0_ffn_eb"], o["L0_ffn_eb3"] = columns(i["L0_ffn_eb1"], i["L0_ffn_eb2"]), row(i["L0_ffn_eb3"])
    o["L1_ffn_gamma"], o["L1_ffn_beta"] = row(i["L1_ffn_gamma"]), row(i["L1_ffn_beta"])
    o["L1_ffn_Wr"], o["L1_ffn_br"] = halves(i["L1_ffn_Wr"]), row(i["L1_ffn_br"])
    def first_parts(w, b, *affine):
        parts = [packed(w), columns(b).transpose(1, 0, 2)]
        if affine:
            g, c = (columns(v).transpose(1, 0, 2) for v in affine)
            parts.append(np.stack([g, c], axis=3).reshape(g.shape[0], P, 2 * KK))
        return np.ascontiguousarray(np.concatenate(parts, axis=2))

    o["L1_ffn_first"] = first_parts(i["L1_ffn_W1"], i["L1_ffn_b1"])
    o["L1_ffn_second"], o["L1_ffn_b2"] = packed(i["L1_ffn_W2"]), row(i["L1_ffn_b2"])
    o["L2_ffn_Wr"], o["L2_ffn_br"] = halves(i["L2_ffn_Wr"]), row(i["L2_ffn_br"])
    o["L2_ffn_first"] = first_parts(i["L2_ffn_W1"], i["L2_ffn_b1"], i["L2_ffn_ln_g"], i["L2_ffn_ln_b"])
    o["L2_ffn_second"], o["L2_ffn_b2"] = packed(i["L2_ffn_W2"]), row(i["L2_ffn_b2"])
    o["L3_ffn_Wr"], o["L3_ffn_br"] = halves(i["L3_ffn_Wr"]), row(i["L3_ffn_br"])
    o["L3_ffn_W"] = packed(i["L3_ffn_W1"], i["L3_ffn_W2"], i["L3_ffn_Wo"])
    o["L3_ffn_bo"] = row(i["L3_ffn_bo"])
    for n in ("b", "g", "be", "m", "v"):
        o[f"L3_ffn_{n}"] = columns(i[f"L3_ffn_{n}1"], i[f"L3_ffn_{n}2"])
    return o


def kernel(**inputs):
    import concourse.bacc as bacc
    from concourse.bass_utils import run_bass_kernel_spmd as run

    nc = bacc.Bacc("TRN2", target_bir_lowering=False, num_devices=1)
    arrays = lay_out(inputs)
    a = {n: nc.dram_tensor(f"in_{n}", v.shape, mybir.dt.from_np(v.dtype), kind="ExternalInput").ap()
         for n, v in arrays.items()}
    out = nc.dram_tensor("out_x", (NODES, D), F32, kind="ExternalOutput").ap()
    program(nc, a, out)
    r = run(nc, [{f"in_{n}": v for n, v in arrays.items()}], core_ids=[0])
    return r.results[0]["out_x"]
```
